# Optimizing a Trainium2 kernel written in Bass

```python
import numpy as np
import jax
import jax.numpy as jnp

def _softmax(x, axis=-1):
    return jax.nn.softmax(x, axis=axis)

def _gelu(x):
    return jax.nn.gelu(x, approximate=True)

def _silu(x):
    return jax.nn.silu(x)

def _sigmoid(x):
    return jax.nn.sigmoid(x)

def _layernorm(x, axis=-1, eps=1e-05):
    m = jnp.mean(x, axis=axis, keepdims=True)
    v = jnp.var(x, axis=axis, keepdims=True)
    return (x - m) / jnp.sqrt(v + eps)

def _scatter_add(tgt, idx, src, axis=0):
    return tgt.at[idx].add(src)

def _segment_sum(src, seg, n):
    return jax.ops.segment_sum(src, seg, n)
kernel_name = 'mk_decoder_postln_d1_seqx_r2_b2821a'

def setup_inputs(seed: int=0):
    np.random.seed(seed)
    _w = jnp.asarray

    def _rec_inputs():
        import jax
        import jax.numpy as jnp
        _rk = jax.random.key(seed)
        x = 7.22e-05 + 1 * jax.random.normal(jax.random.fold_in(_rk, 1), (4, 1024, 512), jnp.float32)
        _lenS = 1024 - jax.random.randint(jax.random.fold_in(_rk, 7), (4,), 0, max(1, 1024 // 4) + 1, jnp.int32)
        _lenS2 = 2048 - jax.random.randint(jax.random.fold_in(_rk, 8), (4,), 0, max(1, 2048 // 4) + 1, jnp.int32)
        _ctx_768P = jax.random.normal(jax.random.fold_in(_rk, 11), (4, 16, 384), jnp.float32)
        _ctx_768c = jax.random.dirichlet(jax.random.fold_in(_rk, 511), 0.3 * jnp.ones((16,), jnp.float32), (4, 2048))
        _ctx_768t = jnp.einsum('bsk,bkd->bsd', _ctx_768c, _ctx_768P)
        _ctx_768t = _ctx_768t * jax.lax.rsqrt(jnp.mean(jnp.square(_ctx_768t)) + 1e-12) * 0.953939
        ctx_768 = 3.88148e-05 + 0.999967 * (_ctx_768t + 0.3 * jax.random.normal(jax.random.fold_in(_rk, 611), (4, 2048, 384), jnp.float32))
        _validS = jnp.arange(1024)[None, :] < _lenS[:, None]
        _validS2 = jnp.arange(2048)[None, :] < _lenS2[:, None]
        _causal = jnp.tril(jnp.ones((1024, 1024), dtype=bool))
        mask_BxS_bf1 = jnp.ones((4, 1024), dtype=bool)
        mask_BxS2_bf1 = jnp.ones((4, 2048), dtype=bool)
        return (x, ctx_768, mask_BxS_bf1, mask_BxS2_bf1)
    x, ctx_768, mask_BxS_bf1, mask_BxS2_bf1 = _rec_inputs()

    def _L0_attn_setup():
        import jax, jax.numpy as jnp
        import numpy as np
        D_MODEL = 512
        N_HEADS = 16
        HEAD_DIM = D_MODEL // N_HEADS
        WINDOW = 128
        B, S = (4, 2048)

        def _window_starts(seq_len, ws):
            stride = ws // 2
            starts = []
            for i in range(0, seq_len, stride):
                end = min(i + ws, seq_len)
                start = max(0, end - ws)
                starts.append(start)
                if end == seq_len:
                    break
            return np.asarray(starts, dtype=np.int32)
        key = jax.random.key(seed)
        ks = jax.random.split(key, 9)
        sc = 0.02
        x = jax.random.normal(ks[0], (B, S, D_MODEL), dtype=jnp.float32)
        Wq = jax.random.normal(ks[1], (D_MODEL, D_MODEL), dtype=jnp.float32) * sc
        bq = jnp.zeros((D_MODEL,), jnp.float32)
        Wk = jax.random.normal(ks[2], (D_MODEL, D_MODEL), dtype=jnp.float32) * sc
        bk = jnp.zeros((D_MODEL,), jnp.float32)
        Wv = jax.random.normal(ks[3], (D_MODEL, D_MODEL), dtype=jnp.float32) * sc
        bv = jnp.zeros((D_MODEL,), jnp.float32)
        Wo = jax.random.normal(ks[4], (D_MODEL, D_MODEL), dtype=jnp.float32) * sc
        bo = jnp.zeros((D_MODEL,), jnp.float32)
        return {'x': x, 'Wq': Wq, 'bq': bq, 'Wk': Wk, 'bk': bk, 'Wv': Wv, 'bv': bv, 'Wo': Wo, 'bo': bo}
    _L0_attn_all = _L0_attn_setup()
    _L0_attn_in = {k: v for k, v in _L0_attn_all.items() if k in ('Wq', 'bq', 'Wk', 'bk', 'Wv', 'bv', 'Wo', 'bo')}
    del _L0_attn_all

    def _L0_xattn_setup():
        import jax, jax.numpy as jnp
        import numpy as np
        B, T, DT, G, DV = (16, 256, 512, 288, 384)
        H, DH = (4, 32)
        INNER = H * DH
        HID = 4 * DT
        N_STATE = 64
        K_TOP = 32

        def layernorm(x, g, b, eps=1e-05):
            m = x.mean(-1, keepdims=True)
            v = x.var(-1, keepdims=True)
            return (x - m) * jax.lax.rsqrt(v + eps) * g + b

        def s4d(x, log_dt, A_re, A_im, C_re, C_im, D_skip):
            Bb, L, D = x.shape
            dt = jnp.exp(log_dt)
            A = A_re + 1j * A_im
            C = C_re + 1j * C_im
            dtA = dt[:, None] * A
            dC = C * (jnp.exp(dtA) - 1.0) / A
            powers = jnp.exp(dtA[:, :, None] * jnp.arange(L))
            K = 2.0 * jnp.einsum('dn,dnl->dl', dC, powers).real
            n = 2 * L
            Kf = jnp.fft.rfft(K, n=n, axis=-1)
            xf = jnp.fft.rfft(x, n=n, axis=1)
            y = jnp.fft.irfft(xf * Kf.T[None], n=n, axis=1)[:, :L]
            return y + x * D_skip
        key = jax.random.key(seed)
        ks = jax.random.split(key, 16)
        s = 0.02
        inp = {'x_text': jax.random.normal(ks[0], (B, T, DT), jnp.float32), 'x_vision': jax.random.normal(ks[1], (B, G, DV), jnp.float32), 'text_mask': jnp.ones((B, T), bool), 'vision_mask': jnp.ones((B, G), bool), 'Wq': jax.random.normal(ks[2], (DT, INNER), jnp.float32) * s, 'Wk': jax.random.normal(ks[3], (DV, INNER), jnp.float32) * s, 'Wv': jax.random.normal(ks[4], (DV, DT), jnp.float32) * s, 'W_film_in': jax.random.normal(ks[5], (DT, 2 * DT), jnp.float32) * s, 'b_film_in': jnp.zeros((2 * DT,), jnp.float32), 'W_film_out': jax.random.normal(ks[6], (DT, 2 * DT), jnp.float32) * s, 'b_film_out': jnp.zeros((2 * DT,), jnp.float32), 'g_norm_in': jnp.ones((DT,), jnp.float32), 'b_norm_in': jnp.zeros((DT,), jnp.float32), 'g_norm_out': jnp.ones((DT,), jnp.float32), 'b_norm_out': jnp.zeros((DT,), jnp.float32), 'g_ffn': jnp.ones((DT,), jnp.float32), 'b_ffn': jnp.zeros((DT,), jnp.float32), 'W1': jax.random.normal(ks[7], (DT, HID), jnp.float32) * s, 'b1': jnp.zeros((HID,), jnp.float32), 'W2': jax.random.normal(ks[8], (HID, DT), jnp.float32) * s, 'b2': jnp.zeros((DT,), jnp.float32), 'log_dt': jnp.log(0.001) + jax.random.uniform(ks[9], (DT,), jnp.float32) * (jnp.log(0.1) - jnp.log(0.001)), 'A_re': -0.5 * jnp.ones((DT, N_STATE), jnp.float32), 'A_im': jnp.tile(jnp.pi * jnp.arange(N_STATE, dtype=jnp.float32), (DT, 1)), 'C_re': jax.random.normal(ks[10], (DT, N_STATE), jnp.float32) * 0.5 ** 0.5, 'C_im': jax.random.normal(ks[11], (DT, N_STATE), jnp.float32) * 0.5 ** 0.5, 'D_skip': jax.random.normal(ks[12], (DT,), jnp.float32), 'mod_gate': jnp.array(0.5, jnp.float32)}
        return inp
    _L0_xattn_all = _L0_xattn_setup()
    _L0_xattn_in = {k: v for k, v in _L0_xattn_all.items() if k in ('Wq', 'Wk', 'Wv', 'W_film_in', 'b_film_in', 'W_film_out', 'b_film_out', 'g_norm_in', 'b_norm_in', 'g_norm_out', 'b_norm_out', 'g_ffn', 'b_ffn', 'W1', 'b1', 'W2', 'b2', 'log_dt', 'A_re', 'A_im', 'C_re', 'C_im', 'D_skip', 'mod_gate')}
    del _L0_xattn_all

    def _L0_ffn_setup():
        import jax, jax.numpy as jnp
        import numpy as np
        D_MODEL = 512
        EXPANSION = 4
        D_HIDDEN = D_MODEL * EXPANSION
        NUM_STAGES = int(np.log2(D_HIDDEN))

        def butterfly(y, weights, dim):
            lead = y.shape[:-1]
            for stage in range(weights.shape[0]):
                s = 2 ** stage
                nb = dim // (2 * s)
                yr = y.reshape(*lead, nb, 2, s)
                a = yr[..., 0, :]
                b = yr[..., 1, :]
                w = weights[stage].reshape(nb, s, 2, 2)
                na = w[..., 0, 0] * a + w[..., 0, 1] * b
                nb2 = w[..., 1, 0] * a + w[..., 1, 1] * b
                y = jnp.stack([na, nb2], axis=-2).reshape(*lead, dim)
            return y
        key = jax.random.key(seed)
        ks = jax.random.split(key, 6)
        B, S = (4, 1024)
        x = jax.random.normal(ks[0], (B, S, D_MODEL), jnp.float32)
        W_exp = jax.random.normal(ks[1], (D_MODEL, D_HIDDEN), jnp.float32) * 0.02
        b_exp = jnp.zeros((D_HIDDEN,), jnp.float32)
        up_weights = jax.random.normal(ks[2], (NUM_STAGES, D_HIDDEN // 2, 2, 2), jnp.float32) * 0.02
        up_bias = jnp.zeros((D_HIDDEN,), jnp.float32)
        down_weights = jax.random.normal(ks[3], (NUM_STAGES, D_HIDDEN // 2, 2, 2), jnp.float32) * 0.02
        W_con = jax.random.normal(ks[4], (D_HIDDEN, D_MODEL), jnp.float32) * 0.02
        b_con = jnp.zeros((D_MODEL,), jnp.float32)
        down_bias = jnp.zeros((D_MODEL,), jnp.float32)
        return dict(x=x, W_exp=W_exp, b_exp=b_exp, up_weights=up_weights, up_bias=up_bias, down_weights=down_weights, W_con=W_con, b_con=b_con, down_bias=down_bias)
    _L0_ffn_all = _L0_ffn_setup()
    _L0_ffn_in = {k: v for k, v in _L0_ffn_all.items() if k in ('W_exp', 'b_exp', 'up_weights', 'up_bias', 'down_weights', 'W_con', 'b_con', 'down_bias')}
    del _L0_ffn_all
    return {'x': x, 'ctx_768': ctx_768, 'mask_BxS_bf1': mask_BxS_bf1, 'mask_BxS2_bf1': mask_BxS2_bf1, 'L0_attn_Wq': _L0_attn_in['Wq'], 'L0_attn_bq': _L0_attn_in['bq'], 'L0_attn_Wk': _L0_attn_in['Wk'], 'L0_attn_bk': _L0_attn_in['bk'], 'L0_attn_Wv': _L0_attn_in['Wv'], 'L0_attn_bv': _L0_attn_in['bv'], 'L0_attn_Wo': _L0_attn_in['Wo'], 'L0_attn_bo': _L0_attn_in['bo'], 'L0_xattn_Wq': _L0_xattn_in['Wq'], 'L0_xattn_Wk': _L0_xattn_in['Wk'], 'L0_xattn_Wv': _L0_xattn_in['Wv'], 'L0_xattn_W_film_in': _L0_xattn_in['W_film_in'], 'L0_xattn_b_film_in': _L0_xattn_in['b_film_in'], 'L0_xattn_W_film_out': _L0_xattn_in['W_film_out'], 'L0_xattn_b_film_out': _L0_xattn_in['b_film_out'], 'L0_xattn_g_norm_in': _L0_xattn_in['g_norm_in'], 'L0_xattn_b_norm_in': _L0_xattn_in['b_norm_in'], 'L0_xattn_g_norm_out': _L0_xattn_in['g_norm_out'], 'L0_xattn_b_norm_out': _L0_xattn_in['b_norm_out'], 'L0_xattn_g_ffn': _L0_xattn_in['g_ffn'], 'L0_xattn_b_ffn': _L0_xattn_in['b_ffn'], 'L0_xattn_W1': _L0_xattn_in['W1'], 'L0_xattn_b1': _L0_xattn_in['b1'], 'L0_xattn_W2': _L0_xattn_in['W2'], 'L0_xattn_b2': _L0_xattn_in['b2'], 'L0_xattn_log_dt': _L0_xattn_in['log_dt'], 'L0_xattn_A_re': _L0_xattn_in['A_re'], 'L0_xattn_A_im': _L0_xattn_in['A_im'], 'L0_xattn_C_re': _L0_xattn_in['C_re'], 'L0_xattn_C_im': _L0_xattn_in['C_im'], 'L0_xattn_D_skip': _L0_xattn_in['D_skip'], 'L0_xattn_mod_gate': _L0_xattn_in['mod_gate'], 'L0_ffn_W_exp': _L0_ffn_in['W_exp'], 'L0_ffn_b_exp': _L0_ffn_in['b_exp'], 'L0_ffn_up_weights': _L0_ffn_in['up_weights'], 'L0_ffn_up_bias': _L0_ffn_in['up_bias'], 'L0_ffn_down_weights': _L0_ffn_in['down_weights'], 'L0_ffn_W_con': _L0_ffn_in['W_con'], 'L0_ffn_b_con': _L0_ffn_in['b_con'], 'L0_ffn_down_bias': _L0_ffn_in['down_bias']}

def reference(x, ctx_768, mask_BxS_bf1, mask_BxS2_bf1, L0_attn_Wq, L0_attn_bq, L0_attn_Wk, L0_attn_bk, L0_attn_Wv, L0_attn_bv, L0_attn_Wo, L0_attn_bo, L0_xattn_Wq, L0_xattn_Wk, L0_xattn_Wv, L0_xattn_W_film_in, L0_xattn_b_film_in, L0_xattn_W_film_out, L0_xattn_b_film_out, L0_xattn_g_norm_in, L0_xattn_b_norm_in, L0_xattn_g_norm_out, L0_xattn_b_norm_out, L0_xattn_g_ffn, L0_xattn_b_ffn, L0_xattn_W1, L0_xattn_b1, L0_xattn_W2, L0_xattn_b2, L0_xattn_log_dt, L0_xattn_A_re, L0_xattn_A_im, L0_xattn_C_re, L0_xattn_C_im, L0_xattn_D_skip, L0_xattn_mod_gate, L0_ffn_W_exp, L0_ffn_b_exp, L0_ffn_up_weights, L0_ffn_up_bias, L0_ffn_down_weights, L0_ffn_W_con, L0_ffn_b_con, L0_ffn_down_bias):
    import jax
    import jax.numpy as jnp

    def _L0_attn_ref(x, Wq, bq, Wk, bk, Wv, bv, Wo, bo):
        import jax, jax.numpy as jnp
        import numpy as np
        D_MODEL = 512
        N_HEADS = 16
        HEAD_DIM = D_MODEL // N_HEADS
        WINDOW = 128
        B, S = (4, 2048)

        def _window_starts(seq_len, ws):
            stride = ws // 2
            starts = []
            for i in range(0, seq_len, stride):
                end = min(i + ws, seq_len)
                start = max(0, end - ws)
                starts.append(start)
                if end == seq_len:
                    break
            return np.asarray(starts, dtype=np.int32)
        Bsz, seq, dm = x.shape
        q = x @ Wq + bq
        k = x @ Wk + bk
        v = x @ Wv + bv
        starts = _window_starts(seq, WINDOW)
        idx = starts[:, None] + np.arange(WINDOW)[None]
        idx_j = jnp.asarray(idx)
        qw = q[:, idx_j, :]
        kw = k[:, idx_j, :]
        vw = v[:, idx_j, :]
        scale = 1.0 / np.sqrt(HEAD_DIM).astype(np.float32)
        scores = jnp.einsum('bwid,bwjd->bwij', qw, kw) * scale
        attn = jax.nn.softmax(scores, axis=-1)
        ow = jnp.einsum('bwij,bwjd->bwid', attn, vw)
        flat_idx = idx_j.reshape(-1)
        out = jnp.zeros_like(q).at[:, flat_idx, :].add(ow.reshape(Bsz, -1, dm))
        counts = jnp.zeros((seq,), jnp.float32).at[flat_idx].add(1.0)
        out = out / counts[None, :, None]
        return out @ Wo + bo

    def _L0_xattn_ref(x_text, x_vision, text_mask, vision_mask, Wq, Wk, Wv, W_film_in, b_film_in, W_film_out, b_film_out, g_norm_in, b_norm_in, g_norm_out, b_norm_out, g_ffn, b_ffn, W1, b1, W2, b2, log_dt, A_re, A_im, C_re, C_im, D_skip, mod_gate):
        import jax, jax.numpy as jnp
        import numpy as np
        B, T, DT, G, DV = (16, 256, 512, 288, 384)
        H, DH = (4, 32)
        INNER = H * DH
        HID = 4 * DT
        N_STATE = 64
        K_TOP = 32

        def layernorm(x, g, b, eps=1e-05):
            m = x.mean(-1, keepdims=True)
            v = x.var(-1, keepdims=True)
            return (x - m) * jax.lax.rsqrt(v + eps) * g + b

        def s4d(x, log_dt, A_re, A_im, C_re, C_im, D_skip):
            Bb, L, D = x.shape
            dt = jnp.exp(log_dt)
            A = A_re + 1j * A_im
            C = C_re + 1j * C_im
            dtA = dt[:, None] * A
            dC = C * (jnp.exp(dtA) - 1.0) / A
            powers = jnp.exp(dtA[:, :, None] * jnp.arange(L))
            K = 2.0 * jnp.einsum('dn,dnl->dl', dC, powers).real
            n = 2 * L
            Kf = jnp.fft.rfft(K, n=n, axis=-1)
            xf = jnp.fft.rfft(x, n=n, axis=1)
            y = jnp.fft.irfft(xf * Kf.T[None], n=n, axis=1)[:, :L]
            return y + x * D_skip
        Bb, Tt, D = x_text.shape
        Gg = x_vision.shape[1]
        Q = (x_text @ Wq).reshape(Bb, Tt, H, DH)
        K = (x_vision @ Wk).reshape(Bb, Gg, H, DH)
        scores = jnp.einsum('bthd,bghd->bhtg', Q, K) / np.sqrt(DH).astype(np.float32)
        scores = jnp.where(vision_mask[:, None, None, :], scores, -jnp.inf)
        topv, topi = jax.lax.top_k(scores, K_TOP)
        probs = jax.nn.softmax(topv, axis=-1)
        bi = jnp.arange(Bb)[:, None, None, None]
        hi = jnp.arange(H)[None, :, None, None]
        ti = jnp.arange(Tt)[None, None, :, None]
        attn = jnp.zeros_like(scores).at[bi, hi, ti, topi].set(probs)
        attn_mean = attn.mean(axis=1)
        V = x_vision @ Wv
        c_t = jnp.einsum('btg,bgd->btd', attn_mean, V)
        c_t = c_t * text_mask[..., None]
        x = layernorm(x_text, g_norm_in, b_norm_in)
        scale_in, shift_in = jnp.split(c_t @ W_film_in + b_film_in, 2, axis=-1)
        x = x * (1.0 + mod_gate * scale_in) + mod_gate * shift_in
        y = s4d(x, log_dt, A_re, A_im, C_re, C_im, D_skip)
        scale_out, shift_out = jnp.split(c_t @ W_film_out + b_film_out, 2, axis=-1)
        y = y * (1.0 + mod_gate * scale_out) + mod_gate * shift_out
        xt = x_text + y
        h = layernorm(xt, g_ffn, b_ffn)
        h = jax.nn.gelu(h @ W1 + b1, approximate=False) @ W2 + b2
        xt = xt + h
        return layernorm(xt, g_norm_out, b_norm_out)

    def _L0_ffn_ref(x, W_exp, b_exp, up_weights, up_bias, down_weights, W_con, b_con, down_bias):
        import jax, jax.numpy as jnp
        import numpy as np
        D_MODEL = 512
        EXPANSION = 4
        D_HIDDEN = D_MODEL * EXPANSION
        NUM_STAGES = int(np.log2(D_HIDDEN))

        def butterfly(y, weights, dim):
            lead = y.shape[:-1]
            for stage in range(weights.shape[0]):
                s = 2 ** stage
                nb = dim // (2 * s)
                yr = y.reshape(*lead, nb, 2, s)
                a = yr[..., 0, :]
                b = yr[..., 1, :]
                w = weights[stage].reshape(nb, s, 2, 2)
                na = w[..., 0, 0] * a + w[..., 0, 1] * b
                nb2 = w[..., 1, 0] * a + w[..., 1, 1] * b
                y = jnp.stack([na, nb2], axis=-2).reshape(*lead, dim)
            return y
        h = jnp.einsum('bsd,dh->bsh', x, W_exp) + b_exp
        h = butterfly(h, up_weights, D_HIDDEN)
        h = jax.nn.gelu(h + up_bias, approximate=False)
        h = butterfly(h, down_weights, D_HIDDEN)
        y = jnp.einsum('bsh,hd->bsd', h, W_con) + b_con
        return y + down_bias
    x = _layernorm(x + _L0_attn_ref(x, L0_attn_Wq, L0_attn_bq, L0_attn_Wk, L0_attn_bk, L0_attn_Wv, L0_attn_bv, L0_attn_Wo, L0_attn_bo), axis=-1)
    x = _layernorm(x + _L0_xattn_ref(x, ctx_768, mask_BxS_bf1, mask_BxS2_bf1, L0_xattn_Wq, L0_xattn_Wk, L0_xattn_Wv, L0_xattn_W_film_in, L0_xattn_b_film_in, L0_xattn_W_film_out, L0_xattn_b_film_out, L0_xattn_g_norm_in, L0_xattn_b_norm_in, L0_xattn_g_norm_out, L0_xattn_b_norm_out, L0_xattn_g_ffn, L0_xattn_b_ffn, L0_xattn_W1, L0_xattn_b1, L0_xattn_W2, L0_xattn_b2, L0_xattn_log_dt, L0_xattn_A_re, L0_xattn_A_im, L0_xattn_C_re, L0_xattn_C_im, L0_xattn_D_skip, L0_xattn_mod_gate), axis=-1)
    x = _layernorm(x + _L0_ffn_ref(x, L0_ffn_W_exp, L0_ffn_b_exp, L0_ffn_up_weights, L0_ffn_up_bias, L0_ffn_down_weights, L0_ffn_W_con, L0_ffn_b_con, L0_ffn_down_bias), axis=-1)
    return x

_drawn_inputs = setup_inputs


def setup_inputs(seed=0):
    import zlib

    import numpy as np

    out = dict(_drawn_inputs(seed))
    spreads = {'L0_attn_bq': (0.0, 0.8),
     'L0_attn_bk': (0.0, 0.8),
     'L0_attn_bv': (0.0, 0.1),
     'L0_attn_bo': (0.0, 0.1),
     'L0_xattn_b_film_in': (0.0, 0.1),
     'L0_xattn_b_film_out': (0.0, 0.284),
     'L0_xattn_g_norm_in': (1.0, 0.2),
     'L0_xattn_b_norm_in': (0.0, 0.1),
     'L0_xattn_g_norm_out': (1.0, 0.2),
     'L0_xattn_b_norm_out': (0.0, 0.1),
     'L0_xattn_g_ffn': (1.0, 0.6),
     'L0_xattn_b_ffn': (0.0, 0.8),
     'L0_xattn_b1': (0.0, 0.523),
     'L0_xattn_b2': (0.0, 0.285),
     'L0_xattn_A_re': (-0.5, 0.2),
     'L0_ffn_b_exp': (0.0, 0.1),
     'L0_ffn_up_bias': (0.0, 0.1),
     'L0_ffn_b_con': (0.0, 0.1),
     'L0_ffn_down_bias': (0.0, 0.1)}
    factors = {'L0_attn_Wq': 3.396, 'L0_attn_Wk': 3.341}
    for name, (base, spread) in spreads.items():
        noise = np.random.default_rng([zlib.crc32(name.encode()), seed]).standard_normal(out[name].shape)
        drawn = base * np.exp(spread * noise) if base else spread * noise
        out[name] = jnp.asarray(drawn.astype(out[name].dtype))
    for name, factor in factors.items():
        out[name] = (out[name] * factor).astype(out[name].dtype)
    return out
```

```python
import math
from contextlib import ExitStack

import numpy as np

import concourse.bass as bass
from concourse import mybir

F32 = mybir.dt.float32
F32R = mybir.dt.float32r
BF16 = mybir.dt.bfloat16
U8 = mybir.dt.uint8
ALU = mybir.AluOpType
ACT = mybir.ActivationFunctionType
AX = mybir.AxisListType

P = 128
B, S, D = 4, 1024, 512
DC = D // P
TILES = B * S // P
TPB = S // P
S2, DV = 2048, 384
VC = DV // P
GC = S2 // P
HEADS, DH = 4, 32
HID = 2048
HC = HID // P
TOPK = 32
NST = 64
EPS = 1e-5
SCALE = 1.0 / math.sqrt(32.0)
BIG = 1.0e30
TAKEN = -3.0e38


class Stage:

    def __init__(self, nc, ctx, name):
        self.nc, self.ctx, self.name, self.sems = nc, ctx, name, []

    def sb(self, name, shape, dt=F32):
        return self.ctx.enter_context(self.nc.sbuf_tensor(f"{self.name}_{name}", shape, dt))

    def psum(self, name, shape, dt=F32):
        return self.ctx.enter_context(self.nc.psum_tensor(f"{self.name}_{name}", shape, dt))

    def sem(self, name):
        self.sems.append(self.ctx.enter_context(self.nc.semaphore(f"{self.name}_{name}")))
        return self.sems[-1]

    def clear(self):
        with self.nc.Block() as block:
            @block.gpsimd
            def _(pool):
                for s in self.sems:
                    pool.sem_clear(s)


def rows(ap, start, n):
    return ap[bass.ds(start, n)]


def mm3(pe, out, w_hi, w_lo, m_hi, m_lo, start, stop):
    pe.matmul(out, w_hi, m_lo, start=start, stop=False)
    pe.matmul(out, w_lo, m_hi, start=False, stop=False)
    return pe.matmul(out, w_hi, m_hi, start=False, stop=stop)



def stage_taps(nc, A, tap_rows, taps_out):
    R = 32
    ROUND = 12582912.0
    LEVELS = 10
    TURN_1 = 6.28125
    TURN_2 = 0.0019350051879882812
    TURN_3 = 2.0 * math.pi - TURN_1 - TURN_2
    G = 16
    with ExitStack() as ctx:
        st = Stage(nc, ctx, "tp")
        sb, psum, sem = st.sb, st.psum, st.sem
        ident = sb("ident", [P, P])
        ldt = sb("ldt", [P, 1])
        dsk = sb("dsk", [P, 1])
        par = sb("par", [P, 4, NST])
        dt = sb("dt", [P, 3])
        dt_bits = sb("dt_bits", [P, 1], mybir.dt.int32)
        z = sb("z", [P, 6, LEVELS, NST])
        z_bits = sb("z_bits", [P, LEVELS, NST], mybir.dt.int32)
        lam = sb("lam", [P, LEVELS // 2, 2, NST])
        big = sb("big", [P, 5, 2, NST])
        w = sb("w", [P, 12, NST])
        ones = sb("ones", [P, NST])
        tab = [sb(f"tab{i}", [P, R, 2, NST]) for i in range(2)]
        tmp = [sb(f"tmp{i}", [P, 2, R // 2, NST]) for i in range(2)]
        tabT = [sb(f"tabT{i}", [P, R, P]) for i in range(2)]
        krow = sb("krow", [R, P, R])
        kd = sb("kd", [P, S])
        kT = sb("kT", [P, 2, P])
        ps_t = psum("ps_t", [P, 2, 4, P])
        ps_k = psum("ps_k", [R, 2, G, R])
        ps_o = psum("ps_o", [P, 2, 512])

        s_id = sem("identity")
        s_ld = sem("loaded")
        s_pow = sem("powers")
        s_tab = [sem(f"table{i}") for i in range(2)]
        s_tr = sem("transposed")
        s_trc = sem("transposed_copied")
        s_k = sem("taps_summed")
        s_kc = sem("taps_copied")
        s_kr = sem("tap_rows_stored")
        s_kd = sem("taps_loaded")
        s_skip = sem("skip_added")
        s_o = sem("taps_turned")
        s_oc = sem("taps_turned_copied")
        s_st = [sem(f"stored{k}") for k in range(2)]

        def grow(eng, table, t, power, n):
            for k in range(n.bit_length() - 1):
                m = 2 ** k
                re, im = table[:, 0:m, 0, :], table[:, 0:m, 1, :]
                pr = power[:, k:k + 1, 0, :].broadcast_to([P, m, NST])
                pi = power[:, k:k + 1, 1, :].broadcast_to([P, m, NST])
                for part, (x, y, op) in enumerate(((pr, pi, ALU.subtract), (pi, pr, ALU.add))):
                    eng.tensor_tensor(t[:, 0, 0:m, :], re, x, ALU.mult)
                    eng.tensor_tensor(t[:, 1, 0:m, :], im, y, ALU.mult)
                    eng.drain()
                    eng.tensor_tensor(table[:, m:2 * m, part, :], t[:, 0, 0:m, :], t[:, 1, 0:m, :], op)
                    eng.drain()

        with nc.Block() as block:

            @block.sync
            def _(sp):
                with sp.Fori(0, DC) as c:
                    sp.wait_ge(s_skip, c)
                    sp.wait_ge(s_tab[1], c)
                    sp.dma_start(ldt[:, :], rows(A["L0_xattn_log_dt"].rearrange("(n o) -> n o", o=1), c * P, P)).then_inc(s_ld, 16)
                    sp.dma_start(dsk[:, :], rows(A["L0_xattn_D_skip"].rearrange("(n o) -> n o", o=1), c * P, P)).then_inc(s_ld, 16)
                    for i, name in enumerate(("A_re", "A_im", "C_re", "C_im")):
                        sp.dma_start(par[:, i, :], rows(A["L0_xattn_" + name], c * P, P)).then_inc(s_ld, 16)
                    sp.wait_ge(s_kc, (P // G) * (c + 1))
                    sp.dma_start(rows(tap_rows, c * P, P).rearrange("d (a r) -> a d r", r=R), krow[:, :, :]).then_inc(s_kr, 16)
                    sp.wait_ge(s_kr, 16 * (c + 1))
                    sp.dma_start(kd[:, :], rows(tap_rows, c * P, P)).then_inc(s_kd, 16)
                    for n in range(S // P):
                        sp.wait_ge(s_oc, (S // P) * c + n + 1)
                        sp.dma_start(taps_out[n * P:(n + 1) * P, bass.ds(c * P, P)], kT[:, n % 2, :]).then_inc(s_st[n % 2], 16)
                for k in range(2):
                    sp.wait_ge(s_st[k], 16 * DC * (S // P) // 2)

            @block.gpsimd
            def _(pool):
                pool.memset(ident[:, :], 0.0)
                pool.memset(ones[:, :], 1.0)
                pool.drain()
                pool.affine_select(out=ident[:, :], in_=ident[:, :], compare_op=ALU.not_equal, fill=1.0,
                                   base=0, pattern=[[-1, P]], channel_multiplier=1)
                pool.drain().then_inc(s_id, 1)
                with pool.Fori(0, DC) as c:
                    pool.wait_ge(s_pow, c + 1)
                    pool.wait_ge(s_trc, 16 * c)
                    pool.tensor_tensor(tab[1][:, 0, 0, :], w[:, 10, :], ones[:, :], ALU.mult)
                    pool.tensor_tensor(tab[1][:, 0, 1, :], w[:, 11, :], ones[:, :], ALU.mult)
                    pool.drain()
                    grow(pool, tab[1], tmp[1], big, R)
                    pool.drain().then_inc(s_tab[1], 1)

            @block.tensor
            def _(pe):
                pe.wait_ge(s_id, 1)
                with pe.Fori(0, DC) as c:
                    for i in range(2):
                        pe.wait_ge(s_tab[i], c + 1)
                        for g in range(8):
                            n = 8 * i + g
                            pe.wait_ge(s_trc, 16 * c + (n - 1 if n >= 1 else 0))
                            for q in range(4):
                                last = pe.transpose(ps_t[:, n % 2, q, :], tab[i][:, 4 * g + q, :, :].rearrange("p a n -> p (a n)"), ident[:, :])
                            last.then_inc(s_tr, 1)
                    pe.wait_ge(s_trc, 16 * (c + 1))
                    for g in range(P // G):
                        pe.wait_ge(s_kc, (P // G) * c + (g - 1 if g >= 1 else 0))
                        for q in range(G):
                            d = g * G + q
                            last = pe.matmul(ps_k[:, g % 2, q, :], tabT[1][:, :, d], tabT[0][:, :, d], start=True, stop=True)
                        last.then_inc(s_k, 1)
                    pe.wait_ge(s_skip, c + 1)
                    pe.wait_ge(s_kd, 16 * (c + 1))
                    for n in range(S // P):
                        pe.wait_ge(s_oc, (S // P) * c + (n - 1 if n >= 1 else 0))
                        pe.transpose(ps_o[:, n % 2, 0:P], kd[:, n * P:(n + 1) * P], ident[:, :]).then_inc(s_o, 1)

            @block.scalar
            def _(act):
                with act.Fori(0, DC) as c:
                    for n in range(16):
                        act.wait_ge(s_tr, 16 * c + n + 1)
                        i, g = n // 8, n % 8
                        act.activation(tabT[i][:, 4 * g:4 * g + 4, :], ps_t[:, n % 2, :, :], ACT.Copy).then_inc(s_trc, 1)
                    act.wait_ge(s_kr, 16 * c)
                    for g in range(P // G):
                        act.wait_ge(s_k, (P // G) * c + g + 1)
                        act.activation(krow[:, g * G:(g + 1) * G, :], ps_k[:, g % 2, :, :], ACT.Copy).then_inc(s_kc, 1)
                    for n in range(S // P):
                        act.wait_ge(s_o, (S // P) * c + n + 1)
                        act.wait_ge(s_st[n % 2], 16 * ((S // P // 2) * c + n // 2))
                        act.activation(kT[:, n % 2, :], ps_o[:, n % 2, 0:P], ACT.Copy).then_inc(s_oc, 1)

            @block.vector
            def _(dve):
                def tt(out, a, b, op):
                    dve.tensor_tensor(out, a, b, op)
                    dve.drain()

                def mul(out, a, x):
                    dve.tensor_scalar(out, a, x, None, ALU.mult)
                    dve.drain()

                def horner(p, v, coefs):
                    mul(p, v, coefs[0])
                    for coef in coefs[1:]:
                        dve.scalar_tensor_tensor(out=p, in0=p, scalar=coef, in1=v, op0=ALU.add, op1=ALU.mult)
                        dve.drain()

                def less_multiples(x, q, inv, parts):
                    dve.tensor_scalar(q, x, inv, ROUND, ALU.mult, ALU.add)
                    dve.drain()
                    dve.tensor_scalar(q, q, -ROUND, None, ALU.add)
                    dve.drain()
                    for part in parts:
                        dve.scalar_tensor_tensor(out=x, in0=q, scalar=-part, in1=x, op0=ALU.mult, op1=ALU.add)
                        dve.drain()

                def exp(x, q, qi, p):
                    dve.tensor_scalar(x, x, -87.0, 88.0, ALU.max, ALU.min)
                    dve.drain()
                    less_multiples(x, q, 1.0 / math.log(2.0), (0.693359375, math.log(2.0) - 0.693359375))
                    horner(p, x, [1.0 / math.factorial(n) for n in range(8, 0, -1)])
                    dve.tensor_scalar(q, q, 127.0, float(2 ** 23), ALU.add, ALU.mult)
                    dve.drain()
                    dve.tensor_copy(qi, q)
                    dve.drain()
                    dve.scalar_tensor_tensor(out=p, in0=p, scalar=1.0, in1=qi.bitcast(F32), op0=ALU.add, op1=ALU.mult)
                    dve.drain()

                with dve.Fori(0, DC) as c:
                    dve.wait_ge(s_ld, 16 * 6 * (c + 1))
                    W = [w[:, i, :] for i in range(12)]
                    are, aim, cre, cim = (par[:, i, :] for i in range(4))
                    dve.tensor_copy(dt[:, 1:2], ldt[:, :])
                    dve.drain()
                    exp(dt[:, 1:2], dt[:, 2:3], dt_bits[:, :], dt[:, 0:1])
                    for k in range(LEVELS):
                        dve.tensor_scalar(z[:, 0, k, :], are, dt[:, 0:1], float(2 ** k), ALU.mult, ALU.mult)
                        dve.tensor_scalar(z[:, 1, k, :], aim, dt[:, 0:1], float(2 ** k), ALU.mult, ALU.mult)
                    dve.drain()
                    X, Y, Q, V, SI, CO = (z[:, i, :, :] for i in range(6))
                    exp(X, Q, z_bits[:, :, :], V)
                    dve.tensor_copy(X, V)
                    dve.drain()
                    less_multiples(Y, Q, 1.0 / (2.0 * math.pi), (TURN_1, TURN_2, TURN_3))
                    mul(Y, Y, 0.25)
                    tt(V, Y, Y, ALU.mult)
                    horner(SI, V, [(-1.0) ** n / math.factorial(2 * n + 1) for n in range(4, 0, -1)])
                    dve.scalar_tensor_tensor(out=SI, in0=SI, scalar=1.0, in1=Y, op0=ALU.add, op1=ALU.mult)
                    horner(CO, V, [(-1.0) ** n / math.factorial(2 * n) for n in range(5, 0, -1)])
                    dve.tensor_scalar(CO, CO, 1.0, None, ALU.add)
                    dve.drain()
                    for _ in range(2):
                        tt(V, SI, SI, ALU.mult)
                        dve.scalar_tensor_tensor(out=SI, in0=SI, scalar=2.0, in1=CO, op0=ALU.mult, op1=ALU.mult)
                        dve.drain()
                        dve.tensor_scalar(CO, V, -2.0, 1.0, ALU.mult, ALU.add)
                        dve.drain()
                    half = LEVELS // 2
                    tt(lam[:, :, 0, :], X[:, 0:half], CO[:, 0:half], ALU.mult)
                    tt(lam[:, :, 1, :], X[:, 0:half], SI[:, 0:half], ALU.mult)
                    tt(big[:, :, 0, :], X[:, half:], CO[:, half:], ALU.mult)
                    dve.scalar_tensor_tensor(out=big[:, :, 1, :], in0=X[:, half:], scalar=-1.0, in1=SI[:, half:],
                                             op0=ALU.mult, op1=ALU.mult)
                    dve.drain()
                    dve.tensor_scalar(W[2], lam[:, 0, 0, :], -1.0, None, ALU.add)
                    dve.drain()
                    li = lam[:, 0, 1, :]
                    tt(W[5], cre, W[2], ALU.mult)
                    tt(W[6], cim, li, ALU.mult)
                    tt(W[7], W[5], W[6], ALU.subtract)
                    tt(W[5], cre, li, ALU.mult)
                    tt(W[6], cim, W[2], ALU.mult)
                    tt(W[8], W[5], W[6], ALU.add)
                    tt(W[5], are, are, ALU.mult)
                    tt(W[6], aim, aim, ALU.mult)
                    tt(W[9], W[5], W[6], ALU.add)
                    dve.reciprocal(W[9], W[9])
                    dve.drain()
                    mul(W[9], W[9], 2.0)
                    tt(W[5], W[7], are, ALU.mult)
                    tt(W[6], W[8], aim, ALU.mult)
                    tt(W[5], W[5], W[6], ALU.add)
                    tt(W[10], W[5], W[9], ALU.mult)
                    tt(W[5], W[7], aim, ALU.mult)
                    tt(W[6], W[8], are, ALU.mult)
                    tt(W[5], W[5], W[6], ALU.subtract)
                    tt(W[11], W[5], W[9], ALU.mult)
                    dve.drain().then_inc(s_pow, 1)
                    dve.wait_ge(s_trc, 16 * c)
                    dve.memset(tab[0][:, 0, 0, :], 1.0)
                    dve.memset(tab[0][:, 0, 1, :], 0.0)
                    dve.drain()
                    grow(dve, tab[0], tmp[0], lam, R)
                    dve.drain().then_inc(s_tab[0], 1)
                    dve.wait_ge(s_kd, 16 * (c + 1))
                    dve.tensor_tensor(kd[:, 0:1], kd[:, 0:1], dsk[:, :], ALU.add).then_inc(s_skip, 1)
        st.clear()



def stage_butterfly(nc, A, w3_out, b3_out, w4_out):
    LOW = 7
    TOP = 4
    PAIRS = HID // 2
    with ExitStack() as ctx:
        st = Stage(nc, ctx, "bf")
        sb, psum, sem = st.sb, st.psum, st.sem
        ident = sb("ident", [P, P])
        e_up = sb("e_up", [P, 2, HID])
        e_dn = sb("e_dn", [P, 2, HID])
        w_up = sb("w_up", [P, PAIRS, 4])
        w_dn = sb("w_dn", [P, PAIRS, 4])
        tmp_up = sb("tmp_up", [P, 2, PAIRS])
        tmp_dn = sb("tmp_dn", [P, 2, PAIRS])
        col_up = sb("col_up", [P, TOP, HC // 2, 4])
        col_dn = sb("col_dn", [P, TOP, HC // 2, 4])
        wx = sb("wx", [P, HID])
        wT = sb("wT", [P, HC, D + 2])
        pair_tmp = sb("pair_tmp", [P, 2, 2, D + 2])
        upb = sb("upb", [P, HC])
        eT = sb("eT", [P, 4, P])
        out_t = sb("out_t", [P, 2, D])
        ps = psum("ps", [P, 2, 512])
        ps_b = psum("ps_b", [P, HC])
        wc = wT

        s_id = sem("identity")
        s_wu = sem("up_stage_weights")
        s_wd = sem("down_stage_weights")
        s_cols = sem("columns_loaded")
        s_wx = sem("w_exp_loaded")
        s_up = sem("up_matrix_stage")
        s_dn = sem("down_matrix_stage")
        s_tr = sem("transposed")
        s_trc = sem("transposed_copied")
        s_mm = sem("block_product")
        s_mmc = sem("block_product_copied")
        s_hi = sem("across_blocks")
        s_r = sem("rows_transposed")
        s_rc = sem("rows_copied")
        s_wc = sem("w_con_loaded")
        s_dhi = sem("down_across_blocks")
        s_eT = sem("down_matrix_transposed")
        s_eTc = sem("down_matrix_transposed_copied")
        s_d = sem("down_product")
        s_dc = sem("down_product_copied")
        s_out = [sem(f"stored{k}") for k in range(2)]
        s_b3 = sem("bias_stored")

        def low_stage(eng, e, w, tmp, s):
            width = 2 ** s
            src = e[:, s % 2, :].rearrange("p (n two s) -> p two n s", two=2, s=width)
            dst = e[:, 1 - s % 2, :].rearrange("p (n two s) -> p two n s", two=2, s=width)
            wv = w[:, :, :].rearrange("p (n s) f -> p f n s", s=width)
            t = [tmp[:, i, :].rearrange("p (n s) -> p n s", s=width) for i in range(2)]
            for o in range(2):
                eng.tensor_tensor(t[0], src[:, 0], wv[:, 2 * o], ALU.mult)
                eng.tensor_tensor(t[1], src[:, 1], wv[:, 2 * o + 1], ALU.mult)
                eng.drain()
                last = eng.tensor_tensor(dst[:, o], t[0], t[1], ALU.add)
                eng.drain()
            return last

        def block_pairs(s):
            w = 2 ** s
            return [(q // w * 2 * w + q % w, q // w * 2 * w + q % w + w) for q in range(HC // 2)]

        def across(eng, x, col, s, width, transposed):
            a10, a01 = (1, 2) if transposed else (2, 1)
            for q, (a, b) in enumerate(block_pairs(s)):
                ta, tb = pair_tmp[:, q % 2, 0, 0:width], pair_tmp[:, q % 2, 1, 0:width]
                xa, xb = x[:, a, 0:width], x[:, b, 0:width]
                eng.tensor_scalar(ta, xa, col[:, s, q, 0:1], None, ALU.mult)
                eng.tensor_scalar(tb, xa, col[:, s, q, a10:a10 + 1], None, ALU.mult)
                eng.drain()
                eng.scalar_tensor_tensor(out=xa, in0=xb, scalar=col[:, s, q, a01:a01 + 1], in1=ta, op0=ALU.mult, op1=ALU.add)
                eng.drain()
                eng.scalar_tensor_tensor(out=xb, in0=xb, scalar=col[:, s, q, 3:4], in1=tb, op0=ALU.mult, op1=ALU.add)
            eng.drain()

        with nc.Block() as block:

            @block.sync
            def _(sp):
                for s in range(LOW):
                    if s >= 1:
                        sp.wait_ge(s_up, s)
                    sp.dma_start(w_up[:, :, :], A["L0_ffn_up_weights"][s:s + 1].rearrange("o k i j -> o k (i j)").broadcast_to([P, PAIRS, 4]))\
                      .then_inc(s_wu, 16)
                    if s == 0:
                        for v, name in ((col_up, "L0_ffn_up_weights"), (col_dn, "L0_ffn_down_weights")):
                            for k in range(TOP):
                                sp.dma_start(v[:, k, :, :], A[name][LOW + k].rearrange("(q p) i j -> p q (i j)", p=P)).then_inc(s_cols, 16)
                        sp.dma_start(wT[:, :, D:D + 1], A["L0_ffn_b_exp"].rearrange("(c p o) -> p c o", p=P, o=1), allow_slow_non_contiguous=True).then_inc(s_cols, 16)
                        sp.dma_start(upb[:, :], A["L0_ffn_up_bias"].rearrange("(c p) -> p c", p=P), allow_slow_non_contiguous=True)\
                          .then_inc(s_cols, 16)
                for c in range(DC):
                    if c >= 1:
                        sp.wait_ge(s_tr, 4 * c)
                    sp.dma_start(wx[:, :], A["L0_ffn_W_exp"][c * P:(c + 1) * P, :]).then_inc(s_wx, 16)
                for n in range(4 * DC):
                    sp.wait_ge(s_rc, n + 1)
                    c, g = n // 4, n % 4
                    sp.dma_start(w3_out[c * P:(c + 1) * P, g * 512:(g + 1) * 512], out_t[:, n % 2, :]).then_inc(s_out[n % 2], 16)
                sp.dma_start(wc[:, :, 0:D], A["L0_ffn_W_con"].rearrange("(c p) n -> p c n", p=P)).then_inc(s_wc, 16)
                for n in range(HC):
                    sp.wait_ge(s_dc, n + 1)
                    sp.dma_start(w4_out[n * P:(n + 1) * P, :], out_t[:, n % 2, :]).then_inc(s_out[n % 2], 16)
                for k in range(2):
                    sp.wait_ge(s_out[k], 16 * (4 * DC + HC) // 2)

            @block.gpsimd
            def _(pool):
                pool.memset(ident[:, :], 0.0)
                pool.drain()
                pool.affine_select(out=ident[:, :], in_=ident[:, :], compare_op=ALU.not_equal, fill=1.0,
                                   base=0, pattern=[[-1, P]], channel_multiplier=1)
                pool.drain().then_inc(s_id, 1)
                for c in range(HC):
                    pool.tensor_copy(e_dn[:, 0, c * P:(c + 1) * P], ident[:, :])
                pool.drain()
                for s in range(LOW):
                    pool.wait_ge(s_wd, 16 * (s + 1))
                    low_stage(pool, e_dn, w_dn, tmp_dn, s)
                    pool.drain().then_inc(s_dn, 1)

            @block.tensor
            def _(pe):
                pe.wait_ge(s_id, 1)
                for c in range(DC):
                    pe.wait_ge(s_wx, 16 * (c + 1))
                    for g in range(4):
                        n = 4 * c + g
                        if n >= 2:
                            pe.wait_ge(s_trc, n - 1)
                        for q in range(4):
                            h = 4 * g + q
                            last = pe.transpose(ps[:, n % 2, q * P:(q + 1) * P], wx[:, h * P:(h + 1) * P], ident[:, :])
                        last.then_inc(s_tr, 1)
                pe.wait_ge(s_trc, 16)
                pe.wait_ge(s_cols, 16 * 10)
                pe.wait_ge(s_up, LOW)
                for h in range(HC):
                    if h >= 2:
                        pe.wait_ge(s_mmc, h - 1)
                    blk = e_up[:, LOW % 2, h * P:(h + 1) * P]
                    pe.matmul(ps_b[:, h:h + 1], blk, wT[:, h, D:D + 1], start=True, stop=True)
                    pe.matmul(ps[:, h % 2, :], blk, wT[:, h, 0:D], start=True, stop=True).then_inc(s_mm, 1)
                pe.wait_ge(s_hi, 1)
                for c in range(DC):
                    for g in range(4):
                        n = 4 * c + g
                        if n >= 2:
                            pe.wait_ge(s_rc, n - 1)
                        for q in range(4):
                            h = 4 * g + q
                            last = pe.transpose(ps[:, n % 2, q * P:(q + 1) * P], wT[:, h, c * P:(c + 1) * P], ident[:, :])
                        last.then_inc(s_r, 1)
                pe.wait_ge(s_rc, 16)
                pe.wait_ge(s_dn, LOW)
                pe.wait_ge(s_dhi, 1)
                for h in range(HC):
                    if h >= 1:
                        pe.wait_ge(s_dc, h)
                    pe.transpose(ps[:, 0, 0:P], e_dn[:, LOW % 2, h * P:(h + 1) * P], ident[:, :]).then_inc(s_eT, 1)
                    pe.wait_ge(s_eTc, h + 1)
                    pe.matmul(ps[:, 1, :], eT[:, 0, :], wc[:, h, 0:D], start=True, stop=True).then_inc(s_d, 1)

            @block.scalar
            def _(act):
                for s in range(LOW):
                    if s >= 1:
                        act.wait_ge(s_dn, s)
                    act.dma_start(w_dn[:, :, :], A["L0_ffn_down_weights"][s:s + 1].rearrange("o k i j -> o k (i j)").broadcast_to([P, PAIRS, 4]))\
                       .then_inc(s_wd, 16)
                    if s == 0:
                        for n in range(16):
                            act.wait_ge(s_tr, n + 1)
                            c, g = n // 4, n % 4
                            act.activation(wT[:, 4 * g:4 * g + 4, c * P:(c + 1) * P], ps[:, n % 2, :].rearrange("p (q t) -> p q t", q=4),
                                           ACT.Copy).then_inc(s_trc, 1)
                for h in range(HC):
                    act.wait_ge(s_mm, h + 1)
                    act.activation(wT[:, h, 0:D], ps[:, h % 2, :], ACT.Copy).then_inc(s_mmc, 1)
                for n in range(16):
                    act.wait_ge(s_r, n + 1)
                    if n >= 2:
                        act.wait_ge(s_out[n % 2], 16 * (n // 2))
                    act.activation(out_t[:, n % 2, :], ps[:, n % 2, :], ACT.Copy).then_inc(s_rc, 1)
                for h in range(HC):
                    act.wait_ge(s_eT, h + 1)
                    act.activation(eT[:, 0, :], ps[:, 0, 0:P], ACT.Copy).then_inc(s_eTc, 1)
                    act.wait_ge(s_d, h + 1)
                    act.wait_ge(s_out[h % 2], 16 * (8 + h // 2))
                    act.activation(out_t[:, h % 2, :], ps[:, 1, :], ACT.Copy).then_inc(s_dc, 1)
                act.wait_ge(s_hi, 1)
                act.dma_start(b3_out.rearrange("(c p) -> p c", p=P), upb[:, :], allow_slow_non_contiguous=True).then_inc(s_b3, 16)
                act.wait_ge(s_b3, 16)

            @block.vector
            def _(dve):
                dve.wait_ge(s_id, 1)
                for c in range(HC):
                    dve.tensor_copy(e_up[:, 0, c * P:(c + 1) * P], ident[:, :])
                dve.drain()
                for s in range(LOW):
                    dve.wait_ge(s_wu, 16 * (s + 1))
                    low_stage(dve, e_up, w_up, tmp_up, s)
                    dve.drain().then_inc(s_up, 1)
                dve.wait_ge(s_mmc, HC)
                dve.tensor_copy(wT[:, :, D:D + 1], ps_b[:, :].rearrange("p (h o) -> p h o", o=1))
                dve.drain()
                for s in range(TOP):
                    across(dve, wT, col_up, s, D + 1, False)
                dve.tensor_tensor(upb[:, :], upb[:, :], wT[:, :, D], ALU.add)
                dve.drain().then_inc(s_hi, 1)
                dve.wait_ge(s_wc, 16)
                for s in reversed(range(TOP)):
                    across(dve, wc, col_dn, s, D, True)
                dve.drain().then_inc(s_dhi, 1)
        st.clear()


def stage_attention(nc, A, x1_out, qt_out):
    with ExitStack() as ctx:
        st = Stage(nc, ctx, "at")
        sb, psum, sem = st.sb, st.psum, st.sem
        ident = sb("ident", [P, P])
        ones = sb("ones", [P, P])
        wq = sb("wq", [P, DC, D])
        wk = sb("wk", [P, DC, D])
        wv = sb("wv", [P, DC, D])
        wo = sb("wo", [P, DC, D])
        wxq = sb("wxq", [P, DC, P])
        bq = sb("bq", [P, DC])
        bk = sb("bk", [P, DC])
        bv = sb("bv", [P, DC])
        bvw = sb("bvw", [P, DC, P])
        bo = sb("bo", [P, D])
        wqT = sb("wqT", [P, DC, D])
        wkT = sb("wkT", [P, DC, D])
        wvT = sb("wvT", [P, DC, D])
        m_qk = sb("m_qk", [P, DC, D])
        w_vo = sb("w_vo", [P, DC, D])
        u_k = sb("u_k", [P, DC])
        u_q = sb("u_q", [P, DC])
        bqk = sb("bqk", [P, 1])
        b_row = sb("b_row", [P, D])
        w_own = sb("w_own", [P, TPB])
        w_oth = sb("w_oth", [P, TPB])
        neghalf = sb("neghalf", [P, 1])
        xk = sb("xk", [P, 2, 2, D])
        xq = sb("xq", [P, 2, D])
        xT = sb("xT", [P, 2, DC, 2 * P])
        tT = sb("tT", [P, DC, P])
        crow = sb("crow", [P, 2, 1])
        sc = sb("sc", [P, 2, 2 * P])
        mx = sb("mx", [P, 2, 2])
        p1 = sb("p1", [P, P])
        p2 = sb("p2", [P, P])
        den = sb("den", [P, 2, 2])
        rec = sb("rec", [P, 2])
        att = sb("att", [P, 2 * P])
        attT = sb("attT", [P, 2, P])
        oT = sb("oT", [P, DC, P])
        res = sb("res", [P, D])
        stats = sb("stats", [P, 6])
        mv = sb("mv", [P, 2])
        rstd = sb("rstd", [P, 1])
        x1 = sb("x1", [P, 2, D])
        x1T = sb("x1T", [P, DC, P])
        qhl = sb("qhl", [P, 2, 2, P], F32R)

        ps_x = psum("ps_x", [P, 2, 2 * 2 * P])
        ps_t = psum("ps_t", [P, DC, P])
        ps_s = psum("ps_s", [P, 2 * P])
        ps_c = psum("ps_c", [P, D])
        ps_a = psum("ps_a", [P, 4, P])
        ps_o = psum("ps_o", [P, DC, P])
        ps_y = psum("ps_y", [P, D])

        s_w = sem("weights_loaded")
        s_const = sem("constants")
        s_wT = sem("weight_transposes")
        s_wTc = sem("weight_transposes_copied")
        s_fold = sem("folded")
        s_foldc = sem("folded_copied")
        s_bvw = sem("bv_widened")
        s_x = [sem(f"x_loaded{k}") for k in range(2)]
        s_xT = sem("x_transposed")
        s_xTc = sem("x_transposed_copied")
        s_t = sem("t_done")
        s_tc = sem("t_copied")
        s_s = sem("scores_done")
        s_crow = sem("score_bias")
        s_sc = sem("scores_copied")
        s_mx = sem("max_done")
        s_p = sem("probs_done")
        s_v = sem("vector_chain")
        s_att = sem("attention_done")
        s_aT = sem("attention_transposed")
        s_aTc = sem("attention_transposed_copied")
        s_o = sem("mix_done")
        s_oc = sem("mix_copied")
        s_y = sem("projected")
        s_var = sem("variance")
        s_rstd = sem("rstd")
        s_x1 = sem("x1_done")
        s_x1T = sem("x1_transposed")
        s_x1Tc = sem("x1_transposed_copied")
        s_q = sem("q_done")
        s_qh = sem("q_hi")
        s_ql = sem("q_lo")
        s_st = [sem(f"x1_stored{k}") for k in range(2)]
        s_sq = [sem(f"q_stored{k}") for k in range(2)]
        x_flat = A["x"].rearrange("b s d -> (b s) d")

        with nc.Block() as block:

            @block.sync
            def _(sp):
                for w, name in ((wq, "L0_attn_Wq"), (wk, "L0_attn_Wk"), (wv, "L0_attn_Wv"), (wo, "L0_attn_Wo")):
                    sp.dma_start(w[:, :, :], A[name].rearrange("(c p) n -> p c n", p=P)).then_inc(s_w, 16)
                sp.dma_start(wxq[:, :, :], A["L0_xattn_Wq"].rearrange("(c p) n -> p c n", p=P)).then_inc(s_w, 16)
                for v, name in ((bq, "L0_attn_bq"), (bk, "L0_attn_bk"), (bv, "L0_attn_bv")):
                    sp.dma_start(v[:, :], A[name].rearrange("(c p) -> p c", p=P), allow_slow_non_contiguous=True).then_inc(s_w, 16)
                sp.dma_start(bo[:, :], A["L0_attn_bo"].rearrange("(o n) -> o n", o=1).broadcast_to([P, D])).then_inc(s_w, 16)
                with sp.Fori(0, B) as b:
                    for j in range(TPB):
                        k = j % 2
                        t0 = b * S + j * P
                        if j >= 2:
                            sp.wait_ge(s_o, b * TPB + (j - 1))
                            sp.wait_ge(s_x1, b * TPB + (j - 1))
                        else:
                            sp.wait_ge(s_o, b * TPB)
                            sp.wait_ge(s_x1, b * TPB)
                        lo = t0 - 64 if j > 0 else t0
                        hi = t0 + P if j < TPB - 1 else t0 + P - 64
                        sp.dma_start(xk[0:64, k, 0, :], rows(x_flat, lo, 64)).then_inc(s_x[k], 16)
                        sp.dma_start(xk[64:128, k, 0, :], rows(x_flat, t0, 64)).then_inc(s_x[k], 16)
                        sp.dma_start(xk[0:64, k, 1, :], rows(x_flat, t0 + 64, 64)).then_inc(s_x[k], 16)
                        sp.dma_start(xk[64:128, k, 1, :], rows(x_flat, hi, 64)).then_inc(s_x[k], 16)
                        sp.dma_start(xq[:, k, :], rows(x_flat, t0, P)).then_inc(s_x[k], 16)

            @block.gpsimd
            def _(pool):
                pool.memset(ident[:, :], 0.0).then_inc(s_const, 1)
                pool.memset(ones[:, :], 1.0).then_inc(s_const, 1)
                pool.memset(neghalf[:, :], -0.5).then_inc(s_const, 1)
                pool.memset(att[:, :], 0.0).then_inc(s_const, 1)
                pool.wait_ge(s_const, 4)
                pool.affine_select(out=ident[:, :], in_=ident[:, :], compare_op=ALU.not_equal, fill=1.0,
                                   base=0, pattern=[[-1, P]], channel_multiplier=1).then_inc(s_const, 1)
                with pool.Fori(0, B) as b:
                    for j in range(TPB):
                        pool.wait_ge(s_var, b * TPB + j + 1)
                        pool.tensor_tensor(rstd[:, :], mv[:, 1:2], neghalf[:, :], ALU.pow).then_inc(s_rstd, 1)

            @block.tensor
            def _(pe):
                pe.wait_ge(s_const, 5)
                pe.wait_ge(s_w, 16 * 9)
                n = 0
                for w in (wq, wk, wv):
                    for c in range(DC):
                        if n >= 2:
                            pe.wait_ge(s_wTc, n - 1)
                        for e in range(DC):
                            last = pe.transpose(ps_x[:, n % 2, e * P:(e + 1) * P], w[:, c, e * P:(e + 1) * P], ident[:, :])
                        last.then_inc(s_wT, 1)
                        n += 1
                pe.wait_ge(s_wTc, 3 * DC)
                n = 0
                for wT, mv_ in ((wqT, wkT), (wvT, wo)):
                    for c in range(DC):
                        if n >= 2:
                            pe.wait_ge(s_foldc, n - 1)
                        for e in range(DC):
                            last = pe.matmul(ps_x[:, n % 2, :], wT[:, e, c * P:(c + 1) * P], mv_[:, e, :],
                                             start=(e == 0), stop=(e == DC - 1))
                        last.then_inc(s_fold, 1)
                        n += 1
                pe.wait_ge(s_bvw, 1)
                for i, (wT, v) in enumerate(((wkT, bq), (wqT, bk))):
                    for c in range(DC):
                        for e in range(DC):
                            pe.matmul(ps_c[:, i * DC + c:i * DC + c + 1], wT[:, e, c * P:(c + 1) * P], v[:, e:e + 1],
                                      start=(e == 0), stop=(e == DC - 1))
                for e in range(DC):
                    pe.matmul(ps_s[:, 0:1], oT[:, e, :], bk[:, e:e + 1], start=(e == 0), stop=(e == DC - 1))
                for e in range(DC):
                    last = pe.matmul(ps_y[:, :], bvw[:, e, :], wo[:, e, :], start=(e == 0), stop=(e == DC - 1))
                last.then_inc(s_fold, 1)
                pe.wait_ge(s_foldc, 2 * DC + 1)

                with pe.Fori(0, B) as b:
                    for j in range(TPB):
                        k, i = j % 2, b * TPB + j
                        pe.wait_ge(s_x[k], 80 * (b * (TPB // 2) + j // 2 + 1))
                        pe.wait_ge(s_xTc, i)
                        for c in range(DC):
                            for h in range(2):
                                last = pe.transpose(ps_x[:, c // 2, (c % 2) * 2 * P + h * P:(c % 2) * 2 * P + (h + 1) * P],
                                                    xk[:, k, h, c * P:(c + 1) * P], ident[:, :])
                        last.then_inc(s_xT, 1)
                        pe.wait_ge(s_xTc, i + 1)
                        pe.wait_ge(s_x1Tc, i)
                        for m in range(DC):
                            for c in range(DC):
                                pe.matmul(ps_t[:, m, :], m_qk[:, c, m * P:(m + 1) * P], xT[:, k, c, 64:64 + P],
                                          start=(c == 0), stop=(c == DC - 1))
                        for c in range(DC):
                            last = pe.matmul(ps_c[:, 0:1], xT[:, k, c, 64:64 + P], u_q[:, c:c + 1],
                                             start=(c == 0), stop=(c == DC - 1))
                        last.then_inc(s_t, 1)
                        pe.wait_ge(s_tc, i + 1)
                        for c in range(DC):
                            last = pe.matmul(ps_s[:, :], tT[:, c, :], xT[:, k, c, :], start=(c == 0), stop=(c == DC - 1))
                        last.then_inc(s_s, 1)
                        pe.wait_ge(s_att, i + 1)
                        for h in range(2):
                            last = pe.transpose(ps_a[:, h, :], att[:, h * P:(h + 1) * P], ident[:, :])
                        last.then_inc(s_aT, 1)
                        pe.wait_ge(s_aTc, i + 1)
                        for c in range(DC):
                            for h in range(2):
                                last = pe.matmul(ps_o[:, c, :], xk[:, k, h, c * P:(c + 1) * P], attT[:, h, :],
                                                 start=(h == 0), stop=(h == 1))
                        last.then_inc(s_o, 1)
                        pe.wait_ge(s_oc, i + 1)
                        for c in range(DC):
                            last = pe.matmul(ps_y[:, :], oT[:, c, :], w_vo[:, c, :], start=(c == 0), stop=(c == DC - 1))
                        last.then_inc(s_y, 1)
                        pe.wait_ge(s_x1, i + 1)
                        for c in range(DC):
                            last = pe.transpose(ps_t[:, c, :], x1[:, k, c * P:(c + 1) * P], ident[:, :])
                        last.then_inc(s_x1T, 1)
                        pe.wait_ge(s_x1Tc, i + 1)
                        pe.wait_ge(s_ql, i)
                        for c in range(DC):
                            last = pe.matmul(ps_c[:, P:2 * P], wxq[:, c, :], x1T[:, c, :], start=(c == 0), stop=(c == DC - 1))
                        last.then_inc(s_q, 1)

            @block.scalar
            def _(act):
                n = 0
                for wT in (wqT, wkT, wvT):
                    for c in range(DC):
                        act.wait_ge(s_wT, n + 1)
                        act.activation(wT[:, :, c * P:(c + 1) * P], ps_x[:, n % 2, :].rearrange("p (e q) -> p e q", e=DC),
                                       ACT.Copy).then_inc(s_wTc, 1)
                        n += 1
                n = 0
                for w in (m_qk, w_vo):
                    for c in range(DC):
                        act.wait_ge(s_fold, n + 1)
                        act.activation(w[:, c, :], ps_x[:, n % 2, :], ACT.Copy).then_inc(s_foldc, 1)
                        n += 1
                with act.Fori(0, B) as b:
                    for j in range(TPB):
                        k, i = j % 2, b * TPB + j
                        act.wait_ge(s_xT, i + 1)
                        for h in range(2):
                            act.activation(xT[:, k, 2 * h:2 * h + 2, :], ps_x[:, h, :].rearrange("p (c q) -> p c q", c=2),
                                           ACT.Copy)
                        act.drain().then_inc(s_xTc, 1)
                        act.wait_ge(s_s, i + 1)
                        act.wait_ge(s_crow, i + 1)
                        act.activation(sc[:, k, :], ps_s[:, :], ACT.Identity, bias=crow[:, k, :], scale=SCALE).then_inc(s_sc, 1)
                        act.wait_ge(s_mx, i + 1)
                        act.activation(p1[:, :], sc[:, k, 64:64 + P], ACT.Exp, bias=mx[:, k, 0:1], accum_out=den[:, k, 0:1])
                        act.activation(p2[0:64, :], sc[0:64, k, 0:P], ACT.Exp, bias=mx[0:64, k, 1:2], accum_out=den[0:64, k, 1:2])
                        act.activation(p2[64:128, :], sc[64:128, k, P:2 * P], ACT.Exp, bias=mx[64:128, k, 1:2],
                                       accum_out=den[64:128, k, 1:2]).then_inc(s_p, 1)
                        act.wait_ge(s_aT, i + 1)
                        act.activation(attT[:, :, :], ps_a[:, 0:2, :], ACT.Copy).then_inc(s_aTc, 1)
                        act.wait_ge(s_o, i + 1)
                        act.activation(oT[:, :, :], ps_o[:, :, :], ACT.Copy).then_inc(s_oc, 1)
                        act.wait_ge(s_x1T, i + 1)
                        act.activation(x1T[:, :, :], ps_t[:, :, :], ACT.Copy).then_inc(s_x1Tc, 1)
                        act.wait_ge(s_q, i + 1)
                        act.wait_ge(s_sq[k], 32 * (b * (TPB // 2) + j // 2))
                        act.activation(qhl[:, k, 0, :], ps_c[:, P:2 * P], ACT.Copy).then_inc(s_qh, 1)
                        act.dma_start(rows(x1_out, i * P, P), x1[:, k, :]).then_inc(s_st[k], 16)
                        act.wait_ge(s_ql, i + 1)
                        for hl in range(2):
                            act.dma_start(qt_out[hl, :, bass.ds(i * P, P)], qhl[:, k, hl, :].bitcast(F32)).then_inc(s_sq[k], 16)
                for k in range(2):
                    act.wait_ge(s_st[k], 16 * TILES // 2)
                    act.wait_ge(s_sq[k], 32 * TILES // 2)

            @block.vector
            def _(dve):
                dve.wait_ge(s_const, 5)
                dve.wait_ge(s_w, 16 * 9)
                for w in (w_own, w_oth):
                    dve.memset(w[:, :], 0.5)
                dve.drain()
                for w, val in ((w_own, 1.0), (w_oth, 0.0)):
                    dve.memset(w[0:64, 0:1], val)
                    dve.memset(w[64:128, TPB - 1:TPB], val)
                for c in range(DC):
                    dve.tensor_scalar(bvw[:, c, :], ones[:, :], bv[:, c:c + 1], None, ALU.mult)
                    last = dve.tensor_scalar(oT[:, c, :], ones[:, :], bq[:, c:c + 1], None, ALU.mult)
                last.then_inc(s_bvw, 1)
                dve.wait_ge(s_fold, 2 * DC + 1)
                dve.tensor_copy(u_k[:, :], ps_c[:, 0:DC])
                dve.tensor_copy(u_q[:, :], ps_c[:, DC:2 * DC])
                dve.tensor_copy(bqk[:, :], ps_s[:, 0:1])
                dve.tensor_tensor(b_row[:, :], ps_y[:, :], bo[:, :], ALU.add).then_inc(s_foldc, 1)
                with dve.Fori(0, B) as b:
                    for j in range(TPB):
                        k, i = j % 2, b * TPB + j
                        v = b * (5 * TPB) + 5 * j
                        dve.wait_ge(s_t, i + 1)
                        for m in range(DC):
                            dve.tensor_scalar(tT[:, m, :], ps_t[:, m, :], u_k[:, m:m + 1], None, ALU.add)
                        dve.tensor_scalar(crow[:, k, :], ps_c[:, 0:1], bqk[:, 0:1], SCALE, ALU.add, ALU.mult).then_inc(s_crow, 1)
                        dve.drain().then_inc(s_tc, 1)
                        dve.wait_ge(s_sc, i + 1)
                        dve.tensor_reduce(mx[:, k, 0:1], sc[:, k, 64:64 + P], AX.X, ALU.max, negate=True)
                        dve.tensor_reduce(mx[0:64, k, 1:2], sc[0:64, k, 0:P], AX.X, ALU.max, negate=True)
                        dve.tensor_reduce(mx[64:128, k, 1:2], sc[64:128, k, P:2 * P], AX.X, ALU.max, negate=True)
                        dve.drain().then_inc(s_mx, 1)
                        dve.wait_ge(s_p, i + 1)
                        dve.reciprocal(rec[:, :], den[:, k, :]).then_inc(s_v, 1)
                        dve.wait_ge(s_v, v + 1)
                        dve.tensor_tensor(rec[:, 0:1], rec[:, 0:1], w_own[:, j:j + 1], ALU.mult)
                        dve.tensor_tensor(rec[:, 1:2], rec[:, 1:2], w_oth[:, j:j + 1], ALU.mult).then_inc(s_v, 1)
                        dve.wait_ge(s_v, v + 2)
                        dve.tensor_scalar(att[:, 64:64 + P], p1[:, :], rec[:, 0:1], None, ALU.mult).then_inc(s_v, 1)
                        dve.tensor_scalar(att[0:64, 0:64], p2[0:64, 0:64], rec[0:64, 1:2], None, ALU.mult)
                        dve.tensor_scalar(att[64:128, 192:256], p2[64:128, 64:128], rec[64:128, 1:2], None, ALU.mult)
                        dve.wait_ge(s_v, v + 3)
                        dve.scalar_tensor_tensor(out=att[0:64, 64:128], in0=p2[0:64, 64:128], scalar=rec[0:64, 1:2],
                                                 in1=att[0:64, 64:128], op0=ALU.mult, op1=ALU.add)
                        dve.scalar_tensor_tensor(out=att[64:128, 128:192], in0=p2[64:128, 0:64], scalar=rec[64:128, 1:2],
                                                 in1=att[64:128, 128:192], op0=ALU.mult, op1=ALU.add)
                        dve.drain().then_inc(s_att, 1)
                        dve.wait_ge(s_y, i + 1)
                        dve.tensor_tensor(res[:, :], ps_y[:, :], xq[:, k, :], ALU.add).then_inc(s_v, 1)
                        dve.wait_ge(s_v, v + 4)
                        dve.tensor_tensor(res[:, :], res[:, :], b_row[:, :], ALU.add).then_inc(s_v, 1)
                        dve.wait_ge(s_v, v + 5)
                        dve.bn_stats(stats[:, :], res[:, :])
                        dve.drain()
                        dve.bn_aggr(mv[:, :], stats[:, :])
                        dve.drain()
                        dve.tensor_scalar(mv[:, 1:2], mv[:, 1:2], EPS, None, ALU.add).then_inc(s_var, 1)
                        dve.wait_ge(s_rstd, i + 1)
                        dve.wait_ge(s_st[k], 16 * (b * (TPB // 2) + j // 2))
                        dve.tensor_scalar(x1[:, k, :], res[:, :], mv[:, 0:1], rstd[:, 0:1], ALU.subtract, ALU.mult)\
                           .then_inc(s_x1, 1)
                        dve.wait_ge(s_qh, i + 1)
                        dve.tensor_tensor(qhl[:, k, 1, :], ps_c[:, P:2 * P], qhl[:, k, 0, :].bitcast(F32), ALU.subtract)\
                           .then_inc(s_ql, 1)
        st.clear()



def stage_cross(nc, A, qt_in, kt_tmp, ac_out):
    SEGS = 32
    SEG = S2 // SEGS
    NCAND = 8 * SEGS
    HT = HEADS * TPB
    with ExitStack() as ctx:
        st = Stage(nc, ctx, "xa")
        sb, psum, sem = st.sb, st.psum, st.sem
        ident = sb("ident", [P, P])
        wk = sb("wk", [P, VC, P])
        raw = sb("raw", [P, 2, 4, DV])
        cT = sb("cT", [P, VC, 4 * P])
        ctx_hl = sb("ctx_hl", [P, 2, GC, DV], F32R)
        khl = sb("khl", [P, 2, 4 * P], F32R)
        ks = sb("ks", [P, HEADS, S2], F32R)
        qs = sb("qs", [P, 2, HEADS, P], F32R)
        row0 = sb("row0", [P, P], BF16)
        mask_u8 = sb("mask_u8", [1, S2], U8)
        mask = sb("mask", [P, S2], BF16)
        ones = sb("ones", [P, 1])
        s_buf = sb("s_buf", [P, 2, S2])
        cand = sb("cand", [P, NCAND])
        cand_b = sb("cand_b", [P, NCAND])
        top = sb("top", [P, 2, TOPK])
        f_junk = sb("f_junk", [P, NCAND + SEGS])
        f_acc = sb("f_acc", [P, 2])
        flag = sb("flag", [P, 2, 1])
        flag_i = sb("flag_i", [1, 2], mybir.dt.int32)
        nmax = sb("nmax", [P, 2, 1])
        e_top = sb("e_top", [P, TOPK])
        den = sb("den", [P, 2, 1])
        lden = sb("lden", [P, 1])
        pbias = sb("pbias", [P, 1])
        prob = sb("prob", [P, S2])
        sel = sb("sel", [P, 2, S2])
        acc = sb("acc", [P, S2])
        aT = sb("aT", [P, 2, GC, P], F32R)
        ac = sb("ac", [P, 2, DV])

        ps_s = psum("ps_s", [P, 4, 512])
        ps_t = psum("ps_t", [P, 2, 4, P])
        ps_ac = psum("ps_ac", [P, DV])
        ps_f = psum("ps_f", [1, 2])

        s_const = sem("constants")
        s_ld = sem("weights_loaded")
        s_ms = sem("mask_loaded")
        s_mask = sem("mask_ready")
        s_raw = [sem(f"raw_loaded{k}") for k in range(2)]
        s_chi = sem("ctx_hi")
        s_clo = sem("ctx_lo")
        s_cT = sem("ctx_transposed")
        s_cTc = sem("ctx_transposed_copied")
        s_k = sem("k_done")
        s_khi = sem("k_hi")
        s_klo = sem("k_lo")
        s_kst = sem("k_stored")
        s_ks = sem("k_stacked")
        s_qs = [sem(f"q_stacked{k}") for k in range(2)]
        s_s = sem("scores_done")
        s_sc = sem("scores_copied")
        s_cand = sem("row_flags_done")
        s_f = sem("flag_summed")
        s_chk = sem("tops_final")
        s_prob = sem("prob_done")
        s_sel = sem("selected")
        s_acc = sem("heads_summed")
        s_aT = sem("attn_transposed")
        s_aTh = sem("attn_hi")
        s_aTl = sem("attn_lo")
        s_ac = sem("mix_done")
        s_acc_c = sem("mix_copied")
        s_st = [sem(f"mix_stored{k}") for k in range(2)]

        with nc.Block() as block:

            @block.sync
            def _(sp):
                sp.dma_start(wk[:, :, :], A["L0_xattn_Wk"].rearrange("(c p) n -> p c n", p=P)).then_inc(s_ld, 16)
                with sp.Fori(0, B) as b:
                    for g in range(4):
                        sp.wait_ge(s_klo, 4 * b + g + 1)
                        sp.dma_start(kt_tmp[:, :, g * 512:(g + 1) * 512].rearrange("h p g -> p h g"),
                                     khl[:, :, :].bitcast(F32)).then_inc(s_kst, 16)
                    sp.wait_ge(s_kst, 64 * (b + 1))
                    for q in range(4):
                        sp.dma_start(ks[32 * q:32 * q + 32, :, :].bitcast(F32),
                                     kt_tmp[q % 2].rearrange("(h e) g -> e h g", e=DH)).then_inc(s_ks, 16)
                    with sp.Fori(0, TPB // 2) as j:
                        for k in range(2):
                            t = b * TPB + 2 * j + k
                            sp.wait_ge(s_ac, b * TPB + 2 * j)
                            for q in range(4):
                                sp.dma_start(qs[32 * q:32 * q + 32, k, :, :].bitcast(F32),
                                             qt_in[q // 2].rearrange("(h e) t -> e h t", e=DH)[:, :, bass.ds(t * P, P)]
                                             ).then_inc(s_qs[k], 16)

            @block.gpsimd
            def _(pool):
                pool.memset(ident[:, :], 0.0).then_inc(s_const, 1)
                pool.memset(ones[:, :], 1.0).then_inc(s_const, 1)
                pool.wait_ge(s_const, 2)
                pool.affine_select(out=ident[:, :], in_=ident[:, :], compare_op=ALU.not_equal, fill=1.0,
                                   base=0, pattern=[[-1, P]], channel_multiplier=1).then_inc(s_const, 1)
                with pool.Fori(0, TILES) as t:
                    pool.wait_ge(s_aT, 4 * t)
                    pool.wait_ge(s_sel, t * HEADS + 2)
                    pool.tensor_tensor(acc[:, :], sel[:, 0, :], sel[:, 1, :], ALU.add).then_inc(s_acc, 2)
                    for h in range(2, HEADS):
                        pool.wait_ge(s_sel, t * HEADS + h + 1)
                        pool.wait_ge(s_acc, t * HEADS + h)
                        pool.tensor_tensor(acc[:, :], acc[:, :], sel[:, h % 2, :], ALU.add).then_inc(s_acc, 1)

            @block.tensor
            def _(pe):
                pe.wait_ge(s_const, 3)
                pe.wait_ge(s_ld, 16)

                def scores(b, t, k, h):
                    n = t * HEADS + h
                    pe.wait_ge(s_sc, n)
                    for c in range(4):
                        pe.matmul(ps_s[:, c, :], qs[:, k, h, :], ks[:, h, c * 512:(c + 1) * 512], start=True, stop=False)
                        last = pe.matmul(ps_s[:, c, :], row0[:, :], mask[:, c * 512:(c + 1) * 512], start=False, stop=True)
                    last.then_inc(s_s, 1)

                def sum_flag(n, k):
                    pe.wait_ge(s_cand, n + 1)
                    pe.matmul(ps_f[:, k:k + 1], flag[:, k, :], ones[:, :], start=True, stop=True).then_inc(s_f, 1)

                def mix(t, k):
                    pe.wait_ge(s_acc, (t + 1) * HEADS)
                    for g in range(4):
                        pe.wait_ge(s_aTl, t * 4 + g - 1) if g >= 1 else pe.wait_ge(s_aTl, t * 4)
                        for q in range(4):
                            c = 4 * g + q
                            last = pe.transpose(ps_t[:, g % 2, q, :], acc[:, c * P:(c + 1) * P], ident[:, :])
                        last.then_inc(s_aT, 1)
                    pe.wait_ge(s_acc_c, t)
                    for g in range(4):
                        pe.wait_ge(s_aTl, t * 4 + g + 1)
                        for q in range(4):
                            c = 4 * g + q
                            last = mm3(pe, ps_ac[:, :], aT[:, 0, c, :], aT[:, 1, c, :],
                                       ctx_hl[:, 0, c, :], ctx_hl[:, 1, c, :], start=(c == 0), stop=(c == GC - 1))
                    last.then_inc(s_ac, 1)

                with pe.Fori(0, B) as b:
                    for g in range(4):
                        pe.wait_ge(s_raw[g % 2], 16 * (2 * b + g // 2 + 1))
                        for c in range(VC):
                            n = 3 * g + c
                            pe.wait_ge(s_cTc, 12 * b + (n - 1 if n >= 1 else 0))
                            for q in range(4):
                                last = pe.transpose(ps_t[:, n % 2, q, :], raw[:, g % 2, q, c * P:(c + 1) * P], ident[:, :])
                            last.then_inc(s_cT, 1)
                        pe.wait_ge(s_cTc, 12 * b + 3 * g + 3)
                        pe.wait_ge(s_klo, 4 * b + g)
                        for c in range(VC):
                            last = pe.matmul(ps_s[:, 0, :], wk[:, c, :], cT[:, c, :], start=(c == 0), stop=(c == VC - 1))
                        last.then_inc(s_k, 1)
                    with pe.Fori(0, TPB // 2) as j:
                        for k in range(2):
                            t = b * TPB + 2 * j + k
                            pe.wait_ge(s_ks, 64 * (b + 1))
                            pe.wait_ge(s_mask, b + 1)
                            pe.wait_ge(s_qs[k], 64 * (b * (TPB // 2) + j + 1))
                            for h in range(HEADS):
                                scores(b, t, k, h)
                                sum_flag(t * HEADS + h, h % 2)
                            mix(t, k)

            @block.scalar
            def _(act):
                def load(b, g):
                    act.wait_ge(s_clo, 4 * b + g - 1 if g >= 2 else 4 * b)
                    act.wait_ge(s_cT, 12 * b + 3 * (g - 1) if g >= 2 else 12 * b)
                    act.dma_start(raw[:, g % 2, :, :],
                                  rows(A["ctx_768"], b, 1)[:, g * 512:(g + 1) * 512, :].rearrange("o (n p) v -> p (o n) v", p=P)
                                  ).then_inc(s_raw[g % 2], 16)

                with act.Fori(0, B) as b:
                    act.wait_ge(s_s, b * HT)
                    act.dma_start(mask_u8[:, :], rows(A["mask_BxS2_bf1"], b, 1)).then_inc(s_ms, 16)
                    load(b, 0)
                    load(b, 1)
                    for g in range(4):
                        act.wait_ge(s_raw[g % 2], 16 * (2 * b + g // 2 + 1))
                        act.wait_ge(s_ac, b * TPB)
                        act.activation(ctx_hl[:, 0, 4 * g:4 * g + 4, :], raw[:, g % 2, :, :], ACT.Copy).then_inc(s_chi, 1)
                        for c in range(VC):
                            n = 3 * g + c
                            act.wait_ge(s_cT, 12 * b + n + 1)
                            act.wait_ge(s_k, 4 * b + g)
                            act.activation(cT[:, c, :], ps_t[:, n % 2, :, :].rearrange("p q t -> p (q t)"), ACT.Copy).then_inc(s_cTc, 1)
                        act.wait_ge(s_k, 4 * b + g + 1)
                        act.wait_ge(s_kst, 64 * b + 16 * g)
                        act.activation(khl[:, 0, :], ps_s[:, 0, :], ACT.Copy).then_inc(s_khi, 1)
                        if g < 2:
                            load(b, g + 2)
                    with act.Fori(0, TPB // 2) as j:
                        for k in range(2):
                            t = b * TPB + 2 * j + k
                            for h in range(HEADS):
                                n = t * HEADS + h
                                act.wait_ge(s_s, n + 1)
                                act.wait_ge(s_sel, n)
                                act.activation(s_buf[:, h % 2, :], ps_s[:, :, :].rearrange("p c n -> p (c n)"), ACT.Copy).then_inc(s_sc, 1)
                                act.wait_ge(s_chk, n + 1)
                                act.activation(e_top[:, :], top[:, h % 2, :], ACT.Exp, bias=nmax[:, h % 2, :], scale=SCALE,
                                               accum_out=den[:, h % 2, :])
                                act.drain()
                                act.activation(lden[:, :], den[:, h % 2, :], ACT.Ln, scale=float(HEADS))
                                act.drain()
                                act.activation(pbias[:, :], lden[:, :], ACT.Identity, bias=nmax[:, h % 2, :], scale=-1.0)
                                act.drain()
                                act.activation(prob[:, :], s_buf[:, h % 2, :], ACT.Exp, bias=pbias[:, :], scale=SCALE).then_inc(s_prob, 1)
                            for g in range(4):
                                act.wait_ge(s_aT, 4 * t + g + 1)
                                act.wait_ge(s_ac, t)
                                act.activation(aT[:, 0, 4 * g:4 * g + 4, :], ps_t[:, g % 2, :, :], ACT.Copy).then_inc(s_aTh, 1)
                            act.wait_ge(s_ac, t + 1)
                            act.wait_ge(s_st[k], 16 * (b * (TPB // 2) + j))
                            act.activation(ac[:, k, :], ps_ac[:, :], ACT.Copy).then_inc(s_acc_c, 1)
                            act.wait_ge(s_acc_c, t + 1)
                            act.dma_start(rows(ac_out, t * P, P), ac[:, k, :]).then_inc(s_st[k], 16)
                for k in range(2):
                    act.wait_ge(s_st[k], 16 * TILES // 2)

            @block.vector
            def _(dve):
                dve.memset(mask[:, :], 0.0)
                dve.memset(row0[:, :], 0.0)
                dve.drain()
                dve.memset(row0[0:1, :], 1.0)

                def candidates(n, k):
                    dve.wait_ge(s_sc, n + 1)
                    dve.memset(f_acc[:, :], 0.0)
                    for g in range(SEGS):
                        dve.max(out=cand[:, 8 * g:8 * g + 8], in_=s_buf[:, k, g * SEG:(g + 1) * SEG])
                    dve.drain()
                    src = cand
                    for r in range(TOPK // 8):
                        dve.max(out=top[:, k, 8 * r:8 * r + 8], in_=src[:, :])
                        dve.drain()
                        if r < TOPK // 8 - 1:
                            dve.match_replace(out=cand_b[:, :], in_to_replace=top[:, k, 8 * r:8 * r + 8], in_values=src[:, :],
                                              imm_value=TAKEN)
                            dve.drain()
                        src = cand_b
                    t32 = top[:, k, TOPK - 1:TOPK]
                    dve.tensor_scalar(f_junk[:, 0:NCAND], cand[:, :], t32, None, ALU.is_ge, ALU.add, accum_out=f_acc[:, 0:1])
                    dve.tensor_scalar(f_junk[:, NCAND:NCAND + SEGS], cand[:, :].rearrange("p (g e) -> p g e", e=8)[:, :, 7], t32, None,
                                      ALU.is_ge, ALU.add, accum_out=f_acc[:, 1:2])
                    dve.tensor_scalar(nmax[:, k, :], top[:, k, 0:1], -SCALE, None, ALU.mult)
                    dve.drain()
                    dve.tensor_scalar(flag[:, k, :], f_acc[:, 0:1], f_acc[:, 1:2], float(-TOPK), ALU.add, ALU.add).then_inc(s_cand, 1)

                def settle(n, k):
                    dve.wait_ge(s_f, n + 1)
                    dve.tensor_copy(flag_i[:, k:k + 1], ps_f[:, k:k + 1])
                    dve.drain()
                    doubt = dve.value_load(flag_i[0:1, k:k + 1], min_val=0, max_val=P * NCAND * 2)
                    with dve.If(doubt > 0):
                        src = s_buf[:, k, :]
                        for r in range(TOPK // 8):
                            dve.max(out=top[:, k, 8 * r:8 * r + 8], in_=src)
                            dve.drain()
                            dve.match_replace(out=sel[:, k, :], in_to_replace=top[:, k, 8 * r:8 * r + 8], in_values=src,
                                              imm_value=TAKEN)
                            dve.drain()
                            src = sel[:, k, :]
                        dve.tensor_scalar(sel[:, k, :], sel[:, k, :], 0.5 * TAKEN, -2.0 * BIG, ALU.is_ge, ALU.mult)
                        dve.drain()
                        dve.tensor_tensor(s_buf[:, k, :], s_buf[:, k, :], sel[:, k, :], ALU.add)
                    dve.drain().then_inc(s_chk, 1)

                def select(n, k):
                    dve.wait_ge(s_prob, n + 1)
                    dve.scalar_tensor_tensor(out=sel[:, k, :], in0=s_buf[:, k, :], scalar=top[:, k, TOPK - 1:TOPK],
                                             in1=prob[:, :], op0=ALU.is_ge, op1=ALU.mult).then_inc(s_sel, 1)

                with dve.Fori(0, B) as b:
                    dve.wait_ge(s_ms, 16 * (b + 1))
                    dve.tensor_scalar(mask[0:1, :], mask_u8[:, :], BIG, -BIG, ALU.mult, ALU.add).then_inc(s_mask, 1)
                    for g in range(4):
                        dve.wait_ge(s_chi, 4 * b + g + 1)
                        dve.tensor_tensor(ctx_hl[:, 1, 4 * g:4 * g + 4, :], raw[:, g % 2, :, :],
                                          ctx_hl[:, 0, 4 * g:4 * g + 4, :].bitcast(F32), ALU.subtract).then_inc(s_clo, 1)
                        dve.wait_ge(s_khi, 4 * b + g + 1)
                        dve.tensor_tensor(khl[:, 1, :], ps_s[:, 0, :], khl[:, 0, :].bitcast(F32), ALU.subtract).then_inc(s_klo, 1)
                    with dve.Fori(0, TPB // 2) as j:
                        for kk in range(2):
                            t = b * TPB + 2 * j + kk
                            for h in range(HEADS):
                                n = t * HEADS + h
                                candidates(n, h % 2)
                                dve.wait_ge(s_acc, n - 1 if h >= 1 else n)
                                settle(n, h % 2)
                                select(n, h % 2)
                            for g in range(4):
                                dve.wait_ge(s_aTh, 4 * t + g + 1)
                                dve.tensor_tensor(aT[:, 1, 4 * g:4 * g + 4, :], ps_t[:, g % 2, :, :],
                                                  aT[:, 0, 4 * g:4 * g + 4, :].bitcast(F32), ALU.subtract).then_inc(s_aTl, 1)
        st.clear()



def stage_film(nc, A, x1_in, ac_in, xin_out, so_out, sh_out):
    NF = 4
    with ExitStack() as ctx:
        st = Stage(nc, ctx, "fi")
        sb, psum, sem = st.sb, st.psum, st.sem
        ident = sb("ident", [P, P])
        neghalf = sb("neghalf", [P, 1])
        gate = sb("gate", [P, 1])
        wv = sb("wv", [P, VC, D])
        wvT = sb("wvT", [P, DC, DV])
        wfilm = sb("wfilm", [P, DC, 2 * D])
        wf = sb("wf", [P, 2, VC, NF, D], F32R)
        bf = sb("bf", [P, NF, D])
        g_in = sb("g_in", [P, D])
        b_in = sb("b_in", [P, D])
        x1 = sb("x1", [P, 2, D])
        ac = sb("ac", [P, 2, DV])
        mask_u8 = sb("mask_u8", [P, 2, 1], U8)
        mask = sb("mask", [P, 2, 1])
        aT = sb("aT", [P, 2, 2, VC, P], F32R)
        stats = sb("stats", [P, 6])
        mv = sb("mv", [P, 2])
        rstd = sb("rstd", [P, 1])
        xn = sb("xn", [P, 2, D])
        mod = sb("mod", [P, 2, NF, D])

        ps_t = psum("ps_t", [P, 2, 512])
        ps_f = psum("ps_f", [P, NF, D])
        ps_w = psum("ps_w", [P, 2, 512])

        s_const = sem("constants")
        s_ld = sem("weights_loaded")
        s_lo_ = sem("film_out_loaded")
        s_wT = sem("wv_transposed")
        s_wTc = sem("wv_transposed_copied")
        s_fold = sem("folded")
        s_foh = sem("folded_hi")
        s_fol = sem("folded_lo")
        s_bf = sem("biases_ready")
        s_in = [sem(f"tile_loaded{k}") for k in range(2)]
        s_t = sem("ac_transposed")
        s_th = sem("ac_hi")
        s_tl = sem("ac_lo")
        s_f = sem("film_done")
        s_fr = sem("film_read")
        s_var = sem("variance")
        s_rstd = sem("rstd")
        s_xn = sem("normalised")
        s_x = sem("input_done")
        s_st = [sem(f"stored{k}") for k in range(2)]

        def bcast(name, n, off=0):
            return A[name].rearrange("(o n) -> o n", o=1)[:, off:off + n].broadcast_to([P, n])

        with nc.Block() as block:

            @block.sync
            def _(sp):
                sp.dma_start(gate[:, :], A["L0_xattn_mod_gate"].rearrange("(o n) -> o n", o=1).broadcast_to([P, 1])).then_inc(s_ld, 16)
                sp.dma_start(wv[:, :, :], A["L0_xattn_Wv"].rearrange("(c p) n -> p c n", p=P)).then_inc(s_ld, 16)
                sp.dma_start(wfilm[:, :, :], A["L0_xattn_W_film_in"].rearrange("(c p) n -> p c n", p=P)).then_inc(s_ld, 16)
                sp.dma_start(g_in[:, :], bcast("L0_xattn_g_norm_in", D)).then_inc(s_ld, 16)
                sp.dma_start(b_in[:, :], bcast("L0_xattn_b_norm_in", D)).then_inc(s_ld, 16)
                for i, name in enumerate(("L0_xattn_b_film_in", "L0_xattn_b_film_out")):
                    sp.dma_start(bf[:, 2 * i:2 * i + 2, :].rearrange("p a n -> p (a n)"), bcast(name, 2 * D)).then_inc(s_ld, 16)
                sp.wait_ge(s_fold, 6)
                sp.dma_start(wfilm[:, :, :], A["L0_xattn_W_film_out"].rearrange("(c p) n -> p c n", p=P)).then_inc(s_lo_, 16)

            @block.gpsimd
            def _(pool):
                pool.memset(ident[:, :], 0.0)
                pool.memset(neghalf[:, :], -0.5)
                pool.drain()
                pool.affine_select(out=ident[:, :], in_=ident[:, :], compare_op=ALU.not_equal, fill=1.0,
                                   base=0, pattern=[[-1, P]], channel_multiplier=1)
                pool.drain().then_inc(s_const, 1)
                with pool.Fori(0, TILES // 2) as j:
                    for k in range(2):
                        t = 2 * j + k
                        pool.wait_ge(s_var, t + 1)
                        pool.tensor_tensor(rstd[:, :], mv[:, 1:2], neghalf[:, :], ALU.pow).then_inc(s_rstd, 1)
                        pool.wait_ge(s_xn, t + 1)
                        pool.tensor_tensor(xn[:, k, :], xn[:, k, :], g_in[:, :], ALU.mult)
                        pool.drain()
                        pool.tensor_tensor(xn[:, k, :], xn[:, k, :], b_in[:, :], ALU.add)
                        pool.drain()
                        pool.wait_ge(s_fr, 4 * t + 2)
                        pool.tensor_tensor(xn[:, k, :], xn[:, k, :], mod[:, k, 0, :], ALU.mult)
                        pool.drain()
                        pool.tensor_tensor(xn[:, k, :], xn[:, k, :], mod[:, k, 1, :], ALU.add)
                        pool.drain().then_inc(s_x, 1)

            @block.tensor
            def _(pe):
                pe.wait_ge(s_const, 1)
                pe.wait_ge(s_ld, 16 * 7)
                for c in range(VC):
                    if c >= 2:
                        pe.wait_ge(s_wTc, c - 1)
                    for e in range(DC):
                        last = pe.transpose(ps_w[:, c % 2, e * P:(e + 1) * P], wv[:, c, e * P:(e + 1) * P], ident[:, :])
                    last.then_inc(s_wT, 1)
                pe.wait_ge(s_wTc, VC)
                n = 0
                for half in range(2):
                    if half:
                        pe.wait_ge(s_lo_, 16)
                    for q in range(2):
                        for c in range(VC):
                            if n >= 2:
                                pe.wait_ge(s_fol, n - 1)
                            for e in range(DC):
                                last = pe.matmul(ps_w[:, n % 2, :], wvT[:, e, c * P:(c + 1) * P], wfilm[:, e, q * D:(q + 1) * D],
                                                 start=(e == 0), stop=(e == DC - 1))
                            last.then_inc(s_fold, 1)
                            n += 1
                pe.wait_ge(s_fol, NF * VC)

                def film(t, k, first=False):
                    pe.wait_ge(s_tl, t + 1)
                    for f in range(NF):
                        if not first:
                            pe.wait_ge(s_fr, NF * (t - 1) + f + 1)
                        for c in range(VC):
                            last = mm3(pe, ps_f[:, f, :], aT[:, k, 0, c, :], aT[:, k, 1, c, :],
                                       wf[:, 0, c, f, :], wf[:, 1, c, f, :], start=(c == 0), stop=(c == VC - 1))
                        last.then_inc(s_f, 1)

                def transposes(k):
                    for c in range(VC):
                        last = pe.transpose(ps_t[:, k, c * P:(c + 1) * P], ac[:, k, c * P:(c + 1) * P], ident[:, :])
                    last.then_inc(s_t, 1)

                for k in range(2):
                    pe.wait_ge(s_in[k], 48)
                    transposes(k)
                film(0, 0, first=True)
                with pe.Fori(1, TILES // 2) as j:
                    for k in range(2):
                        t = 2 * j + k
                        pe.wait_ge(s_in[k], 48 * (j + 1))
                        pe.wait_ge(s_tl, t - 1)
                        transposes(k)
                        film(t - 1, 1 - k)
                film(TILES - 1, 1)

            @block.scalar
            def _(act):
                for c in range(VC):
                    act.wait_ge(s_wT, c + 1)
                    act.activation(wvT[:, :, c * P:(c + 1) * P], ps_w[:, c % 2, :].rearrange("p (e q) -> p e q", e=DC),
                                   ACT.Copy).then_inc(s_wTc, 1)
                n = 0
                for f in range(NF):
                    for c in range(VC):
                        act.wait_ge(s_fold, n + 1)
                        act.activation(wf[:, 0, c, f, :], ps_w[:, n % 2, :], ACT.Identity, scale=gate[:, 0:1]).then_inc(s_foh, 1)
                        n += 1

                text_mask = A["mask_BxS_bf1"].rearrange("b (s o) -> (b s) o", o=1)

                def load(t, k):
                    act.dma_start(x1[:, k, :], rows(x1_in, t * P, P)).then_inc(s_in[k], 16)
                    act.dma_start(ac[:, k, :], rows(ac_in, t * P, P)).then_inc(s_in[k], 16)
                    act.dma_start(mask_u8[:, k, :], rows(text_mask, t * P, P)).then_inc(s_in[k], 16)

                def hi(t, k):
                    act.wait_ge(s_t, t + 1)
                    act.activation(aT[:, k, 0, :, :].rearrange("p c q -> p (c q)"), ps_t[:, k, 0:DV], ACT.Copy).then_inc(s_th, 1)

                def store(t, k):
                    act.wait_ge(s_fr, 4 * t + 4)
                    act.dma_start(rows(so_out, t * P, P), mod[:, k, 2, :]).then_inc(s_st[k], 16)
                    act.dma_start(rows(sh_out, t * P, P), mod[:, k, 3, :]).then_inc(s_st[k], 16)
                    act.wait_ge(s_x, t + 1)
                    act.dma_start(rows(xin_out, t * P, P), xn[:, k, :]).then_inc(s_st[k], 16)

                load(0, 0)
                load(1, 1)
                hi(0, 0)
                hi(1, 1)
                with act.Fori(1, TILES // 2) as j:
                    for k in range(2):
                        store(2 * j + k - 2, k)
                        act.wait_ge(s_t, 2 * j + k - 1)
                        load(2 * j + k, k)
                        hi(2 * j + k, k)
                store(TILES - 2, 0)
                store(TILES - 1, 1)
                for k in range(2):
                    act.wait_ge(s_st[k], 48 * TILES // 2)

            @block.vector
            def _(dve):
                dve.wait_ge(s_ld, 16 * 7)
                dve.tensor_scalar(bf[:, :, :], bf[:, :, :], gate[:, 0:1], None, ALU.mult)
                dve.drain()
                for f in (0, 2):
                    dve.tensor_scalar(bf[:, f, :], bf[:, f, :], 1.0, None, ALU.add)
                dve.drain()
                n = 0
                for f in range(NF):
                    for c in range(VC):
                        dve.wait_ge(s_foh, n + 1)
                        dve.scalar_tensor_tensor(out=wf[:, 1, c, f, :], in0=ps_w[:, n % 2, :], scalar=gate[:, 0:1],
                                                 in1=wf[:, 0, c, f, :].bitcast(F32), op0=ALU.mult, op1=ALU.subtract).then_inc(s_fol, 1)
                        n += 1
                def split(t, k):
                    dve.wait_ge(s_th, t + 1)
                    dve.tensor_tensor(aT[:, k, 1, :, :].rearrange("p c q -> p (c q)"), ps_t[:, k, 0:DV],
                                      aT[:, k, 0, :, :].rearrange("p c q -> p (c q)").bitcast(F32), ALU.subtract).then_inc(s_tl, 1)

                def tile(t, k, j):
                    dve.wait_ge(s_in[k], 48 * (j + 1))
                    dve.tensor_copy(mask[:, k, :], mask_u8[:, k, :])
                    dve.bn_stats(stats[:, :], x1[:, k, :])
                    dve.drain()
                    dve.bn_aggr(mv[:, :], stats[:, :])
                    dve.drain()
                    dve.tensor_scalar(mv[:, 1:2], mv[:, 1:2], EPS, None, ALU.add).then_inc(s_var, 1)
                    dve.wait_ge(s_rstd, t + 1)
                    dve.wait_ge(s_st[k], 48 * j)
                    dve.tensor_scalar(xn[:, k, :], x1[:, k, :], mv[:, 0:1], rstd[:, 0:1], ALU.subtract, ALU.mult).then_inc(s_xn, 1)
                    for f in range(NF):
                        dve.wait_ge(s_f, NF * t + f + 1)
                        dve.scalar_tensor_tensor(out=mod[:, k, f, :], in0=ps_f[:, f, :], scalar=mask[:, k, :], in1=bf[:, f, :],
                                                 op0=ALU.mult, op1=ALU.add).then_inc(s_fr, 1)

                split(0, 0)
                split(1, 1)
                with dve.Fori(0, TILES // 2 - 1) as j:
                    for k in range(2):
                        tile(2 * j + k, k, j)
                        split(2 * j + k + 2, k)
                tile(TILES - 2, 0, TILES // 2 - 1)
                tile(TILES - 1, 1, TILES // 2 - 1)
        st.clear()



def conv_constants():
    t = np.arange(S // 2)[:, None] + 0.5
    fwd, tw = [], []
    for par in range(2):
        m = 2 * np.arange(S // 2)[None, :] + par + 0.5
        ang = np.pi * m * t / S
        fwd.append([np.cos(ang) + np.sin(ang), np.cos(ang) - np.sin(ang)])
        half = np.pi * m[0] / (2 * S)
        tw.append([(np.cos(half) + np.sin(half)) / 2, (np.cos(half) - np.sin(half)) / 2])
    fwd = np.array(fwd)
    inv = fwd.transpose(0, 1, 3, 2) / (2 * S)
    tw = np.array(tw).transpose(1, 0, 2).reshape(2, S)
    return {"dft": fwd.astype(np.float32), "idft": inv.astype(np.float32).copy(), "twiddle": tw.astype(np.float32)}


def make_exchange(pool, flip, ready):
    pool.memset(flip[:, :], 0.0)
    pool.drain()
    pool.affine_select(out=flip[:, :], in_=flip[:, :], compare_op=ALU.not_equal, fill=1.0,
                       base=1 - P, pattern=[[1, P]], channel_multiplier=1)
    pool.drain().then_inc(ready, 1)


def stage_dft(nc, A, xin, taps, y_out):
    TC = S // 2 // P
    MC = S // P
    XIN = 16 * (1 + TC)
    with ExitStack() as ctx:
        st = Stage(nc, ctx, "df")
        sb, psum, sem = st.sb, st.psum, st.sem
        raw = sb("raw", [P, 2, TC, D])
        mats = sb("mats", [P, 2, 2, 2, TC, 512], F32R)
        uv = sb("uv", [P, 2, 2, TC, D], F32R)
        uvf = sb("uvf", [P, 2, TC, D])
        kc = sb("kc", [P, MC, D])
        ks = sb("ks", [P, MC, D])
        tw = sb("tw", [P, 2, MC])
        prod = sb("prod", [P, 2, 4, D])
        yo = sb("yo", [P, 2, 2, D])
        flip = sb("flip", [P, P])
        ps = psum("ps", [P, 2, 2, D])
        ps_rev = psum("ps_rev", [P, TC, D])

        s_tw = sem("twiddle_loaded")
        s_m = sem("matrix_loaded")
        s_mh = sem("matrix_hi")
        s_ml = sem("matrix_lo")
        s_x = sem("x_loaded")
        s_const = sem("exchange_ready")
        s_rev = sem("reversed")
        s_uv = sem("sums_done")
        s_hi = sem("sums_hi")
        s_lo = sem("sums_lo")
        s_f = sem("spectrum")
        s_fr = sem("spectrum_read")
        s_kk = sem("taps_spectrum")
        s_pr = sem("products")
        s_y = sem("y_done")
        s_st = [sem(f"stored{k}") for k in range(2)]

        with nc.Block() as block:

            @block.sync
            def _(sp):
                sp.dma_start(tw[:, :, :], A["twiddle"].rearrange("i (q p) -> p i q", p=P), allow_slow_non_contiguous=True).then_inc(s_tw, 16)
                for n in range(4):
                    if n >= 1:
                        sp.wait_ge(s_ml, n)
                    sp.dma_start(raw[:, 0, :, :], A["dft"][n // 2, n % 2].rearrange("(q p) m -> p q m", p=P)).then_inc(s_m, 16)
                sp.wait_ge(s_ml, 4)

                def load(src, first):
                    sp.dma_start(raw[:, 0, :, :], rows(src, first, S // 2).rearrange("(q p) d -> p q d", p=P)).then_inc(s_x, 16)
                    for c in range(TC):
                        sp.dma_start(raw[:, 1, c, :], rows(src, first + S - (c + 1) * P, P)).then_inc(s_x, 16)

                load(taps, 0)
                with sp.Fori(0, B) as b:
                    sp.wait_ge(s_uv, b + 1)
                    load(xin, b * S)

            @block.gpsimd
            def _(pool):
                make_exchange(pool, flip, s_const)

                def split_v(n):
                    pool.wait_ge(s_hi, n + 1)
                    pool.tensor_tensor(uv[:, 1, 1, :, :], uvf[:, 1, :, :], uv[:, 1, 0, :, :].bitcast(F32), ALU.subtract).then_inc(s_lo, 1)

                split_v(0)
                with pool.Fori(0, B) as b:
                    split_v(b + 1)
                    for q in range(MC):
                        k = q % 2
                        pool.wait_ge(s_pr, MC * b + q + 1)
                        pool.wait_ge(s_st[k], 16 * ((MC // 2) * b + q // 2))
                        pool.tensor_tensor(yo[:, k, 0, :], prod[:, k, 0, :], prod[:, k, 1, :], ALU.add)
                        pool.tensor_tensor(yo[:, k, 1, :], prod[:, k, 2, :], prod[:, k, 3, :], ALU.subtract)
                        pool.drain().then_inc(s_y, 1)

            @block.tensor
            def _(pe):
                def reverse(n):
                    pe.wait_ge(s_x, XIN * (n + 1))
                    pe.wait_ge(s_uv, n)
                    for c in range(TC):
                        last = pe.matmul(ps_rev[:, c, :], flip[:, :], raw[:, 1, c, :], start=True, stop=True)
                    last.then_inc(s_rev, 1)

                def spectrum(n, q):
                    k = q % 2
                    i = MC * n + q
                    if not (isinstance(n, int) and n == 0 and q < 2):
                        pe.wait_ge(s_fr, i - 1)
                    par, mq = q // TC, q % TC
                    for sd in range(2):
                        src = (sd + par) % 2
                        for c in range(TC):
                            last = mm3(pe, ps[:, k, sd, :],
                                       mats[:, 0, par, sd, c, mq * P:(mq + 1) * P], mats[:, 1, par, sd, c, mq * P:(mq + 1) * P],
                                       uv[:, src, 0, c, :], uv[:, src, 1, c, :], start=(c == 0), stop=(c == TC - 1))
                    last.then_inc(s_f, 1)

                def sequence(n, last):
                    pe.wait_ge(s_lo, 2 * n + 2)
                    for q in range(MC):
                        if q == 3 and not last:
                            reverse(n + 1)
                        spectrum(n, q)

                pe.wait_ge(s_const, 1)
                pe.wait_ge(s_ml, 4)
                reverse(0)
                sequence(0, False)
                with pe.Fori(1, B) as n:
                    sequence(n, False)
                sequence(B, True)

            @block.scalar
            def _(act):
                for n in range(4):
                    act.wait_ge(s_m, 16 * (n + 1))
                    act.activation(mats[:, 0, n // 2, n % 2, :, :], raw[:, 0, :, :], ACT.Copy).then_inc(s_mh, 1)

                def hi(n):
                    act.wait_ge(s_uv, n + 1)
                    act.wait_ge(s_f, MC * n)
                    for i in range(2):
                        act.activation(uv[:, i, 0, :, :], uvf[:, i, :, :], ACT.Copy)
                    act.drain().then_inc(s_hi, 1)

                hi(0)
                with act.Fori(0, B) as b:
                    hi(b + 1)
                    for q in range(MC):
                        k = q % 2
                        act.wait_ge(s_y, MC * b + q + 1)
                        act.dma_start(y_out[bass.ds(b, 1), q].rearrange("o i p d -> p (o i) d"), yo[:, k, :, :]).then_inc(s_st[k], 16)
                for k in range(2):
                    act.wait_ge(s_st[k], 16 * B * MC // 2)

            @block.vector
            def _(dve):
                for n in range(4):
                    dve.wait_ge(s_mh, n + 1)
                    dve.tensor_tensor(mats[:, 1, n // 2, n % 2, :, :], raw[:, 0, :, :],
                                      mats[:, 0, n // 2, n % 2, :, :].bitcast(F32), ALU.subtract).then_inc(s_ml, 1)

                def fold(n):
                    dve.wait_ge(s_x, XIN * (n + 1))
                    dve.wait_ge(s_rev, n + 1)
                    dve.wait_ge(s_lo, 2 * n)
                    dve.tensor_tensor(uvf[:, 0, :, :], raw[:, 0, :, :], ps_rev[:, :, :], ALU.add)
                    dve.tensor_tensor(uvf[:, 1, :, :], raw[:, 0, :, :], ps_rev[:, :, :], ALU.subtract)
                    dve.drain().then_inc(s_uv, 1)
                    dve.wait_ge(s_hi, n + 1)
                    dve.tensor_tensor(uv[:, 0, 1, :, :], uvf[:, 0, :, :], uv[:, 0, 0, :, :].bitcast(F32), ALU.subtract).then_inc(s_lo, 1)

                fold(0)
                dve.wait_ge(s_tw, 16)
                for q in range(MC):
                    k = q % 2
                    dve.wait_ge(s_f, q + 1)
                    dve.tensor_scalar(prod[:, k, 0, :], ps[:, k, 0, :], tw[:, 0, q:q + 1], None, ALU.mult)
                    dve.tensor_scalar(prod[:, k, 1, :], ps[:, k, 1, :], tw[:, 0, q:q + 1], None, ALU.mult)
                    dve.drain()
                    dve.scalar_tensor_tensor(out=kc[:, q, :], in0=ps[:, k, 1, :], scalar=tw[:, 1, q:q + 1], in1=prod[:, k, 0, :],
                                             op0=ALU.mult, op1=ALU.add)
                    dve.scalar_tensor_tensor(out=ks[:, q, :], in0=ps[:, k, 0, :], scalar=tw[:, 1, q:q + 1], in1=prod[:, k, 1, :],
                                             op0=ALU.mult, op1=ALU.subtract)
                    dve.drain().then_inc(s_fr, 1)
                with dve.Fori(0, B) as b:
                    fold(b + 1)
                    for q in range(MC):
                        k = q % 2
                        dve.wait_ge(s_f, MC * (b + 1) + q + 1)
                        if q >= 2:
                            dve.wait_ge(s_y, MC * b + q - 1)
                        else:
                            dve.wait_ge(s_y, MC * b)
                        for i, (x, w) in enumerate(((0, kc), (1, ks), (1, kc), (0, ks))):
                            dve.tensor_tensor(prod[:, k, i, :], ps[:, k, x, :], w[:, q, :], ALU.mult)
                        dve.drain().then_inc(s_fr, 1)
                        dve.drain().then_inc(s_pr, 1)
        st.clear()


def stage_idft(nc, A, y_in, conv_out):
    TC = S // 2 // P
    MC = S // P
    with ExitStack() as ctx:
        st = Stage(nc, ctx, "id")
        sb, psum, sem = st.sb, st.psum, st.sem
        raw = sb("raw", [P, 2, 2, D])
        mraw = sb("mraw", [P, TC, 512])
        mats = sb("mats", [P, 2, 2, 2, TC, 512], F32R)
        y = sb("y", [P, MC, 2, 2, D], F32R)
        a_sb = sb("a_sb", [P, 2, D])
        out = sb("out", [P, 2, 2, D])
        flip = sb("flip", [P, P])
        rev = sb("rev", [P, 2, D])
        ps = psum("ps", [P, 2, 2, D])
        ps_rev = psum("ps_rev", [P, 2, D])

        s_m = sem("matrix_loaded")
        s_mh = sem("matrix_hi")
        s_ml = sem("matrix_lo")
        s_y = [sem(f"y_loaded{k}") for k in range(2)]
        s_hi = sem("y_hi")
        s_lo = sem("y_lo")
        s_o = sem("sums_done")
        s_const = sem("exchange_ready")
        s_rev = sem("reversed")
        s_rc = sem("reversed_copied")
        s_a = sem("a_copied")
        s_r = sem("result_done")
        s_st = [sem(f"stored{k}") for k in range(2)]

        with nc.Block() as block:

            @block.sync
            def _(sp):
                for n in range(4):
                    if n >= 1:
                        sp.wait_ge(s_ml, n)
                    sp.dma_start(mraw[:, :, :], A["idft"][n // 2, n % 2].rearrange("(q p) m -> p q m", p=P)).then_inc(s_m, 16)
                with sp.Fori(0, B) as b:
                    for q in range(MC):
                        k = q % 2
                        sp.wait_ge(s_lo, MC * b + q - 1 if q >= 2 else MC * b)
                        sp.dma_start(raw[:, k, :, :], y_in[bass.ds(b, 1), q].rearrange("o i p d -> p (o i) d")).then_inc(s_y[k], 16)

            @block.gpsimd
            def _(pool):
                make_exchange(pool, flip, s_const)
                with pool.Fori(0, B) as b:
                    for t in range(TC):
                        k = t % 2
                        pool.wait_ge(s_r, TC * b + t + 1)
                        pool.dma_start(rows(conv_out, b * S + t * P, P), out[:, k, 0, :]).then_inc(s_st[k], 16)
                        pool.wait_ge(s_rc, TC * b + t + 1)
                        pool.dma_start(rows(conv_out, b * S + S - (t + 1) * P, P), rev[:, k, :]).then_inc(s_st[k], 16)
                for k in range(2):
                    pool.wait_ge(s_st[k], 32 * B * TC // 2)

            @block.tensor
            def _(pe):
                def reverse(b, t):
                    pe.wait_ge(s_r, TC * b + t + 1)
                    pe.wait_ge(s_rc, TC * b + t - 1 if t >= 2 else TC * b)
                    pe.matmul(ps_rev[:, t % 2, :], flip[:, :], out[:, t % 2, 1, :], start=True, stop=True).then_inc(s_rev, 1)

                pe.wait_ge(s_const, 1)
                pe.wait_ge(s_ml, 4)
                with pe.Fori(0, B) as b:
                    pe.wait_ge(s_lo, MC * (b + 1))
                    for t in range(TC):
                        k = t % 2
                        pe.wait_ge(s_r, TC * b + t - 1 if t >= 2 else TC * b)
                        for ab in range(2):
                            for q in range(MC):
                                par, mq = q // TC, q % TC
                                pm = (ab + par) % 2
                                last = mm3(pe, ps[:, k, ab, :],
                                           mats[:, 0, par, pm, mq, t * P:(t + 1) * P], mats[:, 1, par, pm, mq, t * P:(t + 1) * P],
                                           y[:, q, 0, pm, :], y[:, q, 1, pm, :], start=(q == 0), stop=(q == MC - 1))
                        last.then_inc(s_o, 1)
                        if t >= 1:
                            reverse(b, t - 1)
                    reverse(b, TC - 1)

            @block.scalar
            def _(act):
                for n in range(4):
                    act.wait_ge(s_m, 16 * (n + 1))
                    act.activation(mats[:, 0, n // 2, n % 2, :, :], mraw[:, :, :], ACT.Copy).then_inc(s_mh, 1)

                def turned(b, t):
                    k = t % 2
                    act.wait_ge(s_rev, TC * b + t + 1)
                    act.wait_ge(s_st[k], 32 * ((TC // 2) * b + t // 2))
                    act.activation(rev[:, k, :], ps_rev[:, k, :], ACT.Copy).then_inc(s_rc, 1)

                with act.Fori(0, B) as b:
                    act.wait_ge(s_o, TC * b)
                    for q in range(MC):
                        k = q % 2
                        act.wait_ge(s_y[k], 16 * ((MC // 2) * b + q // 2 + 1))
                        act.activation(y[:, q, 0, :, :], raw[:, k, :, :], ACT.Copy).then_inc(s_hi, 1)
                    for t in range(TC):
                        k = t % 2
                        act.wait_ge(s_o, TC * b + t + 1)
                        act.wait_ge(s_r, TC * b + t - 1 if t >= 2 else TC * b)
                        act.activation(a_sb[:, k, :], ps[:, k, 0, :], ACT.Copy).then_inc(s_a, 1)
                        if t >= 1:
                            turned(b, t - 1)
                    turned(b, TC - 1)

            @block.vector
            def _(dve):
                for n in range(4):
                    dve.wait_ge(s_mh, n + 1)
                    dve.tensor_tensor(mats[:, 1, n // 2, n % 2, :, :], mraw[:, :, :],
                                      mats[:, 0, n // 2, n % 2, :, :].bitcast(F32), ALU.subtract).then_inc(s_ml, 1)
                with dve.Fori(0, B) as b:
                    for q in range(MC):
                        dve.wait_ge(s_hi, MC * b + q + 1)
                        dve.tensor_tensor(y[:, q, 1, :, :], raw[:, q % 2, :, :], y[:, q, 0, :, :].bitcast(F32), ALU.subtract)\
                           .then_inc(s_lo, 1)
                    for t in range(TC):
                        k = t % 2
                        dve.wait_ge(s_a, TC * b + t + 1)
                        dve.wait_ge(s_st[k], 32 * ((TC // 2) * b + t // 2))
                        dve.tensor_tensor(out[:, k, 0, :], a_sb[:, k, :], ps[:, k, 1, :], ALU.add)
                        if t >= 2:
                            dve.wait_ge(s_rev, TC * b + t - 1)
                        dve.tensor_tensor(out[:, k, 1, :], a_sb[:, k, :], ps[:, k, 1, :], ALU.subtract)
                        dve.drain().then_inc(s_r, 1)
        st.clear()


def stage_mlp(nc, name, modulated, W_up, b_up, W_down, down_biases, x_in, out, g_ffn=None, b_ffn=None,
              g_out=None, b_out=None, y_in=None, so_in=None, sh_in=None):
    N = 4 * P
    GROUPS = B * S // N
    Q = N // P
    PIECES = 2 * Q * DC
    IN = 64 if modulated else 16
    with ExitStack() as ctx:
        st = Stage(nc, ctx, name)
        sb, psum, sem = st.sb, st.psum, st.sem
        ident = sb("ident", [P, P])
        neghalf = sb("neghalf", [P, 1])
        w1 = sb("w1", [P, 2, DC, HID], F32R)
        w2 = sb("w2", [P, 2, HC, D], F32R)
        b1 = sb("b1", [P, HC])
        b2 = sb("b2", [P, D])
        xt = sb("xt", [P, 2, Q, D])
        h = sb("h", [P, D])
        hT = sb("hT", [P, 2, 2, DC, N], F32R)
        act_hl = sb("act_hl", [P, 2, 2, N], F32R)
        g32 = sb("g32", [P, N])
        stats = sb("stats", [P, 6])
        mv = {v: sb(f"mv_{v}", [P, 2]) for v in "pef"}
        rstd = {v: sb(f"rstd_{v}", [P, 1]) for v in "pef"}
        e = sb("e", [P, 2, D])
        if modulated:
            gf = sb("gf", [P, DC])
            bf = sb("bf", [P, DC])
            g_row = sb("g_row", [P, D])
            b_row = sb("b_row", [P, D])
            y = sb("y", [P, D])
            so = sb("so", [P, D])
            sh = sb("sh", [P, D])
            xr = sb("xr", [P, D])

        ps_h = psum("ps_h", [P, 2, N])
        ps_o = psum("ps_o", [P, Q, D])
        ps_t = psum("ps_t", [P, 2, D])

        s_const = sem("constants")
        s_c = sem("small_loaded")
        s_raw = [sem(f"piece_loaded{k}") for k in range(8)]
        s_whi = sem("weights_hi")
        s_wlo = sem("weights_lo")
        s_bm = sem("bias_products")
        s_in = sem("tile_loaded")
        s_mod = sem("modulated")
        s_var = {v: sem(f"variance_{v}") for v in "pef"}
        s_rstd = {v: sem(f"rstd_{v}") for v in "pef"}
        s_h = sem("h_done")
        s_b2 = sem("bias_added")
        s_tr = sem("h_transposed")
        s_hi = sem("hT_hi")
        s_hT = sem("hT_lo")
        s_m1 = sem("up_done")
        s_g = sem("gelu_done")
        s_gh = sem("gelu_hi")
        s_gl = sem("gelu_lo")
        s_m2 = sem("down_chunk_done")
        s_o = sem("down_done")
        s_add = sem("residual_added")
        s_n1 = sem("inner_norm")
        s_xr = sem("x_again_loaded")
        s_e = sem("outer_sum")
        s_n2 = sem("outer_norm")
        s_st = [sem(f"stored{k}") for k in range(2)]
        s_out = s_n2 if modulated else s_n1

        def in_groups(eng, group):
            group(0, 0, True, False)
            with eng.Fori(0, (GROUPS - 2) // 2) as j:
                for k in range(2):
                    group(2 * j + 1 + k, (1 + k) % 2, False, False)
            group(GROUPS - 1, (GROUPS - 1) % 2, False, True)

        with nc.Block() as block:

            @block.sync
            def _(sp):
                sp.dma_start(b1[:, :], b_up.rearrange("(c p) -> p c", p=P), allow_slow_non_contiguous=True).then_inc(s_c, 16)
                row = lambda v: v.rearrange("(o n) -> o n", o=1).broadcast_to([P, D])
                sp.dma_start(b2[:, :], row(down_biases[0])).then_inc(s_c, 16)
                if modulated:
                    for t, v in ((gf, g_ffn), (bf, b_ffn)):
                        sp.dma_start(t[:, :], v.rearrange("(c p) -> p c", p=P), allow_slow_non_contiguous=True).then_inc(s_c, 16)
                    for t, v in ((g_row, g_out), (b_row, b_out)):
                        sp.dma_start(t[:, :], row(v)).then_inc(s_c, 16)
                else:
                    sp.dma_start(h[:, :], row(down_biases[1])).then_inc(s_c, 16)
                for m in range(PIECES):
                    if m >= 8:
                        sp.wait_ge(s_whi, m - 7)
                        sp.wait_ge(s_wlo, m - 7)
                        if modulated:
                            sp.wait_ge(s_bm, min(m - 7, PIECES // 2))
                    if m < PIECES // 2:
                        c, q = m // Q, m % Q
                        src = W_up[c * P:(c + 1) * P, q * D:(q + 1) * D]
                    else:
                        n = m - PIECES // 2
                        src = W_down[n * P:(n + 1) * P, :]
                    sp.dma_start(xt[:, (m % 8) // Q, m % Q, :], src).then_inc(s_raw[m % 8], 16)

                def again(g, q):
                    i = Q * g + q
                    sp.wait_ge(s_e, i)
                    sp.dma_start(xr[:, :], rows(x_in, i * P, P)).then_inc(s_xr, 16)

                def group(g, slot, first, last):
                    for q in range(Q):
                        if not first:
                            again(g - 1, q)

                if modulated:
                    in_groups(sp, group)
                if modulated:
                    for q in range(Q):
                        again(GROUPS - 1, q)

            @block.gpsimd
            def _(pool):
                pool.memset(ident[:, :], 0.0)
                pool.memset(neghalf[:, :], -0.5)
                pool.drain()
                pool.affine_select(out=ident[:, :], in_=ident[:, :], compare_op=ALU.not_equal, fill=1.0,
                                   base=0, pattern=[[-1, P]], channel_multiplier=1)
                pool.drain().then_inc(s_const, 1)

                def power(v, i):
                    pool.wait_ge(s_var[v], i + 1)
                    pool.tensor_tensor(rstd[v][:, :], mv[v][:, 1:2], neghalf[:, :], ALU.pow).then_inc(s_rstd[v], 1)

                def modulate(g, slot, q):
                    i = Q * g + q
                    pool.wait_ge(s_in, IN * (i + 1))
                    pool.tensor_tensor(y[:, :], y[:, :], so[:, :], ALU.mult)
                    pool.drain()
                    pool.tensor_tensor(y[:, :], y[:, :], sh[:, :], ALU.add)
                    pool.drain()
                    pool.tensor_tensor(xt[:, slot, q, :], xt[:, slot, q, :], y[:, :], ALU.add).then_inc(s_mod, 1)

                def bias(g, slot, q):
                    pool.wait_ge(s_h, Q * g + q + 1)
                    pool.tensor_tensor(xt[:, slot, q, :], xt[:, slot, q, :], b2[:, :], ALU.add).then_inc(s_b2, 1)

                def outer_sum(g, q):
                    i = Q * g + q
                    pool.wait_ge(s_n1, i + 1)
                    ek = e[:, q % 2, :]
                    pool.tensor_tensor(ek, ek, g_row[:, :], ALU.mult)
                    pool.drain()
                    pool.tensor_tensor(ek, ek, b_row[:, :], ALU.add)
                    pool.drain()
                    pool.wait_ge(s_xr, 16 * (i + 1))
                    pool.tensor_tensor(ek, ek, xr[:, :], ALU.add).then_inc(s_e, 1)

                pool.wait_ge(s_c, 16 * (6 if modulated else 3))
                pool.wait_ge(s_wlo, PIECES)
                for q in range(Q):
                    if modulated:
                        modulate(0, 0, q)
                        power("p", q)
                    bias(0, 0, q)

                def group(g, slot, first, last):
                    for n in range(HC):
                        pool.wait_ge(s_gh, HC * g + n + 1)
                        lo, hi = act_hl[:, n % 2, 1, :], act_hl[:, n % 2, 0, :]
                        pool.tensor_tensor(lo, g32[:, :], hi.bitcast(F32), ALU.subtract).then_inc(s_gl, 1)
                        q, phase = n // 3, n % 3
                        if not first:
                            if phase == 0 and q < Q:
                                power("e", Q * (g - 1) + q)
                            if phase == 1 and q < Q and modulated:
                                outer_sum(g - 1, q)
                            if phase == 2 and q < Q and modulated:
                                power("f", Q * (g - 1) + q)
                        if not last:
                            if phase == 2 and q < Q and modulated:
                                modulate(g + 1, 1 - slot, q)
                            if modulated and phase == 0 and 1 <= q <= Q:
                                power("p", Q * (g + 1) + q - 1)
                            if phase == 1 and q >= 1 and q <= Q:
                                bias(g + 1, 1 - slot, q - 1)

                in_groups(pool, group)
                for q in range(Q):
                    i = Q * (GROUPS - 1) + q
                    power("e", i)
                    if modulated:
                        outer_sum(GROUPS - 1, q)
                        power("f", i)

            @block.tensor
            def _(pe):
                pe.wait_ge(s_const, 1)
                if modulated:
                    pe.wait_ge(s_c, 16 * 6)
                    for m in range(PIECES // 2):
                        c, q = m // Q, m % Q
                        pe.wait_ge(s_raw[m % 8], 16 * (m // 8 + 1))
                        for r in range(4):
                            n = 4 * q + r
                            last = pe.matmul(ps_t[:, 0, c * HC + n:c * HC + n + 1], xt[:, (m % 8) // Q, m % Q, r * P:(r + 1) * P],
                                             bf[:, c:c + 1], start=True, stop=True)
                        last.then_inc(s_bm, 1)
                pe.wait_ge(s_wlo, PIECES + 1)

                def turn(g, slot, q):
                    i = Q * g + q
                    pe.wait_ge(s_h, i + 1)
                    if not (isinstance(i, int) and i < 2):
                        pe.wait_ge(s_hT, i - 1)
                    for c in range(DC):
                        last = pe.transpose(ps_t[:, q % 2, c * P:(c + 1) * P], h[:, c * P:(c + 1) * P], ident[:, :])
                    last.then_inc(s_tr, 1)

                def up(g, slot, n, first):
                    if n == 0:
                        pe.wait_ge(s_hT, Q * (g + 1))
                    if not (first and n < 2):
                        pe.wait_ge(s_g, HC * g + n - 1)
                    for c in range(DC):
                        w_hi, w_lo = (w1[:, x, c, n * P:(n + 1) * P] for x in range(2))
                        last = mm3(pe, ps_h[:, n % 2, :], w_hi, w_lo, hT[:, slot, 0, c, :], hT[:, slot, 1, c, :],
                                   start=(c == 0), stop=(c == DC - 1))
                    last.then_inc(s_m1, 1)

                def down(g, n, first):
                    pe.wait_ge(s_gl, HC * g + n + 1)
                    for q in range(Q):
                        if n == 0 and not first:
                            pe.wait_ge(s_add, Q * (g - 1) + q + 1)
                        a_hi, a_lo = (act_hl[:, n % 2, x, q * P:(q + 1) * P] for x in range(2))
                        last = mm3(pe, ps_o[:, q, :], a_hi, a_lo, w2[:, 0, n, :], w2[:, 1, n, :],
                                   start=(n == 0), stop=(n == HC - 1))
                        if n == HC - 1:
                            last.then_inc(s_o, 1)
                    pe.drain().then_inc(s_m2, 1)

                for q in range(Q):
                    turn(0, 0, q)
                up(0, 0, 0, True)

                def group(g, slot, first, last):
                    for n in range(HC):
                        if not last and n >= 5 and (n - 5) % 3 == 0:
                            turn(g + 1, 1 - slot, (n - 5) // 3)
                        if n < HC - 1:
                            up(g, slot, n + 1, first)
                        elif not last:
                            up(g + 1, 1 - slot, 0, False)
                        down(g, n, first)

                in_groups(pe, group)

            @block.scalar
            def _(act):
                act.wait_ge(s_c, 16 * (6 if modulated else 3))
                for m in range(PIECES):
                    raw = xt[:, (m % 8) // Q, m % Q, :]
                    act.wait_ge(s_raw[m % 8], 16 * (m // 8 + 1))
                    if m < PIECES // 2:
                        c, q = m // Q, m % Q
                        act.activation(w1[:, 0, c, q * D:(q + 1) * D], raw, ACT.Identity,
                                       scale=gf[:, c:c + 1] if modulated else 1.0).then_inc(s_whi, 1)
                    else:
                        act.activation(w2[:, 0, m - PIECES // 2, :], raw, ACT.Copy).then_inc(s_whi, 1)

                def load(g, slot, q):
                    i = Q * g + q
                    if modulated:
                        act.wait_ge(s_mod, i)
                        for t, v in ((y, y_in), (so, so_in), (sh, sh_in)):
                            act.dma_start(t[:, :], rows(v, i * P, P)).then_inc(s_in, 16)
                    else:
                        act.wait_ge(s_h, i)
                    act.dma_start(xt[:, slot, q, :], rows(x_in, i * P, P)).then_inc(s_in, 16)

                def hi(g, slot, q):
                    act.wait_ge(s_tr, Q * g + q + 1)
                    if not (isinstance(g, int) and g < 2):
                        act.wait_ge(s_m1, HC * (g - 1))
                    act.activation(hT[:, slot, 0, :, q * P:(q + 1) * P], ps_t[:, q % 2, :].rearrange("p (c t) -> p c t", c=DC),
                                   ACT.Copy).then_inc(s_hi, 1)

                def store(g, q):
                    i = Q * g + q
                    act.wait_ge(s_out, i + 1)
                    act.dma_start(rows(out, i * P, P), e[:, q % 2, :]).then_inc(s_st[q % 2], 16)

                act.wait_ge(s_wlo, PIECES)
                for q in range(Q):
                    load(0, 0, q)
                    hi(0, 0, q)

                def group(g, slot, first, last):
                    for n in range(HC):
                        act.wait_ge(s_m1, HC * g + n + 1)
                        act.wait_ge(s_gl, HC * g + n)
                        act.activation(g32[:, :], ps_h[:, n % 2, :], ACT.Gelu,
                                       bias=b1[:, n:n + 1]).then_inc(s_g, 1)
                        if not last and n % 3 == 1 and n // 3 < Q:
                            if not first:
                                act.wait_ge(s_n1, Q * (g - 1) + n // 3 + 1)
                            load(g + 1, 1 - slot, n // 3)
                        if not last and n >= 5 and (n - 5) % 3 == 0:
                            hi(g + 1, 1 - slot, (n - 5) // 3)
                        if not first and n >= 4 and (n - 4) % 3 == 0 and (n - 4) // 3 < Q:
                            store(g - 1, (n - 4) // 3)

                in_groups(act, group)
                for q in range(Q):
                    store(GROUPS - 1, q)
                for k in range(2):
                    act.wait_ge(s_st[k], 16 * TILES // 2)

            @block.vector
            def _(dve):
                dve.wait_ge(s_c, 16 * (6 if modulated else 3))
                for m in range(PIECES):
                    raw = xt[:, (m % 8) // Q, m % Q, :]
                    dve.wait_ge(s_whi, m + 1)
                    if m < PIECES // 2 and modulated:
                        c, q = m // Q, m % Q
                        dve.scalar_tensor_tensor(out=w1[:, 1, c, q * D:(q + 1) * D], in0=raw, scalar=gf[:, c:c + 1],
                                                 in1=w1[:, 0, c, q * D:(q + 1) * D].bitcast(F32), op0=ALU.mult,
                                                 op1=ALU.subtract).then_inc(s_wlo, 1)
                    else:
                        if m < PIECES // 2:
                            c, q = m // Q, m % Q
                            w_hi, w_lo = (w1[:, x, c, q * D:(q + 1) * D] for x in range(2))
                        else:
                            w_hi, w_lo = (w2[:, x, m - PIECES // 2, :] for x in range(2))
                        dve.tensor_tensor(w_lo, raw, w_hi.bitcast(F32), ALU.subtract).then_inc(s_wlo, 1)
                if modulated:
                    dve.wait_ge(s_bm, PIECES // 2)
                    for c in range(DC):
                        dve.tensor_tensor(b1[:, :], b1[:, :], ps_t[:, 0, c * HC:(c + 1) * HC], ALU.add)
                        dve.drain()
                else:
                    dve.tensor_tensor(b2[:, :], b2[:, :], h[:, :], ALU.add)
                dve.drain().then_inc(s_wlo, 1)

                def variance(v, x):
                    dve.bn_stats(stats[:, :], x)
                    dve.drain()
                    dve.bn_aggr(mv[v][:, :], stats[:, :])
                    dve.drain()
                    dve.tensor_scalar(mv[v][:, 1:2], mv[v][:, 1:2], EPS, None, ALU.add).then_inc(s_var[v], 1)

                def var_p(g, slot, q):
                    i = Q * g + q
                    dve.wait_ge(s_mod, i + 1)
                    variance("p", xt[:, slot, q, :])

                def norm_p(g, slot, q):
                    i = Q * g + q
                    dve.wait_ge(s_tr, i)
                    if modulated:
                        dve.wait_ge(s_rstd["p"], i + 1)
                        dve.tensor_scalar(h[:, :], xt[:, slot, q, :], mv["p"][:, 0:1], rstd["p"][:, 0:1],
                                          ALU.subtract, ALU.mult).then_inc(s_h, 1)
                    else:
                        dve.wait_ge(s_in, IN * (i + 1))
                        dve.tensor_copy(h[:, :], xt[:, slot, q, :]).then_inc(s_h, 1)

                def lo(g, slot, q):
                    dve.wait_ge(s_hi, Q * g + q + 1)
                    dve.tensor_tensor(hT[:, slot, 1, :, q * P:(q + 1) * P], ps_t[:, q % 2, :].rearrange("p (c t) -> p c t", c=DC),
                                      hT[:, slot, 0, :, q * P:(q + 1) * P].bitcast(F32), ALU.subtract).then_inc(s_hT, 1)

                def add(g, slot):
                    for q in range(Q):
                        dve.wait_ge(s_o, Q * g + q + 1)
                        dve.wait_ge(s_b2, Q * g + q + 1)
                        dve.tensor_tensor(xt[:, slot, q, :], ps_o[:, q, :], xt[:, slot, q, :], ALU.add).then_inc(s_add, 1)
                    dve.drain()

                def norm_e(g, slot, q):
                    i = Q * g + q
                    dve.wait_ge(s_rstd["e"], i + 1)
                    dve.wait_ge(s_st[q % 2], 16 * (2 * g + q // 2))
                    dve.tensor_scalar(e[:, q % 2, :], xt[:, slot, q, :], mv["e"][:, 0:1], rstd["e"][:, 0:1],
                                      ALU.subtract, ALU.mult).then_inc(s_n1, 1)

                def var_f(g, q):
                    dve.wait_ge(s_e, Q * g + q + 1)
                    variance("f", e[:, q % 2, :])

                def norm_f(g, q):
                    dve.wait_ge(s_rstd["f"], Q * g + q + 1)
                    dve.tensor_scalar(e[:, q % 2, :], e[:, q % 2, :], mv["f"][:, 0:1], rstd["f"][:, 0:1],
                                      ALU.subtract, ALU.mult).then_inc(s_n2, 1)

                for q in range(Q):
                    if modulated:
                        var_p(0, 0, q)
                    norm_p(0, 0, q)
                    lo(0, 0, q)

                def group(g, slot, first, last):
                    for n in range(HC):
                        q, phase = n // 3, n % 3
                        dve.wait_ge(s_g, HC * g + n + 1)
                        if not (first and n < 2):
                            dve.wait_ge(s_m2, HC * g + n - 1)
                        dve.tensor_copy(act_hl[:, n % 2, 0, :], g32[:, :]).then_inc(s_gh, 1)
                        if not first:
                            if n == 0:
                                add(g - 1, 1 - slot)
                            if phase == 0 and q < Q:
                                variance("e", xt[:, 1 - slot, q, :])
                            if phase == 1 and q < Q:
                                norm_e(g - 1, 1 - slot, q)
                            if modulated:
                                if phase == 2 and q < Q:
                                    var_f(g - 1, q)
                                if phase == 0 and 1 <= q <= Q:
                                    norm_f(g - 1, q - 1)
                        if not last:
                            if modulated and phase == 0 and 1 <= q <= Q:
                                var_p(g + 1, 1 - slot, q - 1)
                            if phase == 1 and q >= 1:
                                norm_p(g + 1, 1 - slot, q - 1)
                            if phase == 2 and q >= 1:
                                lo(g + 1, 1 - slot, q - 1)

                in_groups(dve, group)
                add(GROUPS - 1, (GROUPS - 1) % 2)
                for q in range(Q):
                    variance("e", xt[:, (GROUPS - 1) % 2, q, :])
                    norm_e(GROUPS - 1, (GROUPS - 1) % 2, q)
                    if modulated:
                        var_f(GROUPS - 1, q)
                        norm_f(GROUPS - 1, q)
        st.clear()



def decoder_layer(nc, A, out):
    T = B * S

    def scratch(name, shape):
        return nc.dram_tensor(name, shape, F32, kind="Internal").ap()

    tap_rows, taps = scratch("tap_rows", [D, S]), scratch("taps", [S, D])
    w3, b3, w4 = scratch("w3", [D, HID]), scratch("b3", [HID]), scratch("w4", [HID, D])
    x1, qt = scratch("x1", [T, D]), scratch("qt", [2, P, T])
    kt, ac = scratch("kt", [2, P, S2]), scratch("ac", [T, DV])
    xin, so, sh = (scratch(n, [T, D]) for n in ("xin", "so", "sh"))
    spectrum, conv = scratch("spectrum", [B, 2 * DC, 2, P, D]), scratch("conv", [T, D])
    x2 = scratch("x2", [T, D])

    stage_taps(nc, A, tap_rows, taps)
    stage_butterfly(nc, A, w3, b3, w4)
    stage_attention(nc, A, x1, qt)
    stage_cross(nc, A, qt, kt, ac)
    stage_film(nc, A, x1, ac, xin, so, sh)
    stage_dft(nc, A, xin, taps, spectrum)
    stage_idft(nc, A, spectrum, conv)
    X = "L0_xattn_"
    stage_mlp(nc, "m1", True, A[X + "W1"], A[X + "b1"], A[X + "W2"], [A[X + "b2"]], x1, x2,
              g_ffn=A[X + "g_ffn"], b_ffn=A[X + "b_ffn"], g_out=A[X + "g_norm_out"], b_out=A[X + "b_norm_out"],
              y_in=conv, so_in=so, sh_in=sh)
    stage_mlp(nc, "m2", False, w3, b3, w4, [A["L0_ffn_b_con"], A["L0_ffn_down_bias"]], x2,
              out.rearrange("b s d -> (b s) d"))


def kernel(**inputs):
    import concourse.bacc as bacc
    from concourse.bass_utils import run_bass_kernel_spmd

    nc = bacc.Bacc("TRN2", target_bir_lowering=False, num_devices=1)
    given = {k: np.ascontiguousarray(v) for k, v in inputs.items()}
    given["L0_xattn_mod_gate"] = given["L0_xattn_mod_gate"].reshape(1)
    for name in ("mask_BxS_bf1", "mask_BxS2_bf1"):
        given[name] = given[name].view(np.uint8)
    given.update(conv_constants())
    arrays, aps = {}, {}
    for name, a in given.items():
        arrays[f"in_{name}_dram"] = a
        aps[name] = nc.dram_tensor(f"in_{name}_dram", a.shape, mybir.dt.from_np(a.dtype), kind="ExternalInput").ap()
    out = nc.dram_tensor("out_0_dram", (B, S, D), F32, kind="ExternalOutput").ap()
    decoder_layer(nc, aps, out)
    result = run_bass_kernel_spmd(nc, [arrays], core_ids=[0])
    return result.results[0]["out_0_dram"]
```

```python
import math
from contextlib import ExitStack

import numpy as np

import concourse.bass as bass
from concourse import mybir

F32 = mybir.dt.float32
F32R = mybir.dt.float32r
BF16 = mybir.dt.bfloat16
U8 = mybir.dt.uint8
ALU = mybir.AluOpType
ACT = mybir.ActivationFunctionType
AX = mybir.AxisListType

P = 128
B, S, D = 4, 1024, 512
DC = D // P
TILES = B * S // P
TPB = S // P
S2, DV = 2048, 384
VC = DV // P
GC = S2 // P
HEADS, DH = 4, 32
HID = 2048
HC = HID // P
TOPK = 32
NST = 64
EPS = 1e-5
SCALE = 1.0 / math.sqrt(32.0)
BIG = 1.0e30
TAKEN = -3.0e38


class Stage:

    def __init__(self, nc, ctx, name):
        self.nc, self.ctx, self.name, self.sems = nc, ctx, name, []

    def sb(self, name, shape, dt=F32):
        return self.ctx.enter_context(self.nc.sbuf_tensor(f"{self.name}_{name}", shape, dt))

    def psum(self, name, shape, dt=F32):
        return self.ctx.enter_context(self.nc.psum_tensor(f"{self.name}_{name}", shape, dt))

    def sem(self, name):
        self.sems.append(self.ctx.enter_context(self.nc.semaphore(f"{self.name}_{name}")))
        return self.sems[-1]

    def clear(self):
        with self.nc.Block() as block:
            @block.gpsimd
            def _(pool):
                for s in self.sems:
                    pool.sem_clear(s)


def rows(ap, start, n):
    return ap[bass.ds(start, n)]


def mm3(pe, out, w_hi, w_lo, m_hi, m_lo, start, stop):
    pe.matmul(out, w_hi, m_lo, start=start, stop=False)
    pe.matmul(out, w_lo, m_hi, start=False, stop=False)
    return pe.matmul(out, w_hi, m_hi, start=False, stop=stop)



def stage_taps(nc, A, tap_rows, taps_out):
    R = 32
    ROUND = 12582912.0
    LEVELS = 10
    TURN_1 = 6.28125
    TURN_2 = 0.0019350051879882812
    TURN_3 = 2.0 * math.pi - TURN_1 - TURN_2
    G = 16
    with ExitStack() as ctx:
        st = Stage(nc, ctx, "tp")
        sb, psum, sem = st.sb, st.psum, st.sem
        ident = sb("ident", [P, P])
        ldt = sb("ldt", [P, 1])
        dsk = sb("dsk", [P, 1])
        par = sb("par", [P, 4, NST])
        dt = sb("dt", [P, 3])
        dt_bits = sb("dt_bits", [P, 1], mybir.dt.int32)
        z = sb("z", [P, 6, LEVELS, NST])
        z_bits = sb("z_bits", [P, LEVELS, NST], mybir.dt.int32)
        lam = sb("lam", [P, LEVELS // 2, 2, NST])
        big = sb("big", [P, 5, 2, NST])
        w = sb("w", [P, 12, NST])
        ones = sb("ones", [P, NST])
        tab = [sb(f"tab{i}", [P, R, 2, NST]) for i in range(2)]
        tmp = [sb(f"tmp{i}", [P, 2, R // 2, NST]) for i in range(2)]
        tabT = [sb(f"tabT{i}", [P, R, P]) for i in range(2)]
        krow = sb("krow", [R, P, R])
        kd = sb("kd", [P, S])
        kT = sb("kT", [P, 2, P])
        ps_t = psum("ps_t", [P, 2, 4, P])
        ps_k = psum("ps_k", [R, 2, G, R])
        ps_o = psum("ps_o", [P, 2, 512])

        s_id = sem("identity")
        s_ld = sem("loaded")
        s_pow = sem("powers")
        s_tab = [sem(f"table{i}") for i in range(2)]
        s_tr = sem("transposed")
        s_trc = sem("transposed_copied")
        s_k = sem("taps_summed")
        s_kc = sem("taps_copied")
        s_kr = sem("tap_rows_stored")
        s_kd = sem("taps_loaded")
        s_skip = sem("skip_added")
        s_o = sem("taps_turned")
        s_oc = sem("taps_turned_copied")
        s_st = [sem(f"stored{k}") for k in range(2)]

        def grow(eng, table, t, power, n):
            for k in range(n.bit_length() - 1):
                m = 2 ** k
                re, im = table[:, 0:m, 0, :], table[:, 0:m, 1, :]
                pr = power[:, k:k + 1, 0, :].broadcast_to([P, m, NST])
                pi = power[:, k:k + 1, 1, :].broadcast_to([P, m, NST])
                for part, (x, y, op) in enumerate(((pr, pi, ALU.subtract), (pi, pr, ALU.add))):
                    eng.tensor_tensor(t[:, 0, 0:m, :], re, x, ALU.mult)
                    eng.tensor_tensor(t[:, 1, 0:m, :], im, y, ALU.mult)
                    eng.drain()
                    eng.tensor_tensor(table[:, m:2 * m, part, :], t[:, 0, 0:m, :], t[:, 1, 0:m, :], op)
                    eng.drain()

        with nc.Block() as block:

            @block.sync
            def _(sp):
                with sp.Fori(0, DC) as c:
                    sp.wait_ge(s_skip, c)
                    sp.wait_ge(s_tab[1], c)
                    sp.dma_start(ldt[:, :], rows(A["L0_xattn_log_dt"].rearrange("(n o) -> n o", o=1), c * P, P)).then_inc(s_ld, 16)
                    sp.dma_start(dsk[:, :], rows(A["L0_xattn_D_skip"].rearrange("(n o) -> n o", o=1), c * P, P)).then_inc(s_ld, 16)
                    for i, name in enumerate(("A_re", "A_im", "C_re", "C_im")):
                        sp.dma_start(par[:, i, :], rows(A["L0_xattn_" + name], c * P, P)).then_inc(s_ld, 16)
                    sp.wait_ge(s_kc, (P // G) * (c + 1))
                    sp.dma_start(rows(tap_rows, c * P, P).rearrange("d (a r) -> a d r", r=R), krow[:, :, :]).then_inc(s_kr, 16)
                    sp.wait_ge(s_kr, 16 * (c + 1))
                    sp.dma_start(kd[:, :], rows(tap_rows, c * P, P)).then_inc(s_kd, 16)
                    for n in range(S // P):
                        sp.wait_ge(s_oc, (S // P) * c + n + 1)
                        sp.dma_start(taps_out[n * P:(n + 1) * P, bass.ds(c * P, P)], kT[:, n % 2, :]).then_inc(s_st[n % 2], 16)
                for k in range(2):
                    sp.wait_ge(s_st[k], 16 * DC * (S // P) // 2)

            @block.gpsimd
            def _(pool):
                pool.memset(ident[:, :], 0.0)
                pool.memset(ones[:, :], 1.0)
                pool.drain()
                pool.affine_select(out=ident[:, :], in_=ident[:, :], compare_op=ALU.not_equal, fill=1.0,
                                   base=0, pattern=[[-1, P]], channel_multiplier=1)
                pool.drain().then_inc(s_id, 1)
                with pool.Fori(0, DC) as c:
                    pool.wait_ge(s_pow, c + 1)
                    pool.wait_ge(s_trc, 16 * c)
                    pool.tensor_tensor(tab[1][:, 0, 0, :], w[:, 10, :], ones[:, :], ALU.mult)
                    pool.tensor_tensor(tab[1][:, 0, 1, :], w[:, 11, :], ones[:, :], ALU.mult)
                    pool.drain()
                    grow(pool, tab[1], tmp[1], big, R)
                    pool.drain().then_inc(s_tab[1], 1)

            @block.tensor
            def _(pe):
                pe.wait_ge(s_id, 1)
                with pe.Fori(0, DC) as c:
                    for i in range(2):
                        pe.wait_ge(s_tab[i], c + 1)
                        for g in range(8):
                            n = 8 * i + g
                            pe.wait_ge(s_trc, 16 * c + (n - 1 if n >= 1 else 0))
                            for q in range(4):
                                last = pe.transpose(ps_t[:, n % 2, q, :], tab[i][:, 4 * g + q, :, :].rearrange("p a n -> p (a n)"), ident[:, :])
                            last.then_inc(s_tr, 1)
                    pe.wait_ge(s_trc, 16 * (c + 1))
                    for g in range(P // G):
                        pe.wait_ge(s_kc, (P // G) * c + (g - 1 if g >= 1 else 0))
                        for q in range(G):
                            d = g * G + q
                            last = pe.matmul(ps_k[:, g % 2, q, :], tabT[1][:, :, d], tabT[0][:, :, d], start=True, stop=True)
                        last.then_inc(s_k, 1)
                    pe.wait_ge(s_skip, c + 1)
                    pe.wait_ge(s_kd, 16 * (c + 1))
                    for n in range(S // P):
                        pe.wait_ge(s_oc, (S // P) * c + (n - 1 if n >= 1 else 0))
                        pe.transpose(ps_o[:, n % 2, 0:P], kd[:, n * P:(n + 1) * P], ident[:, :]).then_inc(s_o, 1)

            @block.scalar
            def _(act):
                with act.Fori(0, DC) as c:
                    for n in range(16):
                        act.wait_ge(s_tr, 16 * c + n + 1)
                        i, g = n // 8, n % 8
                        act.activation(tabT[i][:, 4 * g:4 * g + 4, :], ps_t[:, n % 2, :, :], ACT.Copy).then_inc(s_trc, 1)
                    act.wait_ge(s_kr, 16 * c)
                    for g in range(P // G):
                        act.wait_ge(s_k, (P // G) * c + g + 1)
                        act.activation(krow[:, g * G:(g + 1) * G, :], ps_k[:, g % 2, :, :], ACT.Copy).then_inc(s_kc, 1)
                    for n in range(S // P):
                        act.wait_ge(s_o, (S // P) * c + n + 1)
                        act.wait_ge(s_st[n % 2], 16 * ((S // P // 2) * c + n // 2))
                        act.activation(kT[:, n % 2, :], ps_o[:, n % 2, 0:P], ACT.Copy).then_inc(s_oc, 1)

            @block.vector
            def _(dve):
                def tt(out, a, b, op):
                    dve.tensor_tensor(out, a, b, op)
                    dve.drain()

                def mul(out, a, x):
                    dve.tensor_scalar(out, a, x, None, ALU.mult)
                    dve.drain()

                def horner(p, v, coefs):
                    mul(p, v, coefs[0])
                    for coef in coefs[1:]:
                        dve.scalar_tensor_tensor(out=p, in0=p, scalar=coef, in1=v, op0=ALU.add, op1=ALU.mult)
                        dve.drain()

                def less_multiples(x, q, inv, parts):
                    dve.tensor_scalar(q, x, inv, ROUND, ALU.mult, ALU.add)
                    dve.drain()
                    dve.tensor_scalar(q, q, -ROUND, None, ALU.add)
                    dve.drain()
                    for part in parts:
                        dve.scalar_tensor_tensor(out=x, in0=q, scalar=-part, in1=x, op0=ALU.mult, op1=ALU.add)
                        dve.drain()

                def exp(x, q, qi, p):
                    dve.tensor_scalar(x, x, -87.0, 88.0, ALU.max, ALU.min)
                    dve.drain()
                    less_multiples(x, q, 1.0 / math.log(2.0), (0.693359375, math.log(2.0) - 0.693359375))
                    horner(p, x, [1.0 / math.factorial(n) for n in range(8, 0, -1)])
                    dve.tensor_scalar(q, q, 127.0, float(2 ** 23), ALU.add, ALU.mult)
                    dve.drain()
                    dve.tensor_copy(qi, q)
                    dve.drain()
                    dve.scalar_tensor_tensor(out=p, in0=p, scalar=1.0, in1=qi.bitcast(F32), op0=ALU.add, op1=ALU.mult)
                    dve.drain()

                with dve.Fori(0, DC) as c:
                    dve.wait_ge(s_ld, 16 * 6 * (c + 1))
                    W = [w[:, i, :] for i in range(12)]
                    are, aim, cre, cim = (par[:, i, :] for i in range(4))
                    dve.tensor_copy(dt[:, 1:2], ldt[:, :])
                    dve.drain()
                    exp(dt[:, 1:2], dt[:, 2:3], dt_bits[:, :], dt[:, 0:1])
                    for k in range(LEVELS):
                        dve.tensor_scalar(z[:, 0, k, :], are, dt[:, 0:1], float(2 ** k), ALU.mult, ALU.mult)
                        dve.tensor_scalar(z[:, 1, k, :], aim, dt[:, 0:1], float(2 ** k), ALU.mult, ALU.mult)
                    dve.drain()
                    X, Y, Q, V, SI, CO = (z[:, i, :, :] for i in range(6))
                    exp(X, Q, z_bits[:, :, :], V)
                    dve.tensor_copy(X, V)
                    dve.drain()
                    less_multiples(Y, Q, 1.0 / (2.0 * math.pi), (TURN_1, TURN_2, TURN_3))
                    mul(Y, Y, 0.25)
                    tt(V, Y, Y, ALU.mult)
                    horner(SI, V, [(-1.0) ** n / math.factorial(2 * n + 1) for n in range(4, 0, -1)])
                    dve.scalar_tensor_tensor(out=SI, in0=SI, scalar=1.0, in1=Y, op0=ALU.add, op1=ALU.mult)
                    horner(CO, V, [(-1.0) ** n / math.factorial(2 * n) for n in range(5, 0, -1)])
                    dve.tensor_scalar(CO, CO, 1.0, None, ALU.add)
                    dve.drain()
                    for _ in range(2):
                        tt(V, SI, SI, ALU.mult)
                        dve.scalar_tensor_tensor(out=SI, in0=SI, scalar=2.0, in1=CO, op0=ALU.mult, op1=ALU.mult)
                        dve.drain()
                        dve.tensor_scalar(CO, V, -2.0, 1.0, ALU.mult, ALU.add)
                        dve.drain()
                    half = LEVELS // 2
                    tt(lam[:, :, 0, :], X[:, 0:half], CO[:, 0:half], ALU.mult)
                    tt(lam[:, :, 1, :], X[:, 0:half], SI[:, 0:half], ALU.mult)
                    tt(big[:, :, 0, :], X[:, half:], CO[:, half:], ALU.mult)
                    dve.scalar_tensor_tensor(out=big[:, :, 1, :], in0=X[:, half:], scalar=-1.0, in1=SI[:, half:],
                                             op0=ALU.mult, op1=ALU.mult)
                    dve.drain()
                    dve.tensor_scalar(W[2], lam[:, 0, 0, :], -1.0, None, ALU.add)
                    dve.drain()
                    li = lam[:, 0, 1, :]
                    tt(W[5], cre, W[2], ALU.mult)
                    tt(W[6], cim, li, ALU.mult)
                    tt(W[7], W[5], W[6], ALU.subtract)
                    tt(W[5], cre, li, ALU.mult)
                    tt(W[6], cim, W[2], ALU.mult)
                    tt(W[8], W[5], W[6], ALU.add)
                    tt(W[5], are, are, ALU.mult)
                    tt(W[6], aim, aim, ALU.mult)
                    tt(W[9], W[5], W[6], ALU.add)
                    dve.reciprocal(W[9], W[9])
                    dve.drain()
                    mul(W[9], W[9], 2.0)
                    tt(W[5], W[7], are, ALU.mult)
                    tt(W[6], W[8], aim, ALU.mult)
                    tt(W[5], W[5], W[6], ALU.add)
                    tt(W[10], W[5], W[9], ALU.mult)
                    tt(W[5], W[7], aim, ALU.mult)
                    tt(W[6], W[8], are, ALU.mult)
                    tt(W[5], W[5], W[6], ALU.subtract)
                    tt(W[11], W[5], W[9], ALU.mult)
                    dve.drain().then_inc(s_pow, 1)
                    dve.wait_ge(s_trc, 16 * c)
                    dve.memset(tab[0][:, 0, 0, :], 1.0)
                    dve.memset(tab[0][:, 0, 1, :], 0.0)
                    dve.drain()
                    grow(dve, tab[0], tmp[0], lam, R)
                    dve.drain().then_inc(s_tab[0], 1)
                    dve.wait_ge(s_kd, 16 * (c + 1))
                    dve.tensor_tensor(kd[:, 0:1], kd[:, 0:1], dsk[:, :], ALU.add).then_inc(s_skip, 1)
        st.clear()



def stage_butterfly(nc, A, w3_out, b3_out, w4_out):
    LOW = 7
    TOP = 4
    PAIRS = HID // 2
    with ExitStack() as ctx:
        st = Stage(nc, ctx, "bf")
        sb, psum, sem = st.sb, st.psum, st.sem
        ident = sb("ident", [P, P])
        e_up = sb("e_up", [P, 2, HID])
        e_dn = sb("e_dn", [P, 2, HID])
        w_up = sb("w_up", [P, PAIRS, 4])
        w_dn = sb("w_dn", [P, PAIRS, 4])
        tmp_up = sb("tmp_up", [P, 2, PAIRS])
        tmp_dn = sb("tmp_dn", [P, 2, PAIRS])
        col_up = sb("col_up", [P, TOP, HC // 2, 4])
        col_dn = sb("col_dn", [P, TOP, HC // 2, 4])
        wx = sb("wx", [P, HID])
        wT = sb("wT", [P, HC, D + 2])
        pair_tmp = sb("pair_tmp", [P, 2, 2, D + 2])
        upb = sb("upb", [P, HC])
        eT = sb("eT", [P, 4, P])
        out_t = sb("out_t", [P, 2, D])
        ps = psum("ps", [P, 2, 512])
        ps_b = psum("ps_b", [P, HC])
        wc = wT

        s_id = sem("identity")
        s_wu = sem("up_stage_weights")
        s_wd = sem("down_stage_weights")
        s_cols = sem("columns_loaded")
        s_wx = sem("w_exp_loaded")
        s_up = sem("up_matrix_stage")
        s_dn = sem("down_matrix_stage")
        s_tr = sem("transposed")
        s_trc = sem("transposed_copied")
        s_mm = sem("block_product")
        s_mmc = sem("block_product_copied")
        s_hi = sem("across_blocks")
        s_r = sem("rows_transposed")
        s_rc = sem("rows_copied")
        s_wc = sem("w_con_loaded")
        s_dhi = sem("down_across_blocks")
        s_eT = sem("down_matrix_transposed")
        s_eTc = sem("down_matrix_transposed_copied")
        s_d = sem("down_product")
        s_dc = sem("down_product_copied")
        s_out = [sem(f"stored{k}") for k in range(2)]
        s_b3 = sem("bias_stored")

        def low_stage(eng, e, w, tmp, s):
            width = 2 ** s
            src = e[:, s % 2, :].rearrange("p (n two s) -> p two n s", two=2, s=width)
            dst = e[:, 1 - s % 2, :].rearrange("p (n two s) -> p two n s", two=2, s=width)
            wv = w[:, :, :].rearrange("p (n s) f -> p f n s", s=width)
            t = [tmp[:, i, :].rearrange("p (n s) -> p n s", s=width) for i in range(2)]
            for o in range(2):
                eng.tensor_tensor(t[0], src[:, 0], wv[:, 2 * o], ALU.mult)
                eng.tensor_tensor(t[1], src[:, 1], wv[:, 2 * o + 1], ALU.mult)
                eng.drain()
                last = eng.tensor_tensor(dst[:, o], t[0], t[1], ALU.add)
                eng.drain()
            return last

        def block_pairs(s):
            w = 2 ** s
            return [(q // w * 2 * w + q % w, q // w * 2 * w + q % w + w) for q in range(HC // 2)]

        def across(eng, x, col, s, width, transposed):
            a10, a01 = (1, 2) if transposed else (2, 1)
            for q, (a, b) in enumerate(block_pairs(s)):
                ta, tb = pair_tmp[:, q % 2, 0, 0:width], pair_tmp[:, q % 2, 1, 0:width]
                xa, xb = x[:, a, 0:width], x[:, b, 0:width]
                eng.tensor_scalar(ta, xa, col[:, s, q, 0:1], None, ALU.mult)
                eng.tensor_scalar(tb, xa, col[:, s, q, a10:a10 + 1], None, ALU.mult)
                eng.drain()
                eng.scalar_tensor_tensor(out=xa, in0=xb, scalar=col[:, s, q, a01:a01 + 1], in1=ta, op0=ALU.mult, op1=ALU.add)
                eng.drain()
                eng.scalar_tensor_tensor(out=xb, in0=xb, scalar=col[:, s, q, 3:4], in1=tb, op0=ALU.mult, op1=ALU.add)
            eng.drain()

        with nc.Block() as block:

            @block.sync
            def _(sp):
                for s in range(LOW):
                    if s >= 1:
                        sp.wait_ge(s_up, s)
                    sp.dma_start(w_up[:, :, :], A["L0_ffn_up_weights"][s:s + 1].rearrange("o k i j -> o k (i j)").broadcast_to([P, PAIRS, 4]))\
                      .then_inc(s_wu, 16)
                    if s == 0:
                        for v, name in ((col_up, "L0_ffn_up_weights"), (col_dn, "L0_ffn_down_weights")):
                            for k in range(TOP):
                                sp.dma_start(v[:, k, :, :], A[name][LOW + k].rearrange("(q p) i j -> p q (i j)", p=P)).then_inc(s_cols, 16)
                        sp.dma_start(wT[:, :, D:D + 1], A["L0_ffn_b_exp"].rearrange("(c p o) -> p c o", p=P, o=1), allow_slow_non_contiguous=True).then_inc(s_cols, 16)
                        sp.dma_start(upb[:, :], A["L0_ffn_up_bias"].rearrange("(c p) -> p c", p=P), allow_slow_non_contiguous=True)\
                          .then_inc(s_cols, 16)
                for c in range(DC):
                    if c >= 1:
                        sp.wait_ge(s_tr, 4 * c)
                    sp.dma_start(wx[:, :], A["L0_ffn_W_exp"][c * P:(c + 1) * P, :]).then_inc(s_wx, 16)
                for n in range(4 * DC):
                    sp.wait_ge(s_rc, n + 1)
                    c, g = n // 4, n % 4
                    sp.dma_start(w3_out[c * P:(c + 1) * P, g * 512:(g + 1) * 512], out_t[:, n % 2, :]).then_inc(s_out[n % 2], 16)
                sp.dma_start(wc[:, :, 0:D], A["L0_ffn_W_con"].rearrange("(c p) n -> p c n", p=P)).then_inc(s_wc, 16)
                for n in range(HC):
                    sp.wait_ge(s_dc, n + 1)
                    sp.dma_start(w4_out[n * P:(n + 1) * P, :], out_t[:, n % 2, :]).then_inc(s_out[n % 2], 16)
                for k in range(2):
                    sp.wait_ge(s_out[k], 16 * (4 * DC + HC) // 2)

            @block.gpsimd
            def _(pool):
                pool.memset(ident[:, :], 0.0)
                pool.drain()
                pool.affine_select(out=ident[:, :], in_=ident[:, :], compare_op=ALU.not_equal, fill=1.0,
                                   base=0, pattern=[[-1, P]], channel_multiplier=1)
                pool.drain().then_inc(s_id, 1)
                for c in range(HC):
                    pool.tensor_copy(e_dn[:, 0, c * P:(c + 1) * P], ident[:, :])
                pool.drain()
                for s in range(LOW):
                    pool.wait_ge(s_wd, 16 * (s + 1))
                    low_stage(pool, e_dn, w_dn, tmp_dn, s)
                    pool.drain().then_inc(s_dn, 1)

            @block.tensor
            def _(pe):
                pe.wait_ge(s_id, 1)
                for c in range(DC):
                    pe.wait_ge(s_wx, 16 * (c + 1))
                    for g in range(4):
                        n = 4 * c + g
                        if n >= 2:
                            pe.wait_ge(s_trc, n - 1)
                        for q in range(4):
                            h = 4 * g + q
                            last = pe.transpose(ps[:, n % 2, q * P:(q + 1) * P], wx[:, h * P:(h + 1) * P], ident[:, :])
                        last.then_inc(s_tr, 1)
                pe.wait_ge(s_trc, 16)
                pe.wait_ge(s_cols, 16 * 10)
                pe.wait_ge(s_up, LOW)
                for h in range(HC):
                    if h >= 2:
                        pe.wait_ge(s_mmc, h - 1)
                    blk = e_up[:, LOW % 2, h * P:(h + 1) * P]
                    pe.matmul(ps_b[:, h:h + 1], blk, wT[:, h, D:D + 1], start=True, stop=True)
                    pe.matmul(ps[:, h % 2, :], blk, wT[:, h, 0:D], start=True, stop=True).then_inc(s_mm, 1)
                pe.wait_ge(s_hi, 1)
                for c in range(DC):
                    for g in range(4):
                        n = 4 * c + g
                        if n >= 2:
                            pe.wait_ge(s_rc, n - 1)
                        for q in range(4):
                            h = 4 * g + q
                            last = pe.transpose(ps[:, n % 2, q * P:(q + 1) * P], wT[:, h, c * P:(c + 1) * P], ident[:, :])
                        last.then_inc(s_r, 1)
                pe.wait_ge(s_rc, 16)
                pe.wait_ge(s_dn, LOW)
                pe.wait_ge(s_dhi, 1)
                for h in range(HC):
                    if h >= 1:
                        pe.wait_ge(s_dc, h)
                    pe.transpose(ps[:, 0, 0:P], e_dn[:, LOW % 2, h * P:(h + 1) * P], ident[:, :]).then_inc(s_eT, 1)
                    pe.wait_ge(s_eTc, h + 1)
                    pe.matmul(ps[:, 1, :], eT[:, 0, :], wc[:, h, 0:D], start=True, stop=True).then_inc(s_d, 1)

            @block.scalar
            def _(act):
                for s in range(LOW):
                    if s >= 1:
                        act.wait_ge(s_dn, s)
                    act.dma_start(w_dn[:, :, :], A["L0_ffn_down_weights"][s:s + 1].rearrange("o k i j -> o k (i j)").broadcast_to([P, PAIRS, 4]))\
                       .then_inc(s_wd, 16)
                    if s == 0:
                        for n in range(16):
                            act.wait_ge(s_tr, n + 1)
                            c, g = n // 4, n % 4
                            act.activation(wT[:, 4 * g:4 * g + 4, c * P:(c + 1) * P], ps[:, n % 2, :].rearrange("p (q t) -> p q t", q=4),
                                           ACT.Copy).then_inc(s_trc, 1)
                for h in range(HC):
                    act.wait_ge(s_mm, h + 1)
                    act.activation(wT[:, h, 0:D], ps[:, h % 2, :], ACT.Copy).then_inc(s_mmc, 1)
                for n in range(16):
                    act.wait_ge(s_r, n + 1)
                    if n >= 2:
                        act.wait_ge(s_out[n % 2], 16 * (n // 2))
                    act.activation(out_t[:, n % 2, :], ps[:, n % 2, :], ACT.Copy).then_inc(s_rc, 1)
                for h in range(HC):
                    act.wait_ge(s_eT, h + 1)
                    act.activation(eT[:, 0, :], ps[:, 0, 0:P], ACT.Copy).then_inc(s_eTc, 1)
                    act.wait_ge(s_d, h + 1)
                    act.wait_ge(s_out[h % 2], 16 * (8 + h // 2))
                    act.activation(out_t[:, h % 2, :], ps[:, 1, :], ACT.Copy).then_inc(s_dc, 1)
                act.wait_ge(s_hi, 1)
                act.dma_start(b3_out.rearrange("(c p) -> p c", p=P), upb[:, :], allow_slow_non_contiguous=True).then_inc(s_b3, 16)
                act.wait_ge(s_b3, 16)

            @block.vector
            def _(dve):
                dve.wait_ge(s_id, 1)
                for c in range(HC):
                    dve.tensor_copy(e_up[:, 0, c * P:(c + 1) * P], ident[:, :])
                dve.drain()
                for s in range(LOW):
                    dve.wait_ge(s_wu, 16 * (s + 1))
                    low_stage(dve, e_up, w_up, tmp_up, s)
                    dve.drain().then_inc(s_up, 1)
                dve.wait_ge(s_mmc, HC)
                dve.tensor_copy(wT[:, :, D:D + 1], ps_b[:, :].rearrange("p (h o) -> p h o", o=1))
                dve.drain()
                for s in range(TOP):
                    across(dve, wT, col_up, s, D + 1, False)
                dve.tensor_tensor(upb[:, :], upb[:, :], wT[:, :, D], ALU.add)
                dve.drain().then_inc(s_hi, 1)
                dve.wait_ge(s_wc, 16)
                for s in reversed(range(TOP)):
                    across(dve, wc, col_dn, s, D, True)
                dve.drain().then_inc(s_dhi, 1)
        st.clear()


def stage_attention(nc, A, x1_out, qt_out):
    SLOTS = 4
    with ExitStack() as ctx:
        st = Stage(nc, ctx, "at")
        sb, psum, sem = st.sb, st.psum, st.sem
        ident = sb("ident", [P, P])
        ones = sb("ones", [P, P])
        wq = sb("wq", [P, DC, D])
        wk = sb("wk", [P, DC, D])
        wv = sb("wv", [P, DC, D])
        wo = sb("wo", [P, DC, D])
        wxq = sb("wxq", [P, DC, P])
        bq = sb("bq", [P, DC])
        bk = sb("bk", [P, DC])
        bv = sb("bv", [P, DC])
        bvw = sb("bvw", [P, DC, P])
        bo = sb("bo", [P, D])
        wqT = sb("wqT", [P, DC, D])
        wkT = sb("wkT", [P, DC, D])
        wvT = sb("wvT", [P, DC, D])
        m_qk = sb("m_qk", [P, DC, D])
        w_vo = sb("w_vo", [P, DC, D])
        u_k = sb("u_k", [P, DC])
        u_q = sb("u_q", [P, DC])
        bqk = sb("bqk", [P, 1])
        b_row = sb("b_row", [P, D])
        w_own = sb("w_own", [P, TPB])
        w_oth = sb("w_oth", [P, TPB])
        neghalf = sb("neghalf", [P, 1])
        xk = sb("xk", [P, SLOTS, 2, D])
        xq = sb("xq", [P, SLOTS, D])
        xT = sb("xT", [P, 2, DC, 2 * P])
        tT = sb("tT", [P, DC, P])
        crow = sb("crow", [P, 2, 1])
        sc = sb("sc", [P, 2, 2 * P])
        mx = sb("mx", [P, 2, 2])
        p1 = sb("p1", [P, P])
        p2 = sb("p2", [P, P])
        den = sb("den", [P, 2, 2])
        rec = sb("rec", [P, 2])
        att = sb("att", [P, 2 * P])
        attT = sb("attT", [P, 2, P])
        oT = sb("oT", [P, DC, P])
        res = sb("res", [P, D])
        stats = sb("stats", [P, 6])
        mv = sb("mv", [P, 2])
        rstd = sb("rstd", [P, 1])
        x1 = sb("x1", [P, 2, D])
        x1T = sb("x1T", [P, DC, P])
        qhl = sb("qhl", [P, 2, 2, P], F32R)

        ps_x = psum("ps_x", [P, 2, 2 * 2 * P])
        ps_t = psum("ps_t", [P, DC, P])
        ps_s = psum("ps_s", [P, 4 * P])
        ps_c = psum("ps_c", [P, D])
        ps_x1 = psum("ps_x1", [P, DC, P])
        ps_o = psum("ps_o", [P, DC, P])
        ps_y = psum("ps_y", [P, D])

        s_w = sem("weights_loaded")
        s_const = sem("constants")
        s_wT = sem("weight_transposes")
        s_wTc = sem("weight_transposes_copied")
        s_fold = sem("folded")
        s_foldc = sem("folded_copied")
        s_bvw = sem("bv_widened")
        s_x = [sem(f"x_loaded{k}") for k in range(SLOTS)]
        s_xT = sem("x_transposed")
        s_xTc = sem("x_transposed_copied")
        s_t = sem("t_done")
        s_tc = sem("t_copied")
        s_s = sem("scores_done")
        s_crow = sem("score_bias")
        s_sc = sem("scores_copied")
        s_mx = sem("max_done")
        s_p = sem("probs_done")
        s_v = sem("vector_chain")
        s_att = sem("attention_done")
        s_aT = sem("attention_transposed")
        s_aTc = sem("attention_transposed_copied")
        s_o = sem("mix_done")
        s_oc = sem("mix_copied")
        s_y = sem("projected")
        s_var = sem("variance")
        s_rstd = sem("rstd")
        s_x1 = sem("x1_done")
        s_x1T = sem("x1_transposed")
        s_x1Tc = sem("x1_transposed_copied")
        s_q = sem("q_done")
        s_qh = sem("q_hi")
        s_ql = sem("q_lo")
        s_st = [sem(f"x1_stored{k}") for k in range(2)]
        s_sq = [sem(f"q_stored{k}") for k in range(2)]
        x_flat = A["x"].rearrange("b s d -> (b s) d")

        def batches(eng, tile):
            for j in range(TPB):
                tile(0, j, j == 0, False)
            with eng.Fori(1, B - 1) as b:
                for j in range(TPB):
                    tile(b, j, False, False)
            for j in range(TPB):
                tile(B - 1, j, False, j == TPB - 1)

        def after(b, j, d):
            bb, jj = b + (j + d) // TPB, (j + d) % TPB
            return bb, jj

        with nc.Block() as block:

            @block.sync
            def _(sp):
                for w, name in ((wq, "L0_attn_Wq"), (wk, "L0_attn_Wk"), (wv, "L0_attn_Wv"), (wo, "L0_attn_Wo")):
                    sp.dma_start(w[:, :, :], A[name].rearrange("(c p) n -> p c n", p=P)).then_inc(s_w, 16)
                sp.dma_start(wxq[:, :, :], A["L0_xattn_Wq"].rearrange("(c p) n -> p c n", p=P)).then_inc(s_w, 16)
                for v, name in ((bq, "L0_attn_bq"), (bk, "L0_attn_bk"), (bv, "L0_attn_bv")):
                    sp.dma_start(v[:, :], A[name].rearrange("(c p) -> p c", p=P), allow_slow_non_contiguous=True).then_inc(s_w, 16)
                sp.dma_start(bo[:, :], A["L0_attn_bo"].rearrange("(o n) -> o n", o=1).broadcast_to([P, D])).then_inc(s_w, 16)

                def load(b, j, first, last):
                    k, t0, i = j % SLOTS, b * S + j * P, b * TPB + j
                    if not (isinstance(b, int) and i < SLOTS):
                        sp.wait_ge(s_o, i - SLOTS + 1)
                        sp.wait_ge(s_x1, i - SLOTS + 1)
                    lo = t0 - 64 if j > 0 else t0
                    hi = t0 + P if j < TPB - 1 else t0 + P - 64
                    sp.dma_start(xk[0:64, k, 0, :], rows(x_flat, lo, 64)).then_inc(s_x[k], 16)
                    sp.dma_start(xk[64:128, k, 0, :], rows(x_flat, t0, 64)).then_inc(s_x[k], 16)
                    sp.dma_start(xk[0:64, k, 1, :], rows(x_flat, t0 + 64, 64)).then_inc(s_x[k], 16)
                    sp.dma_start(xk[64:128, k, 1, :], rows(x_flat, hi, 64)).then_inc(s_x[k], 16)
                    sp.dma_start(xq[:, k, :], rows(x_flat, t0, P)).then_inc(s_x[k], 16)

                batches(sp, load)

            @block.gpsimd
            def _(pool):
                pool.memset(ident[:, :], 0.0).then_inc(s_const, 1)
                pool.memset(ones[:, :], 1.0).then_inc(s_const, 1)
                pool.memset(neghalf[:, :], -0.5).then_inc(s_const, 1)
                pool.memset(att[:, :], 0.0).then_inc(s_const, 1)
                pool.wait_ge(s_const, 4)
                pool.affine_select(out=ident[:, :], in_=ident[:, :], compare_op=ALU.not_equal, fill=1.0,
                                   base=0, pattern=[[-1, P]], channel_multiplier=1).then_inc(s_const, 1)
                with pool.Fori(0, B) as b:
                    for j in range(TPB):
                        pool.wait_ge(s_var, b * TPB + j + 1)
                        pool.tensor_tensor(rstd[:, :], mv[:, 1:2], neghalf[:, :], ALU.pow).then_inc(s_rstd, 1)

            @block.tensor
            def _(pe):
                pe.wait_ge(s_const, 5)
                pe.wait_ge(s_w, 16 * 9)
                n = 0
                for w in (wq, wk, wv):
                    for c in range(DC):
                        if n >= 2:
                            pe.wait_ge(s_wTc, n - 1)
                        for e in range(DC):
                            last = pe.transpose(ps_x[:, n % 2, e * P:(e + 1) * P], w[:, c, e * P:(e + 1) * P], ident[:, :])
                        last.then_inc(s_wT, 1)
                        n += 1
                pe.wait_ge(s_wTc, 3 * DC)
                n = 0
                for wT, mv_ in ((wqT, wkT), (wvT, wo)):
                    for c in range(DC):
                        if n >= 2:
                            pe.wait_ge(s_foldc, n - 1)
                        for e in range(DC):
                            last = pe.matmul(ps_x[:, n % 2, :], wT[:, e, c * P:(c + 1) * P], mv_[:, e, :],
                                             start=(e == 0), stop=(e == DC - 1))
                        last.then_inc(s_fold, 1)
                        n += 1
                pe.wait_ge(s_bvw, 1)
                for i, (wT, v) in enumerate(((wkT, bq), (wqT, bk))):
                    for c in range(DC):
                        for e in range(DC):
                            pe.matmul(ps_c[:, i * DC + c:i * DC + c + 1], wT[:, e, c * P:(c + 1) * P], v[:, e:e + 1],
                                      start=(e == 0), stop=(e == DC - 1))
                for e in range(DC):
                    pe.matmul(ps_s[:, 0:1], oT[:, e, :], bk[:, e:e + 1], start=(e == 0), stop=(e == DC - 1))
                for e in range(DC):
                    last = pe.matmul(ps_y[:, :], bvw[:, e, :], wo[:, e, :], start=(e == 0), stop=(e == DC - 1))
                last.then_inc(s_fold, 1)
                pe.wait_ge(s_foldc, 2 * DC + 1)


                def x_turned(b, j):
                    k, i = j % 2, b * TPB + j
                    slot = j % SLOTS
                    pe.wait_ge(s_x[slot], 80 * (b * (TPB // SLOTS) + j // SLOTS + 1))
                    pe.wait_ge(s_xTc, i)
                    for c in range(DC):
                        for h in range(2):
                            last = pe.transpose(ps_x[:, c // 2, (c % 2) * 2 * P + h * P:(c % 2) * 2 * P + (h + 1) * P],
                                                xk[:, slot, h, c * P:(c + 1) * P], ident[:, :])
                    last.then_inc(s_xT, 1)

                def queries(b, j):
                    k, i = j % 2, b * TPB + j
                    pe.wait_ge(s_xTc, i + 1)
                    pe.wait_ge(s_tc, i)
                    if not (isinstance(i, int) and i < 3):
                        pe.wait_ge(s_ql, i - 2)
                    for m in range(DC):
                        for c in range(DC):
                            pe.matmul(ps_t[:, m, :], m_qk[:, c, m * P:(m + 1) * P], xT[:, k, c, 64:64 + P],
                                      start=(c == 0), stop=(c == DC - 1))
                    for c in range(DC):
                        last = pe.matmul(ps_c[:, 0:1], xT[:, k, c, 64:64 + P], u_q[:, c:c + 1],
                                         start=(c == 0), stop=(c == DC - 1))
                    last.then_inc(s_t, 1)

                def scores(b, j):
                    k, i = j % 2, b * TPB + j
                    pe.wait_ge(s_tc, i + 1)
                    pe.wait_ge(s_sc, i)
                    for c in range(DC):
                        last = pe.matmul(ps_s[:, 0:2 * P], tT[:, c, :], xT[:, k, c, :], start=(c == 0), stop=(c == DC - 1))
                    last.then_inc(s_s, 1)

                def x1_turned(i, k):
                    pe.wait_ge(s_x1, i + 1)
                    pe.wait_ge(s_x1Tc, i)
                    for c in range(DC):
                        last = pe.transpose(ps_x1[:, c, :], x1[:, k, c * P:(c + 1) * P], ident[:, :])
                    last.then_inc(s_x1T, 1)

                def cross_q(i):
                    pe.wait_ge(s_x1Tc, i + 1)
                    pe.wait_ge(s_crow, min(i + 3, TILES) if isinstance(i, int) else i + 3)
                    pe.wait_ge(s_ql, i)
                    for c in range(DC):
                        last = pe.matmul(ps_c[:, P:2 * P], wxq[:, c, :], x1T[:, c, :], start=(c == 0), stop=(c == DC - 1))
                    last.then_inc(s_q, 1)

                def tile(b, j, first, last):
                    i, slot = b * TPB + j, j % SLOTS
                    if not last:
                        queries(*after(b, j, 1))
                    pe.wait_ge(s_att, i + 1)
                    pe.wait_ge(s_aTc, i)
                    for h in range(2):
                        done = pe.transpose(ps_s[:, (2 + h) * P:(3 + h) * P], att[:, h * P:(h + 1) * P], ident[:, :])
                    done.then_inc(s_aT, 1)
                    if not first:
                        x1_turned(i - 1, (j + 1) % 2)
                    pe.wait_ge(s_aTc, i + 1)
                    pe.wait_ge(s_oc, i)
                    for c in range(DC):
                        for h in range(2):
                            done = pe.matmul(ps_o[:, c, :], xk[:, slot, h, c * P:(c + 1) * P], attT[:, h, :],
                                             start=(h == 0), stop=(h == 1))
                    done.then_inc(s_o, 1)
                    if not first:
                        cross_q(i - 1)
                    if not last:
                        scores(*after(b, j, 1))
                        if not (isinstance(b, int) and i + 2 >= TILES):
                            x_turned(*after(b, j, 2))
                    pe.wait_ge(s_oc, i + 1)
                    pe.wait_ge(s_x1, i)
                    for c in range(DC):
                        done = pe.matmul(ps_y[:, :], oT[:, c, :], w_vo[:, c, :], start=(c == 0), stop=(c == DC - 1))
                    done.then_inc(s_y, 1)

                x_turned(0, 0)
                queries(0, 0)
                scores(0, 0)
                x_turned(0, 1)
                batches(pe, tile)
                x1_turned(TILES - 1, 1)
                cross_q(TILES - 1)

            @block.scalar
            def _(act):
                n = 0
                for wT in (wqT, wkT, wvT):
                    for c in range(DC):
                        act.wait_ge(s_wT, n + 1)
                        act.activation(wT[:, :, c * P:(c + 1) * P], ps_x[:, n % 2, :].rearrange("p (e q) -> p e q", e=DC),
                                       ACT.Copy).then_inc(s_wTc, 1)
                        n += 1
                n = 0
                for w in (m_qk, w_vo):
                    for c in range(DC):
                        act.wait_ge(s_fold, n + 1)
                        act.activation(w[:, c, :], ps_x[:, n % 2, :], ACT.Copy).then_inc(s_foldc, 1)
                        n += 1

                def x_copied(i, k):
                    act.wait_ge(s_xT, i + 1)
                    if not (isinstance(i, int) and i < 2):
                        act.wait_ge(s_s, i - 1)
                    for h in range(2):
                        act.activation(xT[:, k, 2 * h:2 * h + 2, :], ps_x[:, h, :].rearrange("p (c q) -> p c q", c=2),
                                       ACT.Copy)
                    act.drain().then_inc(s_xTc, 1)

                def scores_copied(i, k):
                    act.wait_ge(s_s, i + 1)
                    act.wait_ge(s_crow, i + 1)
                    act.activation(sc[:, k, :], ps_s[:, 0:2 * P], ACT.Identity, bias=crow[:, k, :], scale=SCALE).then_inc(s_sc, 1)

                def exponentials(i, k):
                    act.wait_ge(s_mx, i + 1)
                    act.wait_ge(s_att, i)
                    act.activation(p1[:, :], sc[:, k, 64:64 + P], ACT.Exp, bias=mx[:, k, 0:1], accum_out=den[:, k, 0:1])
                    act.activation(p2[0:64, :], sc[0:64, k, 0:P], ACT.Exp, bias=mx[0:64, k, 1:2], accum_out=den[0:64, k, 1:2])
                    act.activation(p2[64:128, :], sc[64:128, k, P:2 * P], ACT.Exp, bias=mx[64:128, k, 1:2],
                                   accum_out=den[64:128, k, 1:2]).then_inc(s_p, 1)

                def x1_copied(i):
                    act.wait_ge(s_x1T, i + 1)
                    act.wait_ge(s_q, i)
                    act.activation(x1T[:, :, :], ps_x1[:, :, :], ACT.Copy).then_inc(s_x1Tc, 1)

                def q_hi(i, k, stores):
                    act.wait_ge(s_q, i + 1)
                    act.wait_ge(s_sq[k], 32 * stores)
                    act.activation(qhl[:, k, 0, :], ps_c[:, P:2 * P], ACT.Copy).then_inc(s_qh, 1)

                def store(i, k):
                    act.wait_ge(s_ql, i + 1)
                    act.dma_start(rows(x1_out, i * P, P), x1[:, k, :]).then_inc(s_st[k], 16)
                    for hl in range(2):
                        act.dma_start(qt_out[hl, :, bass.ds(i * P, P)], qhl[:, k, hl, :].bitcast(F32)).then_inc(s_sq[k], 16)

                def tile(b, j, first, last):
                    i, k = b * TPB + j, j % 2
                    act.wait_ge(s_aT, i + 1)
                    act.wait_ge(s_o, i)
                    act.activation(attT[:, :, :], ps_s[:, 2 * P:4 * P].rearrange("p (h q) -> p h q", h=2), ACT.Copy).then_inc(s_aTc, 1)
                    if not first:
                        x1_copied(i - 1)
                    act.wait_ge(s_o, i + 1)
                    act.wait_ge(s_y, i)
                    act.activation(oT[:, :, :], ps_o[:, :, :], ACT.Copy).then_inc(s_oc, 1)
                    if not first:
                        q_hi(i - 1, 1 - k, b * (TPB // 2) + (j - 1) // 2)
                    if not last:
                        scores_copied(i + 1, 1 - k)
                        if not (isinstance(b, int) and i + 2 >= TILES):
                            x_copied(i + 2, k)
                        exponentials(i + 1, 1 - k)
                    if not first:
                        store(i - 1, 1 - k)

                x_copied(0, 0)
                scores_copied(0, 0)
                x_copied(1, 1)
                exponentials(0, 0)
                batches(act, tile)
                x1_copied(TILES - 1)
                q_hi(TILES - 1, 1, TILES // 2 - 1)
                store(TILES - 1, 1)
                for k in range(2):
                    act.wait_ge(s_st[k], 16 * TILES // 2)
                    act.wait_ge(s_sq[k], 32 * TILES // 2)

            @block.vector
            def _(dve):
                dve.wait_ge(s_const, 5)
                dve.wait_ge(s_w, 16 * 9)
                for w in (w_own, w_oth):
                    dve.memset(w[:, :], 0.5)
                dve.drain()
                for w, val in ((w_own, 1.0), (w_oth, 0.0)):
                    dve.memset(w[0:64, 0:1], val)
                    dve.memset(w[64:128, TPB - 1:TPB], val)
                for c in range(DC):
                    dve.tensor_scalar(bvw[:, c, :], ones[:, :], bv[:, c:c + 1], None, ALU.mult)
                    last = dve.tensor_scalar(oT[:, c, :], ones[:, :], bq[:, c:c + 1], None, ALU.mult)
                last.then_inc(s_bvw, 1)
                dve.wait_ge(s_fold, 2 * DC + 1)
                dve.tensor_copy(u_k[:, :], ps_c[:, 0:DC])
                dve.tensor_copy(u_q[:, :], ps_c[:, DC:2 * DC])
                dve.tensor_copy(bqk[:, :], ps_s[:, 0:1])
                dve.tensor_tensor(b_row[:, :], ps_y[:, :], bo[:, :], ALU.add).then_inc(s_foldc, 1)

                def queries_copied(i, k):
                    dve.wait_ge(s_t, i + 1)
                    dve.wait_ge(s_s, i)
                    dve.tensor_scalar(crow[:, k, :], ps_c[:, 0:1], bqk[:, 0:1], SCALE, ALU.add, ALU.mult).then_inc(s_crow, 1)
                    for m in range(DC):
                        dve.tensor_scalar(tT[:, m, :], ps_t[:, m, :], u_k[:, m:m + 1], None, ALU.add)
                    dve.drain().then_inc(s_tc, 1)

                def softmax(i, j):
                    k = j % 2
                    dve.wait_ge(s_sc, i + 1)
                    dve.tensor_reduce(mx[:, k, 0:1], sc[:, k, 64:64 + P], AX.X, ALU.max, negate=True)
                    dve.tensor_reduce(mx[0:64, k, 1:2], sc[0:64, k, 0:P], AX.X, ALU.max, negate=True)
                    dve.tensor_reduce(mx[64:128, k, 1:2], sc[64:128, k, P:2 * P], AX.X, ALU.max, negate=True)
                    dve.drain().then_inc(s_mx, 1)
                    dve.wait_ge(s_p, i + 1)
                    dve.reciprocal(rec[:, :], den[:, k, :])
                    dve.drain()
                    dve.tensor_tensor(rec[:, 0:1], rec[:, 0:1], w_own[:, j:j + 1], ALU.mult)
                    dve.tensor_tensor(rec[:, 1:2], rec[:, 1:2], w_oth[:, j:j + 1], ALU.mult)
                    dve.drain()
                    dve.wait_ge(s_aT, i)
                    dve.tensor_scalar(att[:, 64:64 + P], p1[:, :], rec[:, 0:1], None, ALU.mult)
                    dve.tensor_scalar(att[0:64, 0:64], p2[0:64, 0:64], rec[0:64, 1:2], None, ALU.mult)
                    dve.tensor_scalar(att[64:128, 192:256], p2[64:128, 64:128], rec[64:128, 1:2], None, ALU.mult)
                    dve.drain()
                    dve.scalar_tensor_tensor(out=att[0:64, 64:128], in0=p2[0:64, 64:128], scalar=rec[0:64, 1:2],
                                             in1=att[0:64, 64:128], op0=ALU.mult, op1=ALU.add)
                    dve.scalar_tensor_tensor(out=att[64:128, 128:192], in0=p2[64:128, 0:64], scalar=rec[64:128, 1:2],
                                             in1=att[64:128, 128:192], op0=ALU.mult, op1=ALU.add)
                    dve.drain().then_inc(s_att, 1)

                def q_lo(i, k):
                    dve.wait_ge(s_qh, i + 1)
                    dve.tensor_tensor(qhl[:, k, 1, :], ps_c[:, P:2 * P], qhl[:, k, 0, :].bitcast(F32), ALU.subtract)\
                       .then_inc(s_ql, 1)

                def tile(b, j, first, last):
                    i, k, slot = b * TPB + j, j % 2, j % SLOTS
                    if not last:
                        queries_copied(i + 1, 1 - k)
                    if not first:
                        q_lo(i - 1, 1 - k)
                    if not last:
                        softmax(i + 1, (j + 1) % TPB)
                    dve.wait_ge(s_y, i + 1)
                    dve.tensor_tensor(res[:, :], ps_y[:, :], xq[:, slot, :], ALU.add)
                    dve.drain()
                    dve.tensor_tensor(res[:, :], res[:, :], b_row[:, :], ALU.add)
                    dve.drain()
                    dve.bn_stats(stats[:, :], res[:, :])
                    dve.drain()
                    dve.bn_aggr(mv[:, :], stats[:, :])
                    dve.drain()
                    dve.tensor_scalar(mv[:, 1:2], mv[:, 1:2], EPS, None, ALU.add).then_inc(s_var, 1)
                    dve.wait_ge(s_rstd, i + 1)
                    dve.wait_ge(s_st[k], 16 * (b * (TPB // 2) + j // 2))
                    dve.tensor_scalar(x1[:, k, :], res[:, :], mv[:, 0:1], rstd[:, 0:1], ALU.subtract, ALU.mult)\
                       .then_inc(s_x1, 1)

                queries_copied(0, 0)
                softmax(0, 0)
                batches(dve, tile)
                q_lo(TILES - 1, 1)
        st.clear()


def stage_keys(nc, A, kt_out):
    GROUPS = B * S2 // 512
    with ExitStack() as ctx:
        st = Stage(nc, ctx, "ky")
        sb, psum, sem = st.sb, st.psum, st.sem
        ident = sb("ident", [P, P])
        wk = sb("wk", [P, VC, P])
        raw = sb("raw", [P, 2, 4, DV])
        cT = sb("cT", [P, 2, VC, 4 * P])
        khl = sb("khl", [P, 2, 2, 4 * P], F32R)
        ps_t = psum("ps_t", [P, VC, 4 * P])
        ps_k = psum("ps_k", [P, 2, 4 * P])

        s_const = sem("constants")
        s_ld = sem("weights_loaded")
        s_raw = [sem(f"ctx_loaded{k}") for k in range(2)]
        s_t = sem("ctx_transposed")
        s_tc = sem("ctx_transposed_copied")
        s_k = sem("k_done")
        s_hi = sem("k_hi")
        s_lo = sem("k_lo")
        s_st = [sem(f"k_stored{k}") for k in range(2)]
        keys = A["ctx_768"].rearrange("b g v -> (b g) v")

        with nc.Block() as block:

            @block.sync
            def _(sp):
                sp.dma_start(wk[:, :, :], A["L0_xattn_Wk"].rearrange("(c p) n -> p c n", p=P)).then_inc(s_ld, 16)

                def load(g, k):
                    sp.dma_start(raw[:, k, :, :], rows(keys, g * 512, 512).rearrange("(n p) v -> p n v", p=P)).then_inc(s_raw[k], 16)

                load(0, 0)
                load(1, 1)
                with sp.Fori(1, GROUPS // 2) as j:
                    for k in range(2):
                        sp.wait_ge(s_t, VC * (2 * j + k - 1))
                        load(2 * j + k, k)

            @block.gpsimd
            def _(pool):
                pool.memset(ident[:, :], 0.0)
                pool.drain()
                pool.affine_select(out=ident[:, :], in_=ident[:, :], compare_op=ALU.not_equal, fill=1.0,
                                   base=0, pattern=[[-1, P]], channel_multiplier=1)
                pool.drain().then_inc(s_const, 1)

            @block.tensor
            def _(pe):
                pe.wait_ge(s_const, 1)
                pe.wait_ge(s_ld, 16)

                def turn(g, k, nth):
                    pe.wait_ge(s_raw[k], 16 * nth)
                    for c in range(VC):
                        pe.wait_ge(s_tc, VC * (g - 1) + c + 1) if not (isinstance(g, int) and g == 0) else None
                        for q in range(4):
                            last = pe.transpose(ps_t[:, c, q * P:(q + 1) * P], raw[:, k, q, c * P:(c + 1) * P], ident[:, :])
                        last.then_inc(s_t, 1)

                def project(g, k, first=False):
                    pe.wait_ge(s_tc, VC * (g + 1))
                    if not first:
                        pe.wait_ge(s_lo, g - 1)
                    for c in range(VC):
                        last = pe.matmul(ps_k[:, k, :], wk[:, c, :], cT[:, k, c, :], start=(c == 0), stop=(c == VC - 1))
                    last.then_inc(s_k, 1)

                turn(0, 0, 1)
                turn(1, 1, 1)
                project(0, 0, first=True)
                with pe.Fori(1, GROUPS // 2) as j:
                    turn(2 * j, 0, j + 1)
                    project(2 * j - 1, 1)
                    turn(2 * j + 1, 1, j + 1)
                    project(2 * j, 0)
                project(GROUPS - 1, 1)

            @block.scalar
            def _(act):
                def copies(g, k):
                    act.wait_ge(s_k, g - 1) if not (isinstance(g, int) and g == 0) else None
                    for c in range(VC):
                        act.wait_ge(s_t, VC * g + c + 1)
                        act.activation(cT[:, k, c, :], ps_t[:, c, :], ACT.Copy).then_inc(s_tc, 1)

                def hi(g, k, stores):
                    act.wait_ge(s_k, g + 1)
                    act.wait_ge(s_st[k], 16 * stores)
                    act.activation(khl[:, k, 0, :], ps_k[:, k, :], ACT.Copy).then_inc(s_hi, 1)

                def store(g, k):
                    act.wait_ge(s_lo, g + 1)
                    act.dma_start(kt_out[:, :, bass.ds(g * 512, 512)].rearrange("h p g -> p h g"),
                                  khl[:, k, :, :].bitcast(F32)).then_inc(s_st[k], 16)

                copies(0, 0)
                copies(1, 1)
                hi(0, 0, 0)
                with act.Fori(1, GROUPS // 2) as j:
                    copies(2 * j, 0)
                    store(2 * j - 2, 0)
                    hi(2 * j - 1, 1, j - 1)
                    copies(2 * j + 1, 1)
                    store(2 * j - 1, 1)
                    hi(2 * j, 0, j)
                store(GROUPS - 2, 0)
                hi(GROUPS - 1, 1, GROUPS // 2 - 1)
                store(GROUPS - 1, 1)
                for k in range(2):
                    act.wait_ge(s_st[k], 16 * GROUPS // 2)

            @block.vector
            def _(dve):
                with dve.Fori(0, GROUPS // 2) as j:
                    for k in range(2):
                        dve.wait_ge(s_hi, 2 * j + k + 1)
                        dve.tensor_tensor(khl[:, k, 1, :], ps_k[:, k, :], khl[:, k, 0, :].bitcast(F32), ALU.subtract).then_inc(s_lo, 1)
        st.clear()



def stage_cross(nc, A, qt_in, kt_in, ac_out):
    SEGS = 32
    SEG = S2 // SEGS
    NCAND = 8 * SEGS
    HT = HEADS * TPB
    with ExitStack() as ctx:
        st = Stage(nc, ctx, "xa")
        sb, psum, sem = st.sb, st.psum, st.sem
        ident = sb("ident", [P, P])
        raw = sb("raw", [P, 2, 4, DV])
        ctx_hl = sb("ctx_hl", [P, 2, GC, DV], F32R)
        ks = sb("ks", [P, HEADS, S2], F32R)
        qs = sb("qs", [P, 2, HEADS, P], F32R)
        row0 = sb("row0", [P, P], BF16)
        mask_u8 = sb("mask_u8", [1, S2], U8)
        mask = sb("mask", [P, S2], BF16)
        ones = sb("ones", [P, 1])
        s_buf = sb("s_buf", [P, 4, S2])
        cand = sb("cand", [P, NCAND])
        cand_b = sb("cand_b", [P, NCAND])
        top = sb("top", [P, 2, TOPK])
        f_junk = sb("f_junk", [P, NCAND + SEGS])
        f_acc = sb("f_acc", [P, 2])
        flag = sb("flag", [P, 2, 1])
        flag_i = sb("flag_i", [1, 2], mybir.dt.int32)
        nmax = sb("nmax", [P, 2, 1])
        e_top = sb("e_top", [P, TOPK])
        den = sb("den", [P, 2, 1])
        rec = sb("rec", [P, 2, 1])
        prob = sb("prob", [P, 2, S2])
        acc = sb("acc", [P, 2, S2])
        aT = sb("aT", [P, 2, GC, P], F32R)
        ac = sb("ac", [P, 2, DV])

        ps_s = psum("ps_s", [P, 4, 512])
        ps_t = psum("ps_t", [P, 2, 4, P])
        ps_ac = psum("ps_ac", [P, DV])
        ps_f = psum("ps_f", [1, 2])

        s_const = sem("constants")
        s_ms = sem("mask_loaded")
        s_mask = sem("mask_ready")
        s_raw = [sem(f"raw_loaded{k}") for k in range(2)]
        s_chi = sem("ctx_hi")
        s_clo = sem("ctx_lo")
        s_ks = [sem(f"k_stacked{h}") for h in range(HEADS)]
        s_qs = [sem(f"q_stacked{k}") for k in range(2)]
        s_s = sem("scores_done")
        s_sc = sem("scores_copied")
        s_cand = sem("row_flags_done")
        s_f = sem("flag_summed")
        s_chk = sem("tops_final")
        s_den = sem("denominator")
        s_rec = sem("reciprocal")
        s_scl = sem("scaled")
        s_prob = sem("prob_done")
        s_sel = sem("selected")
        s_acc = sem("heads_summed")
        s_aT = sem("attn_transposed")
        s_aTh = sem("attn_hi")
        s_aTl = sem("attn_lo")
        s_ac = sem("mix_done")
        s_acc_c = sem("mix_copied")
        s_st = [sem(f"mix_stored{k}") for k in range(2)]

        def steps(eng, body):
            with eng.Fori(0, B) as b:
                body(b, 0, True, False)
                with eng.Fori(1, TPB // 2 - 1) as j:
                    body(b, j, False, False)
                body(b, TPB // 2 - 1, False, True)

        with nc.Block() as block:

            @block.sync
            def _(sp):
                def keys(b, h):
                    for q in range(4):
                        sp.dma_start(ks[32 * q:32 * q + 32, h, :].bitcast(F32),
                                     kt_in[q % 2][h * DH:(h + 1) * DH, bass.ds(b * S2, S2)]).then_inc(s_ks[h], 16)

                def queries(b, j):
                    for k in range(2):
                        t = b * TPB + 2 * j + k
                        sp.wait_ge(s_s, HEADS * (t - 1))
                        for q in range(4):
                            sp.dma_start(qs[32 * q:32 * q + 32, k, :, :].bitcast(F32),
                                         qt_in[q // 2].rearrange("(h e) t -> e h t", e=DH)[:, :, bass.ds(t * P, P)]
                                         ).then_inc(s_qs[k], 16)

                for h in range(HEADS):
                    keys(0, h)
                for k in range(2):
                    for q in range(4):
                        sp.dma_start(qs[32 * q:32 * q + 32, k, :, :].bitcast(F32),
                                     qt_in[q // 2].rearrange("(h e) t -> e h t", e=DH)[:, :, k * P:(k + 1) * P]).then_inc(s_qs[k], 16)
                with sp.Fori(1, TPB // 2) as j:
                    queries(0, j)
                with sp.Fori(1, B) as b:
                    for h in range(HEADS):
                        sp.wait_ge(s_s, HT * b - HEADS + 1 + h)
                        keys(b, h)
                    with sp.Fori(0, TPB // 2) as j:
                        queries(b, j)

            @block.gpsimd
            def _(pool):
                pool.memset(ident[:, :], 0.0).then_inc(s_const, 1)
                pool.memset(ones[:, :], 1.0).then_inc(s_const, 1)
                pool.wait_ge(s_const, 2)
                pool.affine_select(out=ident[:, :], in_=ident[:, :], compare_op=ALU.not_equal, fill=1.0,
                                   base=0, pattern=[[-1, P]], channel_multiplier=1).then_inc(s_const, 1)
                with pool.Fori(0, TILES // 2) as j:
                    for k in range(2):
                        t = 2 * j + k
                        for h in range(1, HEADS):
                            pool.wait_ge(s_scl, HEADS * t + h + 1)
                            pool.wait_ge(s_acc, 3 * t + h - 1)
                            pool.tensor_tensor(acc[:, k, :], acc[:, k, :], prob[:, h % 2, :], ALU.add).then_inc(s_acc, 1)

            @block.tensor
            def _(pe):
                pe.wait_ge(s_const, 3)

                def scores(n, k, h):
                    pe.wait_ge(s_sc, n)
                    for c in range(4):
                        pe.matmul(ps_s[:, c, :], qs[:, k, h, :], ks[:, h, c * 512:(c + 1) * 512], start=True, stop=False)
                        last = pe.matmul(ps_s[:, c, :], row0[:, :], mask[:, c * 512:(c + 1) * 512], start=False, stop=True)
                    last.then_inc(s_s, 1)

                def sum_flag(n, k):
                    pe.wait_ge(s_cand, n + 1)
                    pe.matmul(ps_f[:, k:k + 1], flag[:, k, :], ones[:, :], start=True, stop=True).then_inc(s_f, 1)

                def turn(t, k, g):
                    if g == 0:
                        pe.wait_ge(s_acc, 3 * (t + 1))
                    pe.wait_ge(s_aTl, t * 4 + g - 1) if g >= 1 else pe.wait_ge(s_aTl, t * 4)
                    for q in range(4):
                        c = 4 * g + q
                        last = pe.transpose(ps_t[:, g % 2, q, :], acc[:, k, c * P:(c + 1) * P], ident[:, :])
                    last.then_inc(s_aT, 1)

                def mix(t, b):
                    pe.wait_ge(s_aTl, t * 4 + 4)
                    pe.wait_ge(s_clo, 4 * (b + 1))
                    pe.wait_ge(s_acc_c, t)
                    for c in range(GC):
                        last = mm3(pe, ps_ac[:, :], aT[:, 0, c, :], aT[:, 1, c, :],
                                   ctx_hl[:, 0, c, :], ctx_hl[:, 1, c, :], start=(c == 0), stop=(c == GC - 1))
                    last.then_inc(s_ac, 1)

                def body(b, j, first, last):
                    if first:
                        pe.wait_ge(s_ks[0], 64 * (b + 1))
                        pe.wait_ge(s_mask, b + 1)
                        pe.wait_ge(s_qs[0], 64 * (b * (TPB // 2) + 1))
                        scores(HT * b, 0, 0)
                    for s in range(2 * HEADS):
                        n = HT * b + 2 * HEADS * j + s
                        h = s % HEADS
                        if not (last and s == 2 * HEADS - 1):
                            if first and s < HEADS - 1:
                                pe.wait_ge(s_ks[s + 1], 64 * (b + 1))
                            k = (s + 1) // HEADS
                            if (s + 1) % HEADS == 0:
                                pe.wait_ge(s_qs[k % 2], 64 * (b * (TPB // 2) + j + 1 + k // 2))
                            scores(n + 1, k % 2, (s + 1) % HEADS)
                        if not (first and s < HEADS):
                            t, k = b * TPB + 2 * j + s // HEADS - 1, (s // HEADS + 1) % 2
                            if h in (1, 2):
                                turn(t, k, 2 * h - 2)
                                turn(t, k, 2 * h - 1)
                            if h == 3:
                                mix(t, b)
                        sum_flag(n, s % 2)
                    if last:
                        t = b * TPB + TPB - 1
                        for g in range(4):
                            turn(t, 1, g)
                        mix(t, b)

                steps(pe, body)

            @block.scalar
            def _(act):
                def load(b, g):
                    act.wait_ge(s_clo, 4 * b + g - 1 if g >= 2 else 4 * b)
                    act.dma_start(raw[:, g % 2, :, :],
                                  rows(A["ctx_768"], b, 1)[:, g * 512:(g + 1) * 512, :].rearrange("o (n p) v -> p (o n) v", p=P)
                                  ).then_inc(s_raw[g % 2], 16)

                def copy(n, slot, fresh):
                    act.wait_ge(s_s, n + 1)
                    if not fresh:
                        act.wait_ge(s_sel, n - 3)
                    act.activation(s_buf[:, slot, :], ps_s[:, :, :].rearrange("p c n -> p (c n)"), ACT.Copy).then_inc(s_sc, 1)

                def scale(n, t, k, h, fresh):
                    act.wait_ge(s_sel, n + 1)
                    if h == 0 and not fresh:
                        act.wait_ge(s_aT, 4 * (t - 1))
                    act.activation(acc[:, k, :] if h == 0 else prob[:, h % 2, :], prob[:, h % 2, :], ACT.Identity,
                                   scale=rec[:, h % 2, :]).then_inc(s_scl, 1)

                def exponentials(n, t, h, begin=False):
                    act.wait_ge(s_chk, n + 1)
                    act.activation(e_top[:, :], top[:, h % 2, :], ACT.Exp, bias=nmax[:, h % 2, :], scale=SCALE,
                                   accum_out=den[:, h % 2, :]).then_inc(s_den, 1)
                    if h == 0:
                        act.wait_ge(s_acc, 3 * t - 1 if not begin else 3 * t)
                    if h == 1:
                        act.wait_ge(s_acc, 3 * t)
                    if h == 2:
                        act.wait_ge(s_scl, n - 1)
                    if h == 3:
                        act.wait_ge(s_acc, 3 * t + 1)
                    act.activation(prob[:, h % 2, :], s_buf[:, h, :], ACT.Exp, bias=nmax[:, h % 2, :], scale=SCALE).then_inc(s_prob, 1)

                def hi(t, g):
                    act.wait_ge(s_aT, 4 * t + g + 1)
                    act.wait_ge(s_ac, t)
                    act.activation(aT[:, 0, 4 * g:4 * g + 4, :], ps_t[:, g % 2, :, :], ACT.Copy).then_inc(s_aTh, 1)

                def mixed(t, k, stores):
                    act.wait_ge(s_ac, t + 1)
                    act.wait_ge(s_st[k], 16 * stores)
                    act.activation(ac[:, k, :], ps_ac[:, :], ACT.Copy, scale=1.0 / HEADS).then_inc(s_acc_c, 1)
                    act.wait_ge(s_acc_c, t + 1)
                    act.dma_start(rows(ac_out, t * P, P), ac[:, k, :]).then_inc(s_st[k], 16)

                def body(b, j, first, last):
                    if first:
                        act.wait_ge(s_s, b * HT)
                        act.dma_start(mask_u8[:, :], rows(A["mask_BxS2_bf1"], b, 1)).then_inc(s_ms, 16)
                        load(b, 0)
                        load(b, 1)
                        for g in range(4):
                            act.wait_ge(s_raw[g % 2], 16 * (2 * b + g // 2 + 1))
                            act.wait_ge(s_ac, b * TPB)
                            act.activation(ctx_hl[:, 0, 4 * g:4 * g + 4, :], raw[:, g % 2, :, :], ACT.Copy).then_inc(s_chi, 1)
                            if g < 2:
                                load(b, g + 2)
                            if g == 1:
                                copy(HT * b, 0, True)
                    for s in range(2 * HEADS):
                        n = HT * b + 2 * HEADS * j + s
                        t, h = b * TPB + 2 * j + s // HEADS, s % HEADS
                        if not (last and s == 2 * HEADS - 1):
                            copy(n + 1, (s + 1) % 4, first and s < 3)
                        if not (first and s == 0):
                            scale(n - 1, t - 1 if h == 0 else t, (s - 1) // HEADS % 2, (s - 1) % HEADS, first)
                        if not (first and s < HEADS):
                            if h in (1, 2):
                                hi(t - 1, 2 * h - 2)
                                hi(t - 1, 2 * h - 1)
                        exponentials(n, t, h, first and s == 0)
                        if h == 0 and not (first and s < 2 * HEADS):
                            mixed(t - 2, s // HEADS, b * (TPB // 2) + j - 1)
                    if last:
                        t = b * TPB + TPB - 1
                        scale(HT * (b + 1) - 1, t, 1, HEADS - 1, False)
                        mixed(t - 1, 0, b * (TPB // 2) + TPB // 2 - 1)
                        for g in range(4):
                            hi(t, g)
                        mixed(t, 1, b * (TPB // 2) + TPB // 2 - 1)

                steps(act, body)
                for k in range(2):
                    act.wait_ge(s_st[k], 16 * TILES // 2)

            @block.vector
            def _(dve):
                dve.memset(mask[:, :], 0.0)
                dve.memset(row0[:, :], 0.0)
                dve.drain()
                dve.memset(row0[0:1, :], 1.0)
                def candidates(n, k, slot):
                    dve.wait_ge(s_sc, n + 1)
                    dve.memset(f_acc[:, :], 0.0)
                    for g in range(SEGS):
                        dve.max(out=cand[:, 8 * g:8 * g + 8], in_=s_buf[:, slot, g * SEG:(g + 1) * SEG])
                    dve.drain()
                    src = cand
                    for r in range(TOPK // 8):
                        dve.max(out=top[:, k, 8 * r:8 * r + 8], in_=src[:, :])
                        dve.drain()
                        if r < TOPK // 8 - 1:
                            dve.match_replace(out=cand_b[:, :], in_to_replace=top[:, k, 8 * r:8 * r + 8], in_values=src[:, :],
                                              imm_value=TAKEN)
                            dve.drain()
                        src = cand_b
                    t32 = top[:, k, TOPK - 1:TOPK]
                    dve.tensor_scalar(f_junk[:, 0:NCAND], cand[:, :], t32, None, ALU.is_ge, ALU.add, accum_out=f_acc[:, 0:1])
                    dve.tensor_scalar(f_junk[:, NCAND:NCAND + SEGS], cand[:, :].rearrange("p (g e) -> p g e", e=8)[:, :, 7], t32, None,
                                      ALU.is_ge, ALU.add, accum_out=f_acc[:, 1:2])
                    dve.tensor_scalar(nmax[:, k, :], top[:, k, 0:1], -SCALE, None, ALU.mult)
                    dve.drain()
                    dve.tensor_scalar(flag[:, k, :], f_acc[:, 0:1], f_acc[:, 1:2], float(-TOPK), ALU.add, ALU.add).then_inc(s_cand, 1)

                def settle(n, k, slot):
                    dve.wait_ge(s_f, n + 1)
                    dve.tensor_copy(flag_i[:, k:k + 1], ps_f[:, k:k + 1])
                    dve.drain()
                    doubt = dve.value_load(flag_i[0:1, k:k + 1], min_val=0, max_val=P * NCAND * 2)
                    with dve.If(doubt > 0):
                        left = prob[:, k, :]
                        src = s_buf[:, slot, :]
                        for r in range(TOPK // 8):
                            dve.max(out=top[:, k, 8 * r:8 * r + 8], in_=src)
                            dve.drain()
                            dve.match_replace(out=left, in_to_replace=top[:, k, 8 * r:8 * r + 8], in_values=src,
                                              imm_value=TAKEN)
                            dve.drain()
                            src = left
                        dve.tensor_scalar(left, left, 0.5 * TAKEN, -2.0 * BIG, ALU.is_ge, ALU.mult)
                        dve.drain()
                        dve.tensor_tensor(s_buf[:, slot, :], s_buf[:, slot, :], left, ALU.add)
                    dve.drain().then_inc(s_chk, 1)

                def select(n, k, slot):
                    dve.wait_ge(s_den, n + 1)
                    dve.reciprocal(rec[:, k, :], den[:, k, :])
                    dve.wait_ge(s_prob, n + 1)
                    dve.scalar_tensor_tensor(out=prob[:, k, :], in0=s_buf[:, slot, :], scalar=top[:, k, TOPK - 1:TOPK],
                                             in1=prob[:, k, :], op0=ALU.is_ge, op1=ALU.mult)
                    dve.drain().then_inc(s_sel, 1)

                def lo(t, g):
                    dve.wait_ge(s_aTh, 4 * t + g + 1)
                    dve.tensor_tensor(aT[:, 1, 4 * g:4 * g + 4, :], ps_t[:, g % 2, :, :],
                                      aT[:, 0, 4 * g:4 * g + 4, :].bitcast(F32), ALU.subtract).then_inc(s_aTl, 1)

                def body(b, j, first, last):
                    if first:
                        dve.wait_ge(s_ms, 16 * (b + 1))
                        dve.tensor_scalar(mask[0:1, :], mask_u8[:, :], BIG, -BIG, ALU.mult, ALU.add).then_inc(s_mask, 1)
                        for g in range(4):
                            dve.wait_ge(s_chi, 4 * b + g + 1)
                            dve.tensor_tensor(ctx_hl[:, 1, 4 * g:4 * g + 4, :], raw[:, g % 2, :, :],
                                              ctx_hl[:, 0, 4 * g:4 * g + 4, :].bitcast(F32), ALU.subtract).then_inc(s_clo, 1)
                    for s in range(2 * HEADS):
                        n = HT * b + 2 * HEADS * j + s
                        t, h = b * TPB + 2 * j + s // HEADS, s % HEADS
                        candidates(n, s % 2, s % 4)
                        if not (first and s == 0):
                            select(n - 1, (s - 1) % 2, (s - 1) % 4)
                        if not (first and s < HEADS) and h in (1, 2):
                            lo(t - 1, 2 * h - 2)
                            lo(t - 1, 2 * h - 1)
                        if h == 0 and not (first and s == 0):
                            dve.wait_ge(s_acc, 3 * t - 1)
                        if h == 1:
                            dve.wait_ge(s_acc, 3 * t)
                        if h == 2:
                            dve.wait_ge(s_scl, n - 1)
                        if h == 3:
                            dve.wait_ge(s_acc, 3 * t + 1)
                        settle(n, s % 2, s % 4)
                    if last:
                        select(HT * (b + 1) - 1, 1, 3)
                        for g in range(4):
                            lo(b * TPB + TPB - 1, g)

                steps(dve, body)
        st.clear()



def stage_film(nc, A, x1_in, ac_in, xin_out, so_out, sh_out):
    NF = 4
    SLOTS = 4
    with ExitStack() as ctx:
        st = Stage(nc, ctx, "fi")
        sb, psum, sem = st.sb, st.psum, st.sem
        ident = sb("ident", [P, P])
        neghalf = sb("neghalf", [P, 1])
        gate = sb("gate", [P, 1])
        wv = sb("wv", [P, VC, D])
        wvT = sb("wvT", [P, DC, DV])
        wfilm = sb("wfilm", [P, DC, 2 * D])
        wf = sb("wf", [P, 2, VC, NF, D], F32R)
        bf = sb("bf", [P, NF, D])
        g_in = sb("g_in", [P, D])
        b_in = sb("b_in", [P, D])
        x1 = sb("x1", [P, SLOTS, D])
        ac = sb("ac", [P, SLOTS, DV])
        mask_u8 = sb("mask_u8", [P, SLOTS, 1], U8)
        mask = sb("mask", [P, SLOTS, 1])
        aT = sb("aT", [P, 2, 2, VC, P], F32R)
        stats = sb("stats", [P, 6])
        mv = sb("mv", [P, 2])
        rstd = sb("rstd", [P, 1])
        xn = sb("xn", [P, SLOTS, D])
        mod = sb("mod", [P, 2, NF, D])

        ps_t = psum("ps_t", [P, 2, 512])
        ps_f = psum("ps_f", [P, NF, D])
        ps_w = psum("ps_w", [P, 2, 512])

        s_const = sem("constants")
        s_ld = sem("weights_loaded")
        s_lo_ = sem("film_out_loaded")
        s_wT = sem("wv_transposed")
        s_wTc = sem("wv_transposed_copied")
        s_fold = sem("folded")
        s_foh = sem("folded_hi")
        s_fol = sem("folded_lo")
        s_bf = sem("biases_ready")
        s_in = [sem(f"tile_loaded{k}") for k in range(SLOTS)]
        s_t = sem("ac_transposed")
        s_th = sem("ac_hi")
        s_tl = sem("ac_lo")
        s_f = sem("film_done")
        s_fr = sem("film_read")
        s_var = sem("variance")
        s_rstd = sem("rstd")
        s_xn = sem("normalised")
        s_x = sem("input_done")
        s_st = [sem(f"stored{k}") for k in range(2)]

        def bcast(name, n, off=0):
            return A[name].rearrange("(o n) -> o n", o=1)[:, off:off + n].broadcast_to([P, n])

        def tiles(eng, tile):
            for k in range(SLOTS):
                tile(k, 0, k, k == 0, False)
            with eng.Fori(1, TILES // SLOTS - 1) as j:
                for k in range(SLOTS):
                    tile(SLOTS * j + k, j, k, False, False)
            for k in range(SLOTS):
                tile(TILES - SLOTS + k, TILES // SLOTS - 1, k, False, k == SLOTS - 1)

        with nc.Block() as block:

            @block.sync
            def _(sp):
                sp.dma_start(gate[:, :], A["L0_xattn_mod_gate"].rearrange("(o n) -> o n", o=1).broadcast_to([P, 1])).then_inc(s_ld, 16)
                sp.dma_start(wv[:, :, :], A["L0_xattn_Wv"].rearrange("(c p) n -> p c n", p=P)).then_inc(s_ld, 16)
                sp.dma_start(wfilm[:, :, :], A["L0_xattn_W_film_in"].rearrange("(c p) n -> p c n", p=P)).then_inc(s_ld, 16)
                sp.dma_start(g_in[:, :], bcast("L0_xattn_g_norm_in", D)).then_inc(s_ld, 16)
                sp.dma_start(b_in[:, :], bcast("L0_xattn_b_norm_in", D)).then_inc(s_ld, 16)
                for i, name in enumerate(("L0_xattn_b_film_in", "L0_xattn_b_film_out")):
                    sp.dma_start(bf[:, 2 * i:2 * i + 2, :].rearrange("p a n -> p (a n)"), bcast(name, 2 * D)).then_inc(s_ld, 16)
                sp.wait_ge(s_fold, 6)
                sp.dma_start(wfilm[:, :, :], A["L0_xattn_W_film_out"].rearrange("(c p) n -> p c n", p=P)).then_inc(s_lo_, 16)

            @block.gpsimd
            def _(pool):
                pool.memset(ident[:, :], 0.0)
                pool.memset(neghalf[:, :], -0.5)
                pool.drain()
                pool.affine_select(out=ident[:, :], in_=ident[:, :], compare_op=ALU.not_equal, fill=1.0,
                                   base=0, pattern=[[-1, P]], channel_multiplier=1)
                pool.drain().then_inc(s_const, 1)

                def base(t, k):
                    pool.wait_ge(s_var, t + 1)
                    pool.tensor_tensor(rstd[:, :], mv[:, 1:2], neghalf[:, :], ALU.pow).then_inc(s_rstd, 1)
                    pool.wait_ge(s_xn, t + 1)
                    pool.tensor_tensor(xn[:, k, :], xn[:, k, :], g_in[:, :], ALU.mult)
                    pool.drain()
                    pool.tensor_tensor(xn[:, k, :], xn[:, k, :], b_in[:, :], ALU.add)
                    pool.drain()

                def tile(t, j, k, first, last):
                    if not last:
                        base(t + 1, (k + 1) % SLOTS)
                    pool.wait_ge(s_fr, NF * t + 2)
                    pool.tensor_tensor(xn[:, k, :], xn[:, k, :], mod[:, k % 2, 0, :], ALU.mult)
                    pool.drain()
                    pool.tensor_tensor(xn[:, k, :], xn[:, k, :], mod[:, k % 2, 1, :], ALU.add).then_inc(s_x, 1)

                base(0, 0)
                tiles(pool, tile)

            @block.tensor
            def _(pe):
                pe.wait_ge(s_const, 1)
                pe.wait_ge(s_ld, 16 * 7)
                for c in range(VC):
                    if c >= 2:
                        pe.wait_ge(s_wTc, c - 1)
                    for e in range(DC):
                        last = pe.transpose(ps_w[:, c % 2, e * P:(e + 1) * P], wv[:, c, e * P:(e + 1) * P], ident[:, :])
                    last.then_inc(s_wT, 1)
                pe.wait_ge(s_wTc, VC)
                n = 0
                for half in range(2):
                    if half:
                        pe.wait_ge(s_lo_, 16)
                    for q in range(2):
                        for c in range(VC):
                            if n >= 2:
                                pe.wait_ge(s_fol, n - 1)
                            for e in range(DC):
                                last = pe.matmul(ps_w[:, n % 2, :], wvT[:, e, c * P:(c + 1) * P], wfilm[:, e, q * D:(q + 1) * D],
                                                 start=(e == 0), stop=(e == DC - 1))
                            last.then_inc(s_fold, 1)
                            n += 1
                pe.wait_ge(s_fol, NF * VC)

                def film(t, k, first):
                    pe.wait_ge(s_tl, t + 1)
                    for f in range(NF):
                        if not first:
                            pe.wait_ge(s_fr, NF * (t - 1) + f + 1)
                        for c in range(VC):
                            last = mm3(pe, ps_f[:, f, :], aT[:, k, 0, c, :], aT[:, k, 1, c, :],
                                       wf[:, 0, c, f, :], wf[:, 1, c, f, :], start=(c == 0), stop=(c == VC - 1))
                        last.then_inc(s_f, 1)

                def turn(t, k, loads):
                    pe.wait_ge(s_in[k], 48 * loads)
                    if not (isinstance(t, int) and t < 2):
                        pe.wait_ge(s_tl, t - 1)
                    for c in range(VC):
                        last = pe.transpose(ps_t[:, k % 2, c * P:(c + 1) * P], ac[:, k, c * P:(c + 1) * P], ident[:, :])
                    last.then_inc(s_t, 1)

                def tile(t, j, k, first, last):
                    if not last:
                        turn(t + 1, (k + 1) % SLOTS, j + (k + 1) // SLOTS + 1)
                    film(t, k % 2, first)

                turn(0, 0, 1)
                tiles(pe, tile)

            @block.scalar
            def _(act):
                for c in range(VC):
                    act.wait_ge(s_wT, c + 1)
                    act.activation(wvT[:, :, c * P:(c + 1) * P], ps_w[:, c % 2, :].rearrange("p (e q) -> p e q", e=DC),
                                   ACT.Copy).then_inc(s_wTc, 1)
                n = 0
                for f in range(NF):
                    for c in range(VC):
                        act.wait_ge(s_fold, n + 1)
                        act.activation(wf[:, 0, c, f, :], ps_w[:, n % 2, :], ACT.Identity, scale=gate[:, 0:1]).then_inc(s_foh, 1)
                        n += 1

                text_mask = A["mask_BxS_bf1"].rearrange("b (s o) -> (b s) o", o=1)

                def load(t, k, fresh=False):
                    if not fresh:
                        act.wait_ge(s_xn, t - SLOTS + 1)
                        act.wait_ge(s_t, t - SLOTS + 1)
                        act.wait_ge(s_fr, NF * (t - SLOTS + 1))
                    act.dma_start(x1[:, k, :], rows(x1_in, t * P, P)).then_inc(s_in[k], 16)
                    act.dma_start(ac[:, k, :], rows(ac_in, t * P, P)).then_inc(s_in[k], 16)
                    act.dma_start(mask_u8[:, k, :], rows(text_mask, t * P, P)).then_inc(s_in[k], 16)

                def hi(t, k):
                    act.wait_ge(s_t, t + 1)
                    if not (isinstance(t, int) and t < 2):
                        act.wait_ge(s_f, NF * (t - 1))
                    act.activation(aT[:, k, 0, :, :].rearrange("p c q -> p (c q)"), ps_t[:, k, 0:DV], ACT.Copy).then_inc(s_th, 1)

                def store(t, k):
                    act.wait_ge(s_fr, NF * (t + 1))
                    act.dma_start(rows(so_out, t * P, P), mod[:, k % 2, 2, :]).then_inc(s_st[k % 2], 16)
                    act.dma_start(rows(sh_out, t * P, P), mod[:, k % 2, 3, :]).then_inc(s_st[k % 2], 16)
                    act.wait_ge(s_x, t + 1)
                    act.dma_start(rows(xin_out, t * P, P), xn[:, k, :]).then_inc(s_st[k % 2], 16)

                def tile(t, j, k, first, last):
                    if not (isinstance(t, int) and t + 2 >= TILES):
                        load(t + 2, (k + 2) % SLOTS, fresh=isinstance(t, int) and t + 2 < SLOTS)
                    if not last:
                        hi(t + 1, (k + 1) % 2)
                    if not first:
                        store(t - 1, (k - 1) % SLOTS)

                load(0, 0, fresh=True)
                load(1, 1, fresh=True)
                hi(0, 0)
                tiles(act, tile)
                store(TILES - 1, SLOTS - 1)
                for k in range(2):
                    act.wait_ge(s_st[k], 48 * TILES // 2)

            @block.vector
            def _(dve):
                dve.wait_ge(s_ld, 16 * 7)
                dve.tensor_scalar(bf[:, :, :], bf[:, :, :], gate[:, 0:1], None, ALU.mult)
                dve.drain()
                for f in (0, 2):
                    dve.tensor_scalar(bf[:, f, :], bf[:, f, :], 1.0, None, ALU.add)
                dve.drain()
                n = 0
                for f in range(NF):
                    for c in range(VC):
                        dve.wait_ge(s_foh, n + 1)
                        dve.scalar_tensor_tensor(out=wf[:, 1, c, f, :], in0=ps_w[:, n % 2, :], scalar=gate[:, 0:1],
                                                 in1=wf[:, 0, c, f, :].bitcast(F32), op0=ALU.mult, op1=ALU.subtract).then_inc(s_fol, 1)
                        n += 1

                def split(t, k):
                    dve.wait_ge(s_th, t + 1)
                    dve.tensor_tensor(aT[:, k, 1, :, :].rearrange("p c q -> p (c q)"), ps_t[:, k, 0:DV],
                                      aT[:, k, 0, :, :].rearrange("p c q -> p (c q)").bitcast(F32), ALU.subtract).then_inc(s_tl, 1)

                def variance(t, k, loads):
                    dve.wait_ge(s_in[k], 48 * loads)
                    dve.tensor_copy(mask[:, k, :], mask_u8[:, k, :])
                    dve.bn_stats(stats[:, :], x1[:, k, :])
                    dve.drain()
                    dve.bn_aggr(mv[:, :], stats[:, :])
                    dve.drain()
                    dve.tensor_scalar(mv[:, 1:2], mv[:, 1:2], EPS, None, ALU.add).then_inc(s_var, 1)

                def norm(t, k):
                    dve.wait_ge(s_rstd, t + 1)
                    dve.tensor_scalar(xn[:, k, :], x1[:, k, :], mv[:, 0:1], rstd[:, 0:1], ALU.subtract, ALU.mult).then_inc(s_xn, 1)

                def modulate(t, k, f):
                    dve.wait_ge(s_f, NF * t + f + 1)
                    dve.scalar_tensor_tensor(out=mod[:, k % 2, f, :], in0=ps_f[:, f, :], scalar=mask[:, k, :], in1=bf[:, f, :],
                                             op0=ALU.mult, op1=ALU.add).then_inc(s_fr, 1)

                def tile(t, j, k, first, last):
                    if not last:
                        split(t + 1, (k + 1) % 2)
                        variance(t + 1, (k + 1) % SLOTS, j + (k + 1) // SLOTS + 1)
                    dve.wait_ge(s_st[k % 2], 48 * (j * 2 + k // 2))
                    modulate(t, k, 0)
                    modulate(t, k, 1)
                    if not last:
                        norm(t + 1, (k + 1) % SLOTS)
                    modulate(t, k, 2)
                    modulate(t, k, 3)

                split(0, 0)
                variance(0, 0, 1)
                norm(0, 0)
                tiles(dve, tile)
        st.clear()



def conv_constants():
    t = np.arange(S // 2)[:, None] + 0.5
    fwd, tw = [], []
    for par in range(2):
        m = 2 * np.arange(S // 2)[None, :] + par + 0.5
        ang = np.pi * m * t / S
        fwd.append([np.cos(ang) + np.sin(ang), np.cos(ang) - np.sin(ang)])
        half = np.pi * m[0] / (2 * S)
        tw.append([(np.cos(half) + np.sin(half)) / 2, (np.cos(half) - np.sin(half)) / 2])
    fwd = np.array(fwd)
    inv = fwd.transpose(0, 1, 3, 2) / (2 * S)
    tw = np.array(tw).transpose(1, 0, 2).reshape(2, S)
    return {"dft": fwd.astype(np.float32), "idft": inv.astype(np.float32).copy(), "twiddle": tw.astype(np.float32)}


def make_exchange(pool, flip, ready):
    pool.memset(flip[:, :], 0.0)
    pool.drain()
    pool.affine_select(out=flip[:, :], in_=flip[:, :], compare_op=ALU.not_equal, fill=1.0,
                       base=1 - P, pattern=[[1, P]], channel_multiplier=1)
    pool.drain().then_inc(ready, 1)


def stage_dft(nc, A, xin, taps, y_out):
    TC = S // 2 // P
    MC = S // P
    XIN = 16 * (1 + TC)
    with ExitStack() as ctx:
        st = Stage(nc, ctx, "df")
        sb, psum, sem = st.sb, st.psum, st.sem
        raw = sb("raw", [P, 2, TC, D])
        mats = sb("mats", [P, 2, 2, 2, TC, 512], F32R)
        uv = sb("uv", [P, 2, 2, TC, D], F32R)
        uvf = sb("uvf", [P, 2, TC, D])
        kc = sb("kc", [P, MC, D])
        ks = sb("ks", [P, MC, D])
        tw = sb("tw", [P, 2, MC])
        prod = sb("prod", [P, 2, 4, D])
        yo = sb("yo", [P, 2, 2, D])
        flip = sb("flip", [P, P])
        ps = psum("ps", [P, 2, 2, D])
        ps_rev = psum("ps_rev", [P, TC, D])

        s_tw = sem("twiddle_loaded")
        s_m = sem("matrix_loaded")
        s_mh = sem("matrix_hi")
        s_ml = sem("matrix_lo")
        s_x = sem("x_loaded")
        s_const = sem("exchange_ready")
        s_rev = sem("reversed")
        s_uv = sem("sums_done")
        s_hi = sem("sums_hi")
        s_lo = sem("sums_lo")
        s_f = sem("spectrum")
        s_fr = sem("spectrum_read")
        s_kk = sem("taps_spectrum")
        s_pr = sem("products")
        s_y = sem("y_done")
        s_st = [sem(f"stored{k}") for k in range(2)]

        with nc.Block() as block:

            @block.sync
            def _(sp):
                sp.dma_start(tw[:, :, :], A["twiddle"].rearrange("i (q p) -> p i q", p=P), allow_slow_non_contiguous=True).then_inc(s_tw, 16)
                for n in range(4):
                    if n >= 1:
                        sp.wait_ge(s_ml, n)
                    sp.dma_start(raw[:, 0, :, :], A["dft"][n // 2, n % 2].rearrange("(q p) m -> p q m", p=P)).then_inc(s_m, 16)
                sp.wait_ge(s_ml, 4)

                def load(src, first):
                    sp.dma_start(raw[:, 0, :, :], rows(src, first, S // 2).rearrange("(q p) d -> p q d", p=P)).then_inc(s_x, 16)
                    for c in range(TC):
                        sp.dma_start(raw[:, 1, c, :], rows(src, first + S - (c + 1) * P, P)).then_inc(s_x, 16)

                load(taps, 0)
                with sp.Fori(0, B) as b:
                    sp.wait_ge(s_uv, b + 1)
                    load(xin, b * S)

            @block.gpsimd
            def _(pool):
                make_exchange(pool, flip, s_const)

                def split_v(n):
                    pool.wait_ge(s_hi, n + 1)
                    pool.tensor_tensor(uv[:, 1, 1, :, :], uvf[:, 1, :, :], uv[:, 1, 0, :, :].bitcast(F32), ALU.subtract).then_inc(s_lo, 1)

                split_v(0)
                with pool.Fori(0, B) as b:
                    split_v(b + 1)
                    for q in range(MC):
                        k = q % 2
                        pool.wait_ge(s_pr, MC * b + q + 1)
                        pool.wait_ge(s_st[k], 16 * ((MC // 2) * b + q // 2))
                        pool.tensor_tensor(yo[:, k, 0, :], prod[:, k, 0, :], prod[:, k, 1, :], ALU.add)
                        pool.tensor_tensor(yo[:, k, 1, :], prod[:, k, 2, :], prod[:, k, 3, :], ALU.subtract)
                        pool.drain().then_inc(s_y, 1)

            @block.tensor
            def _(pe):
                def reverse(n):
                    pe.wait_ge(s_x, XIN * (n + 1))
                    pe.wait_ge(s_uv, n)
                    for c in range(TC):
                        last = pe.matmul(ps_rev[:, c, :], flip[:, :], raw[:, 1, c, :], start=True, stop=True)
                    last.then_inc(s_rev, 1)

                def spectrum(n, q):
                    k = q % 2
                    i = MC * n + q
                    if not (isinstance(n, int) and n == 0 and q < 2):
                        pe.wait_ge(s_fr, i - 1)
                    par, mq = q // TC, q % TC
                    for sd in range(2):
                        src = (sd + par) % 2
                        for c in range(TC):
                            last = mm3(pe, ps[:, k, sd, :],
                                       mats[:, 0, par, sd, c, mq * P:(mq + 1) * P], mats[:, 1, par, sd, c, mq * P:(mq + 1) * P],
                                       uv[:, src, 0, c, :], uv[:, src, 1, c, :], start=(c == 0), stop=(c == TC - 1))
                    last.then_inc(s_f, 1)

                def sequence(n, last):
                    pe.wait_ge(s_lo, 2 * n + 2)
                    for q in range(MC):
                        if q == 3 and not last:
                            reverse(n + 1)
                        spectrum(n, q)

                pe.wait_ge(s_const, 1)
                pe.wait_ge(s_ml, 4)
                reverse(0)
                sequence(0, False)
                with pe.Fori(1, B) as n:
                    sequence(n, False)
                sequence(B, True)

            @block.scalar
            def _(act):
                for n in range(4):
                    act.wait_ge(s_m, 16 * (n + 1))
                    act.activation(mats[:, 0, n // 2, n % 2, :, :], raw[:, 0, :, :], ACT.Copy).then_inc(s_mh, 1)

                def hi(n):
                    act.wait_ge(s_uv, n + 1)
                    act.wait_ge(s_f, MC * n)
                    for i in range(2):
                        act.activation(uv[:, i, 0, :, :], uvf[:, i, :, :], ACT.Copy)
                    act.drain().then_inc(s_hi, 1)

                hi(0)
                with act.Fori(0, B) as b:
                    hi(b + 1)
                    for q in range(MC):
                        k = q % 2
                        act.wait_ge(s_y, MC * b + q + 1)
                        act.dma_start(y_out[bass.ds(b, 1), q].rearrange("o i p d -> p (o i) d"), yo[:, k, :, :]).then_inc(s_st[k], 16)
                for k in range(2):
                    act.wait_ge(s_st[k], 16 * B * MC // 2)

            @block.vector
            def _(dve):
                for n in range(4):
                    dve.wait_ge(s_mh, n + 1)
                    dve.tensor_tensor(mats[:, 1, n // 2, n % 2, :, :], raw[:, 0, :, :],
                                      mats[:, 0, n // 2, n % 2, :, :].bitcast(F32), ALU.subtract).then_inc(s_ml, 1)

                def fold(n):
                    dve.wait_ge(s_x, XIN * (n + 1))
                    dve.wait_ge(s_rev, n + 1)
                    dve.wait_ge(s_lo, 2 * n)
                    dve.tensor_tensor(uvf[:, 0, :, :], raw[:, 0, :, :], ps_rev[:, :, :], ALU.add)
                    dve.tensor_tensor(uvf[:, 1, :, :], raw[:, 0, :, :], ps_rev[:, :, :], ALU.subtract)
                    dve.drain().then_inc(s_uv, 1)
                    dve.wait_ge(s_hi, n + 1)
                    dve.tensor_tensor(uv[:, 0, 1, :, :], uvf[:, 0, :, :], uv[:, 0, 0, :, :].bitcast(F32), ALU.subtract).then_inc(s_lo, 1)

                fold(0)
                dve.wait_ge(s_tw, 16)
                for q in range(MC):
                    k = q % 2
                    dve.wait_ge(s_f, q + 1)
                    dve.tensor_scalar(prod[:, k, 0, :], ps[:, k, 0, :], tw[:, 0, q:q + 1], None, ALU.mult)
                    dve.tensor_scalar(prod[:, k, 1, :], ps[:, k, 1, :], tw[:, 0, q:q + 1], None, ALU.mult)
                    dve.drain()
                    dve.scalar_tensor_tensor(out=kc[:, q, :], in0=ps[:, k, 1, :], scalar=tw[:, 1, q:q + 1], in1=prod[:, k, 0, :],
                                             op0=ALU.mult, op1=ALU.add)
                    dve.scalar_tensor_tensor(out=ks[:, q, :], in0=ps[:, k, 0, :], scalar=tw[:, 1, q:q + 1], in1=prod[:, k, 1, :],
                                             op0=ALU.mult, op1=ALU.subtract)
                    dve.drain().then_inc(s_fr, 1)
                with dve.Fori(0, B) as b:
                    fold(b + 1)
                    for q in range(MC):
                        k = q % 2
                        dve.wait_ge(s_f, MC * (b + 1) + q + 1)
                        if q >= 2:
                            dve.wait_ge(s_y, MC * b + q - 1)
                        else:
                            dve.wait_ge(s_y, MC * b)
                        for i, (x, w) in enumerate(((0, kc), (1, ks), (1, kc), (0, ks))):
                            dve.tensor_tensor(prod[:, k, i, :], ps[:, k, x, :], w[:, q, :], ALU.mult)
                        dve.drain().then_inc(s_fr, 1)
                        dve.drain().then_inc(s_pr, 1)
        st.clear()


def stage_idft(nc, A, y_in, conv_out):
    TC = S // 2 // P
    MC = S // P
    with ExitStack() as ctx:
        st = Stage(nc, ctx, "id")
        sb, psum, sem = st.sb, st.psum, st.sem
        raw = sb("raw", [P, 2, 2, D])
        mraw = sb("mraw", [P, TC, 512])
        mats = sb("mats", [P, 2, 2, 2, TC, 512], F32R)
        y = sb("y", [P, MC, 2, 2, D], F32R)
        a_sb = sb("a_sb", [P, 2, D])
        out = sb("out", [P, 2, 2, D])
        flip = sb("flip", [P, P])
        rev = sb("rev", [P, 2, D])
        ps = psum("ps", [P, 2, 2, D])
        ps_rev = psum("ps_rev", [P, 2, D])

        s_m = sem("matrix_loaded")
        s_mh = sem("matrix_hi")
        s_ml = sem("matrix_lo")
        s_y = [sem(f"y_loaded{k}") for k in range(2)]
        s_hi = sem("y_hi")
        s_lo = sem("y_lo")
        s_o = sem("sums_done")
        s_const = sem("exchange_ready")
        s_rev = sem("reversed")
        s_rc = sem("reversed_copied")
        s_a = sem("a_copied")
        s_r = sem("result_done")
        s_st = [sem(f"stored{k}") for k in range(2)]

        with nc.Block() as block:

            @block.sync
            def _(sp):
                for n in range(4):
                    if n >= 1:
                        sp.wait_ge(s_ml, n)
                    sp.dma_start(mraw[:, :, :], A["idft"][n // 2, n % 2].rearrange("(q p) m -> p q m", p=P)).then_inc(s_m, 16)
                with sp.Fori(0, B) as b:
                    for q in range(MC):
                        k = q % 2
                        sp.wait_ge(s_lo, MC * b + q - 1 if q >= 2 else MC * b)
                        sp.dma_start(raw[:, k, :, :], y_in[bass.ds(b, 1), q].rearrange("o i p d -> p (o i) d")).then_inc(s_y[k], 16)

            @block.gpsimd
            def _(pool):
                make_exchange(pool, flip, s_const)
                with pool.Fori(0, B) as b:
                    for t in range(TC):
                        k = t % 2
                        pool.wait_ge(s_r, TC * b + t + 1)
                        pool.dma_start(rows(conv_out, b * S + t * P, P), out[:, k, 0, :]).then_inc(s_st[k], 16)
                        pool.wait_ge(s_rc, TC * b + t + 1)
                        pool.dma_start(rows(conv_out, b * S + S - (t + 1) * P, P), rev[:, k, :]).then_inc(s_st[k], 16)
                for k in range(2):
                    pool.wait_ge(s_st[k], 32 * B * TC // 2)

            @block.tensor
            def _(pe):
                def reverse(b, t):
                    pe.wait_ge(s_r, TC * b + t + 1)
                    pe.wait_ge(s_rc, TC * b + t - 1 if t >= 2 else TC * b)
                    pe.matmul(ps_rev[:, t % 2, :], flip[:, :], out[:, t % 2, 1, :], start=True, stop=True).then_inc(s_rev, 1)

                pe.wait_ge(s_const, 1)
                pe.wait_ge(s_ml, 4)
                with pe.Fori(0, B) as b:
                    pe.wait_ge(s_lo, MC * (b + 1))
                    for t in range(TC):
                        k = t % 2
                        pe.wait_ge(s_r, TC * b + t - 1 if t >= 2 else TC * b)
                        for ab in range(2):
                            for q in range(MC):
                                par, mq = q // TC, q % TC
                                pm = (ab + par) % 2
                                last = mm3(pe, ps[:, k, ab, :],
                                           mats[:, 0, par, pm, mq, t * P:(t + 1) * P], mats[:, 1, par, pm, mq, t * P:(t + 1) * P],
                                           y[:, q, 0, pm, :], y[:, q, 1, pm, :], start=(q == 0), stop=(q == MC - 1))
                        last.then_inc(s_o, 1)
                        if t >= 1:
                            reverse(b, t - 1)
                    reverse(b, TC - 1)

            @block.scalar
            def _(act):
                for n in range(4):
                    act.wait_ge(s_m, 16 * (n + 1))
                    act.activation(mats[:, 0, n // 2, n % 2, :, :], mraw[:, :, :], ACT.Copy).then_inc(s_mh, 1)

                def turned(b, t):
                    k = t % 2
                    act.wait_ge(s_rev, TC * b + t + 1)
                    act.wait_ge(s_st[k], 32 * ((TC // 2) * b + t // 2))
                    act.activation(rev[:, k, :], ps_rev[:, k, :], ACT.Copy).then_inc(s_rc, 1)

                with act.Fori(0, B) as b:
                    act.wait_ge(s_o, TC * b)
                    for q in range(MC):
                        k = q % 2
                        act.wait_ge(s_y[k], 16 * ((MC // 2) * b + q // 2 + 1))
                        act.activation(y[:, q, 0, :, :], raw[:, k, :, :], ACT.Copy).then_inc(s_hi, 1)
                    for t in range(TC):
                        k = t % 2
                        act.wait_ge(s_o, TC * b + t + 1)
                        act.wait_ge(s_r, TC * b + t - 1 if t >= 2 else TC * b)
                        act.activation(a_sb[:, k, :], ps[:, k, 0, :], ACT.Copy).then_inc(s_a, 1)
                        if t >= 1:
                            turned(b, t - 1)
                    turned(b, TC - 1)

            @block.vector
            def _(dve):
                for n in range(4):
                    dve.wait_ge(s_mh, n + 1)
                    dve.tensor_tensor(mats[:, 1, n // 2, n % 2, :, :], mraw[:, :, :],
                                      mats[:, 0, n // 2, n % 2, :, :].bitcast(F32), ALU.subtract).then_inc(s_ml, 1)
                with dve.Fori(0, B) as b:
                    for q in range(MC):
                        dve.wait_ge(s_hi, MC * b + q + 1)
                        dve.tensor_tensor(y[:, q, 1, :, :], raw[:, q % 2, :, :], y[:, q, 0, :, :].bitcast(F32), ALU.subtract)\
                           .then_inc(s_lo, 1)
                    for t in range(TC):
                        k = t % 2
                        dve.wait_ge(s_a, TC * b + t + 1)
                        dve.wait_ge(s_st[k], 32 * ((TC // 2) * b + t // 2))
                        dve.tensor_tensor(out[:, k, 0, :], a_sb[:, k, :], ps[:, k, 1, :], ALU.add)
                        if t >= 2:
                            dve.wait_ge(s_rev, TC * b + t - 1)
                        dve.tensor_tensor(out[:, k, 1, :], a_sb[:, k, :], ps[:, k, 1, :], ALU.subtract)
                        dve.drain().then_inc(s_r, 1)
        st.clear()


def stage_mlp(nc, name, modulated, W_up, b_up, W_down, down_biases, x_in, out, g_ffn=None, b_ffn=None,
              g_out=None, b_out=None, y_in=None, so_in=None, sh_in=None):
    N = 4 * P
    GROUPS = B * S // N
    Q = N // P
    PIECES = 2 * Q * DC
    IN = 64 if modulated else 16
    with ExitStack() as ctx:
        st = Stage(nc, ctx, name)
        sb, psum, sem = st.sb, st.psum, st.sem
        ident = sb("ident", [P, P])
        neghalf = sb("neghalf", [P, 1])
        w1 = sb("w1", [P, 2, DC, HID], F32R)
        w2 = sb("w2", [P, 2, HC, D], F32R)
        b1 = sb("b1", [P, HC])
        b2 = sb("b2", [P, D])
        xt = sb("xt", [P, 2, Q, D])
        h = sb("h", [P, D])
        hT = sb("hT", [P, 2, 2, DC, N], F32R)
        act_hl = sb("act_hl", [P, 2, 2, N], F32R)
        g32 = sb("g32", [P, N])
        stats = sb("stats", [P, 6])
        mv = {v: sb(f"mv_{v}", [P, 2]) for v in "pef"}
        rstd = {v: sb(f"rstd_{v}", [P, 1]) for v in "pef"}
        e = sb("e", [P, 2, D])
        if modulated:
            gf = sb("gf", [P, DC])
            bf = sb("bf", [P, DC])
            g_row = sb("g_row", [P, D])
            b_row = sb("b_row", [P, D])
            y = sb("y", [P, D])
            so = sb("so", [P, D])
            sh = sb("sh", [P, D])
            xr = sb("xr", [P, D])

        ps_h = psum("ps_h", [P, 2, N])
        ps_o = psum("ps_o", [P, Q, D])
        ps_t = psum("ps_t", [P, 2, D])

        s_const = sem("constants")
        s_c = sem("small_loaded")
        s_raw = [sem(f"piece_loaded{k}") for k in range(8)]
        s_whi = sem("weights_hi")
        s_wlo = sem("weights_lo")
        s_bm = sem("bias_products")
        s_in = sem("tile_loaded")
        s_mod = sem("modulated")
        s_var = {v: sem(f"variance_{v}") for v in "pef"}
        s_rstd = {v: sem(f"rstd_{v}") for v in "pef"}
        s_h = sem("h_done")
        s_b2 = sem("bias_added")
        s_tr = sem("h_transposed")
        s_hi = sem("hT_hi")
        s_hT = sem("hT_lo")
        s_m1 = sem("up_done")
        s_g = sem("gelu_done")
        s_gh = sem("gelu_hi")
        s_gl = sem("gelu_lo")
        s_m2 = sem("down_chunk_done")
        s_o = sem("down_done")
        s_add = sem("residual_added")
        s_n1 = sem("inner_norm")
        s_xr = sem("x_again_loaded")
        s_e = sem("outer_sum")
        s_n2 = sem("outer_norm")
        s_st = [sem(f"stored{k}") for k in range(2)]
        s_out = s_n2 if modulated else s_n1

        def in_groups(eng, group):
            group(0, 0, True, False)
            with eng.Fori(0, (GROUPS - 2) // 2) as j:
                for k in range(2):
                    group(2 * j + 1 + k, (1 + k) % 2, False, False)
            group(GROUPS - 1, (GROUPS - 1) % 2, False, True)

        with nc.Block() as block:

            @block.sync
            def _(sp):
                sp.dma_start(b1[:, :], b_up.rearrange("(c p) -> p c", p=P), allow_slow_non_contiguous=True).then_inc(s_c, 16)
                row = lambda v: v.rearrange("(o n) -> o n", o=1).broadcast_to([P, D])
                sp.dma_start(b2[:, :], row(down_biases[0])).then_inc(s_c, 16)
                if modulated:
                    for t, v in ((gf, g_ffn), (bf, b_ffn)):
                        sp.dma_start(t[:, :], v.rearrange("(c p) -> p c", p=P), allow_slow_non_contiguous=True).then_inc(s_c, 16)
                    for t, v in ((g_row, g_out), (b_row, b_out)):
                        sp.dma_start(t[:, :], row(v)).then_inc(s_c, 16)
                else:
                    sp.dma_start(h[:, :], row(down_biases[1])).then_inc(s_c, 16)
                for m in range(PIECES):
                    if m >= 8:
                        sp.wait_ge(s_whi, m - 7)
                        sp.wait_ge(s_wlo, m - 7)
                        if modulated:
                            sp.wait_ge(s_bm, min(m - 7, PIECES // 2))
                    if m < PIECES // 2:
                        c, q = m // Q, m % Q
                        src = W_up[c * P:(c + 1) * P, q * D:(q + 1) * D]
                    else:
                        n = m - PIECES // 2
                        src = W_down[n * P:(n + 1) * P, :]
                    sp.dma_start(xt[:, (m % 8) // Q, m % Q, :], src).then_inc(s_raw[m % 8], 16)

                def again(g, q):
                    i = Q * g + q
                    sp.wait_ge(s_e, i)
                    sp.dma_start(xr[:, :], rows(x_in, i * P, P)).then_inc(s_xr, 16)

                def group(g, slot, first, last):
                    for q in range(Q):
                        if not first:
                            again(g - 1, q)

                if modulated:
                    in_groups(sp, group)
                if modulated:
                    for q in range(Q):
                        again(GROUPS - 1, q)

            @block.gpsimd
            def _(pool):
                pool.memset(ident[:, :], 0.0)
                pool.memset(neghalf[:, :], -0.5)
                pool.drain()
                pool.affine_select(out=ident[:, :], in_=ident[:, :], compare_op=ALU.not_equal, fill=1.0,
                                   base=0, pattern=[[-1, P]], channel_multiplier=1)
                pool.drain().then_inc(s_const, 1)

                def power(v, i):
                    pool.wait_ge(s_var[v], i + 1)
                    pool.tensor_tensor(rstd[v][:, :], mv[v][:, 1:2], neghalf[:, :], ALU.pow).then_inc(s_rstd[v], 1)

                def modulate(g, slot, q):
                    i = Q * g + q
                    pool.wait_ge(s_in, IN * (i + 1))
                    pool.tensor_tensor(y[:, :], y[:, :], so[:, :], ALU.mult)
                    pool.drain()
                    pool.tensor_tensor(y[:, :], y[:, :], sh[:, :], ALU.add)
                    pool.drain()
                    pool.tensor_tensor(xt[:, slot, q, :], xt[:, slot, q, :], y[:, :], ALU.add).then_inc(s_mod, 1)

                def bias(g, slot, q):
                    pool.wait_ge(s_h, Q * g + q + 1)
                    pool.tensor_tensor(xt[:, slot, q, :], xt[:, slot, q, :], b2[:, :], ALU.add).then_inc(s_b2, 1)

                def outer_sum(g, q):
                    i = Q * g + q
                    pool.wait_ge(s_n1, i + 1)
                    ek = e[:, q % 2, :]
                    pool.tensor_tensor(ek, ek, g_row[:, :], ALU.mult)
                    pool.drain()
                    pool.tensor_tensor(ek, ek, b_row[:, :], ALU.add)
                    pool.drain()
                    pool.wait_ge(s_xr, 16 * (i + 1))
                    pool.tensor_tensor(ek, ek, xr[:, :], ALU.add).then_inc(s_e, 1)

                pool.wait_ge(s_c, 16 * (6 if modulated else 3))
                pool.wait_ge(s_wlo, PIECES)
                for q in range(Q):
                    if modulated:
                        modulate(0, 0, q)
                        power("p", q)
                    bias(0, 0, q)

                def group(g, slot, first, last):
                    for n in range(HC):
                        pool.wait_ge(s_gh, HC * g + n + 1)
                        lo, hi = act_hl[:, n % 2, 1, :], act_hl[:, n % 2, 0, :]
                        pool.tensor_tensor(lo, g32[:, :], hi.bitcast(F32), ALU.subtract).then_inc(s_gl, 1)
                        q, phase = n // 3, n % 3
                        if not first:
                            if phase == 0 and q < Q:
                                power("e", Q * (g - 1) + q)
                            if phase == 1 and q < Q and modulated:
                                outer_sum(g - 1, q)
                            if phase == 2 and q < Q and modulated:
                                power("f", Q * (g - 1) + q)
                        if not last:
                            if phase == 2 and q < Q and modulated:
                                modulate(g + 1, 1 - slot, q)
                            if modulated and phase == 0 and 1 <= q <= Q:
                                power("p", Q * (g + 1) + q - 1)
                            if phase == 1 and q >= 1 and q <= Q:
                                bias(g + 1, 1 - slot, q - 1)

                in_groups(pool, group)
                for q in range(Q):
                    i = Q * (GROUPS - 1) + q
                    power("e", i)
                    if modulated:
                        outer_sum(GROUPS - 1, q)
                        power("f", i)

            @block.tensor
            def _(pe):
                pe.wait_ge(s_const, 1)
                if modulated:
                    pe.wait_ge(s_c, 16 * 6)
                    for m in range(PIECES // 2):
                        c, q = m // Q, m % Q
                        pe.wait_ge(s_raw[m % 8], 16 * (m // 8 + 1))
                        for r in range(4):
                            n = 4 * q + r
                            last = pe.matmul(ps_t[:, 0, c * HC + n:c * HC + n + 1], xt[:, (m % 8) // Q, m % Q, r * P:(r + 1) * P],
                                             bf[:, c:c + 1], start=True, stop=True)
                        last.then_inc(s_bm, 1)
                pe.wait_ge(s_wlo, PIECES + 1)

                def turn(g, slot, q):
                    i = Q * g + q
                    pe.wait_ge(s_h, i + 1)
                    if not (isinstance(i, int) and i < 2):
                        pe.wait_ge(s_hT, i - 1)
                    for c in range(DC):
                        last = pe.transpose(ps_t[:, q % 2, c * P:(c + 1) * P], h[:, c * P:(c + 1) * P], ident[:, :])
                    last.then_inc(s_tr, 1)

                def up(g, slot, n, first):
                    if n == 0:
                        pe.wait_ge(s_hT, Q * (g + 1))
                    if not (first and n < 2):
                        pe.wait_ge(s_g, HC * g + n - 1)
                    for c in range(DC):
                        w_hi, w_lo = (w1[:, x, c, n * P:(n + 1) * P] for x in range(2))
                        last = mm3(pe, ps_h[:, n % 2, :], w_hi, w_lo, hT[:, slot, 0, c, :], hT[:, slot, 1, c, :],
                                   start=(c == 0), stop=(c == DC - 1))
                    last.then_inc(s_m1, 1)

                def down(g, n, first):
                    pe.wait_ge(s_gl, HC * g + n + 1)
                    for q in range(Q):
                        if n == 0 and not first:
                            pe.wait_ge(s_add, Q * (g - 1) + q + 1)
                        a_hi, a_lo = (act_hl[:, n % 2, x, q * P:(q + 1) * P] for x in range(2))
                        last = mm3(pe, ps_o[:, q, :], a_hi, a_lo, w2[:, 0, n, :], w2[:, 1, n, :],
                                   start=(n == 0), stop=(n == HC - 1))
                        if n == HC - 1:
                            last.then_inc(s_o, 1)
                    pe.drain().then_inc(s_m2, 1)

                for q in range(Q):
                    turn(0, 0, q)
                up(0, 0, 0, True)

                def group(g, slot, first, last):
                    for n in range(HC):
                        if not last and n >= 5 and (n - 5) % 3 == 0:
                            turn(g + 1, 1 - slot, (n - 5) // 3)
                        if n < HC - 1:
                            up(g, slot, n + 1, first)
                        elif not last:
                            up(g + 1, 1 - slot, 0, False)
                        down(g, n, first)

                in_groups(pe, group)

            @block.scalar
            def _(act):
                act.wait_ge(s_c, 16 * (6 if modulated else 3))
                for m in range(PIECES):
                    raw = xt[:, (m % 8) // Q, m % Q, :]
                    act.wait_ge(s_raw[m % 8], 16 * (m // 8 + 1))
                    if m < PIECES // 2:
                        c, q = m // Q, m % Q
                        act.activation(w1[:, 0, c, q * D:(q + 1) * D], raw, ACT.Identity,
                                       scale=gf[:, c:c + 1] if modulated else 1.0).then_inc(s_whi, 1)
                    else:
                        act.activation(w2[:, 0, m - PIECES // 2, :], raw, ACT.Copy).then_inc(s_whi, 1)

                def load(g, slot, q):
                    i = Q * g + q
                    if modulated:
                        act.wait_ge(s_mod, i)
                        for t, v in ((y, y_in), (so, so_in), (sh, sh_in)):
                            act.dma_start(t[:, :], rows(v, i * P, P)).then_inc(s_in, 16)
                    else:
                        act.wait_ge(s_h, i)
                    act.dma_start(xt[:, slot, q, :], rows(x_in, i * P, P)).then_inc(s_in, 16)

                def hi(g, slot, q):
                    act.wait_ge(s_tr, Q * g + q + 1)
                    if not (isinstance(g, int) and g < 2):
                        act.wait_ge(s_m1, HC * (g - 1))
                    act.activation(hT[:, slot, 0, :, q * P:(q + 1) * P], ps_t[:, q % 2, :].rearrange("p (c t) -> p c t", c=DC),
                                   ACT.Copy).then_inc(s_hi, 1)

                def store(g, q):
                    i = Q * g + q
                    act.wait_ge(s_out, i + 1)
                    act.dma_start(rows(out, i * P, P), e[:, q % 2, :]).then_inc(s_st[q % 2], 16)

                act.wait_ge(s_wlo, PIECES)
                for q in range(Q):
                    load(0, 0, q)
                    hi(0, 0, q)

                def group(g, slot, first, last):
                    for n in range(HC):
                        act.wait_ge(s_m1, HC * g + n + 1)
                        act.wait_ge(s_gl, HC * g + n)
                        act.activation(g32[:, :], ps_h[:, n % 2, :], ACT.Gelu,
                                       bias=b1[:, n:n + 1]).then_inc(s_g, 1)
                        if not last and n % 3 == 1 and n // 3 < Q:
                            if not first:
                                act.wait_ge(s_n1, Q * (g - 1) + n // 3 + 1)
                            load(g + 1, 1 - slot, n // 3)
                        if not last and n >= 5 and (n - 5) % 3 == 0:
                            hi(g + 1, 1 - slot, (n - 5) // 3)
                        if not first and n >= 4 and (n - 4) % 3 == 0 and (n - 4) // 3 < Q:
                            store(g - 1, (n - 4) // 3)

                in_groups(act, group)
                for q in range(Q):
                    store(GROUPS - 1, q)
                for k in range(2):
                    act.wait_ge(s_st[k], 16 * TILES // 2)

            @block.vector
            def _(dve):
                dve.wait_ge(s_c, 16 * (6 if modulated else 3))
                for m in range(PIECES):
                    raw = xt[:, (m % 8) // Q, m % Q, :]
                    dve.wait_ge(s_whi, m + 1)
                    if m < PIECES // 2 and modulated:
                        c, q = m // Q, m % Q
                        dve.scalar_tensor_tensor(out=w1[:, 1, c, q * D:(q + 1) * D], in0=raw, scalar=gf[:, c:c + 1],
                                                 in1=w1[:, 0, c, q * D:(q + 1) * D].bitcast(F32), op0=ALU.mult,
                                                 op1=ALU.subtract).then_inc(s_wlo, 1)
                    else:
                        if m < PIECES // 2:
                            c, q = m // Q, m % Q
                            w_hi, w_lo = (w1[:, x, c, q * D:(q + 1) * D] for x in range(2))
                        else:
                            w_hi, w_lo = (w2[:, x, m - PIECES // 2, :] for x in range(2))
                        dve.tensor_tensor(w_lo, raw, w_hi.bitcast(F32), ALU.subtract).then_inc(s_wlo, 1)
                if modulated:
                    dve.wait_ge(s_bm, PIECES // 2)
                    for c in range(DC):
                        dve.tensor_tensor(b1[:, :], b1[:, :], ps_t[:, 0, c * HC:(c + 1) * HC], ALU.add)
                        dve.drain()
                else:
                    dve.tensor_tensor(b2[:, :], b2[:, :], h[:, :], ALU.add)
                dve.drain().then_inc(s_wlo, 1)

                def variance(v, x):
                    dve.bn_stats(stats[:, :], x)
                    dve.drain()
                    dve.bn_aggr(mv[v][:, :], stats[:, :])
                    dve.drain()
                    dve.tensor_scalar(mv[v][:, 1:2], mv[v][:, 1:2], EPS, None, ALU.add).then_inc(s_var[v], 1)

                def var_p(g, slot, q):
                    i = Q * g + q
                    dve.wait_ge(s_mod, i + 1)
                    variance("p", xt[:, slot, q, :])

                def norm_p(g, slot, q):
                    i = Q * g + q
                    dve.wait_ge(s_tr, i)
                    if modulated:
                        dve.wait_ge(s_rstd["p"], i + 1)
                        dve.tensor_scalar(h[:, :], xt[:, slot, q, :], mv["p"][:, 0:1], rstd["p"][:, 0:1],
                                          ALU.subtract, ALU.mult).then_inc(s_h, 1)
                    else:
                        dve.wait_ge(s_in, IN * (i + 1))
                        dve.tensor_copy(h[:, :], xt[:, slot, q, :]).then_inc(s_h, 1)

                def lo(g, slot, q):
                    dve.wait_ge(s_hi, Q * g + q + 1)
                    dve.tensor_tensor(hT[:, slot, 1, :, q * P:(q + 1) * P], ps_t[:, q % 2, :].rearrange("p (c t) -> p c t", c=DC),
                                      hT[:, slot, 0, :, q * P:(q + 1) * P].bitcast(F32), ALU.subtract).then_inc(s_hT, 1)

                def add(g, slot):
                    for q in range(Q):
                        dve.wait_ge(s_o, Q * g + q + 1)
                        dve.wait_ge(s_b2, Q * g + q + 1)
                        dve.tensor_tensor(xt[:, slot, q, :], ps_o[:, q, :], xt[:, slot, q, :], ALU.add).then_inc(s_add, 1)
                    dve.drain()

                def norm_e(g, slot, q):
                    i = Q * g + q
                    dve.wait_ge(s_rstd["e"], i + 1)
                    dve.wait_ge(s_st[q % 2], 16 * (2 * g + q // 2))
                    dve.tensor_scalar(e[:, q % 2, :], xt[:, slot, q, :], mv["e"][:, 0:1], rstd["e"][:, 0:1],
                                      ALU.subtract, ALU.mult).then_inc(s_n1, 1)

                def var_f(g, q):
                    dve.wait_ge(s_e, Q * g + q + 1)
                    variance("f", e[:, q % 2, :])

                def norm_f(g, q):
                    dve.wait_ge(s_rstd["f"], Q * g + q + 1)
                    dve.tensor_scalar(e[:, q % 2, :], e[:, q % 2, :], mv["f"][:, 0:1], rstd["f"][:, 0:1],
                                      ALU.subtract, ALU.mult).then_inc(s_n2, 1)

                for q in range(Q):
                    if modulated:
                        var_p(0, 0, q)
                    norm_p(0, 0, q)
                    lo(0, 0, q)

                def group(g, slot, first, last):
                    for n in range(HC):
                        q, phase = n // 3, n % 3
                        dve.wait_ge(s_g, HC * g + n + 1)
                        if not (first and n < 2):
                            dve.wait_ge(s_m2, HC * g + n - 1)
                        dve.tensor_copy(act_hl[:, n % 2, 0, :], g32[:, :]).then_inc(s_gh, 1)
                        if not first:
                            if n == 0:
                                add(g - 1, 1 - slot)
                            if phase == 0 and q < Q:
                                variance("e", xt[:, 1 - slot, q, :])
                            if phase == 1 and q < Q:
                                norm_e(g - 1, 1 - slot, q)
                            if modulated:
                                if phase == 2 and q < Q:
                                    var_f(g - 1, q)
                                if phase == 0 and 1 <= q <= Q:
                                    norm_f(g - 1, q - 1)
                        if not last:
                            if modulated and phase == 0 and 1 <= q <= Q:
                                var_p(g + 1, 1 - slot, q - 1)
                            if phase == 1 and q >= 1:
                                norm_p(g + 1, 1 - slot, q - 1)
                            if phase == 2 and q >= 1:
                                lo(g + 1, 1 - slot, q - 1)

                in_groups(dve, group)
                add(GROUPS - 1, (GROUPS - 1) % 2)
                for q in range(Q):
                    variance("e", xt[:, (GROUPS - 1) % 2, q, :])
                    norm_e(GROUPS - 1, (GROUPS - 1) % 2, q)
                    if modulated:
                        var_f(GROUPS - 1, q)
                        norm_f(GROUPS - 1, q)
        st.clear()



def decoder_layer(nc, A, out):
    T = B * S

    def scratch(name, shape):
        return nc.dram_tensor(name, shape, F32, kind="Internal").ap()

    tap_rows, taps = scratch("tap_rows", [D, S]), scratch("taps", [S, D])
    w3, b3, w4 = scratch("w3", [D, HID]), scratch("b3", [HID]), scratch("w4", [HID, D])
    x1, qt = scratch("x1", [T, D]), scratch("qt", [2, P, T])
    kt, ac = scratch("kt", [2, P, B * S2]), scratch("ac", [T, DV])
    xin, so, sh = (scratch(n, [T, D]) for n in ("xin", "so", "sh"))
    spectrum, conv = scratch("spectrum", [B, 2 * DC, 2, P, D]), scratch("conv", [T, D])
    x2 = scratch("x2", [T, D])

    stage_taps(nc, A, tap_rows, taps)
    stage_butterfly(nc, A, w3, b3, w4)
    stage_attention(nc, A, x1, qt)
    stage_keys(nc, A, kt)
    stage_cross(nc, A, qt, kt, ac)
    stage_film(nc, A, x1, ac, xin, so, sh)
    stage_dft(nc, A, xin, taps, spectrum)
    stage_idft(nc, A, spectrum, conv)
    X = "L0_xattn_"
    stage_mlp(nc, "m1", True, A[X + "W1"], A[X + "b1"], A[X + "W2"], [A[X + "b2"]], x1, x2,
              g_ffn=A[X + "g_ffn"], b_ffn=A[X + "b_ffn"], g_out=A[X + "g_norm_out"], b_out=A[X + "b_norm_out"],
              y_in=conv, so_in=so, sh_in=sh)
    stage_mlp(nc, "m2", False, w3, b3, w4, [A["L0_ffn_b_con"], A["L0_ffn_down_bias"]], x2,
              out.rearrange("b s d -> (b s) d"))


def kernel(**inputs):
    import concourse.bacc as bacc
    from concourse.bass_utils import run_bass_kernel_spmd

    nc = bacc.Bacc("TRN2", target_bir_lowering=False, num_devices=1)
    given = {k: np.ascontiguousarray(v) for k, v in inputs.items()}
    given["L0_xattn_mod_gate"] = given["L0_xattn_mod_gate"].reshape(1)
    for name in ("mask_BxS_bf1", "mask_BxS2_bf1"):
        given[name] = given[name].view(np.uint8)
    given.update(conv_constants())
    arrays, aps = {}, {}
    for name, a in given.items():
        arrays[f"in_{name}_dram"] = a
        aps[name] = nc.dram_tensor(f"in_{name}_dram", a.shape, mybir.dt.from_np(a.dtype), kind="ExternalInput").ap()
    out = nc.dram_tensor("out_0_dram", (B, S, D), F32, kind="ExternalOutput").ap()
    decoder_layer(nc, aps, out)
    result = run_bass_kernel_spmd(nc, [arrays], core_ids=[0])
    return result.results[0]["out_0_dram"]
```

```python
import math
from contextlib import ExitStack

import numpy as np

import concourse.bass as bass
from concourse import mybir

F32 = mybir.dt.float32
F32R = mybir.dt.float32r
BF16 = mybir.dt.bfloat16
U8 = mybir.dt.uint8
ALU = mybir.AluOpType
ACT = mybir.ActivationFunctionType
AX = mybir.AxisListType

P = 128
B, S, D = 4, 1024, 512
DC = D // P
TILES = B * S // P
TPB = S // P
S2, DV = 2048, 384
VC = DV // P
GC = S2 // P
HEADS, DH = 4, 32
HID = 2048
HC = HID // P
TOPK = 32
NST = 64
EPS = 1e-5
SCALE = 1.0 / math.sqrt(32.0)
BIG = 1.0e30
TAKEN = -3.0e38


class Stage:

    def __init__(self, nc, ctx, name):
        self.nc, self.ctx, self.name, self.sems = nc, ctx, name, []

    def sb(self, name, shape, dt=F32):
        return self.ctx.enter_context(self.nc.sbuf_tensor(f"{self.name}_{name}", shape, dt))

    def psum(self, name, shape, dt=F32):
        return self.ctx.enter_context(self.nc.psum_tensor(f"{self.name}_{name}", shape, dt))

    def sem(self, name):
        self.sems.append(self.ctx.enter_context(self.nc.semaphore(f"{self.name}_{name}")))
        return self.sems[-1]

    def clear(self):
        with self.nc.Block() as block:
            @block.gpsimd
            def _(pool):
                for s in self.sems:
                    pool.sem_clear(s)


def rows(ap, start, n):
    return ap[bass.ds(start, n)]


def mm3(pe, out, w_hi, w_lo, m_hi, m_lo, start, stop):
    pe.matmul(out, w_hi, m_lo, start=start, stop=False)
    pe.matmul(out, w_lo, m_hi, start=False, stop=False)
    return pe.matmul(out, w_hi, m_hi, start=False, stop=stop)



def stage_taps(nc, A, tap_rows, taps_out):
    R = 32
    ROUND = 12582912.0
    LEVELS = 10
    TURN_1 = 6.28125
    TURN_2 = 0.0019350051879882812
    TURN_3 = 2.0 * math.pi - TURN_1 - TURN_2
    G = 16
    with ExitStack() as ctx:
        st = Stage(nc, ctx, "tp")
        sb, psum, sem = st.sb, st.psum, st.sem
        ident = sb("ident", [P, P])
        ldt = sb("ldt", [P, 1])
        dsk = sb("dsk", [P, DC])
        par = sb("par", [P, 4, NST])
        dt = sb("dt", [P, 3])
        dt_bits = sb("dt_bits", [P, 1], mybir.dt.int32)
        z = sb("z", [P, 6, LEVELS, NST])
        z_bits = sb("z_bits", [P, LEVELS, NST], mybir.dt.int32)
        lam = sb("lam", [P, LEVELS // 2, 2, NST])
        big = sb("big", [P, 5, 2, NST])
        w = sb("w", [P, 12, NST])
        ones = sb("ones", [P, NST])
        tab = [sb(f"tab{i}", [P, R, 2, NST]) for i in range(2)]
        tmp = [sb(f"tmp{i}", [P, 2, R // 2, NST]) for i in range(2)]
        tabT = [sb(f"tabT{i}", [P, R, P]) for i in range(2)]
        krow = sb("krow", [R, P, R])
        kd = sb("kd", [P, S])
        kT = sb("kT", [P, 2, P])
        ps_t = psum("ps_t", [P, 2, 4, P])
        ps_k = psum("ps_k", [R, 2, G, R])
        ps_o = psum("ps_o", [P, 2, 512])

        s_id = sem("identity")
        s_ld = sem("loaded")
        s_dsk = sem("skip_loaded")
        s_pow = sem("powers")
        s_tab = [sem(f"table{i}") for i in range(2)]
        s_tr = sem("transposed")
        s_trc = sem("transposed_copied")
        s_k = sem("taps_summed")
        s_kc = sem("taps_copied")
        s_kr = sem("tap_rows_stored")
        s_kd = sem("taps_loaded")
        s_skip = sem("skip_added")
        s_o = sem("taps_turned")
        s_oc = sem("taps_turned_copied")
        s_st = [sem(f"stored{k}") for k in range(2)]

        def grow(eng, table, t, power, n):
            for k in range(n.bit_length() - 1):
                m = 2 ** k
                re, im = table[:, 0:m, 0, :], table[:, 0:m, 1, :]
                pr = power[:, k:k + 1, 0, :].broadcast_to([P, m, NST])
                pi = power[:, k:k + 1, 1, :].broadcast_to([P, m, NST])
                for part, (x, y, op) in enumerate(((pr, pi, ALU.subtract), (pi, pr, ALU.add))):
                    eng.tensor_tensor(t[:, 0, 0:m, :], re, x, ALU.mult)
                    eng.tensor_tensor(t[:, 1, 0:m, :], im, y, ALU.mult)
                    eng.drain()
                    eng.tensor_tensor(table[:, m:2 * m, part, :], t[:, 0, 0:m, :], t[:, 1, 0:m, :], op)
                    eng.drain()

        with nc.Block() as block:

            @block.sync
            def _(sp):
                def load(c):
                    sp.dma_start(ldt[:, :], rows(A["L0_xattn_log_dt"].rearrange("(n o) -> n o", o=1), c * P, P)).then_inc(s_ld, 16)
                    for i, name in enumerate(("A_re", "A_im", "C_re", "C_im")):
                        sp.dma_start(par[:, i, :], rows(A["L0_xattn_" + name], c * P, P)).then_inc(s_ld, 16)

                def through_dram(c):
                    sp.wait_ge(s_kc, (P // G) * (c + 1))
                    sp.dma_start(rows(tap_rows, c * P, P).rearrange("d (a r) -> a d r", r=R), krow[:, :, :]).then_inc(s_kr, 16)
                    sp.wait_ge(s_kr, 16 * (c + 1))
                    sp.dma_start(kd[:, :], rows(tap_rows, c * P, P)).then_inc(s_kd, 16)
                    for n in range(S // P):
                        sp.wait_ge(s_oc, (S // P) * c + n + 1)
                        sp.dma_start(taps_out[n * P:(n + 1) * P, bass.ds(c * P, P)], kT[:, n % 2, :]).then_inc(s_st[n % 2], 16)

                sp.dma_start(dsk[:, :], A["L0_xattn_D_skip"].rearrange("(c p) -> p c", p=P), allow_slow_non_contiguous=True).then_inc(s_dsk, 16)
                load(0)
                for c in range(DC):
                    if c + 1 < DC:
                        sp.wait_ge(s_pow, c + 1)
                        load(c + 1)
                    through_dram(c)
                for k in range(2):
                    sp.wait_ge(s_st[k], 16 * DC * (S // P) // 2)

            @block.gpsimd
            def _(pool):
                pool.memset(ident[:, :], 0.0)
                pool.memset(ones[:, :], 1.0)
                pool.drain()
                pool.affine_select(out=ident[:, :], in_=ident[:, :], compare_op=ALU.not_equal, fill=1.0,
                                   base=0, pattern=[[-1, P]], channel_multiplier=1)
                pool.drain().then_inc(s_id, 1)
                with pool.Fori(0, DC) as c:
                    pool.wait_ge(s_pow, c + 1)
                    pool.wait_ge(s_trc, 16 * c)
                    pool.tensor_tensor(tab[1][:, 0, 0, :], w[:, 10, :], ones[:, :], ALU.mult)
                    pool.tensor_tensor(tab[1][:, 0, 1, :], w[:, 11, :], ones[:, :], ALU.mult)
                    pool.drain()
                    grow(pool, tab[1], tmp[1], big, R)
                    pool.drain().then_inc(s_tab[1], 1)

            @block.tensor
            def _(pe):
                pe.wait_ge(s_id, 1)
                with pe.Fori(0, DC) as c:
                    for i in range(2):
                        pe.wait_ge(s_tab[i], c + 1)
                        for g in range(8):
                            n = 8 * i + g
                            pe.wait_ge(s_trc, 16 * c + (n - 1 if n >= 1 else 0))
                            for q in range(4):
                                last = pe.transpose(ps_t[:, n % 2, q, :], tab[i][:, 4 * g + q, :, :].rearrange("p a n -> p (a n)"), ident[:, :])
                            last.then_inc(s_tr, 1)
                    pe.wait_ge(s_trc, 16 * (c + 1))
                    for g in range(P // G):
                        pe.wait_ge(s_kc, (P // G) * c + (g - 1 if g >= 1 else 0))
                        for q in range(G):
                            d = g * G + q
                            last = pe.matmul(ps_k[:, g % 2, q, :], tabT[1][:, :, d], tabT[0][:, :, d], start=True, stop=True)
                        last.then_inc(s_k, 1)
                    pe.wait_ge(s_skip, c + 1)
                    pe.wait_ge(s_kd, 16 * (c + 1))
                    for n in range(S // P):
                        pe.wait_ge(s_oc, (S // P) * c + (n - 1 if n >= 1 else 0))
                        pe.transpose(ps_o[:, n % 2, 0:P], kd[:, n * P:(n + 1) * P], ident[:, :]).then_inc(s_o, 1)

            @block.scalar
            def _(act):
                with act.Fori(0, DC) as c:
                    for n in range(16):
                        act.wait_ge(s_tr, 16 * c + n + 1)
                        i, g = n // 8, n % 8
                        act.activation(tabT[i][:, 4 * g:4 * g + 4, :], ps_t[:, n % 2, :, :], ACT.Copy).then_inc(s_trc, 1)
                    act.wait_ge(s_kr, 16 * c)
                    for g in range(P // G):
                        act.wait_ge(s_k, (P // G) * c + g + 1)
                        act.activation(krow[:, g * G:(g + 1) * G, :], ps_k[:, g % 2, :, :], ACT.Copy).then_inc(s_kc, 1)
                    for n in range(S // P):
                        act.wait_ge(s_o, (S // P) * c + n + 1)
                        act.wait_ge(s_st[n % 2], 16 * ((S // P // 2) * c + n // 2))
                        act.activation(kT[:, n % 2, :], ps_o[:, n % 2, 0:P], ACT.Copy).then_inc(s_oc, 1)

            @block.vector
            def _(dve):
                def tt(out, a, b, op):
                    dve.tensor_tensor(out, a, b, op)
                    dve.drain()

                def mul(out, a, x):
                    dve.tensor_scalar(out, a, x, None, ALU.mult)
                    dve.drain()

                def horner(p, v, coefs):
                    mul(p, v, coefs[0])
                    for coef in coefs[1:]:
                        dve.scalar_tensor_tensor(out=p, in0=p, scalar=coef, in1=v, op0=ALU.add, op1=ALU.mult)
                        dve.drain()

                def less_multiples(x, q, inv, parts):
                    dve.tensor_scalar(q, x, inv, ROUND, ALU.mult, ALU.add)
                    dve.drain()
                    dve.tensor_scalar(q, q, -ROUND, None, ALU.add)
                    dve.drain()
                    for part in parts:
                        dve.scalar_tensor_tensor(out=x, in0=q, scalar=-part, in1=x, op0=ALU.mult, op1=ALU.add)
                        dve.drain()

                def exp(x, q, qi, p):
                    dve.tensor_scalar(x, x, -87.0, 88.0, ALU.max, ALU.min)
                    dve.drain()
                    less_multiples(x, q, 1.0 / math.log(2.0), (0.693359375, math.log(2.0) - 0.693359375))
                    horner(p, x, [1.0 / math.factorial(n) for n in range(8, 0, -1)])
                    dve.tensor_scalar(q, q, 127.0, float(2 ** 23), ALU.add, ALU.mult)
                    dve.drain()
                    dve.tensor_copy(qi, q)
                    dve.drain()
                    dve.scalar_tensor_tensor(out=p, in0=p, scalar=1.0, in1=qi.bitcast(F32), op0=ALU.add, op1=ALU.mult)
                    dve.drain()

                def skip(c):
                    dve.wait_ge(s_kd, 16 * (c + 1))
                    dve.tensor_tensor(kd[:, 0:1], kd[:, 0:1], dsk[:, c:c + 1], ALU.add).then_inc(s_skip, 1)

                dve.wait_ge(s_dsk, 16)
                for c in range(DC):
                    dve.wait_ge(s_ld, 16 * 5 * (c + 1))
                    W = [w[:, i, :] for i in range(12)]
                    are, aim, cre, cim = (par[:, i, :] for i in range(4))
                    dve.tensor_copy(dt[:, 1:2], ldt[:, :])
                    dve.drain()
                    exp(dt[:, 1:2], dt[:, 2:3], dt_bits[:, :], dt[:, 0:1])
                    for k in range(LEVELS):
                        dve.tensor_scalar(z[:, 0, k, :], are, dt[:, 0:1], float(2 ** k), ALU.mult, ALU.mult)
                        dve.tensor_scalar(z[:, 1, k, :], aim, dt[:, 0:1], float(2 ** k), ALU.mult, ALU.mult)
                    dve.drain()
                    X, Y, Q, V, SI, CO = (z[:, i, :, :] for i in range(6))
                    exp(X, Q, z_bits[:, :, :], V)
                    dve.tensor_copy(X, V)
                    dve.drain()
                    less_multiples(Y, Q, 1.0 / (2.0 * math.pi), (TURN_1, TURN_2, TURN_3))
                    mul(Y, Y, 0.25)
                    tt(V, Y, Y, ALU.mult)
                    horner(SI, V, [(-1.0) ** n / math.factorial(2 * n + 1) for n in range(4, 0, -1)])
                    dve.scalar_tensor_tensor(out=SI, in0=SI, scalar=1.0, in1=Y, op0=ALU.add, op1=ALU.mult)
                    horner(CO, V, [(-1.0) ** n / math.factorial(2 * n) for n in range(5, 0, -1)])
                    dve.tensor_scalar(CO, CO, 1.0, None, ALU.add)
                    dve.drain()
                    for _ in range(2):
                        tt(V, SI, SI, ALU.mult)
                        dve.scalar_tensor_tensor(out=SI, in0=SI, scalar=2.0, in1=CO, op0=ALU.mult, op1=ALU.mult)
                        dve.drain()
                        dve.tensor_scalar(CO, V, -2.0, 1.0, ALU.mult, ALU.add)
                        dve.drain()
                    half = LEVELS // 2
                    if c >= 1:
                        dve.wait_ge(s_tab[1], c)
                    tt(lam[:, :, 0, :], X[:, 0:half], CO[:, 0:half], ALU.mult)
                    tt(lam[:, :, 1, :], X[:, 0:half], SI[:, 0:half], ALU.mult)
                    tt(big[:, :, 0, :], X[:, half:], CO[:, half:], ALU.mult)
                    dve.scalar_tensor_tensor(out=big[:, :, 1, :], in0=X[:, half:], scalar=-1.0, in1=SI[:, half:],
                                             op0=ALU.mult, op1=ALU.mult)
                    dve.drain()
                    dve.tensor_scalar(W[2], lam[:, 0, 0, :], -1.0, None, ALU.add)
                    dve.drain()
                    li = lam[:, 0, 1, :]
                    tt(W[5], cre, W[2], ALU.mult)
                    tt(W[6], cim, li, ALU.mult)
                    tt(W[7], W[5], W[6], ALU.subtract)
                    tt(W[5], cre, li, ALU.mult)
                    tt(W[6], cim, W[2], ALU.mult)
                    tt(W[8], W[5], W[6], ALU.add)
                    tt(W[5], are, are, ALU.mult)
                    tt(W[6], aim, aim, ALU.mult)
                    tt(W[9], W[5], W[6], ALU.add)
                    dve.reciprocal(W[9], W[9])
                    dve.drain()
                    mul(W[9], W[9], 2.0)
                    tt(W[5], W[7], are, ALU.mult)
                    tt(W[6], W[8], aim, ALU.mult)
                    tt(W[5], W[5], W[6], ALU.add)
                    tt(W[10], W[5], W[9], ALU.mult)
                    tt(W[5], W[7], aim, ALU.mult)
                    tt(W[6], W[8], are, ALU.mult)
                    tt(W[5], W[5], W[6], ALU.subtract)
                    tt(W[11], W[5], W[9], ALU.mult)
                    dve.drain().then_inc(s_pow, 1)
                    if c >= 1:
                        skip(c - 1)
                    dve.wait_ge(s_trc, 16 * c)
                    dve.memset(tab[0][:, 0, 0, :], 1.0)
                    dve.memset(tab[0][:, 0, 1, :], 0.0)
                    dve.drain()
                    grow(dve, tab[0], tmp[0], lam, R)
                    dve.drain().then_inc(s_tab[0], 1)
                skip(DC - 1)
        st.clear()



def stage_butterfly(nc, A, w3_out, b3_out, w4_out):
    LOW = 7
    TOP = 4
    PAIRS = HID // 2
    with ExitStack() as ctx:
        st = Stage(nc, ctx, "bf")
        sb, psum, sem = st.sb, st.psum, st.sem
        ident = sb("ident", [P, P])
        e_up = sb("e_up", [P, 2, HID])
        e_dn = sb("e_dn", [P, 2, HID])
        w_up = sb("w_up", [P, 2, PAIRS, 4])
        w_dn = sb("w_dn", [P, 2, PAIRS, 4])
        tmp_up = sb("tmp_up", [P, 2, PAIRS])
        tmp_dn = sb("tmp_dn", [P, 2, PAIRS])
        col_up = sb("col_up", [P, TOP, HC // 2, 4])
        col_dn = sb("col_dn", [P, TOP, HC // 2, 4])
        wx = sb("wx", [P, HID])
        wT = sb("wT", [P, HC, D + 2])
        wc = sb("wc", [P, HC, D])
        pair_tmp = sb("pair_tmp", [P, 2, 2, D + 2])
        upb = sb("upb", [P, HC])
        eT = sb("eT", [P, 2, P])
        out_t = sb("out_t", [P, 2, D])
        ps = psum("ps", [P, 2, 512])
        ps_b = psum("ps_b", [P, HC])
        ps_e = psum("ps_e", [P, 2, 512])

        s_id = sem("identity")
        s_wu = [sem(f"up_stage_weights{k}") for k in range(2)]
        s_wd = [sem(f"down_stage_weights{k}") for k in range(2)]
        s_cols = sem("columns_loaded")
        s_wx = sem("w_exp_loaded")
        s_up = sem("up_matrix_stage")
        s_dn = sem("down_matrix_stage")
        s_tr = sem("transposed")
        s_trc = sem("transposed_copied")
        s_mm = sem("block_product")
        s_mmc = sem("block_product_copied")
        s_hi = sem("across_blocks")
        s_r = sem("rows_transposed")
        s_rc = sem("rows_copied")
        s_wc = sem("w_con_loaded")
        s_dhi = sem("down_across_blocks")
        s_eT = sem("down_matrix_transposed")
        s_eTc = sem("down_matrix_transposed_copied")
        s_d = sem("down_product")
        s_dc = sem("down_product_copied")
        s_out = [sem(f"stored{k}") for k in range(2)]
        s_b3 = sem("bias_stored")

        def low_stage(eng, e, w, tmp, s):
            width = 2 ** s
            src = e[:, s % 2, :].rearrange("p (n two s) -> p two n s", two=2, s=width)
            dst = e[:, 1 - s % 2, :].rearrange("p (n two s) -> p two n s", two=2, s=width)
            wv = w[:, s % 2, :, :].rearrange("p (n s) f -> p f n s", s=width)
            t = [tmp[:, i, :].rearrange("p (n s) -> p n s", s=width) for i in range(2)]
            for o in range(2):
                eng.tensor_tensor(t[0], src[:, 0], wv[:, 2 * o], ALU.mult)
                eng.tensor_tensor(t[1], src[:, 1], wv[:, 2 * o + 1], ALU.mult)
                eng.drain()
                last = eng.tensor_tensor(dst[:, o], t[0], t[1], ALU.add)
                eng.drain()
            return last

        def block_pairs(s):
            w = 2 ** s
            return [(q // w * 2 * w + q % w, q // w * 2 * w + q % w + w) for q in range(HC // 2)]

        def across(eng, x, col, s, width, transposed):
            a10, a01 = (1, 2) if transposed else (2, 1)
            for q, (a, b) in enumerate(block_pairs(s)):
                ta, tb = pair_tmp[:, q % 2, 0, 0:width], pair_tmp[:, q % 2, 1, 0:width]
                xa, xb = x[:, a, 0:width], x[:, b, 0:width]
                eng.tensor_scalar(ta, xa, col[:, s, q, 0:1], None, ALU.mult)
                eng.tensor_scalar(tb, xa, col[:, s, q, a10:a10 + 1], None, ALU.mult)
                eng.drain()
                eng.scalar_tensor_tensor(out=xa, in0=xb, scalar=col[:, s, q, a01:a01 + 1], in1=ta, op0=ALU.mult, op1=ALU.add)
                eng.drain()
                eng.scalar_tensor_tensor(out=xb, in0=xb, scalar=col[:, s, q, 3:4], in1=tb, op0=ALU.mult, op1=ALU.add)
            eng.drain()

        with nc.Block() as block:

            @block.sync
            def _(sp):
                def down_stage_weights(s):
                    if s >= 2:
                        sp.wait_ge(s_dn, s - 1)
                    sp.dma_start(w_dn[:, s % 2, :, :], A["L0_ffn_down_weights"][s:s + 1].rearrange("o k i j -> o k (i j)").broadcast_to([P, PAIRS, 4]))\
                      .then_inc(s_wd[s % 2], 16)

                down_stage_weights(0)
                for v, name in ((col_up, "L0_ffn_up_weights"), (col_dn, "L0_ffn_down_weights")):
                    for k in range(TOP):
                        sp.dma_start(v[:, k, :, :], A[name][LOW + k].rearrange("(q p) i j -> p q (i j)", p=P)).then_inc(s_cols, 16)
                sp.dma_start(wT[:, :, D:D + 1], A["L0_ffn_b_exp"].rearrange("(c p o) -> p c o", p=P, o=1), allow_slow_non_contiguous=True).then_inc(s_cols, 16)
                sp.dma_start(upb[:, :], A["L0_ffn_up_bias"].rearrange("(c p) -> p c", p=P), allow_slow_non_contiguous=True)\
                  .then_inc(s_cols, 16)
                for c in range(DC):
                    if c >= 1:
                        sp.wait_ge(s_tr, 4 * c)
                    sp.dma_start(wx[:, :], A["L0_ffn_W_exp"][c * P:(c + 1) * P, :]).then_inc(s_wx, 16)
                for s in range(1, LOW):
                    down_stage_weights(s)
                    if s == 2:
                        sp.dma_start(wc[:, :, :], A["L0_ffn_W_con"].rearrange("(c p) n -> p c n", p=P)).then_inc(s_wc, 16)
                for n in range(HC):
                    sp.wait_ge(s_dc, n + 1)
                    sp.dma_start(w4_out[n * P:(n + 1) * P, :], out_t[:, n % 2, :]).then_inc(s_out[n % 2], 16)
                for n in range(4 * DC):
                    sp.wait_ge(s_rc, n + 1)
                    c, g = n // 4, n % 4
                    sp.dma_start(w3_out[c * P:(c + 1) * P, g * 512:(g + 1) * 512], out_t[:, n % 2, :]).then_inc(s_out[n % 2], 16)
                for k in range(2):
                    sp.wait_ge(s_out[k], 16 * (4 * DC + HC) // 2)

            @block.gpsimd
            def _(pool):
                pool.memset(ident[:, :], 0.0)
                pool.drain()
                pool.affine_select(out=ident[:, :], in_=ident[:, :], compare_op=ALU.not_equal, fill=1.0,
                                   base=0, pattern=[[-1, P]], channel_multiplier=1)
                pool.drain().then_inc(s_id, 1)
                for c in range(HC):
                    pool.tensor_copy(e_dn[:, 0, c * P:(c + 1) * P], ident[:, :])
                pool.drain()
                for s in range(LOW):
                    pool.wait_ge(s_wd[s % 2], 16 * (s // 2 + 1))
                    low_stage(pool, e_dn, w_dn, tmp_dn, s)
                    pool.drain().then_inc(s_dn, 1)

            @block.tensor
            def _(pe):
                pe.wait_ge(s_id, 1)
                for c in range(DC):
                    pe.wait_ge(s_wx, 16 * (c + 1))
                    for g in range(4):
                        n = 4 * c + g
                        if n >= 2:
                            pe.wait_ge(s_trc, n - 1)
                        for q in range(4):
                            h = 4 * g + q
                            last = pe.transpose(ps[:, n % 2, q * P:(q + 1) * P], wx[:, h * P:(h + 1) * P], ident[:, :])
                        last.then_inc(s_tr, 1)
                pe.wait_ge(s_trc, 16)
                pe.wait_ge(s_cols, 16 * 10)
                pe.wait_ge(s_up, LOW)
                for h in range(HC):
                    if h >= 2:
                        pe.wait_ge(s_mmc, h - 1)
                    blk = e_up[:, LOW % 2, h * P:(h + 1) * P]
                    pe.matmul(ps_b[:, h:h + 1], blk, wT[:, h, D:D + 1], start=True, stop=True)
                    pe.matmul(ps[:, h % 2, :], blk, wT[:, h, 0:D], start=True, stop=True).then_inc(s_mm, 1)
                pe.wait_ge(s_mmc, HC)
                pe.wait_ge(s_dn, LOW)
                pe.wait_ge(s_dhi, 1)

                def down_turned(h):
                    if h >= 2:
                        pe.wait_ge(s_eTc, h - 1)
                    pe.transpose(ps_e[:, h % 2, 0:P], e_dn[:, LOW % 2, h * P:(h + 1) * P], ident[:, :]).then_inc(s_eT, 1)

                down_turned(0)
                for h in range(HC):
                    if h + 1 < HC:
                        down_turned(h + 1)
                    pe.wait_ge(s_eTc, h + 1)
                    if h >= 2:
                        pe.wait_ge(s_dc, h - 1)
                    pe.matmul(ps[:, h % 2, :], eT[:, h % 2, :], wc[:, h, :], start=True, stop=True).then_inc(s_d, 1)
                pe.wait_ge(s_hi, 1)
                pe.wait_ge(s_dc, HC)
                for c in range(DC):
                    for g in range(4):
                        n = 4 * c + g
                        if n >= 2:
                            pe.wait_ge(s_rc, n - 1)
                        for q in range(4):
                            h = 4 * g + q
                            last = pe.transpose(ps[:, n % 2, q * P:(q + 1) * P], wT[:, h, c * P:(c + 1) * P], ident[:, :])
                        last.then_inc(s_r, 1)

            @block.scalar
            def _(act):
                def up_stage_weights(s):
                    if s >= 2:
                        act.wait_ge(s_up, s - 1)
                    act.dma_start(w_up[:, s % 2, :, :], A["L0_ffn_up_weights"][s:s + 1].rearrange("o k i j -> o k (i j)").broadcast_to([P, PAIRS, 4]))\
                       .then_inc(s_wu[s % 2], 16)

                up_stage_weights(0)
                up_stage_weights(1)
                for n in range(16):
                    act.wait_ge(s_tr, n + 1)
                    c, g = n // 4, n % 4
                    act.activation(wT[:, 4 * g:4 * g + 4, c * P:(c + 1) * P], ps[:, n % 2, :].rearrange("p (q t) -> p q t", q=4),
                                   ACT.Copy).then_inc(s_trc, 1)
                    if g == 3:
                        up_stage_weights(c + 2)
                for s in range(DC + 2, LOW):
                    up_stage_weights(s)
                for h in range(HC):
                    act.wait_ge(s_mm, h + 1)
                    act.activation(wT[:, h, 0:D], ps[:, h % 2, :], ACT.Copy).then_inc(s_mmc, 1)
                def down_copied(h):
                    act.wait_ge(s_eT, h + 1)
                    if h >= 2:
                        act.wait_ge(s_d, h - 1)
                    act.activation(eT[:, h % 2, :], ps_e[:, h % 2, 0:P], ACT.Copy).then_inc(s_eTc, 1)

                down_copied(0)
                for h in range(HC):
                    if h + 1 < HC:
                        down_copied(h + 1)
                    act.wait_ge(s_d, h + 1)
                    if h >= 2:
                        act.wait_ge(s_out[h % 2], 16 * (h // 2))
                    act.activation(out_t[:, h % 2, :], ps[:, h % 2, :], ACT.Copy).then_inc(s_dc, 1)
                for n in range(16):
                    act.wait_ge(s_r, n + 1)
                    act.wait_ge(s_out[n % 2], 16 * (HC // 2 + n // 2))
                    act.activation(out_t[:, n % 2, :], ps[:, n % 2, :], ACT.Copy).then_inc(s_rc, 1)
                act.wait_ge(s_hi, 1)
                act.dma_start(b3_out.rearrange("(c p) -> p c", p=P), upb[:, :], allow_slow_non_contiguous=True).then_inc(s_b3, 16)
                act.wait_ge(s_b3, 16)

            @block.vector
            def _(dve):
                dve.wait_ge(s_id, 1)
                for c in range(HC):
                    dve.tensor_copy(e_up[:, 0, c * P:(c + 1) * P], ident[:, :])
                dve.drain()
                for s in range(LOW):
                    dve.wait_ge(s_wu[s % 2], 16 * (s // 2 + 1))
                    low_stage(dve, e_up, w_up, tmp_up, s)
                    dve.drain().then_inc(s_up, 1)
                dve.wait_ge(s_wc, 16)
                dve.wait_ge(s_cols, 16 * 10)
                for s in reversed(range(TOP)):
                    across(dve, wc, col_dn, s, D, True)
                dve.drain().then_inc(s_dhi, 1)
                dve.wait_ge(s_mmc, HC)
                dve.tensor_copy(wT[:, :, D:D + 1], ps_b[:, :].rearrange("p (h o) -> p h o", o=1))
                dve.drain()
                for s in range(TOP):
                    across(dve, wT, col_up, s, D + 1, False)
                dve.tensor_tensor(upb[:, :], upb[:, :], wT[:, :, D], ALU.add)
                dve.drain().then_inc(s_hi, 1)
        st.clear()


def stage_attention(nc, A, x1_out, qt_out):
    SLOTS = 4
    with ExitStack() as ctx:
        st = Stage(nc, ctx, "at")
        sb, psum, sem = st.sb, st.psum, st.sem
        ident = sb("ident", [P, P])
        ones = sb("ones", [P, P])
        wq = sb("wq", [P, DC, D])
        wk = sb("wk", [P, DC, D])
        wv = sb("wv", [P, DC, D])
        wo = sb("wo", [P, DC, D])
        wxq = sb("wxq", [P, DC, P])
        bq = sb("bq", [P, DC])
        bk = sb("bk", [P, DC])
        bv = sb("bv", [P, DC])
        bvw = sb("bvw", [P, DC, P])
        bo = sb("bo", [P, D])
        wqT = sb("wqT", [P, DC, D])
        wkT = sb("wkT", [P, DC, D])
        wvT = sb("wvT", [P, DC, D])
        m_qk = sb("m_qk", [P, DC, D])
        w_vo = sb("w_vo", [P, DC, D])
        u_k = sb("u_k", [P, DC])
        u_q = sb("u_q", [P, DC])
        bqk = sb("bqk", [P, 1])
        b_row = sb("b_row", [P, D])
        w_own = sb("w_own", [P, TPB])
        w_oth = sb("w_oth", [P, TPB])
        neghalf = sb("neghalf", [P, 1])
        xk = sb("xk", [P, SLOTS, 2, D])
        xq = sb("xq", [P, SLOTS, D])
        xT = sb("xT", [P, 2, DC, 2 * P])
        tT = sb("tT", [P, DC, P])
        crow = sb("crow", [P, 2, 1])
        sc = sb("sc", [P, 2, 2 * P])
        mx = sb("mx", [P, 2, 2])
        p1 = sb("p1", [P, P])
        p2 = sb("p2", [P, P])
        den = sb("den", [P, 2, 2])
        rec = sb("rec", [P, 2])
        att = sb("att", [P, 2 * P])
        attT = sb("attT", [P, 2, P])
        oT = sb("oT", [P, DC, P])
        res = sb("res", [P, D])
        stats = sb("stats", [P, 6])
        mv = sb("mv", [P, 2])
        rstd = sb("rstd", [P, 1])
        x1 = sb("x1", [P, 2, D])
        x1T = sb("x1T", [P, DC, P])
        qhl = sb("qhl", [P, 2, 2, P], F32R)

        ps_x = psum("ps_x", [P, 2, 2 * 2 * P])
        ps_t = psum("ps_t", [P, DC, P])
        ps_s = psum("ps_s", [P, 4 * P])
        ps_c = psum("ps_c", [P, D])
        ps_x1 = psum("ps_x1", [P, DC, P])
        ps_o = psum("ps_o", [P, DC, P])
        ps_y = psum("ps_y", [P, D])

        s_w = sem("weights_loaded")
        s_const = sem("constants")
        s_wT = sem("weight_transposes")
        s_wTc = sem("weight_transposes_copied")
        s_fold = sem("folded")
        s_foldc = sem("folded_copied")
        s_bvw = sem("bv_widened")
        s_x = [sem(f"x_loaded{k}") for k in range(SLOTS)]
        s_xT = sem("x_transposed")
        s_xTc = sem("x_transposed_copied")
        s_t = sem("t_done")
        s_tc = sem("t_copied")
        s_s = sem("scores_done")
        s_crow = sem("score_bias")
        s_sc = sem("scores_copied")
        s_mx = sem("max_done")
        s_p = sem("probs_done")
        s_att = sem("attention_done")
        s_aT = sem("attention_transposed")
        s_aTc = sem("attention_transposed_copied")
        s_o = sem("mix_done")
        s_oc = sem("mix_copied")
        s_y = sem("projected")
        s_var = sem("variance")
        s_rstd = sem("rstd")
        s_x1 = sem("x1_done")
        s_x1T = sem("x1_transposed")
        s_x1Tc = sem("x1_transposed_copied")
        s_q = sem("q_done")
        s_qh = sem("q_hi")
        s_ql = sem("q_lo")
        s_st = [sem(f"x1_stored{k}") for k in range(2)]
        s_sq = [sem(f"q_stored{k}") for k in range(2)]
        x_flat = A["x"].rearrange("b s d -> (b s) d")

        def batches(eng, tile):
            for j in range(TPB):
                tile(0, j, j == 0, False)
            with eng.Fori(1, B - 1) as b:
                for j in range(TPB):
                    tile(b, j, False, False)
            for j in range(TPB):
                tile(B - 1, j, False, j == TPB - 1)

        def after(b, j, d):
            bb, jj = b + (j + d) // TPB, (j + d) % TPB
            return bb, jj

        with nc.Block() as block:

            @block.sync
            def _(sp):
                for w, name in ((wq, "L0_attn_Wq"), (wk, "L0_attn_Wk"), (wv, "L0_attn_Wv"), (wo, "L0_attn_Wo")):
                    sp.dma_start(w[:, :, :], A[name].rearrange("(c p) n -> p c n", p=P)).then_inc(s_w, 16)
                sp.dma_start(wxq[:, :, :], A["L0_xattn_Wq"].rearrange("(c p) n -> p c n", p=P)).then_inc(s_w, 16)
                for v, name in ((bq, "L0_attn_bq"), (bk, "L0_attn_bk"), (bv, "L0_attn_bv")):
                    sp.dma_start(v[:, :], A[name].rearrange("(c p) -> p c", p=P), allow_slow_non_contiguous=True).then_inc(s_w, 16)
                sp.dma_start(bo[:, :], A["L0_attn_bo"].rearrange("(o n) -> o n", o=1).broadcast_to([P, D])).then_inc(s_w, 16)

                def load(b, j, first, last):
                    k, t0, i = j % SLOTS, b * S + j * P, b * TPB + j
                    if not (isinstance(b, int) and i < SLOTS):
                        sp.wait_ge(s_o, i - SLOTS + 1)
                        sp.wait_ge(s_x1, i - SLOTS + 1)
                    lo = t0 - 64 if j > 0 else t0
                    hi = t0 + P if j < TPB - 1 else t0 + P - 64
                    sp.dma_start(xk[0:64, k, 0, :], rows(x_flat, lo, 64)).then_inc(s_x[k], 16)
                    sp.dma_start(xk[64:128, k, 0, :], rows(x_flat, t0, 64)).then_inc(s_x[k], 16)
                    sp.dma_start(xk[0:64, k, 1, :], rows(x_flat, t0 + 64, 64)).then_inc(s_x[k], 16)
                    sp.dma_start(xk[64:128, k, 1, :], rows(x_flat, hi, 64)).then_inc(s_x[k], 16)
                    sp.dma_start(xq[:, k, :], rows(x_flat, t0, P)).then_inc(s_x[k], 16)

                batches(sp, load)

            @block.gpsimd
            def _(pool):
                pool.memset(ident[:, :], 0.0).then_inc(s_const, 1)
                pool.memset(ones[:, :], 1.0).then_inc(s_const, 1)
                pool.memset(neghalf[:, :], -0.5).then_inc(s_const, 1)
                pool.memset(att[:, :], 0.0).then_inc(s_const, 1)
                pool.wait_ge(s_const, 4)
                pool.affine_select(out=ident[:, :], in_=ident[:, :], compare_op=ALU.not_equal, fill=1.0,
                                   base=0, pattern=[[-1, P]], channel_multiplier=1).then_inc(s_const, 1)
                with pool.Fori(0, B) as b:
                    for j in range(TPB):
                        pool.wait_ge(s_var, b * TPB + j + 1)
                        pool.tensor_tensor(rstd[:, :], mv[:, 1:2], neghalf[:, :], ALU.pow).then_inc(s_rstd, 1)

            @block.tensor
            def _(pe):
                pe.wait_ge(s_const, 5)
                pe.wait_ge(s_w, 16 * 9)
                n = 0
                for w in (wq, wk, wv):
                    for c in range(DC):
                        if n >= 2:
                            pe.wait_ge(s_wTc, n - 1)
                        for e in range(DC):
                            last = pe.transpose(ps_x[:, n % 2, e * P:(e + 1) * P], w[:, c, e * P:(e + 1) * P], ident[:, :])
                        last.then_inc(s_wT, 1)
                        n += 1
                pe.wait_ge(s_wTc, 3 * DC)
                n = 0
                for wT, mv_ in ((wqT, wkT), (wvT, wo)):
                    for c in range(DC):
                        if n >= 2:
                            pe.wait_ge(s_foldc, n - 1)
                        for e in range(DC):
                            last = pe.matmul(ps_x[:, n % 2, :], wT[:, e, c * P:(c + 1) * P], mv_[:, e, :],
                                             start=(e == 0), stop=(e == DC - 1))
                        last.then_inc(s_fold, 1)
                        n += 1
                pe.wait_ge(s_bvw, 1)
                for i, (wT, v) in enumerate(((wkT, bq), (wqT, bk))):
                    for c in range(DC):
                        for e in range(DC):
                            pe.matmul(ps_c[:, i * DC + c:i * DC + c + 1], wT[:, e, c * P:(c + 1) * P], v[:, e:e + 1],
                                      start=(e == 0), stop=(e == DC - 1))
                for e in range(DC):
                    pe.matmul(ps_s[:, 0:1], oT[:, e, :], bk[:, e:e + 1], start=(e == 0), stop=(e == DC - 1))
                for e in range(DC):
                    last = pe.matmul(ps_y[:, :], bvw[:, e, :], wo[:, e, :], start=(e == 0), stop=(e == DC - 1))
                last.then_inc(s_fold, 1)
                pe.wait_ge(s_foldc, 2 * DC + 1)


                def x_turned(b, j):
                    k, i = j % 2, b * TPB + j
                    slot = j % SLOTS
                    pe.wait_ge(s_x[slot], 80 * (b * (TPB // SLOTS) + j // SLOTS + 1))
                    pe.wait_ge(s_xTc, i)
                    for c in range(DC):
                        for h in range(2):
                            last = pe.transpose(ps_x[:, c // 2, (c % 2) * 2 * P + h * P:(c % 2) * 2 * P + (h + 1) * P],
                                                xk[:, slot, h, c * P:(c + 1) * P], ident[:, :])
                    last.then_inc(s_xT, 1)

                def queries(b, j):
                    k, i = j % 2, b * TPB + j
                    pe.wait_ge(s_xTc, i + 1)
                    pe.wait_ge(s_tc, i)
                    if not (isinstance(i, int) and i < 3):
                        pe.wait_ge(s_ql, i - 2)
                    for m in range(DC):
                        for c in range(DC):
                            pe.matmul(ps_t[:, m, :], m_qk[:, c, m * P:(m + 1) * P], xT[:, k, c, 64:64 + P],
                                      start=(c == 0), stop=(c == DC - 1))
                    for c in range(DC):
                        last = pe.matmul(ps_c[:, 0:1], xT[:, k, c, 64:64 + P], u_q[:, c:c + 1],
                                         start=(c == 0), stop=(c == DC - 1))
                    last.then_inc(s_t, 1)

                def scores(b, j):
                    k, i = j % 2, b * TPB + j
                    pe.wait_ge(s_tc, i + 1)
                    pe.wait_ge(s_sc, i)
                    for c in range(DC):
                        last = pe.matmul(ps_s[:, 0:2 * P], tT[:, c, :], xT[:, k, c, :], start=(c == 0), stop=(c == DC - 1))
                    last.then_inc(s_s, 1)

                def x1_turned(i, k):
                    pe.wait_ge(s_x1, i + 1)
                    pe.wait_ge(s_x1Tc, i)
                    for c in range(DC):
                        last = pe.transpose(ps_x1[:, c, :], x1[:, k, c * P:(c + 1) * P], ident[:, :])
                    last.then_inc(s_x1T, 1)

                def cross_q(i):
                    pe.wait_ge(s_x1Tc, i + 1)
                    pe.wait_ge(s_crow, min(i + 3, TILES) if isinstance(i, int) else i + 3)
                    pe.wait_ge(s_ql, i)
                    for c in range(DC):
                        last = pe.matmul(ps_c[:, P:2 * P], wxq[:, c, :], x1T[:, c, :], start=(c == 0), stop=(c == DC - 1))
                    last.then_inc(s_q, 1)

                def tile(b, j, first, last):
                    i, slot = b * TPB + j, j % SLOTS
                    if not last:
                        queries(*after(b, j, 1))
                    pe.wait_ge(s_att, i + 1)
                    pe.wait_ge(s_aTc, i)
                    for h in range(2):
                        done = pe.transpose(ps_s[:, (2 + h) * P:(3 + h) * P], att[:, h * P:(h + 1) * P], ident[:, :])
                    done.then_inc(s_aT, 1)
                    if not first:
                        x1_turned(i - 1, (j + 1) % 2)
                    pe.wait_ge(s_aTc, i + 1)
                    pe.wait_ge(s_oc, i)
                    for c in range(DC):
                        for h in range(2):
                            done = pe.matmul(ps_o[:, c, :], xk[:, slot, h, c * P:(c + 1) * P], attT[:, h, :],
                                             start=(h == 0), stop=(h == 1))
                    done.then_inc(s_o, 1)
                    if not first:
                        cross_q(i - 1)
                    if not last:
                        scores(*after(b, j, 1))
                        if not (isinstance(b, int) and i + 2 >= TILES):
                            x_turned(*after(b, j, 2))
                    pe.wait_ge(s_oc, i + 1)
                    pe.wait_ge(s_x1, i)
                    for c in range(DC):
                        done = pe.matmul(ps_y[:, :], oT[:, c, :], w_vo[:, c, :], start=(c == 0), stop=(c == DC - 1))
                    done.then_inc(s_y, 1)

                x_turned(0, 0)
                queries(0, 0)
                scores(0, 0)
                x_turned(0, 1)
                batches(pe, tile)
                x1_turned(TILES - 1, 1)
                cross_q(TILES - 1)

            @block.scalar
            def _(act):
                n = 0
                for wT in (wqT, wkT, wvT):
                    for c in range(DC):
                        act.wait_ge(s_wT, n + 1)
                        act.activation(wT[:, :, c * P:(c + 1) * P], ps_x[:, n % 2, :].rearrange("p (e q) -> p e q", e=DC),
                                       ACT.Copy).then_inc(s_wTc, 1)
                        n += 1
                n = 0
                for w in (m_qk, w_vo):
                    for c in range(DC):
                        act.wait_ge(s_fold, n + 1)
                        act.activation(w[:, c, :], ps_x[:, n % 2, :], ACT.Copy).then_inc(s_foldc, 1)
                        n += 1

                def x_copied(i, k):
                    act.wait_ge(s_xT, i + 1)
                    if not (isinstance(i, int) and i < 2):
                        act.wait_ge(s_s, i - 1)
                    for h in range(2):
                        act.activation(xT[:, k, 2 * h:2 * h + 2, :], ps_x[:, h, :].rearrange("p (c q) -> p c q", c=2),
                                       ACT.Copy)
                    act.drain().then_inc(s_xTc, 1)

                def scores_copied(i, k):
                    act.wait_ge(s_s, i + 1)
                    act.wait_ge(s_crow, i + 1)
                    act.activation(sc[:, k, :], ps_s[:, 0:2 * P], ACT.Identity, bias=crow[:, k, :], scale=SCALE).then_inc(s_sc, 1)

                def exponentials(i, k):
                    act.wait_ge(s_mx, i + 1)
                    act.wait_ge(s_att, i)
                    act.activation(p1[:, :], sc[:, k, 64:64 + P], ACT.Exp, bias=mx[:, k, 0:1], accum_out=den[:, k, 0:1])
                    act.activation(p2[0:64, :], sc[0:64, k, 0:P], ACT.Exp, bias=mx[0:64, k, 1:2], accum_out=den[0:64, k, 1:2])
                    act.activation(p2[64:128, :], sc[64:128, k, P:2 * P], ACT.Exp, bias=mx[64:128, k, 1:2],
                                   accum_out=den[64:128, k, 1:2]).then_inc(s_p, 1)

                def x1_copied(i):
                    act.wait_ge(s_x1T, i + 1)
                    act.wait_ge(s_q, i)
                    act.activation(x1T[:, :, :], ps_x1[:, :, :], ACT.Copy).then_inc(s_x1Tc, 1)

                def q_hi(i, k, stores):
                    act.wait_ge(s_q, i + 1)
                    act.wait_ge(s_sq[k], 32 * stores)
                    act.activation(qhl[:, k, 0, :], ps_c[:, P:2 * P], ACT.Copy).then_inc(s_qh, 1)

                def store(i, k):
                    act.wait_ge(s_ql, i + 1)
                    act.dma_start(rows(x1_out, i * P, P), x1[:, k, :]).then_inc(s_st[k], 16)
                    for hl in range(2):
                        act.dma_start(qt_out[hl, :, bass.ds(i * P, P)], qhl[:, k, hl, :].bitcast(F32)).then_inc(s_sq[k], 16)

                def tile(b, j, first, last):
                    i, k = b * TPB + j, j % 2
                    act.wait_ge(s_aT, i + 1)
                    act.wait_ge(s_o, i)
                    act.activation(attT[:, :, :], ps_s[:, 2 * P:4 * P].rearrange("p (h q) -> p h q", h=2), ACT.Copy).then_inc(s_aTc, 1)
                    if not first:
                        x1_copied(i - 1)
                    act.wait_ge(s_o, i + 1)
                    act.wait_ge(s_y, i)
                    act.activation(oT[:, :, :], ps_o[:, :, :], ACT.Copy).then_inc(s_oc, 1)
                    if not first:
                        q_hi(i - 1, 1 - k, b * (TPB // 2) + (j - 1) // 2)
                    if not last:
                        scores_copied(i + 1, 1 - k)
                        if not (isinstance(b, int) and i + 2 >= TILES):
                            x_copied(i + 2, k)
                        exponentials(i + 1, 1 - k)
                    if not first:
                        store(i - 1, 1 - k)

                x_copied(0, 0)
                scores_copied(0, 0)
                x_copied(1, 1)
                exponentials(0, 0)
                batches(act, tile)
                x1_copied(TILES - 1)
                q_hi(TILES - 1, 1, TILES // 2 - 1)
                store(TILES - 1, 1)
                for k in range(2):
                    act.wait_ge(s_st[k], 16 * TILES // 2)
                    act.wait_ge(s_sq[k], 32 * TILES // 2)

            @block.vector
            def _(dve):
                dve.wait_ge(s_const, 5)
                dve.wait_ge(s_w, 16 * 9)
                for w in (w_own, w_oth):
                    dve.memset(w[:, :], 0.5)
                dve.drain()
                for w, val in ((w_own, 1.0), (w_oth, 0.0)):
                    dve.memset(w[0:64, 0:1], val)
                    dve.memset(w[64:128, TPB - 1:TPB], val)
                for c in range(DC):
                    dve.tensor_scalar(bvw[:, c, :], ones[:, :], bv[:, c:c + 1], None, ALU.mult)
                    last = dve.tensor_scalar(oT[:, c, :], ones[:, :], bq[:, c:c + 1], None, ALU.mult)
                last.then_inc(s_bvw, 1)
                dve.wait_ge(s_fold, 2 * DC + 1)
                dve.tensor_copy(u_k[:, :], ps_c[:, 0:DC])
                dve.tensor_copy(u_q[:, :], ps_c[:, DC:2 * DC])
                dve.tensor_copy(bqk[:, :], ps_s[:, 0:1])
                dve.tensor_tensor(b_row[:, :], ps_y[:, :], bo[:, :], ALU.add).then_inc(s_foldc, 1)

                def queries_copied(i, k):
                    dve.wait_ge(s_t, i + 1)
                    dve.wait_ge(s_s, i)
                    dve.tensor_scalar(crow[:, k, :], ps_c[:, 0:1], bqk[:, 0:1], SCALE, ALU.add, ALU.mult).then_inc(s_crow, 1)
                    for m in range(DC):
                        dve.tensor_scalar(tT[:, m, :], ps_t[:, m, :], u_k[:, m:m + 1], None, ALU.add)
                    dve.drain().then_inc(s_tc, 1)

                def softmax(i, j):
                    k = j % 2
                    dve.wait_ge(s_sc, i + 1)
                    dve.tensor_reduce(mx[:, k, 0:1], sc[:, k, 64:64 + P], AX.X, ALU.max, negate=True)
                    dve.tensor_reduce(mx[0:64, k, 1:2], sc[0:64, k, 0:P], AX.X, ALU.max, negate=True)
                    dve.tensor_reduce(mx[64:128, k, 1:2], sc[64:128, k, P:2 * P], AX.X, ALU.max, negate=True)
                    dve.drain().then_inc(s_mx, 1)
                    dve.wait_ge(s_p, i + 1)
                    dve.reciprocal(rec[:, :], den[:, k, :])
                    dve.drain()
                    dve.tensor_tensor(rec[:, 0:1], rec[:, 0:1], w_own[:, j:j + 1], ALU.mult)
                    dve.tensor_tensor(rec[:, 1:2], rec[:, 1:2], w_oth[:, j:j + 1], ALU.mult)
                    dve.drain()
                    dve.wait_ge(s_aT, i)
                    dve.tensor_scalar(att[:, 64:64 + P], p1[:, :], rec[:, 0:1], None, ALU.mult)
                    dve.tensor_scalar(att[0:64, 0:64], p2[0:64, 0:64], rec[0:64, 1:2], None, ALU.mult)
                    dve.tensor_scalar(att[64:128, 192:256], p2[64:128, 64:128], rec[64:128, 1:2], None, ALU.mult)
                    dve.drain()
                    dve.scalar_tensor_tensor(out=att[0:64, 64:128], in0=p2[0:64, 64:128], scalar=rec[0:64, 1:2],
                                             in1=att[0:64, 64:128], op0=ALU.mult, op1=ALU.add)
                    dve.scalar_tensor_tensor(out=att[64:128, 128:192], in0=p2[64:128, 0:64], scalar=rec[64:128, 1:2],
                                             in1=att[64:128, 128:192], op0=ALU.mult, op1=ALU.add)
                    dve.drain().then_inc(s_att, 1)

                def q_lo(i, k):
                    dve.wait_ge(s_qh, i + 1)
                    dve.tensor_tensor(qhl[:, k, 1, :], ps_c[:, P:2 * P], qhl[:, k, 0, :].bitcast(F32), ALU.subtract)\
                       .then_inc(s_ql, 1)

                def tile(b, j, first, last):
                    i, k, slot = b * TPB + j, j % 2, j % SLOTS
                    if not last:
                        queries_copied(i + 1, 1 - k)
                    if not first:
                        q_lo(i - 1, 1 - k)
                    if not last:
                        softmax(i + 1, (j + 1) % TPB)
                    dve.wait_ge(s_y, i + 1)
                    dve.tensor_tensor(res[:, :], ps_y[:, :], xq[:, slot, :], ALU.add)
                    dve.drain()
                    dve.tensor_tensor(res[:, :], res[:, :], b_row[:, :], ALU.add)
                    dve.drain()
                    dve.bn_stats(stats[:, :], res[:, :])
                    dve.drain()
                    dve.bn_aggr(mv[:, :], stats[:, :])
                    dve.drain()
                    dve.tensor_scalar(mv[:, 1:2], mv[:, 1:2], EPS, None, ALU.add).then_inc(s_var, 1)
                    dve.wait_ge(s_rstd, i + 1)
                    dve.wait_ge(s_st[k], 16 * (b * (TPB // 2) + j // 2))
                    dve.tensor_scalar(x1[:, k, :], res[:, :], mv[:, 0:1], rstd[:, 0:1], ALU.subtract, ALU.mult)\
                       .then_inc(s_x1, 1)

                queries_copied(0, 0)
                softmax(0, 0)
                batches(dve, tile)
                q_lo(TILES - 1, 1)
        st.clear()


def stage_keys(nc, A, kt_out):
    GROUPS = B * S2 // 512
    with ExitStack() as ctx:
        st = Stage(nc, ctx, "ky")
        sb, psum, sem = st.sb, st.psum, st.sem
        ident = sb("ident", [P, P])
        wk = sb("wk", [P, VC, P])
        raw = sb("raw", [P, 2, 4, DV])
        cT = sb("cT", [P, 2, VC, 4 * P])
        khl = sb("khl", [P, 2, 2, 4 * P], F32R)
        ps_t = psum("ps_t", [P, VC, 4 * P])
        ps_k = psum("ps_k", [P, 2, 4 * P])

        s_const = sem("constants")
        s_ld = sem("weights_loaded")
        s_raw = [sem(f"ctx_loaded{k}") for k in range(2)]
        s_t = sem("ctx_transposed")
        s_tc = sem("ctx_transposed_copied")
        s_k = sem("k_done")
        s_hi = sem("k_hi")
        s_lo = sem("k_lo")
        s_st = [sem(f"k_stored{k}") for k in range(2)]
        keys = A["ctx_768"].rearrange("b g v -> (b g) v")

        with nc.Block() as block:

            @block.sync
            def _(sp):
                sp.dma_start(wk[:, :, :], A["L0_xattn_Wk"].rearrange("(c p) n -> p c n", p=P)).then_inc(s_ld, 16)

                def load(g, k):
                    sp.dma_start(raw[:, k, :, :], rows(keys, g * 512, 512).rearrange("(n p) v -> p n v", p=P)).then_inc(s_raw[k], 16)

                load(0, 0)
                load(1, 1)
                with sp.Fori(1, GROUPS // 2) as j:
                    for k in range(2):
                        sp.wait_ge(s_t, VC * (2 * j + k - 1))
                        load(2 * j + k, k)

            @block.gpsimd
            def _(pool):
                pool.memset(ident[:, :], 0.0)
                pool.drain()
                pool.affine_select(out=ident[:, :], in_=ident[:, :], compare_op=ALU.not_equal, fill=1.0,
                                   base=0, pattern=[[-1, P]], channel_multiplier=1)
                pool.drain().then_inc(s_const, 1)

            @block.tensor
            def _(pe):
                pe.wait_ge(s_const, 1)
                pe.wait_ge(s_ld, 16)

                def turn(g, k, nth):
                    pe.wait_ge(s_raw[k], 16 * nth)
                    for c in range(VC):
                        if not (isinstance(g, int) and g == 0):
                            pe.wait_ge(s_tc, VC * (g - 1) + c + 1)
                        for q in range(4):
                            last = pe.transpose(ps_t[:, c, q * P:(q + 1) * P], raw[:, k, q, c * P:(c + 1) * P], ident[:, :])
                        last.then_inc(s_t, 1)

                def project(g, k, first=False):
                    pe.wait_ge(s_tc, VC * (g + 1))
                    if not first:
                        pe.wait_ge(s_lo, g - 1)
                    for c in range(VC):
                        last = pe.matmul(ps_k[:, k, :], wk[:, c, :], cT[:, k, c, :], start=(c == 0), stop=(c == VC - 1))
                    last.then_inc(s_k, 1)

                turn(0, 0, 1)
                turn(1, 1, 1)
                project(0, 0, first=True)
                with pe.Fori(1, GROUPS // 2) as j:
                    turn(2 * j, 0, j + 1)
                    project(2 * j - 1, 1)
                    turn(2 * j + 1, 1, j + 1)
                    project(2 * j, 0)
                project(GROUPS - 1, 1)

            @block.scalar
            def _(act):
                def copies(g, k):
                    if not (isinstance(g, int) and g < 2):
                        act.wait_ge(s_k, g - 1)
                    for c in range(VC):
                        act.wait_ge(s_t, VC * g + c + 1)
                        act.activation(cT[:, k, c, :], ps_t[:, c, :], ACT.Copy).then_inc(s_tc, 1)

                def hi(g, k, stores):
                    act.wait_ge(s_k, g + 1)
                    act.wait_ge(s_st[k], 16 * stores)
                    act.activation(khl[:, k, 0, :], ps_k[:, k, :], ACT.Copy).then_inc(s_hi, 1)

                def store(g, k):
                    act.wait_ge(s_lo, g + 1)
                    act.dma_start(kt_out[:, :, bass.ds(g * 512, 512)].rearrange("h p g -> p h g"),
                                  khl[:, k, :, :].bitcast(F32)).then_inc(s_st[k], 16)

                copies(0, 0)
                copies(1, 1)
                hi(0, 0, 0)
                with act.Fori(1, GROUPS // 2) as j:
                    copies(2 * j, 0)
                    store(2 * j - 2, 0)
                    hi(2 * j - 1, 1, j - 1)
                    copies(2 * j + 1, 1)
                    store(2 * j - 1, 1)
                    hi(2 * j, 0, j)
                store(GROUPS - 2, 0)
                hi(GROUPS - 1, 1, GROUPS // 2 - 1)
                store(GROUPS - 1, 1)
                for k in range(2):
                    act.wait_ge(s_st[k], 16 * GROUPS // 2)

            @block.vector
            def _(dve):
                with dve.Fori(0, GROUPS // 2) as j:
                    for k in range(2):
                        dve.wait_ge(s_hi, 2 * j + k + 1)
                        dve.tensor_tensor(khl[:, k, 1, :], ps_k[:, k, :], khl[:, k, 0, :].bitcast(F32), ALU.subtract).then_inc(s_lo, 1)
        st.clear()



def stage_cross(nc, A, qt_in, kt_in, ac_out):
    SEGS = 32
    SEG = S2 // SEGS
    NCAND = 8 * SEGS
    HT = HEADS * TPB
    PAIRS = TPB // 2
    with ExitStack() as ctx:
        st = Stage(nc, ctx, "xa")
        sb, psum, sem = st.sb, st.psum, st.sem
        ident = sb("ident", [P, P])
        raw = sb("raw", [P, 2, 4, DV])
        ctx_hl = sb("ctx_hl", [P, 2, GC, DV], F32R)
        ks = sb("ks", [P, HEADS, S2], F32R)
        qs = sb("qs", [P, 2, HEADS, P], F32R)
        row0 = sb("row0", [P, P], BF16)
        mask_u8 = sb("mask_u8", [1, S2], U8)
        mask = sb("mask", [P, S2], BF16)
        ones = sb("ones", [P, 1])
        s_buf = sb("s_buf", [P, 4, S2])
        cand = sb("cand", [P, NCAND])
        cand_b = sb("cand_b", [P, NCAND])
        top = sb("top", [P, 2, TOPK])
        f_junk = sb("f_junk", [P, NCAND])
        f_weight = sb("f_weight", [P, NCAND])
        flag = sb("flag", [P, 2, 1])
        flag_i = sb("flag_i", [1, 2], mybir.dt.int32)
        nmax = sb("nmax", [P, 2, 1])
        e_top = sb("e_top", [P, TOPK])
        den = sb("den", [P, 2, 1])
        rec = sb("rec", [P, 2, 1])
        prob = sb("prob", [P, 2, S2])
        acc = sb("acc", [P, 2, S2])
        a32 = sb("a32", [P, 2, 4, P])
        aT = sb("aT", [P, 2, GC, P], F32R)
        ac = sb("ac", [P, 2, DV])

        ps_s = psum("ps_s", [P, 4, 512])
        ps_t = psum("ps_t", [P, 2, 4, P])
        ps_ac = psum("ps_ac", [P, DV])
        ps_f = psum("ps_f", [1, 2])

        s_const = sem("constants")
        s_ms = sem("mask_loaded")
        s_mask = sem("mask_ready")
        s_raw = [sem(f"raw_loaded{k}") for k in range(2)]
        s_chi = sem("ctx_hi")
        s_clo = sem("ctx_lo")
        s_ks = [sem(f"k_stacked{h}") for h in range(HEADS)]
        s_qs = [sem(f"q_stacked{k}") for k in range(2)]
        s_s = sem("scores_done")
        s_sc = sem("scores_copied")
        s_cand = sem("row_flags_done")
        s_f = sem("flag_summed")
        s_chk = sem("tops_final")
        s_den = sem("denominator")
        s_scl = sem("scaled")
        s_prob = sem("prob_done")
        s_sel = sem("selected")
        s_acc = sem("heads_summed")
        s_aT = sem("attn_transposed")
        s_aTh = sem("attn_hi")
        s_aTl = sem("attn_lo")
        s_a32 = sem("attn_copied")
        s_ac = sem("mix_done")
        s_acc_c = sem("mix_copied")
        s_st = [sem(f"mix_stored{k}") for k in range(2)]

        def steps(eng, body):
            def batch(b, start, end):
                body(b, 0, start, False)
                with eng.Fori(1, PAIRS - 1) as j:
                    body(b, j, False, False)
                body(b, PAIRS - 1, False, end)

            batch(0, True, False)
            with eng.Fori(1, B - 1) as b:
                batch(b, False, False)
            batch(B - 1, False, True)

        def is_pair(j, which):
            return isinstance(j, int) and j == which

        with nc.Block() as block:

            @block.sync
            def _(sp):
                def keys(b, h):
                    for q in range(4):
                        sp.dma_start(ks[32 * q:32 * q + 32, h, :].bitcast(F32),
                                     kt_in[q % 2][h * DH:(h + 1) * DH, bass.ds(b * S2, S2)]).then_inc(s_ks[h], 16)

                def queries(b, j):
                    for k in range(2):
                        t = b * TPB + 2 * j + k
                        sp.wait_ge(s_s, HEADS * (t - 1))
                        for q in range(4):
                            sp.dma_start(qs[32 * q:32 * q + 32, k, :, :].bitcast(F32),
                                         qt_in[q // 2].rearrange("(h e) t -> e h t", e=DH)[:, :, bass.ds(t * P, P)]
                                         ).then_inc(s_qs[k], 16)

                for k in range(2):
                    for q in range(4):
                        sp.dma_start(qs[32 * q:32 * q + 32, k, :, :].bitcast(F32),
                                     qt_in[q // 2].rearrange("(h e) t -> e h t", e=DH)[:, :, k * P:(k + 1) * P]).then_inc(s_qs[k], 16)
                for h in range(HEADS):
                    keys(0, h)
                with sp.Fori(1, TPB // 2) as j:
                    queries(0, j)
                with sp.Fori(1, B) as b:
                    for h in range(HEADS):
                        sp.wait_ge(s_s, HT * b - HEADS + 1 + h)
                        keys(b, h)
                    with sp.Fori(0, TPB // 2) as j:
                        queries(b, j)

            @block.gpsimd
            def _(pool):
                pool.memset(ident[:, :], 0.0).then_inc(s_const, 1)
                pool.memset(ones[:, :], 1.0).then_inc(s_const, 1)
                pool.wait_ge(s_const, 2)
                pool.affine_select(out=ident[:, :], in_=ident[:, :], compare_op=ALU.not_equal, fill=1.0,
                                   base=0, pattern=[[-1, P]], channel_multiplier=1).then_inc(s_const, 1)

                def lo(t, g):
                    pool.wait_ge(s_aTh, 4 * t + g + 1)
                    pool.wait_ge(s_a32, 4 * t + g + 1)
                    pool.tensor_tensor(aT[:, 1, 4 * g:4 * g + 4, :], a32[:, g % 2, :, :],
                                       aT[:, 0, 4 * g:4 * g + 4, :].bitcast(F32), ALU.subtract).then_inc(s_aTl, 1)

                def context_lo(b, g):
                    pool.wait_ge(s_chi, 4 * b + g + 1)
                    pool.tensor_tensor(ctx_hl[:, 1, 4 * g:4 * g + 4, :], raw[:, g % 2, :, :],
                                       ctx_hl[:, 0, 4 * g:4 * g + 4, :].bitcast(F32), ALU.subtract).then_inc(s_clo, 1)

                def body(b, j, start, end):
                    for k in range(2):
                        t = b * TPB + 2 * j + k
                        if is_pair(j, 0) and k == 1:
                            context_lo(b, 0)
                            context_lo(b, 1)
                        if not (start and k == 0):
                            for g in range(4):
                                lo(t - 1, g)
                        if is_pair(j, 0) and k == 1:
                            context_lo(b, 2)
                            context_lo(b, 3)
                        for h in range(1, HEADS):
                            pool.wait_ge(s_scl, HEADS * t + h + 1)
                            pool.wait_ge(s_acc, 3 * t + h - 1)
                            pool.tensor_tensor(acc[:, k, :], acc[:, k, :], prob[:, h % 2, :], ALU.add).then_inc(s_acc, 1)
                    if end:
                        for g in range(4):
                            lo(TILES - 1, g)

                steps(pool, body)

            @block.tensor
            def _(pe):
                pe.wait_ge(s_const, 3)

                def scores(n, k, h):
                    pe.wait_ge(s_sc, n)
                    for c in range(4):
                        pe.matmul(ps_s[:, c, :], qs[:, k, h, :], ks[:, h, c * 512:(c + 1) * 512], start=True, stop=False)
                        last = pe.matmul(ps_s[:, c, :], row0[:, :], mask[:, c * 512:(c + 1) * 512], start=False, stop=True)
                    last.then_inc(s_s, 1)

                def sum_flag(n, k):
                    pe.wait_ge(s_cand, n + 1)
                    pe.matmul(ps_f[:, k:k + 1], flag[:, k, :], ones[:, :], start=True, stop=True).then_inc(s_f, 1)

                def turn(t, k, g):
                    if g == 0:
                        pe.wait_ge(s_acc, 3 * (t + 1))
                    pe.wait_ge(s_a32, t * 4 + g - 1 if g >= 1 else t * 4)
                    for q in range(4):
                        c = 4 * g + q
                        last = pe.transpose(ps_t[:, g % 2, q, :], acc[:, k, c * P:(c + 1) * P], ident[:, :])
                    last.then_inc(s_aT, 1)

                def mix(t, b):
                    pe.wait_ge(s_aTl, t * 4 + 4)
                    pe.wait_ge(s_clo, 4 * (b + 1))
                    pe.wait_ge(s_acc_c, t)
                    for c in range(GC):
                        last = mm3(pe, ps_ac[:, :], aT[:, 0, c, :], aT[:, 1, c, :],
                                   ctx_hl[:, 0, c, :], ctx_hl[:, 1, c, :], start=(c == 0), stop=(c == GC - 1))
                    last.then_inc(s_ac, 1)

                def body(b, j, start, end):
                    for s in range(2 * HEADS):
                        n = HT * b + 2 * HEADS * j + s
                        h = s % HEADS
                        if not (end and s == 2 * HEADS - 1):
                            if is_pair(j, 0) and s < HEADS - 1:
                                pe.wait_ge(s_ks[s + 1], 64 * (b + 1))
                            if is_pair(j, PAIRS - 1) and s == 2 * HEADS - 1:
                                pe.wait_ge(s_ks[0], 64 * (b + 2))
                                pe.wait_ge(s_mask, b + 2)
                            k = (s + 1) // HEADS
                            if (s + 1) % HEADS == 0:
                                pe.wait_ge(s_qs[k % 2], 64 * (b * PAIRS + j + 1 + k // 2))
                            scores(n + 1, k % 2, (s + 1) % HEADS)
                        if not (start and s < HEADS):
                            t, k = b * TPB + 2 * j + s // HEADS - 1, (s // HEADS + 1) % 2
                            if h in (1, 2):
                                turn(t, k, 2 * h - 2)
                                turn(t, k, 2 * h - 1)
                        sum_flag(n, s % 2)
                        if h == 3 and not (start and s < HEADS):
                            mix(t, b - 1 if is_pair(j, 0) and s < HEADS else b)
                    if end:
                        for g in range(4):
                            turn(TILES - 1, 1, g)
                        mix(TILES - 1, B - 1)

                pe.wait_ge(s_ks[0], 64)
                pe.wait_ge(s_mask, 1)
                pe.wait_ge(s_qs[0], 64)
                scores(0, 0, 0)
                steps(pe, body)

            @block.scalar
            def _(act):
                def load_mask(b):
                    act.dma_start(mask_u8[:, :], rows(A["mask_BxS2_bf1"], b, 1)).then_inc(s_ms, 16)

                def load(b, g):
                    act.dma_start(raw[:, g % 2, :, :],
                                  rows(A["ctx_768"], b, 1)[:, g * 512:(g + 1) * 512, :].rearrange("o (n p) v -> p (o n) v", p=P)
                                  ).then_inc(s_raw[g % 2], 16)

                def context_hi(b, g):
                    act.wait_ge(s_raw[g % 2], 16 * (2 * b + g // 2 + 1))
                    act.wait_ge(s_ac, b * TPB)
                    act.activation(ctx_hl[:, 0, 4 * g:4 * g + 4, :], raw[:, g % 2, :, :], ACT.Copy).then_inc(s_chi, 1)

                def copy(n, slot, fresh):
                    act.wait_ge(s_s, n + 1)
                    if not fresh:
                        act.wait_ge(s_sel, n - 3)
                    act.activation(s_buf[:, slot, :], ps_s[:, :, :].rearrange("p c n -> p (c n)"), ACT.Copy).then_inc(s_sc, 1)

                def scale(n, t, k, h, fresh):
                    act.wait_ge(s_sel, n + 1)
                    if h == 0 and not fresh:
                        act.wait_ge(s_aT, 4 * (t - 1))
                    act.activation(acc[:, k, :] if h == 0 else prob[:, h % 2, :], prob[:, h % 2, :], ACT.Identity,
                                   scale=rec[:, h % 2, :]).then_inc(s_scl, 1)

                def exponentials(n, t, h, begin=False):
                    act.wait_ge(s_chk, n + 1)
                    act.activation(e_top[:, :], top[:, h % 2, :], ACT.Exp, bias=nmax[:, h % 2, :], scale=SCALE,
                                   accum_out=den[:, h % 2, :]).then_inc(s_den, 1)
                    if h == 0 and not begin:
                        act.wait_ge(s_acc, 3 * t - 1)
                    if h == 1:
                        act.wait_ge(s_acc, 3 * t)
                    if h == 2:
                        act.wait_ge(s_scl, n - 1)
                    if h == 3:
                        act.wait_ge(s_acc, 3 * t + 1)
                    act.activation(prob[:, h % 2, :], s_buf[:, h, :], ACT.Exp, bias=nmax[:, h % 2, :], scale=SCALE).then_inc(s_prob, 1)

                def hi(t, g):
                    act.wait_ge(s_aT, 4 * t + g + 1)
                    act.wait_ge(s_ac, t)
                    act.activation(aT[:, 0, 4 * g:4 * g + 4, :], ps_t[:, g % 2, :, :], ACT.Copy).then_inc(s_aTh, 1)
                    act.wait_ge(s_aTl, 4 * t + g - 1 if g >= 1 else 4 * t)
                    act.activation(a32[:, g % 2, :, :], ps_t[:, g % 2, :, :], ACT.Copy).then_inc(s_a32, 1)

                def mixed(t, k, stores):
                    act.wait_ge(s_ac, t + 1)
                    act.wait_ge(s_st[k], 16 * stores)
                    act.activation(ac[:, k, :], ps_ac[:, :], ACT.Copy, scale=1.0 / HEADS).then_inc(s_acc_c, 1)
                    act.wait_ge(s_acc_c, t + 1)
                    act.dma_start(rows(ac_out, t * P, P), ac[:, k, :]).then_inc(s_st[k], 16)

                def body(b, j, start, end):
                    for s in range(2 * HEADS):
                        n = HT * b + 2 * HEADS * j + s
                        t, h = b * TPB + 2 * j + s // HEADS, s % HEADS
                        if not (end and s == 2 * HEADS - 1):
                            copy(n + 1, (s + 1) % 4, start and s < 3)
                        if not (start and s == 0):
                            scale(n - 1, t - 1 if h == 0 else t, (s - 1) // HEADS % 2, (s - 1) % HEADS, start)
                        if not (start and s < HEADS):
                            if h in (1, 2):
                                hi(t - 1, 2 * h - 2)
                                hi(t - 1, 2 * h - 1)
                        if start and s == 1:
                            load(0, 0)
                            load(0, 1)
                        if is_pair(j, 0):
                            if s == 4:
                                context_hi(b, 0)
                                context_hi(b, 1)
                            if s == 6:
                                context_hi(b, 2)
                                context_hi(b, 3)
                            if s == 5:
                                act.wait_ge(s_clo, 4 * b + 1)
                                load(b, 2)
                                act.wait_ge(s_clo, 4 * b + 2)
                                load(b, 3)
                        if is_pair(j, PAIRS - 1) and not end and s == 0:
                            act.wait_ge(s_mask, b + 1)
                            load_mask(b + 1)
                            act.wait_ge(s_clo, 4 * (b + 1))
                            load(b + 1, 0)
                            load(b + 1, 1)
                        exponentials(n, t, h, start and s == 0)
                        if h == 0 and not start:
                            mixed(t - 2, s // HEADS, b * PAIRS + j - 1)
                    if end:
                        scale(HT * B - 1, TILES - 1, 1, HEADS - 1, False)
                        mixed(TILES - 2, 0, TILES // 2 - 1)
                        for g in range(4):
                            hi(TILES - 1, g)
                        mixed(TILES - 1, 1, TILES // 2 - 1)

                load_mask(0)
                copy(0, 0, True)
                steps(act, body)
                for k in range(2):
                    act.wait_ge(s_st[k], 16 * TILES // 2)

            @block.vector
            def _(dve):
                dve.memset(mask[:, :], 0.0)
                dve.memset(row0[:, :], 0.0)
                dve.drain()
                dve.memset(row0[0:1, :], 1.0)
                dve.memset(f_weight[:, :], 1.0)
                dve.drain()
                dve.memset(f_weight[:, :].rearrange("p (g e) -> p g e", e=8)[:, :, 7], 2.0)
                def candidates(n, k, slot):
                    dve.wait_ge(s_sc, n + 1)
                    dve.memset(flag[:, k, :], 0.0)
                    for g in range(SEGS):
                        dve.max(out=cand[:, 8 * g:8 * g + 8], in_=s_buf[:, slot, g * SEG:(g + 1) * SEG])
                    dve.drain()
                    src = cand
                    for r in range(TOPK // 8):
                        dve.max(out=top[:, k, 8 * r:8 * r + 8], in_=src[:, :])
                        dve.drain()
                        if r < TOPK // 8 - 1:
                            dve.match_replace(out=cand_b[:, :], in_to_replace=top[:, k, 8 * r:8 * r + 8], in_values=src[:, :],
                                              imm_value=TAKEN)
                            dve.drain()
                        src = cand_b
                    dve.scalar_tensor_tensor(out=f_junk[:, :], in0=cand[:, :], scalar=top[:, k, TOPK - 1:TOPK],
                                             in1=f_weight[:, :], op0=ALU.is_ge, op1=ALU.mult, accum_out=flag[:, k, :])
                    dve.tensor_scalar(nmax[:, k, :], top[:, k, 0:1], -SCALE, None, ALU.mult)
                    dve.drain().then_inc(s_cand, 1)

                def settle(n, k, slot):
                    dve.wait_ge(s_f, n + 1)
                    dve.tensor_copy(flag_i[:, k:k + 1], ps_f[:, k:k + 1])
                    dve.drain()
                    doubt = dve.value_load(flag_i[0:1, k:k + 1], min_val=0, max_val=P * NCAND * 2)
                    with dve.If(doubt > P * TOPK):
                        left = prob[:, k, :]
                        src = s_buf[:, slot, :]
                        for r in range(TOPK // 8):
                            dve.max(out=top[:, k, 8 * r:8 * r + 8], in_=src)
                            dve.drain()
                            dve.match_replace(out=left, in_to_replace=top[:, k, 8 * r:8 * r + 8], in_values=src,
                                              imm_value=TAKEN)
                            dve.drain()
                            src = left
                        dve.tensor_scalar(left, left, 0.5 * TAKEN, -2.0 * BIG, ALU.is_ge, ALU.mult)
                        dve.drain()
                        dve.tensor_tensor(s_buf[:, slot, :], s_buf[:, slot, :], left, ALU.add)
                    dve.drain().then_inc(s_chk, 1)

                def select(n, k, slot):
                    dve.wait_ge(s_den, n + 1)
                    dve.reciprocal(rec[:, k, :], den[:, k, :])
                    dve.wait_ge(s_prob, n + 1)
                    dve.scalar_tensor_tensor(out=prob[:, k, :], in0=s_buf[:, slot, :], scalar=top[:, k, TOPK - 1:TOPK],
                                             in1=prob[:, k, :], op0=ALU.is_ge, op1=ALU.mult)
                    dve.drain().then_inc(s_sel, 1)

                def make_mask(b):
                    dve.wait_ge(s_ms, 16 * (b + 1))
                    dve.wait_ge(s_s, HT * b)
                    dve.tensor_scalar(mask[0:1, :], mask_u8[:, :], BIG, -BIG, ALU.mult, ALU.add).then_inc(s_mask, 1)

                def body(b, j, start, end):
                    for s in range(2 * HEADS):
                        n = HT * b + 2 * HEADS * j + s
                        t, h = b * TPB + 2 * j + s // HEADS, s % HEADS
                        if is_pair(j, PAIRS - 1) and not end and s == 2 * HEADS - 1:
                            make_mask(b + 1)
                        candidates(n, s % 2, s % 4)
                        if not (start and s == 0):
                            select(n - 1, (s - 1) % 2, (s - 1) % 4)
                        if h == 0 and not (start and s == 0):
                            dve.wait_ge(s_acc, 3 * t - 1)
                        if h == 1:
                            dve.wait_ge(s_acc, 3 * t)
                        if h == 2:
                            dve.wait_ge(s_scl, n - 1)
                        if h == 3:
                            dve.wait_ge(s_acc, 3 * t + 1)
                        settle(n, s % 2, s % 4)
                    if end:
                        select(HT * B - 1, 1, 3)

                make_mask(0)
                steps(dve, body)
        st.clear()



def stage_film(nc, A, x1_in, ac_in, xin_out, so_out, sh_out):
    NF = 4
    SLOTS = 4
    with ExitStack() as ctx:
        st = Stage(nc, ctx, "fi")
        sb, psum, sem = st.sb, st.psum, st.sem
        ident = sb("ident", [P, P])
        neghalf = sb("neghalf", [P, 1])
        gate = sb("gate", [P, 1])
        wv = sb("wv", [P, VC, D])
        wvT = sb("wvT", [P, DC, DV])
        wfilm = sb("wfilm", [P, DC, 2 * D])
        wf = sb("wf", [P, 2, VC, NF, D], F32R)
        bf = sb("bf", [P, NF, D])
        g_in = sb("g_in", [P, D])
        b_in = sb("b_in", [P, D])
        x1 = sb("x1", [P, SLOTS, D])
        ac = sb("ac", [P, SLOTS, DV])
        mask_u8 = sb("mask_u8", [P, SLOTS, 1], U8)
        mask = sb("mask", [P, SLOTS, 1])
        aT = sb("aT", [P, 2, 2, VC, P], F32R)
        stats = sb("stats", [P, 6])
        mv = sb("mv", [P, 2])
        rstd = sb("rstd", [P, 1])
        xn = sb("xn", [P, SLOTS, D])
        mod = sb("mod", [P, 2, NF, D])

        ps_t = psum("ps_t", [P, 2, 512])
        ps_f = psum("ps_f", [P, NF, D])
        ps_w = psum("ps_w", [P, 2, 512])

        s_const = sem("constants")
        s_ld = sem("weights_loaded")
        s_lo_ = sem("film_out_loaded")
        s_wT = sem("wv_transposed")
        s_wTc = sem("wv_transposed_copied")
        s_fold = sem("folded")
        s_foh = sem("folded_hi")
        s_fol = sem("folded_lo")
        s_in = [sem(f"tile_loaded{k}") for k in range(SLOTS)]
        s_t = sem("ac_transposed")
        s_th = sem("ac_hi")
        s_tl = sem("ac_lo")
        s_f = sem("film_done")
        s_fr = sem("film_read")
        s_var = sem("variance")
        s_rstd = sem("rstd")
        s_xn = sem("normalised")
        s_x = sem("input_done")
        s_st = [sem(f"stored{k}") for k in range(2)]

        def bcast(name, n, off=0):
            return A[name].rearrange("(o n) -> o n", o=1)[:, off:off + n].broadcast_to([P, n])

        def tiles(eng, tile):
            for k in range(SLOTS):
                tile(k, 0, k, k == 0, False)
            with eng.Fori(1, TILES // SLOTS - 1) as j:
                for k in range(SLOTS):
                    tile(SLOTS * j + k, j, k, False, False)
            for k in range(SLOTS):
                tile(TILES - SLOTS + k, TILES // SLOTS - 1, k, False, k == SLOTS - 1)

        with nc.Block() as block:

            @block.sync
            def _(sp):
                sp.dma_start(gate[:, :], A["L0_xattn_mod_gate"].rearrange("(o n) -> o n", o=1).broadcast_to([P, 1])).then_inc(s_ld, 16)
                sp.dma_start(wv[:, :, :], A["L0_xattn_Wv"].rearrange("(c p) n -> p c n", p=P)).then_inc(s_ld, 16)
                sp.dma_start(wfilm[:, :, :], A["L0_xattn_W_film_in"].rearrange("(c p) n -> p c n", p=P)).then_inc(s_ld, 16)
                sp.dma_start(g_in[:, :], bcast("L0_xattn_g_norm_in", D)).then_inc(s_ld, 16)
                sp.dma_start(b_in[:, :], bcast("L0_xattn_b_norm_in", D)).then_inc(s_ld, 16)
                for i, name in enumerate(("L0_xattn_b_film_in", "L0_xattn_b_film_out")):
                    sp.dma_start(bf[:, 2 * i:2 * i + 2, :].rearrange("p a n -> p (a n)"), bcast(name, 2 * D)).then_inc(s_ld, 16)
                sp.wait_ge(s_fold, 6)
                sp.dma_start(wfilm[:, :, :], A["L0_xattn_W_film_out"].rearrange("(c p) n -> p c n", p=P)).then_inc(s_lo_, 16)

            @block.gpsimd
            def _(pool):
                pool.memset(ident[:, :], 0.0)
                pool.memset(neghalf[:, :], -0.5)
                pool.drain()
                pool.affine_select(out=ident[:, :], in_=ident[:, :], compare_op=ALU.not_equal, fill=1.0,
                                   base=0, pattern=[[-1, P]], channel_multiplier=1)
                pool.drain().then_inc(s_const, 1)

                def base(t, k):
                    pool.wait_ge(s_var, t + 1)
                    pool.tensor_tensor(rstd[:, :], mv[:, 1:2], neghalf[:, :], ALU.pow).then_inc(s_rstd, 1)
                    pool.wait_ge(s_xn, t + 1)
                    pool.tensor_tensor(xn[:, k, :], xn[:, k, :], g_in[:, :], ALU.mult)
                    pool.drain()
                    pool.tensor_tensor(xn[:, k, :], xn[:, k, :], b_in[:, :], ALU.add)
                    pool.drain()

                def tile(t, j, k, first, last):
                    if not last:
                        base(t + 1, (k + 1) % SLOTS)
                    pool.wait_ge(s_fr, NF * t + 2)
                    pool.tensor_tensor(xn[:, k, :], xn[:, k, :], mod[:, k % 2, 0, :], ALU.mult)
                    pool.drain()
                    pool.tensor_tensor(xn[:, k, :], xn[:, k, :], mod[:, k % 2, 1, :], ALU.add).then_inc(s_x, 1)

                base(0, 0)
                tiles(pool, tile)

            @block.tensor
            def _(pe):
                pe.wait_ge(s_const, 1)
                pe.wait_ge(s_ld, 16 * 7)
                for c in range(VC):
                    if c >= 2:
                        pe.wait_ge(s_wTc, c - 1)
                    for e in range(DC):
                        last = pe.transpose(ps_w[:, c % 2, e * P:(e + 1) * P], wv[:, c, e * P:(e + 1) * P], ident[:, :])
                    last.then_inc(s_wT, 1)
                pe.wait_ge(s_wTc, VC)
                n = 0
                for half in range(2):
                    if half:
                        pe.wait_ge(s_lo_, 16)
                    for q in range(2):
                        for c in range(VC):
                            if n >= 2:
                                pe.wait_ge(s_fol, n - 1)
                            for e in range(DC):
                                last = pe.matmul(ps_w[:, n % 2, :], wvT[:, e, c * P:(c + 1) * P], wfilm[:, e, q * D:(q + 1) * D],
                                                 start=(e == 0), stop=(e == DC - 1))
                            last.then_inc(s_fold, 1)
                            n += 1
                pe.wait_ge(s_fol, NF * VC)

                def film(t, k, first):
                    pe.wait_ge(s_tl, t + 1)
                    for f in range(NF):
                        if not first:
                            pe.wait_ge(s_fr, NF * (t - 1) + f + 1)
                        for c in range(VC):
                            last = mm3(pe, ps_f[:, f, :], aT[:, k, 0, c, :], aT[:, k, 1, c, :],
                                       wf[:, 0, c, f, :], wf[:, 1, c, f, :], start=(c == 0), stop=(c == VC - 1))
                        last.then_inc(s_f, 1)

                def turn(t, k, loads):
                    pe.wait_ge(s_in[k], 48 * loads)
                    if not (isinstance(t, int) and t < 2):
                        pe.wait_ge(s_tl, t - 1)
                    for c in range(VC):
                        last = pe.transpose(ps_t[:, k % 2, c * P:(c + 1) * P], ac[:, k, c * P:(c + 1) * P], ident[:, :])
                    last.then_inc(s_t, 1)

                def tile(t, j, k, first, last):
                    if not last:
                        turn(t + 1, (k + 1) % SLOTS, j + (k + 1) // SLOTS + 1)
                    film(t, k % 2, first)

                turn(0, 0, 1)
                tiles(pe, tile)

            @block.scalar
            def _(act):
                for c in range(VC):
                    act.wait_ge(s_wT, c + 1)
                    act.activation(wvT[:, :, c * P:(c + 1) * P], ps_w[:, c % 2, :].rearrange("p (e q) -> p e q", e=DC),
                                   ACT.Copy).then_inc(s_wTc, 1)
                n = 0
                for f in range(NF):
                    for c in range(VC):
                        act.wait_ge(s_fold, n + 1)
                        act.activation(wf[:, 0, c, f, :], ps_w[:, n % 2, :], ACT.Identity, scale=gate[:, 0:1]).then_inc(s_foh, 1)
                        n += 1

                text_mask = A["mask_BxS_bf1"].rearrange("b (s o) -> (b s) o", o=1)

                def load(t, k, fresh=False):
                    if not fresh:
                        act.wait_ge(s_xn, t - SLOTS + 1)
                        act.wait_ge(s_t, t - SLOTS + 1)
                        act.wait_ge(s_fr, NF * (t - SLOTS + 1))
                    act.dma_start(x1[:, k, :], rows(x1_in, t * P, P)).then_inc(s_in[k], 16)
                    act.dma_start(ac[:, k, :], rows(ac_in, t * P, P)).then_inc(s_in[k], 16)
                    act.dma_start(mask_u8[:, k, :], rows(text_mask, t * P, P)).then_inc(s_in[k], 16)

                def hi(t, k):
                    act.wait_ge(s_t, t + 1)
                    if not (isinstance(t, int) and t < 2):
                        act.wait_ge(s_f, NF * (t - 1))
                    act.activation(aT[:, k, 0, :, :].rearrange("p c q -> p (c q)"), ps_t[:, k, 0:DV], ACT.Copy).then_inc(s_th, 1)

                def store(t, k):
                    act.wait_ge(s_fr, NF * (t + 1))
                    act.dma_start(rows(so_out, t * P, P), mod[:, k % 2, 2, :]).then_inc(s_st[k % 2], 16)
                    act.dma_start(rows(sh_out, t * P, P), mod[:, k % 2, 3, :]).then_inc(s_st[k % 2], 16)
                    act.wait_ge(s_x, t + 1)
                    act.dma_start(rows(xin_out, t * P, P), xn[:, k, :]).then_inc(s_st[k % 2], 16)

                def tile(t, j, k, first, last):
                    if not (isinstance(t, int) and t + 2 >= TILES):
                        load(t + 2, (k + 2) % SLOTS, fresh=isinstance(t, int) and t + 2 < SLOTS)
                    if not last:
                        hi(t + 1, (k + 1) % 2)
                    if not first:
                        store(t - 1, (k - 1) % SLOTS)

                load(0, 0, fresh=True)
                load(1, 1, fresh=True)
                hi(0, 0)
                tiles(act, tile)
                store(TILES - 1, SLOTS - 1)
                for k in range(2):
                    act.wait_ge(s_st[k], 48 * TILES // 2)

            @block.vector
            def _(dve):
                dve.wait_ge(s_ld, 16 * 7)
                dve.tensor_scalar(bf[:, :, :], bf[:, :, :], gate[:, 0:1], None, ALU.mult)
                dve.drain()
                for f in (0, 2):
                    dve.tensor_scalar(bf[:, f, :], bf[:, f, :], 1.0, None, ALU.add)
                dve.drain()
                n = 0
                for f in range(NF):
                    for c in range(VC):
                        dve.wait_ge(s_foh, n + 1)
                        dve.scalar_tensor_tensor(out=wf[:, 1, c, f, :], in0=ps_w[:, n % 2, :], scalar=gate[:, 0:1],
                                                 in1=wf[:, 0, c, f, :].bitcast(F32), op0=ALU.mult, op1=ALU.subtract).then_inc(s_fol, 1)
                        n += 1

                def split(t, k):
                    dve.wait_ge(s_th, t + 1)
                    dve.tensor_tensor(aT[:, k, 1, :, :].rearrange("p c q -> p (c q)"), ps_t[:, k, 0:DV],
                                      aT[:, k, 0, :, :].rearrange("p c q -> p (c q)").bitcast(F32), ALU.subtract).then_inc(s_tl, 1)

                def variance(t, k, loads):
                    dve.wait_ge(s_in[k], 48 * loads)
                    dve.tensor_copy(mask[:, k, :], mask_u8[:, k, :])
                    dve.bn_stats(stats[:, :], x1[:, k, :])
                    dve.drain()
                    dve.bn_aggr(mv[:, :], stats[:, :])
                    dve.drain()
                    dve.tensor_scalar(mv[:, 1:2], mv[:, 1:2], EPS, None, ALU.add).then_inc(s_var, 1)

                def norm(t, k):
                    dve.wait_ge(s_rstd, t + 1)
                    dve.tensor_scalar(xn[:, k, :], x1[:, k, :], mv[:, 0:1], rstd[:, 0:1], ALU.subtract, ALU.mult).then_inc(s_xn, 1)

                def modulate(t, k, f):
                    dve.wait_ge(s_f, NF * t + f + 1)
                    dve.scalar_tensor_tensor(out=mod[:, k % 2, f, :], in0=ps_f[:, f, :], scalar=mask[:, k, :], in1=bf[:, f, :],
                                             op0=ALU.mult, op1=ALU.add).then_inc(s_fr, 1)

                def tile(t, j, k, first, last):
                    if not last:
                        split(t + 1, (k + 1) % 2)
                        variance(t + 1, (k + 1) % SLOTS, j + (k + 1) // SLOTS + 1)
                    dve.wait_ge(s_st[k % 2], 48 * (j * 2 + k // 2))
                    modulate(t, k, 0)
                    modulate(t, k, 1)
                    if not last:
                        norm(t + 1, (k + 1) % SLOTS)
                    modulate(t, k, 2)
                    modulate(t, k, 3)

                split(0, 0)
                variance(0, 0, 1)
                norm(0, 0)
                tiles(dve, tile)
        st.clear()



def conv_constants():
    t = np.arange(S // 2)[:, None] + 0.5
    fwd, tw = [], []
    for par in range(2):
        m = 2 * np.arange(S // 2)[None, :] + par + 0.5
        ang = np.pi * m * t / S
        fwd.append([np.cos(ang) + np.sin(ang), np.cos(ang) - np.sin(ang)])
        half = np.pi * m[0] / (2 * S)
        tw.append([(np.cos(half) + np.sin(half)) / 2, (np.cos(half) - np.sin(half)) / 2])
    fwd = np.array(fwd)
    inv = fwd.transpose(0, 1, 3, 2) / (2 * S)
    tw = np.array(tw).transpose(1, 0, 2).reshape(2, S)
    return {"dft": fwd.astype(np.float32), "idft": inv.astype(np.float32).copy(), "twiddle": tw.astype(np.float32)}


def make_exchange(pool, flip, ready):
    pool.memset(flip[:, :], 0.0)
    pool.drain()
    pool.affine_select(out=flip[:, :], in_=flip[:, :], compare_op=ALU.not_equal, fill=1.0,
                       base=1 - P, pattern=[[1, P]], channel_multiplier=1)
    pool.drain().then_inc(ready, 1)


def stage_dft(nc, A, xin, taps, y_out):
    TC = S // 2 // P
    MC = S // P
    XIN = 16 * (1 + TC)
    with ExitStack() as ctx:
        st = Stage(nc, ctx, "df")
        sb, psum, sem = st.sb, st.psum, st.sem
        raw = sb("raw", [P, 2, TC, D])
        mats = sb("mats", [P, 2, 2, 2, TC, 512], F32R)
        uv = sb("uv", [P, 2, 2, TC, D], F32R)
        uvf = sb("uvf", [P, 2, TC, D])
        kc = sb("kc", [P, MC, D])
        ks = sb("ks", [P, MC, D])
        tw = sb("tw", [P, 2, MC])
        prod = sb("prod", [P, 2, 4, D])
        yo = sb("yo", [P, 2, 2, D])
        flip = sb("flip", [P, P])
        ps = psum("ps", [P, 2, 2, D])
        ps_rev = psum("ps_rev", [P, TC, D])

        s_tw = sem("twiddle_loaded")
        s_m = [sem(f"matrix_loaded{k}") for k in range(2)]
        s_mh = sem("matrix_hi")
        s_ml = sem("matrix_lo")
        s_x = sem("x_loaded")
        s_const = sem("exchange_ready")
        s_rev = sem("reversed")
        s_uv = sem("sums_done")
        s_hi = sem("sums_hi")
        s_lo = sem("sums_lo")
        s_f = sem("spectrum")
        s_fr = sem("spectrum_read")
        s_pr = sem("products")
        s_y = sem("y_done")
        s_st = [sem(f"stored{k}") for k in range(2)]

        with nc.Block() as block:

            @block.sync
            def _(sp):
                sp.dma_start(tw[:, :, :], A["twiddle"].rearrange("i (q p) -> p i q", p=P), allow_slow_non_contiguous=True).then_inc(s_tw, 16)
                for n in range(4):
                    if n >= 2:
                        sp.wait_ge(s_ml, n - 1)
                    sp.dma_start(raw[:, n % 2, :, :], A["dft"][n // 2, n % 2].rearrange("(q p) m -> p q m", p=P)).then_inc(s_m[n % 2], 16)
                sp.wait_ge(s_ml, 4)

                def load(src, first):
                    sp.dma_start(raw[:, 0, :, :], rows(src, first, S // 2).rearrange("(q p) d -> p q d", p=P)).then_inc(s_x, 16)
                    for c in range(TC):
                        sp.dma_start(raw[:, 1, c, :], rows(src, first + S - (c + 1) * P, P)).then_inc(s_x, 16)

                load(taps, 0)
                with sp.Fori(0, B) as b:
                    sp.wait_ge(s_uv, b + 1)
                    load(xin, b * S)

            @block.gpsimd
            def _(pool):
                make_exchange(pool, flip, s_const)

                def sequence(b, last):
                    for q in range(MC):
                        k = q % 2
                        pool.wait_ge(s_pr, MC * b + q + 1)
                        pool.wait_ge(s_st[k], 16 * ((MC // 2) * b + q // 2))
                        pool.tensor_tensor(yo[:, k, 0, :], prod[:, k, 0, :], prod[:, k, 1, :], ALU.add)
                        pool.tensor_tensor(yo[:, k, 1, :], prod[:, k, 2, :], prod[:, k, 3, :], ALU.subtract)
                        pool.drain().then_inc(s_y, 1)

                with pool.Fori(0, B - 1) as b:
                    sequence(b, False)
                sequence(B - 1, True)

            @block.tensor
            def _(pe):
                def reverse(n):
                    pe.wait_ge(s_x, XIN * (n + 1))
                    pe.wait_ge(s_uv, n)
                    for c in range(TC):
                        last = pe.matmul(ps_rev[:, c, :], flip[:, :], raw[:, 1, c, :], start=True, stop=True)
                    last.then_inc(s_rev, 1)

                def spectrum(n, q):
                    k = q % 2
                    i = MC * n + q
                    if not (isinstance(n, int) and n == 0 and q < 2):
                        pe.wait_ge(s_fr, i - 1)
                    par, mq = q // TC, q % TC
                    for sd in range(2):
                        src = (sd + par) % 2
                        if q == 0:
                            pe.wait_ge(s_lo, 2 * n + 1 + src)
                        for c in range(TC):
                            last = mm3(pe, ps[:, k, sd, :],
                                       mats[:, 0, par, sd, c, mq * P:(mq + 1) * P], mats[:, 1, par, sd, c, mq * P:(mq + 1) * P],
                                       uv[:, src, 0, c, :], uv[:, src, 1, c, :], start=(c == 0), stop=(c == TC - 1))
                    last.then_inc(s_f, 1)

                def sequence(n, last):
                    for q in range(MC):
                        if q == 3 and not last:
                            reverse(n + 1)
                        spectrum(n, q)

                pe.wait_ge(s_const, 1)
                pe.wait_ge(s_ml, 4)
                reverse(0)
                sequence(0, False)
                with pe.Fori(1, B) as n:
                    sequence(n, False)
                sequence(B, True)

            @block.scalar
            def _(act):
                for n in range(4):
                    act.wait_ge(s_m[n % 2], 16 * (n // 2 + 1))
                    act.activation(mats[:, 0, n // 2, n % 2, :, :], raw[:, n % 2, :, :], ACT.Copy).then_inc(s_mh, 1)

                def hi(n):
                    act.wait_ge(s_uv, n + 1)
                    act.wait_ge(s_f, MC * n)
                    for i in range(2):
                        act.activation(uv[:, i, 0, :, :], uvf[:, i, :, :], ACT.Copy).then_inc(s_hi, 1)

                def sequence(b, last):
                    for q in range(MC):
                        k = q % 2
                        if q == MC - 2 and not last:
                            hi(b + 2)
                        act.wait_ge(s_y, MC * b + q + 1)
                        act.dma_start(y_out[bass.ds(b, 1), q].rearrange("o i p d -> p (o i) d"), yo[:, k, :, :]).then_inc(s_st[k], 16)

                hi(0)
                hi(1)
                with act.Fori(0, B - 1) as b:
                    sequence(b, False)
                sequence(B - 1, True)
                for k in range(2):
                    act.wait_ge(s_st[k], 16 * B * MC // 2)

            @block.vector
            def _(dve):
                for n in range(4):
                    dve.wait_ge(s_mh, n + 1)
                    dve.tensor_tensor(mats[:, 1, n // 2, n % 2, :, :], raw[:, n % 2, :, :],
                                      mats[:, 0, n // 2, n % 2, :, :].bitcast(F32), ALU.subtract).then_inc(s_ml, 1)

                def fold(n):
                    dve.wait_ge(s_x, XIN * (n + 1))
                    dve.wait_ge(s_rev, n + 1)
                    dve.wait_ge(s_lo, 2 * n)
                    dve.tensor_tensor(uvf[:, 0, :, :], raw[:, 0, :, :], ps_rev[:, :, :], ALU.add)
                    dve.tensor_tensor(uvf[:, 1, :, :], raw[:, 0, :, :], ps_rev[:, :, :], ALU.subtract)
                    dve.drain().then_inc(s_uv, 1)

                def split(n):
                    for i in range(2):
                        dve.wait_ge(s_hi, 2 * n + i + 1)
                        dve.tensor_tensor(uv[:, i, 1, :, :], uvf[:, i, :, :], uv[:, i, 0, :, :].bitcast(F32), ALU.subtract).then_inc(s_lo, 1)

                fold(0)
                split(0)
                dve.wait_ge(s_tw, 16)
                for q in range(MC):
                    if q == MC - 2:
                        fold(1)
                    k = q % 2
                    dve.wait_ge(s_f, q + 1)
                    dve.tensor_scalar(prod[:, k, 0, :], ps[:, k, 0, :], tw[:, 0, q:q + 1], None, ALU.mult)
                    dve.tensor_scalar(prod[:, k, 1, :], ps[:, k, 1, :], tw[:, 0, q:q + 1], None, ALU.mult)
                    dve.drain()
                    dve.scalar_tensor_tensor(out=kc[:, q, :], in0=ps[:, k, 1, :], scalar=tw[:, 1, q:q + 1], in1=prod[:, k, 0, :],
                                             op0=ALU.mult, op1=ALU.add)
                    dve.scalar_tensor_tensor(out=ks[:, q, :], in0=ps[:, k, 0, :], scalar=tw[:, 1, q:q + 1], in1=prod[:, k, 1, :],
                                             op0=ALU.mult, op1=ALU.subtract)
                    dve.drain().then_inc(s_fr, 1)

                def sequence(b, last):
                    split(b + 1)
                    for q in range(MC):
                        k = q % 2
                        if q == MC - 2 and not last:
                            fold(b + 2)
                        dve.wait_ge(s_f, MC * (b + 1) + q + 1)
                        if q >= 2:
                            dve.wait_ge(s_y, MC * b + q - 1)
                        else:
                            dve.wait_ge(s_y, MC * b)
                        for i, (x, w) in enumerate(((0, kc), (1, ks), (1, kc), (0, ks))):
                            dve.tensor_tensor(prod[:, k, i, :], ps[:, k, x, :], w[:, q, :], ALU.mult)
                        dve.drain().then_inc(s_fr, 1)
                        dve.drain().then_inc(s_pr, 1)

                with dve.Fori(0, B - 1) as b:
                    sequence(b, False)
                sequence(B - 1, True)
        st.clear()


def stage_idft(nc, A, y_in, conv_out):
    TC = S // 2 // P
    MC = S // P
    with ExitStack() as ctx:
        st = Stage(nc, ctx, "id")
        sb, psum, sem = st.sb, st.psum, st.sem
        raw = sb("raw", [P, 2, 2, D])
        mraw = sb("mraw", [P, 2, TC, 512])
        mats = sb("mats", [P, 2, 2, 2, TC, 512], F32R)
        y = sb("y", [P, MC, 2, 2, D], F32R)
        a_sb = sb("a_sb", [P, 2, D])
        out = sb("out", [P, 2, 2, D])
        flip = sb("flip", [P, P])
        rev = sb("rev", [P, 2, D])
        ps = psum("ps", [P, 2, 2, D])
        ps_rev = psum("ps_rev", [P, 2, D])

        s_m = [sem(f"matrix_loaded{k}") for k in range(2)]
        s_mh = sem("matrix_hi")
        s_ml = sem("matrix_lo")
        s_y = [sem(f"y_loaded{k}") for k in range(2)]
        s_hi = sem("y_hi")
        s_lo = sem("y_lo")
        s_o = sem("sums_done")
        s_used = sem("chunk_multiplied")
        s_const = sem("exchange_ready")
        s_rev = sem("reversed")
        s_rc = sem("reversed_copied")
        s_a = sem("a_copied")
        s_r = sem("result_done")
        s_st = [sem(f"stored{k}") for k in range(2)]

        def batches(eng, batch):
            batch(0, True, False)
            with eng.Fori(1, B - 1) as b:
                batch(b, False, False)
            batch(B - 1, False, True)

        with nc.Block() as block:

            @block.sync
            def _(sp):
                for n in range(4):
                    if n >= 2:
                        sp.wait_ge(s_ml, n - 1)
                    sp.dma_start(mraw[:, n % 2, :, :], A["idft"][n // 2, n % 2].rearrange("(q p) m -> p q m", p=P)).then_inc(s_m[n % 2], 16)
                with sp.Fori(0, B) as b:
                    for q in range(MC):
                        k = q % 2
                        sp.wait_ge(s_lo, MC * b + q - 1 if q >= 2 else MC * b)
                        sp.dma_start(raw[:, k, :, :], y_in[bass.ds(b, 1), q].rearrange("o i p d -> p (o i) d")).then_inc(s_y[k], 16)

            @block.gpsimd
            def _(pool):
                make_exchange(pool, flip, s_const)
                with pool.Fori(0, B) as b:
                    for t in range(TC):
                        k = t % 2
                        pool.wait_ge(s_r, TC * b + t + 1)
                        pool.dma_start(rows(conv_out, b * S + t * P, P), out[:, k, 0, :]).then_inc(s_st[k], 16)
                        pool.wait_ge(s_rc, TC * b + t + 1)
                        pool.dma_start(rows(conv_out, b * S + S - (t + 1) * P, P), rev[:, k, :]).then_inc(s_st[k], 16)
                for k in range(2):
                    pool.wait_ge(s_st[k], 32 * B * TC // 2)

            @block.tensor
            def _(pe):
                def reverse(n, k):
                    pe.wait_ge(s_r, n + 1)
                    if not (isinstance(n, int) and n < 2):
                        pe.wait_ge(s_rc, n - 1)
                    pe.matmul(ps_rev[:, k, :], flip[:, :], out[:, k, 1, :], start=True, stop=True).then_inc(s_rev, 1)

                def batch(b, first, last):
                    for t in range(TC):
                        k, n = t % 2, TC * b + t
                        if not (first and t < 2):
                            pe.wait_ge(s_r, n - 1)
                        for q in range(MC):
                            if t == 0:
                                pe.wait_ge(s_lo, MC * b + q + 1)
                            for ab in range(2):
                                par, mq = q // TC, q % TC
                                pm = (ab + par) % 2
                                done = mm3(pe, ps[:, k, ab, :],
                                           mats[:, 0, par, pm, mq, t * P:(t + 1) * P], mats[:, 1, par, pm, mq, t * P:(t + 1) * P],
                                           y[:, q, 0, pm, :], y[:, q, 1, pm, :], start=(q == 0), stop=(q == MC - 1))
                            if t == TC - 1:
                                done.then_inc(s_used, 1)
                        pe.drain().then_inc(s_o, 1)
                        if not (first and t == 0):
                            reverse(n - 1, 1 - k)

                pe.wait_ge(s_const, 1)
                pe.wait_ge(s_ml, 4)
                batches(pe, batch)
                reverse(B * TC - 1, 1)

            @block.scalar
            def _(act):
                for n in range(4):
                    act.wait_ge(s_m[n % 2], 16 * (n // 2 + 1))
                    act.activation(mats[:, 0, n // 2, n % 2, :, :], mraw[:, n % 2, :, :], ACT.Copy).then_inc(s_mh, 1)

                def turned(n, k, stores):
                    act.wait_ge(s_rev, n + 1)
                    act.wait_ge(s_st[k], 32 * stores)
                    act.activation(rev[:, k, :], ps_rev[:, k, :], ACT.Copy).then_inc(s_rc, 1)

                def hi(b):
                    for q in range(MC):
                        act.wait_ge(s_y[q % 2], 16 * ((MC // 2) * b + q // 2 + 1))
                        if not (isinstance(b, int) and b == 0):
                            act.wait_ge(s_used, MC * (b - 1) + q + 1)
                        act.activation(y[:, q, 0, :, :], raw[:, q % 2, :, :], ACT.Copy).then_inc(s_hi, 1)

                def batch(b, first, last):
                    for t in range(TC):
                        k, n = t % 2, TC * b + t
                        if t == TC - 1 and not last:
                            hi(b + 1)
                        act.wait_ge(s_o, n + 1)
                        if not (first and t < 2):
                            act.wait_ge(s_r, n - 1)
                        act.activation(a_sb[:, k, :], ps[:, k, 0, :], ACT.Copy).then_inc(s_a, 1)
                        if not (first and t == 0):
                            turned(n - 1, 1 - k, (TC // 2) * b + (t - 1) // 2)

                hi(0)
                batches(act, batch)
                turned(B * TC - 1, 1, B * TC // 2 - 1)

            @block.vector
            def _(dve):
                for n in range(4):
                    dve.wait_ge(s_mh, n + 1)
                    dve.tensor_tensor(mats[:, 1, n // 2, n % 2, :, :], mraw[:, n % 2, :, :],
                                      mats[:, 0, n // 2, n % 2, :, :].bitcast(F32), ALU.subtract).then_inc(s_ml, 1)

                def lo(b):
                    for q in range(MC):
                        dve.wait_ge(s_hi, MC * b + q + 1)
                        dve.tensor_tensor(y[:, q, 1, :, :], raw[:, q % 2, :, :], y[:, q, 0, :, :].bitcast(F32), ALU.subtract)\
                           .then_inc(s_lo, 1)

                def batch(b, first, last):
                    for t in range(TC):
                        k, n = t % 2, TC * b + t
                        if t == TC - 1 and not last:
                            lo(b + 1)
                        dve.wait_ge(s_a, n + 1)
                        dve.wait_ge(s_st[k], 32 * ((TC // 2) * b + t // 2))
                        if not (first and t < 2):
                            dve.wait_ge(s_rev, n - 1)
                        dve.tensor_tensor(out[:, k, 0, :], a_sb[:, k, :], ps[:, k, 1, :], ALU.add)
                        dve.tensor_tensor(out[:, k, 1, :], a_sb[:, k, :], ps[:, k, 1, :], ALU.subtract)
                        dve.drain().then_inc(s_r, 1)

                lo(0)
                batches(dve, batch)
        st.clear()


def stage_mlp(nc, name, modulated, W_up, b_up, W_down, down_biases, x_in, out, g_ffn=None, b_ffn=None,
              g_out=None, b_out=None, y_in=None, so_in=None, sh_in=None):
    N = 4 * P
    GROUPS = B * S // N
    Q = N // P
    PIECES = 2 * Q * DC
    FIRST, STEP = 3, PIECES // Q
    IN = 64 if modulated else 16
    with ExitStack() as ctx:
        st = Stage(nc, ctx, name)
        sb, psum, sem = st.sb, st.psum, st.sem
        ident = sb("ident", [P, P])
        neghalf = sb("neghalf", [P, 1])
        w1 = sb("w1", [P, 2, DC, HID], F32R)
        w2 = sb("w2", [P, 2, HC, D], F32R)
        b1 = sb("b1", [P, HC])
        b2 = sb("b2", [P, D])
        xt = sb("xt", [P, 2, Q, D])
        h = sb("h", [P, D])
        hT = sb("hT", [P, 2, 2, DC, N], F32R)
        act_hl = sb("act_hl", [P, 2, 2, N], F32R)
        g32 = sb("g32", [P, N])
        stats = sb("stats", [P, 6])
        mv = {v: sb(f"mv_{v}", [P, 2]) for v in "pef"}
        rstd = {v: sb(f"rstd_{v}", [P, 1]) for v in "pef"}
        e = sb("e", [P, 2, D])
        if modulated:
            gf = sb("gf", [P, DC])
            bf = sb("bf", [P, DC])
            g_row = sb("g_row", [P, D])
            b_row = sb("b_row", [P, D])
            y = sb("y", [P, D])
            so = sb("so", [P, D])
            sh = sb("sh", [P, D])
            xr = sb("xr", [P, D])

        ps_h = psum("ps_h", [P, 2, N])
        ps_o = psum("ps_o", [P, Q, D])
        ps_t = psum("ps_t", [P, 2, D])

        s_const = sem("constants")
        s_c = sem("small_loaded")
        s_raw = [sem(f"piece_loaded{k}") for k in range(Q)]
        s_whi = sem("weights_hi")
        s_wlo = sem("weights_lo")
        s_bm = sem("bias_products")
        s_b1 = sem("up_bias_ready")
        s_in = sem("tile_loaded")
        s_mod = sem("modulated")
        s_var = {v: sem(f"variance_{v}") for v in "pef"}
        s_rstd = {v: sem(f"rstd_{v}") for v in "pef"}
        s_h = sem("h_done")
        s_b2 = sem("bias_added")
        s_tr = sem("h_transposed")
        s_hi = sem("hT_hi")
        s_hT = sem("hT_lo")
        s_m1 = sem("up_done")
        s_g = sem("gelu_done")
        s_gh = sem("gelu_hi")
        s_gl = sem("gelu_lo")
        s_m2 = sem("down_chunk_done")
        s_o = sem("down_done")
        s_add = sem("residual_added")
        s_n1 = sem("inner_norm")
        s_xr = sem("x_again_loaded")
        s_e = sem("outer_sum")
        s_n2 = sem("outer_norm")
        s_st = [sem(f"stored{k}") for k in range(2)]
        s_out = s_n2 if modulated else s_n1

        def in_groups(eng, group):
            group(0, 0, True, False)
            with eng.Fori(0, (GROUPS - 2) // 2) as j:
                for k in range(2):
                    group(2 * j + 1 + k, (1 + k) % 2, False, False)
            group(GROUPS - 1, (GROUPS - 1) % 2, False, True)

        with nc.Block() as block:

            @block.sync
            def _(sp):
                sp.dma_start(b1[:, :], b_up.rearrange("(c p) -> p c", p=P), allow_slow_non_contiguous=True).then_inc(s_c, 16)
                row = lambda v: v.rearrange("(o n) -> o n", o=1).broadcast_to([P, D])
                sp.dma_start(b2[:, :], row(down_biases[0])).then_inc(s_c, 16)
                if modulated:
                    for t, v in ((gf, g_ffn), (bf, b_ffn)):
                        sp.dma_start(t[:, :], v.rearrange("(c p) -> p c", p=P), allow_slow_non_contiguous=True).then_inc(s_c, 16)
                    for t, v in ((g_row, g_out), (b_row, b_out)):
                        sp.dma_start(t[:, :], row(v)).then_inc(s_c, 16)
                else:
                    sp.dma_start(h[:, :], row(down_biases[1])).then_inc(s_c, 16)
                for m in range(PIECES):
                    if m >= Q:
                        sp.wait_ge(s_whi, m - Q + 1)
                        sp.wait_ge(s_wlo, m - Q + 1)
                        if modulated:
                            sp.wait_ge(s_bm, min(m - Q + 1, PIECES // 2))
                    if m < PIECES // 2:
                        c, q = m // Q, m % Q
                        src = W_up[c * P:(c + 1) * P, q * D:(q + 1) * D]
                    else:
                        n = m - PIECES // 2
                        src = W_down[n * P:(n + 1) * P, :]
                    sp.dma_start(xt[:, 1, m % Q, :], src).then_inc(s_raw[m % Q], 16)

                def again(g, q):
                    i = Q * g + q
                    sp.wait_ge(s_e, i)
                    sp.dma_start(xr[:, :], rows(x_in, i * P, P)).then_inc(s_xr, 16)

                def group(g, slot, first, last):
                    for q in range(Q):
                        if not first:
                            again(g - 1, q)

                if modulated:
                    in_groups(sp, group)
                if modulated:
                    for q in range(Q):
                        again(GROUPS - 1, q)

            @block.gpsimd
            def _(pool):
                pool.memset(ident[:, :], 0.0)
                pool.memset(neghalf[:, :], -0.5)
                pool.drain()
                pool.affine_select(out=ident[:, :], in_=ident[:, :], compare_op=ALU.not_equal, fill=1.0,
                                   base=0, pattern=[[-1, P]], channel_multiplier=1)
                pool.drain().then_inc(s_const, 1)

                def power(v, i):
                    pool.wait_ge(s_var[v], i + 1)
                    pool.tensor_tensor(rstd[v][:, :], mv[v][:, 1:2], neghalf[:, :], ALU.pow).then_inc(s_rstd[v], 1)

                def modulate(g, slot, q):
                    i = Q * g + q
                    pool.wait_ge(s_in, IN * (i + 1))
                    pool.tensor_tensor(y[:, :], y[:, :], so[:, :], ALU.mult)
                    pool.drain()
                    pool.tensor_tensor(y[:, :], y[:, :], sh[:, :], ALU.add)
                    pool.drain()
                    pool.tensor_tensor(xt[:, slot, q, :], xt[:, slot, q, :], y[:, :], ALU.add).then_inc(s_mod, 1)

                def bias(g, slot, q):
                    pool.wait_ge(s_h, Q * g + q + 1)
                    pool.tensor_tensor(xt[:, slot, q, :], xt[:, slot, q, :], b2[:, :], ALU.add).then_inc(s_b2, 1)

                def outer_sum(g, q):
                    i = Q * g + q
                    pool.wait_ge(s_n1, i + 1)
                    ek = e[:, q % 2, :]
                    pool.tensor_tensor(ek, ek, g_row[:, :], ALU.mult)
                    pool.drain()
                    pool.tensor_tensor(ek, ek, b_row[:, :], ALU.add)
                    pool.drain()
                    pool.wait_ge(s_xr, 16 * (i + 1))
                    pool.tensor_tensor(ek, ek, xr[:, :], ALU.add).then_inc(s_e, 1)

                pool.wait_ge(s_c, 16 * (6 if modulated else 3))
                if not modulated:
                    pool.wait_ge(s_b1, 1)
                for q in range(Q):
                    if modulated:
                        modulate(0, 0, q)
                        power("p", q)
                    bias(0, 0, q)

                def group(g, slot, first, last):
                    for n in range(HC):
                        pool.wait_ge(s_gh, HC * g + n + 1)
                        lo, hi = act_hl[:, n % 2, 1, :], act_hl[:, n % 2, 0, :]
                        pool.tensor_tensor(lo, g32[:, :], hi.bitcast(F32), ALU.subtract).then_inc(s_gl, 1)
                        q, phase = n // 3, n % 3
                        if not first:
                            if phase == 0 and q < Q:
                                power("e", Q * (g - 1) + q)
                            if phase == 1 and q < Q and modulated:
                                outer_sum(g - 1, q)
                            if phase == 2 and q < Q and modulated:
                                power("f", Q * (g - 1) + q)
                        if not last:
                            if phase == 2 and q < Q and modulated:
                                modulate(g + 1, 1 - slot, q)
                            if modulated and phase == 0 and 1 <= q <= Q:
                                power("p", Q * (g + 1) + q - 1)
                            if phase == 1 and q >= 1 and q <= Q:
                                bias(g + 1, 1 - slot, q - 1)

                in_groups(pool, group)
                for q in range(Q):
                    power("e", Q * (GROUPS - 1) + q)
                    if modulated:
                        power("f", Q * (GROUPS - 1) + q)

            @block.tensor
            def _(pe):
                pe.wait_ge(s_const, 1)
                def turn(g, slot, q):
                    i = Q * g + q
                    pe.wait_ge(s_h, i + 1)
                    if not (isinstance(i, int) and i < 2):
                        pe.wait_ge(s_hT, i - 1)
                    for c in range(DC):
                        last = pe.transpose(ps_t[:, q % 2, c * P:(c + 1) * P], h[:, c * P:(c + 1) * P], ident[:, :])
                    last.then_inc(s_tr, 1)

                def up(g, slot, n, first):
                    if n == 0:
                        pe.wait_ge(s_hT, Q * (g + 1))
                    if not (first and n < 2):
                        pe.wait_ge(s_g, HC * g + n - 1)
                    for c in range(DC):
                        w_hi, w_lo = (w1[:, x, c, n * P:(n + 1) * P] for x in range(2))
                        last = mm3(pe, ps_h[:, n % 2, :], w_hi, w_lo, hT[:, slot, 0, c, :], hT[:, slot, 1, c, :],
                                   start=(c == 0), stop=(c == DC - 1))
                    last.then_inc(s_m1, 1)

                def down(g, n, first):
                    pe.wait_ge(s_gl, HC * g + n + 1)
                    for q in range(Q):
                        if n == 0 and not first:
                            pe.wait_ge(s_add, Q * (g - 1) + q + 1)
                        a_hi, a_lo = (act_hl[:, n % 2, x, q * P:(q + 1) * P] for x in range(2))
                        last = mm3(pe, ps_o[:, q, :], a_hi, a_lo, w2[:, 0, n, :], w2[:, 1, n, :],
                                   start=(n == 0), stop=(n == HC - 1))
                        if n == HC - 1:
                            last.then_inc(s_o, 1)
                    if n == HC - 1:
                        pe.drain().then_inc(s_m2, 1)
                    else:
                        last.then_inc(s_m2, 1)

                if modulated:
                    pe.wait_ge(s_c, 16 * 6)
                    for m in range(PIECES // 2):
                        c, q = m // Q, m % Q
                        pe.wait_ge(s_raw[m % Q], 16 * (m // Q + 1))
                        for r in range(4):
                            n = 4 * q + r
                            last = pe.matmul(ps_o[:, 0, c * HC + n:c * HC + n + 1], xt[:, 1, m % Q, r * P:(r + 1) * P],
                                             bf[:, c:c + 1], start=True, stop=True)
                        last.then_inc(s_bm, 1)
                        if m % STEP == FIRST:
                            turn(0, 0, m // STEP)
                    pe.wait_ge(s_b1, 1)

                for q in range(Q // 2 if modulated else 0, Q):
                    turn(0, 0, q)
                pe.wait_ge(s_wlo, PIECES)
                up(0, 0, 0, True)

                def group(g, slot, first, last):
                    for n in range(HC):
                        if not last and n >= 5 and (n - 5) % 3 == 0:
                            turn(g + 1, 1 - slot, (n - 5) // 3)
                        if n < HC - 1:
                            up(g, slot, n + 1, first)
                        elif not last:
                            up(g + 1, 1 - slot, 0, False)
                        down(g, n, first)

                in_groups(pe, group)

            @block.scalar
            def _(act):
                act.wait_ge(s_c, 16 * (6 if modulated else 3))
                def load(g, slot, q):
                    i = Q * g + q
                    if modulated:
                        act.wait_ge(s_mod, i)
                        for t, v in ((y, y_in), (so, so_in), (sh, sh_in)):
                            act.dma_start(t[:, :], rows(v, i * P, P)).then_inc(s_in, 16)
                    else:
                        act.wait_ge(s_h, i)
                    act.dma_start(xt[:, slot, q, :], rows(x_in, i * P, P)).then_inc(s_in, 16)

                def hi(g, slot, q):
                    act.wait_ge(s_tr, Q * g + q + 1)
                    if not (isinstance(g, int) and g < 2):
                        act.wait_ge(s_m1, HC * (g - 1))
                    act.activation(hT[:, slot, 0, :, q * P:(q + 1) * P], ps_t[:, q % 2, :].rearrange("p (c t) -> p c t", c=DC),
                                   ACT.Copy).then_inc(s_hi, 1)

                def store(g, q):
                    i = Q * g + q
                    act.wait_ge(s_out, i + 1)
                    act.dma_start(rows(out, i * P, P), e[:, q % 2, :]).then_inc(s_st[q % 2], 16)

                load(0, 0, 0)
                for m in range(PIECES):
                    raw = xt[:, 1, m % Q, :]
                    act.wait_ge(s_raw[m % Q], 16 * (m // Q + 1))
                    if m < PIECES // 2:
                        c, q = m // Q, m % Q
                        act.activation(w1[:, 0, c, q * D:(q + 1) * D], raw, ACT.Identity,
                                       scale=gf[:, c:c + 1] if modulated else 1.0).then_inc(s_whi, 1)
                    else:
                        act.activation(w2[:, 0, m - PIECES // 2, :], raw, ACT.Copy).then_inc(s_whi, 1)
                    if m % STEP == FIRST:
                        q = m // STEP
                        hi(0, 0, q)
                        if q + 1 < Q:
                            load(0, 0, q + 1)

                def group(g, slot, first, last):
                    for n in range(HC):
                        act.wait_ge(s_m1, HC * g + n + 1)
                        act.wait_ge(s_gl, HC * g + n)
                        act.activation(g32[:, :], ps_h[:, n % 2, :], ACT.Gelu,
                                       bias=b1[:, n:n + 1]).then_inc(s_g, 1)
                        if not last and n % 3 == 1 and n // 3 < Q:
                            if not first:
                                act.wait_ge(s_n1, Q * (g - 1) + n // 3 + 1)
                            elif n == 1:
                                act.wait_ge(s_wlo, PIECES)
                            load(g + 1, 1 - slot, n // 3)
                        if not last and n >= 5 and (n - 5) % 3 == 0:
                            hi(g + 1, 1 - slot, (n - 5) // 3)
                        if not first and n >= 4 and (n - 4) % 3 == 0 and (n - 4) // 3 < Q:
                            store(g - 1, (n - 4) // 3)

                in_groups(act, group)
                for q in range(Q):
                    store(GROUPS - 1, q)
                for k in range(2):
                    act.wait_ge(s_st[k], 16 * TILES // 2)

            @block.vector
            def _(dve):
                dve.wait_ge(s_c, 16 * (6 if modulated else 3))
                if not modulated:
                    dve.tensor_tensor(b2[:, :], b2[:, :], h[:, :], ALU.add)
                    dve.drain().then_inc(s_b1, 1)

                def variance(v, x):
                    dve.bn_stats(stats[:, :], x)
                    dve.drain()
                    dve.bn_aggr(mv[v][:, :], stats[:, :])
                    dve.drain()
                    dve.tensor_scalar(mv[v][:, 1:2], mv[v][:, 1:2], EPS, None, ALU.add).then_inc(s_var[v], 1)

                def var_p(g, slot, q):
                    i = Q * g + q
                    dve.wait_ge(s_mod, i + 1)
                    variance("p", xt[:, slot, q, :])

                def norm_p(g, slot, q):
                    i = Q * g + q
                    dve.wait_ge(s_tr, i)
                    if modulated:
                        dve.wait_ge(s_rstd["p"], i + 1)
                        dve.tensor_scalar(h[:, :], xt[:, slot, q, :], mv["p"][:, 0:1], rstd["p"][:, 0:1],
                                          ALU.subtract, ALU.mult).then_inc(s_h, 1)
                    else:
                        dve.wait_ge(s_in, IN * (i + 1))
                        dve.tensor_copy(h[:, :], xt[:, slot, q, :]).then_inc(s_h, 1)

                def lo(g, slot, q):
                    dve.wait_ge(s_hi, Q * g + q + 1)
                    dve.tensor_tensor(hT[:, slot, 1, :, q * P:(q + 1) * P], ps_t[:, q % 2, :].rearrange("p (c t) -> p c t", c=DC),
                                      hT[:, slot, 0, :, q * P:(q + 1) * P].bitcast(F32), ALU.subtract).then_inc(s_hT, 1)

                def add(g, slot):
                    for q in range(Q):
                        dve.wait_ge(s_o, Q * g + q + 1)
                        dve.wait_ge(s_b2, Q * g + q + 1)
                        dve.tensor_tensor(xt[:, slot, q, :], ps_o[:, q, :], xt[:, slot, q, :], ALU.add).then_inc(s_add, 1)
                    dve.drain()

                def norm_e(g, slot, q):
                    i = Q * g + q
                    dve.wait_ge(s_rstd["e"], i + 1)
                    dve.wait_ge(s_st[q % 2], 16 * (2 * g + q // 2))
                    dve.tensor_scalar(e[:, q % 2, :], xt[:, slot, q, :], mv["e"][:, 0:1], rstd["e"][:, 0:1],
                                      ALU.subtract, ALU.mult).then_inc(s_n1, 1)

                def var_f(g, q):
                    dve.wait_ge(s_e, Q * g + q + 1)
                    variance("f", e[:, q % 2, :])

                def norm_f(g, q):
                    dve.wait_ge(s_rstd["f"], Q * g + q + 1)
                    dve.tensor_scalar(e[:, q % 2, :], e[:, q % 2, :], mv["f"][:, 0:1], rstd["f"][:, 0:1],
                                      ALU.subtract, ALU.mult).then_inc(s_n2, 1)

                for m in range(PIECES):
                    raw = xt[:, 1, m % Q, :]
                    dve.wait_ge(s_whi, m + 1)
                    if m < PIECES // 2 and modulated:
                        c, q = m // Q, m % Q
                        dve.scalar_tensor_tensor(out=w1[:, 1, c, q * D:(q + 1) * D], in0=raw, scalar=gf[:, c:c + 1],
                                                 in1=w1[:, 0, c, q * D:(q + 1) * D].bitcast(F32), op0=ALU.mult,
                                                 op1=ALU.subtract).then_inc(s_wlo, 1)
                    else:
                        if m < PIECES // 2:
                            c, q = m // Q, m % Q
                            w_hi, w_lo = (w1[:, x, c, q * D:(q + 1) * D] for x in range(2))
                        else:
                            w_hi, w_lo = (w2[:, x, m - PIECES // 2, :] for x in range(2))
                        dve.tensor_tensor(w_lo, raw, w_hi.bitcast(F32), ALU.subtract).then_inc(s_wlo, 1)
                    if m == PIECES // 2 - 1 and modulated:
                        dve.wait_ge(s_bm, PIECES // 2)
                        for c in range(DC):
                            dve.tensor_tensor(b1[:, :], b1[:, :], ps_o[:, 0, c * HC:(c + 1) * HC], ALU.add)
                            dve.drain()
                        dve.drain().then_inc(s_b1, 1)
                    if m % STEP == FIRST:
                        q = m // STEP
                        if modulated:
                            var_p(0, 0, q)
                        norm_p(0, 0, q)
                        lo(0, 0, q)

                def group(g, slot, first, last):
                    for n in range(HC):
                        q, phase = n // 3, n % 3
                        dve.wait_ge(s_g, HC * g + n + 1)
                        if not (first and n < 2):
                            dve.wait_ge(s_m2, HC * g + n - 1)
                        dve.tensor_copy(act_hl[:, n % 2, 0, :], g32[:, :]).then_inc(s_gh, 1)
                        if not first:
                            if n == 0:
                                add(g - 1, 1 - slot)
                            if phase == 0 and q < Q:
                                variance("e", xt[:, 1 - slot, q, :])
                            if phase == 1 and q < Q:
                                norm_e(g - 1, 1 - slot, q)
                            if modulated:
                                if phase == 2 and q < Q:
                                    var_f(g - 1, q)
                                if phase == 0 and 1 <= q <= Q:
                                    norm_f(g - 1, q - 1)
                        if not last:
                            if modulated and phase == 0 and 1 <= q <= Q:
                                var_p(g + 1, 1 - slot, q - 1)
                            if phase == 1 and q >= 1:
                                norm_p(g + 1, 1 - slot, q - 1)
                            if phase == 2 and q >= 1:
                                lo(g + 1, 1 - slot, q - 1)

                in_groups(dve, group)
                add(GROUPS - 1, (GROUPS - 1) % 2)
                for q in range(Q):
                    i = Q * (GROUPS - 1) + q
                    variance("e", xt[:, (GROUPS - 1) % 2, q, :])
                    norm_e(GROUPS - 1, (GROUPS - 1) % 2, q)
                    if modulated:
                        dve.drain()
                        ek = e[:, q % 2, :]
                        dve.tensor_tensor(ek, ek, g_row[:, :], ALU.mult)
                        dve.drain()
                        dve.tensor_tensor(ek, ek, b_row[:, :], ALU.add)
                        dve.drain()
                        dve.wait_ge(s_xr, 16 * (i + 1))
                        dve.tensor_tensor(ek, ek, xr[:, :], ALU.add)
                        dve.drain().then_inc(s_e, 1)
                        variance("f", ek)
                        norm_f(GROUPS - 1, q)
        st.clear()



def decoder_layer(nc, A, out):
    T = B * S

    def scratch(name, shape):
        return nc.dram_tensor(name, shape, F32, kind="Internal").ap()

    tap_rows, taps = scratch("tap_rows", [D, S]), scratch("taps", [S, D])
    w3, b3, w4 = scratch("w3", [D, HID]), scratch("b3", [HID]), scratch("w4", [HID, D])
    x1, qt = scratch("x1", [T, D]), scratch("qt", [2, P, T])
    kt, ac = scratch("kt", [2, P, B * S2]), scratch("ac", [T, DV])
    xin, so, sh = (scratch(n, [T, D]) for n in ("xin", "so", "sh"))
    spectrum, conv = scratch("spectrum", [B, 2 * DC, 2, P, D]), scratch("conv", [T, D])
    x2 = scratch("x2", [T, D])

    stage_taps(nc, A, tap_rows, taps)
    stage_butterfly(nc, A, w3, b3, w4)
    stage_attention(nc, A, x1, qt)
    stage_keys(nc, A, kt)
    stage_cross(nc, A, qt, kt, ac)
    stage_film(nc, A, x1, ac, xin, so, sh)
    stage_dft(nc, A, xin, taps, spectrum)
    stage_idft(nc, A, spectrum, conv)
    X = "L0_xattn_"
    stage_mlp(nc, "m1", True, A[X + "W1"], A[X + "b1"], A[X + "W2"], [A[X + "b2"]], x1, x2,
              g_ffn=A[X + "g_ffn"], b_ffn=A[X + "b_ffn"], g_out=A[X + "g_norm_out"], b_out=A[X + "b_norm_out"],
              y_in=conv, so_in=so, sh_in=sh)
    stage_mlp(nc, "m2", False, w3, b3, w4, [A["L0_ffn_b_con"], A["L0_ffn_down_bias"]], x2,
              out.rearrange("b s d -> (b s) d"))


def kernel(**inputs):
    import concourse.bacc as bacc
    from concourse.bass_utils import run_bass_kernel_spmd

    nc = bacc.Bacc("TRN2", target_bir_lowering=False, num_devices=1)
    given = {k: np.ascontiguousarray(v) for k, v in inputs.items()}
    given["L0_xattn_mod_gate"] = given["L0_xattn_mod_gate"].reshape(1)
    for name in ("mask_BxS_bf1", "mask_BxS2_bf1"):
        given[name] = given[name].view(np.uint8)
    given.update(conv_constants())
    arrays, aps = {}, {}
    for name, a in given.items():
        arrays[f"in_{name}_dram"] = a
        aps[name] = nc.dram_tensor(f"in_{name}_dram", a.shape, mybir.dt.from_np(a.dtype), kind="ExternalInput").ap()
    out = nc.dram_tensor("out_0_dram", (B, S, D), F32, kind="ExternalOutput").ap()
    decoder_layer(nc, aps, out)
    result = run_bass_kernel_spmd(nc, [arrays], core_ids=[0])
    return result.results[0]["out_0_dram"]
```
